# Optimizing a Trainium2 kernel written in Bass

```python
import numpy as np
import jax
import jax.numpy as jnp

def _softmax(x, axis=-1):
    return jax.nn.softmax(x, axis=axis)

def _gelu(x):
    return jax.nn.gelu(x, approximate=True)

def _silu(x):
    return jax.nn.silu(x)

def _sigmoid(x):
    return jax.nn.sigmoid(x)

def _layernorm(x, axis=-1, eps=1e-05):
    m = jnp.mean(x, axis=axis, keepdims=True)
    v = jnp.var(x, axis=axis, keepdims=True)
    return (x - m) / jnp.sqrt(v + eps)

def _scatter_add(tgt, idx, src, axis=0):
    return tgt.at[idx].add(src)

def _segment_sum(src, seg, n):
    return jax.ops.segment_sum(src, seg, n)
kernel_name = 'mk_adaln_d2_jaxref_r4_612406'

def setup_inputs(seed: int=0):
    np.random.seed(seed)
    _w = jnp.asarray

    def _L0_attn_setup():
        import jax, jax.numpy as jnp
        import numpy as np
        B, N, D_IN, D_OUT = (4, 512, 256, 256)
        key = jax.random.key(seed)
        ks = jax.random.split(key, 7)
        s_in = 1.0 / np.sqrt(D_IN)
        return {'X': jax.random.normal(ks[0], (B, N, D_IN), dtype=jnp.float32), 'Wq': jax.random.uniform(ks[1], (D_IN, D_OUT), jnp.float32, -s_in, s_in), 'bq': jax.random.uniform(ks[2], (D_OUT,), jnp.float32, -s_in, s_in), 'Wk': jax.random.uniform(ks[3], (D_IN, D_OUT), jnp.float32, -s_in, s_in), 'bk': jax.random.uniform(ks[4], (D_OUT,), jnp.float32, -s_in, s_in), 'Wv': jax.random.uniform(ks[5], (D_IN, D_OUT), jnp.float32, -s_in, s_in), 'bv': jax.random.uniform(ks[6], (D_OUT,), jnp.float32, -s_in, s_in)}
    _L0_attn_in = _L0_attn_setup()

    def _L0_ffn_setup():
        import jax, jax.numpy as jnp
        import numpy as np
        DIM = 256
        DEPTH = 2
        HEADS = 8
        DIM_HEAD = 64
        WINDOW = 128
        INNER = HEADS * DIM_HEAD
        HID = int(DIM * 4 * 2 / 3)
        B, N = (2, 2048)
        QK_SCALE = 8.0

        def shift_token(t):
            t1, t2 = jnp.split(t, 2, axis=-1)
            t2 = jnp.pad(t2, ((0, 0), (1, 0), (0, 0)))[:, :-1]
            return jnp.concatenate([t1, t2], axis=-1)

        def l2norm(t):
            return t / jnp.clip(jnp.linalg.norm(t, axis=-1, keepdims=True), 1e-12)

        def rotate_half(x):
            x1, x2 = jnp.split(x, 2, axis=-1)
            return jnp.concatenate([-x2, x1], axis=-1)

        def rotary_xpos(q, k):
            n = q.shape[-2]
            half_idx = jnp.arange(0, DIM_HEAD, 2, dtype=jnp.float32)
            inv_freq = 1.0 / 10000.0 ** (half_idx / DIM_HEAD)
            t = jnp.arange(n, dtype=jnp.float32)
            freqs = t[:, None] * inv_freq[None, :]
            freqs = jnp.concatenate([freqs, freqs], axis=-1)
            base = (half_idx + 0.4 * DIM_HEAD) / (1.4 * DIM_HEAD)
            power = (t - n // 2) / float(WINDOW // 2)
            scale = base[None, :] ** power[:, None]
            scale = jnp.concatenate([scale, scale], axis=-1)
            cos, sin = (jnp.cos(freqs), jnp.sin(freqs))
            q = q * cos * scale + rotate_half(q) * sin * scale
            k = k * cos / scale + rotate_half(k) * sin / scale
            return (q, k)

        def local_attention(q, k, v):
            b, h, n, d = q.shape
            w = n // WINDOW
            bq = q.reshape(b, h, w, WINDOW, d) * QK_SCALE
            bk = k.reshape(b, h, w, WINDOW, d)
            bv = v.reshape(b, h, w, WINDOW, d)

            def look_around(t):
                p = jnp.pad(t, ((0, 0), (0, 0), (1, 0), (0, 0), (0, 0)))
                return jnp.concatenate([p[:, :, :w], p[:, :, 1:]], axis=3)
            bk, bv = (look_around(bk), look_around(bv))
            bt = jnp.arange(n).reshape(w, WINDOW)
            btp = jnp.pad(bt, ((1, 0), (0, 0)), constant_values=-1)
            btk = jnp.concatenate([btp[:w], btp[1:]], axis=1)
            sim = jnp.einsum('bhwid,bhwjd->bhwij', bq, bk)
            i = bt[:, :, None]
            j = btk[:, None, :]
            mask = (i < j) | (i > j + WINDOW) | (j == -1)
            sim = jnp.where(mask, -jnp.finfo(sim.dtype).max, sim)
            attn = jax.nn.softmax(sim, axis=-1)
            out = jnp.einsum('bhwij,bhwjd->bhwid', attn, bv)
            return out.reshape(b, h, n, d)

        def _layer(x, wqkv, qs, ksc, wo, lg, lb, w1, b1, w2, b2):
            b, n, _ = x.shape
            h = shift_token(x)
            qkv = h @ wqkv
            q, k, v = jnp.split(qkv, 3, axis=-1)
            to_heads = lambda t: t.reshape(b, n, HEADS, DIM_HEAD).transpose(0, 2, 1, 3)
            q, k, v = (to_heads(q), to_heads(k), to_heads(v))
            q = l2norm(q) * qs
            k = l2norm(k) * ksc
            q, k = rotary_xpos(q, k)
            o = local_attention(q, k, v)
            o = o.transpose(0, 2, 1, 3).reshape(b, n, INNER)
            x = x + o @ wo
            h = shift_token(x)
            mu = h.mean(-1, keepdims=True)
            var = h.var(-1, keepdims=True)
            h = (h - mu) / jnp.sqrt(var + 1e-05) * lg + lb
            h = h @ w1 + b1
            a, g = jnp.split(h, 2, axis=-1)
            h = a * jax.nn.gelu(g, approximate=False)
            x = x + h @ w2 + b2
            return x
        key = jax.random.key(seed)
        ks = jax.random.split(key, 6)
        return {'x': jax.random.normal(ks[0], (B, N, DIM), jnp.float32), 'wqkv': jax.random.normal(ks[1], (DEPTH, DIM, 3 * INNER), jnp.float32) * 0.02, 'q_scale': jnp.ones((DEPTH, DIM_HEAD), jnp.float32), 'k_scale': jnp.ones((DEPTH, DIM_HEAD), jnp.float32), 'wo': jax.random.normal(ks[2], (DEPTH, INNER, DIM), jnp.float32) * 0.02, 'ln_g': jnp.ones((DEPTH, DIM), jnp.float32), 'ln_b': jnp.zeros((DEPTH, DIM), jnp.float32), 'w1': jax.random.normal(ks[3], (DEPTH, DIM, 2 * HID), jnp.float32) * 0.02, 'b1': jnp.zeros((DEPTH, 2 * HID), jnp.float32), 'w2': jax.random.normal(ks[4], (DEPTH, HID, DIM), jnp.float32) * 0.02, 'b2': jnp.zeros((DEPTH, DIM), jnp.float32)}
    _L0_ffn_in = _L0_ffn_setup()
    _L0_c = _w((lambda *s: np.random.randn(*s).astype(np.float32) * 0.05)(1, 256))
    _L0_wmod = _w((lambda *s: np.random.randn(*s).astype(np.float32) * 0.05)(256, 6 * 256) * 256 ** (-0.5))

    def _L1_attn_setup():
        import jax, jax.numpy as jnp
        import numpy as np
        NUM_HEADS = 16
        THETA = 10000.0

        def _rope(x, theta):
            S, d_k = (x.shape[1], x.shape[-1])
            k = jnp.arange(d_k // 2, dtype=jnp.float32)
            inv_freq = theta ** (-2.0 * k / d_k)
            ang = jnp.arange(S, dtype=jnp.float32)[:, None] * inv_freq
            cos = jnp.cos(ang)[None, :, None, :]
            sin = jnp.sin(ang)[None, :, None, :]
            x_even = x[..., 0::2]
            x_odd = x[..., 1::2]
            y_even = cos * x_even - sin * x_odd
            y_odd = sin * x_even + cos * x_odd
            y = jnp.stack([y_even, y_odd], axis=-1)
            return y.reshape(x.shape)
        key = jax.random.key(seed)
        ks = jax.random.split(key, 5)
        B, S, D = (2, 512, 256)
        std = 1.0 / np.sqrt(D)
        return {'in_features': jax.random.normal(ks[0], (B, S, D), dtype=jnp.float32), 'W_Q': jax.random.normal(ks[1], (D, D), dtype=jnp.float32) * std, 'W_K': jax.random.normal(ks[2], (D, D), dtype=jnp.float32) * std, 'W_V': jax.random.normal(ks[3], (D, D), dtype=jnp.float32) * std, 'W_O': jax.random.normal(ks[4], (D, D), dtype=jnp.float32) * std}
    _L1_attn_in = _L1_attn_setup()

    def _L1_ffn_setup():
        import jax, jax.numpy as jnp
        import numpy as np
        N, T, D = (4, 1024, 256)
        NUM_EXPERTS = 8
        EXPERT_CAP = 2.0
        MLP_RATIO = 4
        HIDDEN = MLP_RATIO * D
        key = jax.random.key(seed)
        k1, k2, k3, k4 = jax.random.split(key, 4)
        x = jax.random.normal(k1, (N, T, D), dtype=jnp.float32)
        gate_w = jax.random.truncated_normal(k2, -2.0, 2.0, (D, NUM_EXPERTS), dtype=jnp.float32) * 0.02
        w1 = jax.random.normal(k3, (NUM_EXPERTS, D, HIDDEN), dtype=jnp.float32) * 0.02
        w2 = jax.random.normal(k4, (NUM_EXPERTS, HIDDEN, D), dtype=jnp.float32) * 0.02
        return {'x': x, 'gate_w': gate_w, 'w1': w1, 'w2': w2}
    _L1_ffn_in = _L1_ffn_setup()
    _L1_c = _w((lambda *s: np.random.randn(*s).astype(np.float32) * 0.05)(1, 256))
    _L1_wmod = _w((lambda *s: np.random.randn(*s).astype(np.float32) * 0.05)(256, 6 * 256) * 256 ** (-0.5))
    _d = {'L0_attn_X': _L0_attn_in['X'], 'L0_attn_Wq': _L0_attn_in['Wq'], 'L0_attn_bq': _L0_attn_in['bq'], 'L0_attn_Wk': _L0_attn_in['Wk'], 'L0_attn_bk': _L0_attn_in['bk'], 'L0_attn_Wv': _L0_attn_in['Wv'], 'L0_attn_bv': _L0_attn_in['bv'], 'L0_ffn_wqkv': _L0_ffn_in['wqkv'], 'L0_ffn_q_scale': _L0_ffn_in['q_scale'], 'L0_ffn_k_scale': _L0_ffn_in['k_scale'], 'L0_ffn_wo': _L0_ffn_in['wo'], 'L0_ffn_ln_g': _L0_ffn_in['ln_g'], 'L0_ffn_ln_b': _L0_ffn_in['ln_b'], 'L0_ffn_w1': _L0_ffn_in['w1'], 'L0_ffn_b1': _L0_ffn_in['b1'], 'L0_ffn_w2': _L0_ffn_in['w2'], 'L0_ffn_b2': _L0_ffn_in['b2'], 'L0_c': _L0_c, 'L0_wmod': _L0_wmod, 'L1_attn_W_Q': _L1_attn_in['W_Q'], 'L1_attn_W_K': _L1_attn_in['W_K'], 'L1_attn_W_V': _L1_attn_in['W_V'], 'L1_attn_W_O': _L1_attn_in['W_O'], 'L1_ffn_gate_w': _L1_ffn_in['gate_w'], 'L1_ffn_w1': _L1_ffn_in['w1'], 'L1_ffn_w2': _L1_ffn_in['w2'], 'L1_c': _L1_c, 'L1_wmod': _L1_wmod}
    _x0 = _d['L0_attn_X']
    _d['L0_attn_X'] = jax.random.normal(jax.random.fold_in(jax.random.key(seed), 1), (1, 4096, 256), dtype=_x0.dtype)
    del _x0
    return _d

def reference(L0_attn_X, L0_attn_Wq, L0_attn_bq, L0_attn_Wk, L0_attn_bk, L0_attn_Wv, L0_attn_bv, L0_ffn_wqkv, L0_ffn_q_scale, L0_ffn_k_scale, L0_ffn_wo, L0_ffn_ln_g, L0_ffn_ln_b, L0_ffn_w1, L0_ffn_b1, L0_ffn_w2, L0_ffn_b2, L0_c, L0_wmod, L1_attn_W_Q, L1_attn_W_K, L1_attn_W_V, L1_attn_W_O, L1_ffn_gate_w, L1_ffn_w1, L1_ffn_w2, L1_c, L1_wmod):

    def _L0_attn_ref(X, Wq, bq, Wk, bk, Wv, bv):
        import jax, jax.numpy as jnp
        import numpy as np
        B, N, D_IN, D_OUT = (4, 512, 256, 256)
        q = jnp.einsum('bnd,de->bne', X, Wq) + bq
        k = jnp.einsum('bnd,de->bne', X, Wk) + bk
        v = jnp.einsum('bnd,de->bne', X, Wv) + bv
        scores = jnp.einsum('bne,bme->bnm', q, k)
        weights = jax.nn.softmax(scores, axis=-1)
        return jnp.einsum('bnm,bme->bne', weights, v)

    def _L0_ffn_ref(x, wqkv, q_scale, k_scale, wo, ln_g, ln_b, w1, b1, w2, b2):
        import jax, jax.numpy as jnp
        import numpy as np
        DIM = 256
        DEPTH = 2
        HEADS = 8
        DIM_HEAD = 64
        WINDOW = 128
        INNER = HEADS * DIM_HEAD
        HID = int(DIM * 4 * 2 / 3)
        B, N = (2, 2048)
        QK_SCALE = 8.0

        def shift_token(t):
            t1, t2 = jnp.split(t, 2, axis=-1)
            t2 = jnp.pad(t2, ((0, 0), (1, 0), (0, 0)))[:, :-1]
            return jnp.concatenate([t1, t2], axis=-1)

        def l2norm(t):
            return t / jnp.clip(jnp.linalg.norm(t, axis=-1, keepdims=True), 1e-12)

        def rotate_half(x):
            x1, x2 = jnp.split(x, 2, axis=-1)
            return jnp.concatenate([-x2, x1], axis=-1)

        def rotary_xpos(q, k):
            n = q.shape[-2]
            half_idx = jnp.arange(0, DIM_HEAD, 2, dtype=jnp.float32)
            inv_freq = 1.0 / 10000.0 ** (half_idx / DIM_HEAD)
            t = jnp.arange(n, dtype=jnp.float32)
            freqs = t[:, None] * inv_freq[None, :]
            freqs = jnp.concatenate([freqs, freqs], axis=-1)
            base = (half_idx + 0.4 * DIM_HEAD) / (1.4 * DIM_HEAD)
            power = (t - n // 2) / float(WINDOW // 2)
            scale = base[None, :] ** power[:, None]
            scale = jnp.concatenate([scale, scale], axis=-1)
            cos, sin = (jnp.cos(freqs), jnp.sin(freqs))
            q = q * cos * scale + rotate_half(q) * sin * scale
            k = k * cos / scale + rotate_half(k) * sin / scale
            return (q, k)

        def local_attention(q, k, v):
            b, h, n, d = q.shape
            w = n // WINDOW
            bq = q.reshape(b, h, w, WINDOW, d) * QK_SCALE
            bk = k.reshape(b, h, w, WINDOW, d)
            bv = v.reshape(b, h, w, WINDOW, d)

            def look_around(t):
                p = jnp.pad(t, ((0, 0), (0, 0), (1, 0), (0, 0), (0, 0)))
                return jnp.concatenate([p[:, :, :w], p[:, :, 1:]], axis=3)
            bk, bv = (look_around(bk), look_around(bv))
            bt = jnp.arange(n).reshape(w, WINDOW)
            btp = jnp.pad(bt, ((1, 0), (0, 0)), constant_values=-1)
            btk = jnp.concatenate([btp[:w], btp[1:]], axis=1)
            sim = jnp.einsum('bhwid,bhwjd->bhwij', bq, bk)
            i = bt[:, :, None]
            j = btk[:, None, :]
            mask = (i < j) | (i > j + WINDOW) | (j == -1)
            sim = jnp.where(mask, -jnp.finfo(sim.dtype).max, sim)
            attn = jax.nn.softmax(sim, axis=-1)
            out = jnp.einsum('bhwij,bhwjd->bhwid', attn, bv)
            return out.reshape(b, h, n, d)

        def _layer(x, wqkv, qs, ksc, wo, lg, lb, w1, b1, w2, b2):
            b, n, _ = x.shape
            h = shift_token(x)
            qkv = h @ wqkv
            q, k, v = jnp.split(qkv, 3, axis=-1)
            to_heads = lambda t: t.reshape(b, n, HEADS, DIM_HEAD).transpose(0, 2, 1, 3)
            q, k, v = (to_heads(q), to_heads(k), to_heads(v))
            q = l2norm(q) * qs
            k = l2norm(k) * ksc
            q, k = rotary_xpos(q, k)
            o = local_attention(q, k, v)
            o = o.transpose(0, 2, 1, 3).reshape(b, n, INNER)
            x = x + o @ wo
            h = shift_token(x)
            mu = h.mean(-1, keepdims=True)
            var = h.var(-1, keepdims=True)
            h = (h - mu) / jnp.sqrt(var + 1e-05) * lg + lb
            h = h @ w1 + b1
            a, g = jnp.split(h, 2, axis=-1)
            h = a * jax.nn.gelu(g, approximate=False)
            x = x + h @ w2 + b2
            return x
        for l in range(DEPTH):
            x = _layer(x, wqkv[l], q_scale[l], k_scale[l], wo[l], ln_g[l], ln_b[l], w1[l], b1[l], w2[l], b2[l])
        return x

    def _L1_attn_ref(in_features, W_Q, W_K, W_V, W_O):
        import jax, jax.numpy as jnp
        import numpy as np
        NUM_HEADS = 16
        THETA = 10000.0

        def _rope(x, theta):
            S, d_k = (x.shape[1], x.shape[-1])
            k = jnp.arange(d_k // 2, dtype=jnp.float32)
            inv_freq = theta ** (-2.0 * k / d_k)
            ang = jnp.arange(S, dtype=jnp.float32)[:, None] * inv_freq
            cos = jnp.cos(ang)[None, :, None, :]
            sin = jnp.sin(ang)[None, :, None, :]
            x_even = x[..., 0::2]
            x_odd = x[..., 1::2]
            y_even = cos * x_even - sin * x_odd
            y_odd = sin * x_even + cos * x_odd
            y = jnp.stack([y_even, y_odd], axis=-1)
            return y.reshape(x.shape)
        B, S, D = in_features.shape
        H = NUM_HEADS
        d_k = D // H
        scale = 1.0 / np.sqrt(np.float32(d_k))
        q = jnp.einsum('kd,bsd->bsk', W_Q, in_features).reshape(B, S, H, d_k)
        k = jnp.einsum('kd,bsd->bsk', W_K, in_features).reshape(B, S, H, d_k)
        v = jnp.einsum('vd,bsd->bsv', W_V, in_features).reshape(B, S, H, d_k)
        q = _rope(q, THETA)
        k = _rope(k, THETA)
        q = q.transpose(0, 2, 1, 3)
        k = k.transpose(0, 2, 1, 3)
        v = v.transpose(0, 2, 1, 3)
        scores = jnp.einsum('bhqd,bhkd->bhqk', q, k) * scale
        causal = jnp.tril(jnp.ones((S, S), dtype=bool))
        scores = jnp.where(causal[None, None], scores, -jnp.inf)
        attn = jax.nn.softmax(scores, axis=-1)
        out = jnp.einsum('bhqk,bhkd->bhqd', attn, v)
        out = out.transpose(0, 2, 1, 3).reshape(B, S, D)
        return jnp.einsum('dv,bsv->bsd', W_O, out)

    def _L1_ffn_ref(x, gate_w, w1, w2):
        import jax, jax.numpy as jnp
        import numpy as np
        N, T, D = (4, 1024, 256)
        NUM_EXPERTS = 8
        EXPERT_CAP = 2.0
        MLP_RATIO = 4
        HIDDEN = MLP_RATIO * D
        x = x.astype(jnp.float32)
        n, t, d = x.shape
        k = int(EXPERT_CAP * t / NUM_EXPERTS)
        scores = jnp.einsum('ntd,de->nte', x, gate_w)
        probs = jax.nn.softmax(scores, axis=-1)
        probs = jnp.transpose(probs, (0, 2, 1))
        g, m = jax.lax.top_k(probs, k)
        xin = jax.vmap(lambda xb, mb: xb[mb])(x, m)
        h = jax.nn.gelu(jnp.einsum('nekd,edf->nekf', xin, w1))
        h = jnp.einsum('nekf,efd->nekd', h, w2)
        weighted = g[..., None] * h
        flat_idx = (m + jnp.arange(n, dtype=m.dtype)[:, None, None] * t).reshape(-1)
        out = jnp.zeros((n * t, d), dtype=jnp.float32).at[flat_idx].add(weighted.reshape(-1, d))
        out = out.reshape(n, t, d)
        return out.astype(jnp.bfloat16)
    x = L0_attn_X
    mod = (_silu(L0_c) @ L0_wmod).reshape(L0_c.shape[0], 6, 1, -1)
    sa, ca, ga, sb, cb, gb = (mod[:, 0], mod[:, 1], mod[:, 2], mod[:, 3], mod[:, 4], mod[:, 5])
    ga = (2 * (ga >= 0) - 1) * jnp.maximum(jnp.abs(ga), 0.25)
    gb = (2 * (gb >= 0) - 1) * jnp.maximum(jnp.abs(gb), 0.25)
    h = _layernorm(x, axis=-1) * (1 + ca) + sa
    x = x + ga * _L0_attn_ref(h, L0_attn_Wq, L0_attn_bq, L0_attn_Wk, L0_attn_bk, L0_attn_Wv, L0_attn_bv)
    h = _layernorm(x, axis=-1) * (1 + cb) + sb
    x = x + gb * _L0_ffn_ref(h, L0_ffn_wqkv, L0_ffn_q_scale, L0_ffn_k_scale, L0_ffn_wo, L0_ffn_ln_g, L0_ffn_ln_b, L0_ffn_w1, L0_ffn_b1, L0_ffn_w2, L0_ffn_b2)
    mod = (_silu(L1_c) @ L1_wmod).reshape(L1_c.shape[0], 6, 1, -1)
    sa, ca, ga, sb, cb, gb = (mod[:, 0], mod[:, 1], mod[:, 2], mod[:, 3], mod[:, 4], mod[:, 5])
    ga = (2 * (ga >= 0) - 1) * jnp.maximum(jnp.abs(ga), 0.25)
    gb = (2 * (gb >= 0) - 1) * jnp.maximum(jnp.abs(gb), 0.25)
    h = _layernorm(x, axis=-1) * (1 + ca) + sa
    x = x + ga * _L1_attn_ref(h, L1_attn_W_Q, L1_attn_W_K, L1_attn_W_V, L1_attn_W_O)
    h = _layernorm(x, axis=-1) * (1 + cb) + sb
    x = x + gb * _L1_ffn_ref(h, L1_ffn_gate_w, L1_ffn_w1, L1_ffn_w2)
    return x

_drawn_inputs = setup_inputs


def setup_inputs(seed=0):
    import zlib

    import numpy as np

    out = dict(_drawn_inputs(seed))
    spreads = {'L0_ffn_q_scale': (1.0, 0.6),
     'L0_ffn_k_scale': (1.0, 0.6),
     'L0_ffn_ln_g': (1.0, 0.6),
     'L0_ffn_ln_b': (0.0, 0.8),
     'L0_ffn_b1': (0.0, 0.8),
     'L0_ffn_b2': (0.0, 0.416)}
    factors = {'L0_attn_bq': 3.993,
     'L0_attn_bk': 64.0,
     'L0_attn_bv': 6.138,
     'L0_ffn_wqkv': 7.673,
     'L0_ffn_wo': 7.462,
     'L0_ffn_w1': 4.808,
     'L0_ffn_w2': 4.791,
     'L1_attn_W_Q': 16.873,
     'L1_attn_W_K': 14.772,
     'L1_ffn_gate_w': 8.0,
     'L1_ffn_w1': 8.0,
     'L1_ffn_w2': 8.0,
     'L1_attn_W_V': 3.303,
     'L1_attn_W_O': 3.302}
    for name, (base, spread) in spreads.items():
        noise = np.random.default_rng([zlib.crc32(name.encode()), seed]).standard_normal(out[name].shape)
        drawn = base * np.exp(spread * noise) if base else spread * noise
        out[name] = jnp.asarray(drawn.astype(out[name].dtype))
    for name, factor in factors.items():
        out[name] = (out[name] * factor).astype(out[name].dtype)
    return out
```

```python
from contextlib import ExitStack, contextmanager

import numpy as np

import concourse.bass as bass
from concourse import mybir

F32 = mybir.dt.float32
F16 = mybir.dt.float16
BF16 = mybir.dt.bfloat16
I32 = mybir.dt.int32
U32 = mybir.dt.uint32
ACT = mybir.ActivationFunctionType
ALU = mybir.AluOpType
AX = mybir.AxisListType

P = 128
N = 4096
D = 256
KD = D // P
TILES = N // P
CHUNK = 512
TPC = CHUNK // P
CHUNKS = N // CHUNK
LN_EPS = 1e-5

DEPTH, HEADS, DH, WINDOW = 2, 8, 64, 128
INNER = HEADS * DH
HID = D * 4 * 2 // 3
QK_SCALE = 8.0
HALF = DH // 2
ROTARY_N = 4096

L1_HEADS, L1_DH = 16, 16
EXPERTS, TOPK, EHID = 8, 1024, 1024

CREDIT = 64


def need(eng, sem, n):
    eng.wait_ge(sem, n + CREDIT)


def credit(eng, *sems):
    for sem in sems:
        eng.sem_inc(sem, CREDIT)


class Memory:
    pass


@contextmanager
def stage(nc, name, *names):
    with ExitStack() as ctx:
        sems = [ctx.enter_context(nc.semaphore(f"{name}_{n}")) for n in names]
        with nc.Block() as block:
            yield block, dict(zip(names, sems))
        numbers = [sem.num for sem in sems]
        nc.all_engine_barrier(sems_to_clear=range(min(numbers), max(numbers) + 1))


def in_pairs(eng, count, step):
    with eng.Fori(0, count // 2) as k:
        step(k * 2, 0)
        step(k * 2 + 1, 1)


def ahead_in_pairs(eng, count, first, second):
    first(0, 0)
    with eng.Fori(0, count // 2 - 1) as k:
        first(k * 2 + 1, 1)
        second(k * 2, 0)
        first(k * 2 + 2, 0)
        second(k * 2 + 1, 1)
    first(count - 1, 1)
    second(count - 2, 0)
    second(count - 1, 1)



def modulation(nc, m, name, c, wmod):
    with ExitStack() as ctx:
        ccol = ctx.enter_context(nc.sbuf_tensor(f"{name}_ccol", [P, KD], F32))
        crep = ctx.enter_context(nc.sbuf_tensor(f"{name}_crep", [P, KD, P], F32))
        w = ctx.enter_context(nc.sbuf_tensor(f"{name}_wmod", [P, KD, 6 * D], F32))
        sign = ctx.enter_context(nc.sbuf_tensor(f"{name}_sign", [P, 2, D], F32))
        size = ctx.enter_context(nc.sbuf_tensor(f"{name}_size", [P, 2, D], F32))
        modb = m.modb[:, :, :].rearrange("p i d -> p (i d)")
        gates = m.modb[:, 2:6:3, :]
        with stage(nc, name, "c_in", "w_in", "silu", "rep", "col_mm", "row_mm", "col_ev", "row_ev", "dve") as (block, s):

            @block.sync
            def _(sp):
                sp.dma_start(ccol[:, :], c.rearrange("o (k p) -> p (o k)", p=P),
                             allow_slow_non_contiguous=True).then_inc(s["c_in"], 16)
                sp.dma_start(w[:, :, :], wmod.rearrange("(k p) e -> p k e", p=P)).then_inc(s["w_in"], 16)

            @block.scalar
            def _(act):
                act.wait_ge(s["c_in"], 16)
                act.activation(ccol[:, :], ccol[:, :], ACT.Silu).then_inc(s["silu"], 1)

            @block.tensor
            def _(pe):
                pe.wait_ge(s["w_in"], 16)
                pe.wait_ge(s["silu"], 1)
                for j in range(6 * KD):
                    for k in range(KD):
                        mm = pe.matmul(m.ps[:, 0, j:j + 1], w[:, k, j * P:(j + 1) * P], ccol[:, k:k + 1],
                                       start=(k == 0), stop=(k == KD - 1))
                mm.then_inc(s["col_mm"], 1)
                pe.wait_ge(s["rep"], 1)
                for j in range(3):
                    for k in range(KD):
                        mm = pe.matmul(m.ps[:, 1 + j, :], crep[:, k, :], w[:, k, j * 512:(j + 1) * 512],
                                       start=(k == 0), stop=(k == KD - 1))
                mm.then_inc(s["row_mm"], 1)

            @block.vector
            def _(dve):
                dve.wait_ge(s["silu"], 1)
                dve.tensor_copy(crep[:, :, :], ccol[:, :].unsqueeze(2).broadcast_to([P, KD, P])).then_inc(s["rep"], 1)
                dve.wait_ge(s["col_mm"], 1)
                dve.tensor_copy(m.modc[:, :], m.ps[:, 0, 0:6 * KD]).then_inc(s["col_ev"], 1)
                dve.wait_ge(s["row_mm"], 1)
                dve.tensor_copy(modb, m.ps[:, 1:4, :].rearrange("p b e -> p (b e)")).then_inc(s["row_ev"], 1)
                dve.wait_ge(s["col_ev"], 1)
                scales = m.modc[:, :].rearrange("p (i k) -> p i k", k=KD)[:, 1:6:3, :]
                dve.tensor_scalar(scales, scales, 1.0, None, ALU.add).then_inc(s["dve"], 1)
                dve.wait_ge(s["row_ev"], 1)
                rows = m.modb[:, 1:6:3, :]
                dve.tensor_scalar(rows, rows, 1.0, None, ALU.add).then_inc(s["dve"], 1)
                dve.tensor_scalar(sign[:, :, :], gates, 0.0, 2.0, ALU.is_ge, ALU.mult).then_inc(s["dve"], 1)
                dve.scalar_tensor_tensor(size[:, :, :], gates, -1.0, gates, ALU.mult, ALU.max).then_inc(s["dve"], 1)
                dve.wait_ge(s["dve"], 4)
                dve.tensor_scalar(size[:, :, :], size[:, :, :], 0.25, None, ALU.max).then_inc(s["dve"], 1)
                dve.wait_ge(s["dve"], 5)
                dve.scalar_tensor_tensor(gates, sign[:, :, :], -1.0, size[:, :, :], ALU.add, ALU.mult)



def norm_statistics(nc, m, name):
    with ExitStack() as ctx:
        six = ctx.enter_context(nc.sbuf_tensor(f"{name}_six", [P, TILES, 6], F32))
        half_gap = ctx.enter_context(nc.sbuf_tensor(f"{name}_half_gap", [P, TILES], F32))
        var = ctx.enter_context(nc.sbuf_tensor(f"{name}_var", [P, TILES], F32))
        with stage(nc, name, "six", "dve", "var", "rstd") as (block, s):

            @block.vector
            def _(dve):
                with dve.Fori(0, TILES // 4) as k:
                    for u in range(4):
                        t = bass.ts(k * 4 + u, 1)
                        dve.bn_stats(six[:, t, :], m.x[:, t, :]).then_inc(s["six"], 1)
                dve.wait_ge(s["six"], TILES)
                even, odd, sq_even, sq_odd = six[:, :, 1], six[:, :, 4], six[:, :, 2], six[:, :, 5]
                dve.tensor_tensor(half_gap[:, :], even, odd, ALU.subtract).then_inc(s["dve"], 1)
                dve.tensor_tensor(m.mean[:, :], even, odd, ALU.add).then_inc(s["dve"], 1)
                dve.tensor_tensor(var[:, :], sq_even, sq_odd, ALU.add).then_inc(s["dve"], 1)
                dve.wait_ge(s["dve"], 3)
                dve.tensor_scalar(m.mean[:, :], m.mean[:, :], 0.5, None, ALU.mult)
                dve.tensor_scalar(var[:, :], var[:, :], 1.0 / D, LN_EPS, ALU.mult, ALU.add).then_inc(s["dve"], 1)
                dve.scalar_tensor_tensor(half_gap[:, :], half_gap[:, :], 0.25, half_gap[:, :], ALU.mult, ALU.mult).then_inc(s["dve"], 1)
                dve.wait_ge(s["dve"], 5)
                dve.tensor_tensor(m.rstd[:, :], var[:, :], half_gap[:, :], ALU.add).then_inc(s["var"], 1)

            @block.gpsimd
            def _(pool):
                pool.wait_ge(s["var"], 1)
                pool.tensor_tensor(m.rstd[:, :], m.rstd[:, :], m.minus_half[:, 0:TILES], ALU.pow).then_inc(s["rstd"], 1)



def attention0_projections(nc, m, a):
    with ExitStack() as ctx:
        def sb(name, shape, dt=F32):
            return ctx.enter_context(nc.sbuf_tensor(f"a0_{name}", shape, dt))

        w = {n: sb(f"w{n}", [P, KD, D]) for n in "qkv"}
        bcol = {n: sb(f"b{n}", [P, KD]) for n in "qk"}
        bv = sb("bv", [P, D])
        normed = sb("normed", [P, 2, TPC, D])
        ht = sb("ht", [P, 2, KD, CHUNK])
        v = sb("v_whole", [P, 2, 2, D])
        with stage(nc, "a0", "w_in", "normed", "turned", "ht", "mm", "high", "ev", "v", "v_high", "v_low") as (block, s):

            @block.sync
            def _(sp):
                for n in "qkv":
                    sp.dma_start(w[n][:, :, :], a[f"W{n}"].rearrange("(k p) e -> p k e", p=P)).then_inc(s["w_in"], 16)
                for n in "qk":
                    sp.dma_start(bcol[n][:, :], a[f"b{n}"].rearrange("(k p) -> p k", p=P),
                                 allow_slow_non_contiguous=True).then_inc(s["w_in"], 16)
                sp.dma_start(bv[:, :], a["bv"].partition_broadcast(P)).then_inc(s["w_in"], 16)

            @block.vector
            def _(dve):
                credit(dve, s["normed"], s["ev"], s["v"])
                dve.wait_ge(s["w_in"], 16 * 6)

                def norm(c, u):
                    need(dve, s["turned"], KD * (c - 1))
                    for j in range(TPC):
                        t = c * TPC + j
                        n = dve.tensor_scalar(normed[:, u, j:j + 1, :], m.x[:, bass.ts(t, 1), :], m.mean[:, bass.ts(t, 1)],
                                              m.rstd[:, bass.ts(t, 1)], ALU.subtract, ALU.mult)
                    n.then_inc(s["normed"], 1)

                def outputs(c, u):
                    for n in range(2 * KD):
                        need(dve, s["high"], 2 * KD * c + n + 1)
                        to, b = (m.qt, bcol["q"]) if n < KD else (m.kt, bcol["k"])
                        dve.scalar_tensor_tensor(to[:, n % KD, 1, bass.ts(c, CHUNK)], m.ps[:, 2 + n, :], b[:, n % KD:n % KD + 1],
                                                 to[:, n % KD, 0, bass.ts(c, CHUNK)], ALU.add, ALU.subtract).then_inc(s["ev"], 1)
                    for b in range(2):
                        need(dve, s["mm"], 6 * c + 2 * KD + b + 1)
                        need(dve, s["v_low"], 2 * (c - 1) + b + 1)
                        dve.tensor_tensor(v[:, b, :, :], m.ps[:, 6 + b, :].rearrange("p (j e) -> p j e", e=D),
                                          bv[:, :].unsqueeze(1).broadcast_to([P, 2, D]), ALU.add).then_inc(s["v"], 1)

                ahead_in_pairs(dve, CHUNKS, norm, outputs)

            @block.scalar
            def _(act):
                credit(act, s["ht"], s["high"], s["v_high"])
                act.wait_ge(s["w_in"], 16 * 6)

                def high(c, u):
                    for n in range(2 * KD):
                        need(act, s["mm"], 6 * c + n + 1)
                        to, b = (m.qt, bcol["q"]) if n < KD else (m.kt, bcol["k"])
                        act.activation(to[:, n % KD, 0, bass.ts(c, CHUNK)], m.ps[:, 2 + n, :], ACT.Identity,
                                       bias=b[:, n % KD:n % KD + 1]).then_inc(s["high"], 1)
                    for b in range(2):
                        need(act, s["v"], 2 * c + b + 1)
                        act.copy(m.v[:, bass.ts(c * 2 + b, 2), 0, :], v[:, b, :, :]).then_inc(s["v_high"], 1)

                def scaled(c, u):
                    need(act, s["mm"], 6 * (c - 1))
                    for k in range(KD):
                        need(act, s["turned"], KD * c + k + 1)
                        act.activation(ht[:, u, k, :], m.ps[:, k, :], ACT.Identity, bias=m.modc[:, k:k + 1],
                                       scale=m.modc[:, KD + k:KD + k + 1]).then_inc(s["ht"], 1)

                ahead_in_pairs(act, CHUNKS, scaled, high)

            @block.gpsimd
            def _(pool):
                credit(pool, s["v_low"])

                def low(c, u):
                    for b in range(2):
                        need(pool, s["v_high"], 2 * c + b + 1)
                        pool.tensor_tensor(m.v[:, bass.ts(c * 2 + b, 2), 1, :], v[:, b, :, :], m.v[:, bass.ts(c * 2 + b, 2), 0, :],
                                           ALU.subtract).then_inc(s["v_low"], 1)

                in_pairs(pool, CHUNKS, low)

            @block.tensor
            def _(pe):
                credit(pe, s["turned"], s["mm"])
                pe.wait_ge(s["w_in"], 16 * 6)

                def turn(c, u):
                    need(pe, s["normed"], c + 1)
                    for k in range(KD):
                        need(pe, s["ht"], KD * (c - 1) + k + 1)
                        for j in range(TPC):
                            t = pe.transpose(m.ps[:, k, j * P:(j + 1) * P], normed[:, u, j, k * P:(k + 1) * P], m.ident[:, :])
                        t.then_inc(s["turned"], 1)

                def products(c, u):
                    need(pe, s["ht"], KD * (c + 1))
                    for n in range(2 * KD):
                        need(pe, s["ev"], 2 * KD * (c - 1) + n + 1)
                        o = n % KD
                        for k in range(KD):
                            mm = pe.matmul(m.ps[:, 2 + n, :], w["qk"[n // KD]][:, k, o * P:(o + 1) * P], ht[:, u, k, :],
                                           start=(k == 0), stop=(k == KD - 1))
                        mm.then_inc(s["mm"], 1)
                    for b in range(2):
                        need(pe, s["v"], 2 * (c - 1) + b + 1)
                        for j in range(2):
                            for k in range(KD):
                                mm = pe.matmul(m.ps[:, 6 + b, j * D:(j + 1) * D],
                                               ht[:, u, k, (2 * b + j) * P:(2 * b + j + 1) * P], w["v"][:, k, :],
                                               start=(k == 0), stop=(k == KD - 1))
                        mm.then_inc(s["mm"], 1)

                ahead_in_pairs(pe, CHUNKS, turn, products)


def attention0(nc, m):
    KC = N // CHUNK
    PIECES = 4
    PIECE = N // PIECES
    CPP = KC // PIECES
    with ExitStack() as ctx:
        def sb(name, shape, dt=F32):
            return ctx.enter_context(nc.sbuf_tensor(f"s0_{name}", shape, dt))

        scores = sb("scores", [P, 2, N])
        parts = sb("parts", [P, 2, N], F16)
        pt = sb("pt", [P, 2, 2, CHUNK], F16)
        top = sb("top", [P, 2, KC])
        minus_top = sb("minus_top", [P, 2])
        total = sb("total", [P, 2])
        rtotal = sb("rtotal", [P, 2])
        add = sb("add", [P, 2, D])
        with stage(nc, "s0", "mm", "copied", "max", "top", "exp", "high", "low", "turned", "pt_act", "pt_dve", "pv", "recip", "summed",
                   "gated", "x") as (block, s):

            def run(step, loop):
                with loop(0, TILES // 2 - 1) as k:
                    step(k * 2, 0)
                    step(k * 2 + 1, 1)
                step(TILES - 2, 0)
                step(TILES - 1, 1)

            def exists(i):
                return not isinstance(i, int) or i < TILES

            def turned_bank(c):
                return m.ps[:, 4 + c % 2, :].bitcast(F16)

            @block.gpsimd
            def _(pool):
                credit(pool, s["x"])

                def residual(i, u):
                    need(pool, s["gated"], i + 1)
                    x = m.x[:, bass.ts(i, 1), :]
                    pool.tensor_tensor(x, x, add[:, u:u + 1, :], ALU.add).then_inc(s["x"], 1)

                in_pairs(pool, TILES, residual)

            @block.tensor
            def _(pe):
                credit(pe, s["mm"], s["turned"], s["pv"])

                def score(i):
                    for c in range(KC):
                        need(pe, s["copied"], KC * i + c - 4 + 1)
                        keys = slice(c * CHUNK, (c + 1) * CHUNK)
                        terms = [(k, a, b) for k in range(KD) for a, b in ((0, 0), (0, 1), (1, 0))]
                        for n, (k, a, b) in enumerate(terms):
                            mm = pe.matmul(m.ps[:, c % 4, :], m.qt[:, k, a, bass.ts(i, P)], m.kt[:, k, b, keys],
                                           start=(n == 0), stop=(n == len(terms) - 1))
                        mm.then_inc(s["mm"], 1)

                def turn(i, c):
                    need(pe, s["low"], PIECES * i + c // CPP + 1)
                    if c % 2:
                        need(pe, s["pt_dve"], KC // 2 * i + c // 2)
                    else:
                        need(pe, s["pt_act"], KC // 2 * i + c // 2)
                    for part in range(2):
                        for j in range(TPC):
                            kt = c * TPC + j
                            t = pe.transpose(turned_bank(c)[:, (part * TPC + j) * P:(part * TPC + j + 1) * P],
                                             parts[:, part, kt * P:(kt + 1) * P], m.ident16[:, :])
                    t.then_inc(s["turned"], 1)

                def weigh(i, u):
                    turn(i, 0)
                    need(pe, s["summed"], 2 * (i - 1))
                    for c in range(KC):
                        if c + 1 < KC:
                            turn(i, c + 1)
                        need(pe, s["pt_dve" if c % 2 else "pt_act"], KC // 2 * i + c // 2 + 1)
                        for j in range(TPC):
                            kt = c * TPC + j
                            pe.matmul(m.ps[:, 6 + u, :], pt[:, c % 2, 0, j * P:(j + 1) * P], m.v[:, kt, :, :].rearrange("p i e -> p (i e)"),
                                      start=(kt == 0), stop=False, skip_group_check=True)
                            mm = pe.matmul(m.ps[:, 6 + u, 0:D], pt[:, c % 2, 1, j * P:(j + 1) * P], m.v[:, kt, 0, :],
                                           start=False, stop=(kt == TILES - 1), skip_group_check=True)
                        mm.then_inc(s["pv"], 1)

                def step(i, u):
                    if exists(i + 1):
                        score(i + 1)
                    weigh(i, u)

                score(0)
                run(step, pe.Fori)

            @block.vector
            def _(dve):
                credit(dve, s["copied"], s["max"], s["top"], s["low"], s["pt_dve"], s["recip"], s["summed"], s["gated"])

                def row_max(i, u, c):
                    need(dve, s["mm"], KC * i + c + 1)
                    dve.tensor_scalar(scores[:, u, c * CHUNK:(c + 1) * CHUNK], m.ps[:, c % 4, :], 1.0, None, ALU.mult, ALU.max,
                                      accum_out=top[:, u, c:c + 1]).then_inc(s["copied"], 1)

                def row_top(i, u):
                    need(dve, s["copied"], KC * (i + 1))
                    dve.tensor_reduce(minus_top[:, u:u + 1], top[:, u, :], AX.X, ALU.max, negate=True).then_inc(s["max"], 1)
                    need(dve, s["max"], i + 1)
                    dve.tensor_scalar(minus_top[:, u:u + 1], minus_top[:, u:u + 1], float(10 * np.log(2)), None, ALU.add).then_inc(s["top"], 1)

                def low(i, u, g):
                    need(dve, s["high"], PIECES * i + g + 1)
                    piece = slice(g * PIECE, (g + 1) * PIECE)
                    dve.tensor_tensor(parts[:, 1, piece], scores[:, u, piece], parts[:, 0, piece], ALU.subtract).then_inc(s["low"], 1)

                def step(i, u):
                    for c in range(KC):
                        if exists(i + 1):
                            row_max(i + 1, 1 - u, c)
                        if c >= KC - PIECES:
                            low(i, u, c - (KC - PIECES))
                    if exists(i + 1):
                        row_top(i + 1, 1 - u)
                    dve.reciprocal(rtotal[:, u:u + 1], total[:, u:u + 1]).then_inc(s["recip"], 1)
                    for c in range(1, KC, 2):
                        need(dve, s["turned"], KC * i + c + 1)
                        need(dve, s["pv"], KC * i + c - 2 + 1)
                        dve.tensor_copy(pt[:, c % 2, :, :].rearrange("p i k -> p (i k)"), turned_bank(c)).then_inc(s["pt_dve"], 1)
                    need(dve, s["recip"], i + 1)
                    need(dve, s["pv"], KC * (i + 1))
                    need(dve, s["x"], i - 1)
                    dve.tensor_copy(add[:, u, :], m.ps[:, 6 + u, D:2 * D]).then_inc(s["summed"], 1)
                    need(dve, s["summed"], 2 * i + 1)
                    dve.tensor_tensor(add[:, u, :], m.ps[:, 6 + u, 0:D], add[:, u, :], ALU.add).then_inc(s["summed"], 1)
                    need(dve, s["summed"], 2 * i + 2)
                    dve.scalar_tensor_tensor(add[:, u, :], add[:, u, :], rtotal[:, u:u + 1], m.modb[:, 2, :],
                                             ALU.mult, ALU.mult).then_inc(s["gated"], 1)

                for c in range(KC):
                    row_max(0, 0, c)
                row_top(0, 0)
                run(step, dve.Fori)

            @block.scalar
            def _(act):
                credit(act, s["exp"], s["high"], s["pt_act"])

                def step(i, u):
                    need(act, s["top"], i + 1)
                    need(act, s["recip"], i - 1)
                    act.activation(scores[:, u, :], scores[:, u, :], ACT.Exp, bias=minus_top[:, u:u + 1],
                                   accum_out=total[:, u:u + 1]).then_inc(s["exp"], 1)
                    need(act, s["exp"], i + 1)
                    need(act, s["turned"], KC * i)
                    for g in range(PIECES):
                        piece = slice(g * PIECE, (g + 1) * PIECE)
                        act.copy(parts[:, 0, piece], scores[:, u, piece]).then_inc(s["high"], 1)
                    for c in range(0, KC, 2):
                        need(act, s["turned"], KC * i + c + 1)
                        need(act, s["pv"], KC * i + c - 2 + 1)
                        act.copy(pt[:, c % 2, :, :].rearrange("p i k -> p (i k)"), turned_bank(c)).then_inc(s["pt_act"], 1)

                run(step, act.Fori)



def transformer_input(nc, m):
    with ExitStack() as ctx:
        normed = ctx.enter_context(nc.sbuf_tensor("y0_normed", [P, 2, TPC, D], F32))
        with stage(nc, "y0", "normed", "scaled", "y") as (block, s):

            @block.vector
            def _(dve):
                credit(dve, s["normed"])

                def norm(c, u):
                    need(dve, s["y"], c - 1)
                    for j in range(TPC):
                        t = bass.ts(c * TPC + j, 1)
                        n = dve.tensor_scalar(normed[:, u, j:j + 1, :], m.x[:, t, :], m.mean[:, t], m.rstd[:, t], ALU.subtract, ALU.mult)
                    n.then_inc(s["normed"], 1)

                in_pairs(dve, CHUNKS, norm)

            @block.gpsimd
            def _(pool):
                credit(pool, s["scaled"], s["y"])

                def shift_scale(c, u):
                    need(pool, s["normed"], c + 1)
                    pool.tensor_tensor(normed[:, u, :, :], normed[:, u, :, :], m.modb[:, 4:5, :].broadcast_to([P, TPC, D]),
                                       ALU.mult).then_inc(s["scaled"], 1)
                    need(pool, s["scaled"], c + 1)
                    pool.tensor_tensor(m.y[:, bass.ts(c, TPC), :], normed[:, u, :, :], m.modb[:, 3:4, :].broadcast_to([P, TPC, D]),
                                       ALU.add).then_inc(s["y"], 1)

                in_pairs(pool, CHUNKS, shift_scale)


def transformer_output(nc, m):
    with stage(nc, "y1", "gated", "x") as (block, s):

        @block.vector
        def _(dve):
            with dve.Fori(0, CHUNKS) as c:
                y = m.y[:, bass.ts(c, TPC), :]
                dve.tensor_tensor(y, y, m.modb[:, 5:6, :].broadcast_to([P, TPC, D]), ALU.mult).then_inc(s["gated"], 1)

        @block.gpsimd
        def _(pool):
            with pool.Fori(0, CHUNKS) as c:
                pool.wait_ge(s["gated"], c + 1)
                x = m.x[:, bass.ts(c, TPC), :]
                pool.tensor_tensor(x, x, m.y[:, bass.ts(c, TPC), :], ALU.add).then_inc(s["x"], 1)


def layer_of(weights, layer):
    return weights[bass.ts(layer, 1)]


def local_attention(nc, m, a, layer):
    QK = 2 * INNER
    PAIRS = HEADS // 2
    NEG = -1e30
    with ExitStack() as ctx:
        def sb(name, shape, dt=F32):
            return ctx.enter_context(nc.sbuf_tensor(f"la_{name}", shape, dt))

        wqkv = sb("wqkv", [P, KD, 3 * INNER])
        wo = sb("wo", [P, INNER // P, D])
        table = sb("table", [P, TILES, 4, HALF])
        gain = sb("gain", [P, 2, 2, HALF])
        gain_rot = sb("gain_rot", [P, 2, 2, HALF])
        mask = sb("mask", [P, 3, 2, P])
        y_now = sb("y_now", [P, 2, D])
        yt = sb("yt", [P, 2, KD, P + 4])
        cs = sb("cs", [P, 2, 2, 2 * DH])
        squares = sb("squares", [P, QK])
        straight = sb("straight", [P, 2, QK])
        crossed = sb("crossed", [P, QK])
        ss = sb("ss", [P, 2 * HEADS])
        rnorm = sb("rnorm", [P, 2 * HEADS])
        qscale = sb("qscale", [P, 2, HEADS])
        qz = sb("qz", [P, HEADS, P])
        kt = sb("kt", [P, PAIRS, 2, P])
        v = sb("v", [P, 2, INNER])
        scores = sb("scores", [P, HEADS, 2 * P])
        top = sb("top", [P, HEADS])
        bias = sb("bias", [P, HEADS])
        minus_qscale = sb("minus_qscale", [P, HEADS])
        total = sb("total", [P, HEADS])
        rtotal = sb("rtotal", [P, HEADS])
        pt = sb("pt", [P, PAIRS, 4, P])
        o = sb("o", [P, INNER])
        ot = sb("ot", [P, INNER // P, P])
        Q_BANK, K_BANK, V_BANK, TURN, SCORE, PTURN, OUT = 0, 1, 2, 3, 4, 6, 7

        def run(step, loop):
            for i in range(-3, 2):
                step(i, i % 2)
            with loop(1, TILES // 2 - 2) as k:
                step(k * 2, 0)
                step(k * 2 + 1, 1)
            for i in range(TILES - 4, TILES + 1):
                step(i, i % 2)

        def exists(w):
            return not isinstance(w, int) or 0 <= w < TILES

        with stage(nc, "la", "w_in", "consts", "const_step", "y_now", "y_t", "yt", "qk_mm", "v_mm", "cs", "rot", "squares", "summed", "ss", "rnorm", "crossed",
                   "qk", "qk_t", "qk_ev", "v", "score", "masked", "bias", "exp", "p_t", "p_act", "p_dve", "pv", "recip",
                   "o", "o_t", "ot", "proj", "y") as (block, s):

            @block.sync
            def _(sp):
                sp.dma_start(wqkv[:, :, :], layer_of(a["wqkv"], layer).rearrange("o (k p) e -> p (o k) e", p=P)).then_inc(s["w_in"], 16)
                sp.dma_start(wo[:, :, :], layer_of(a["wo"], layer).rearrange("o (k p) e -> p (o k) e", p=P)).then_inc(s["w_in"], 16)
                sp.dma_start(table[:, :, :, :], a["rotary"].rearrange("(t p) i d -> p t i d", p=P)).then_inc(s["w_in"], 16)
                for n, name in enumerate(("q_scale", "k_scale")):
                    src = layer_of(a[name], layer).rearrange("o d -> (o d)")
                    sp.dma_start(gain[:, n, :, :].rearrange("p h d -> p (h d)"), src.partition_broadcast(P)).then_inc(s["w_in"], 16)

            @block.gpsimd
            def _(pool):
                credit(pool, s["y_now"], s["cs"], s["rnorm"], s["crossed"], s["qk"])
                pool.memset(mask[:, :, :, :], 0.0)
                pool.memset(yt[:, :, :, :], 0.0)
                pool.memset(qz[:, :, :], 0.0)
                pool.memset(kt[:, :, :, :], 0.0)
                pool.memset(v[:, :, :], 0.0).then_inc(s["const_step"], 1)
                pool.wait_ge(s["const_step"], 1)
                for own in (mask[:, 0, 0, :], mask[:, 1, 1, :], mask[:, 2, 0, :]):
                    pool.affine_select(own, own, pattern=[[-1, P]], compare_op=ALU.is_ge, fill=NEG, base=0, channel_multiplier=1)
                for before in (mask[:, 0, 1, :], mask[:, 1, 0, :]):
                    pool.affine_select(before, before, pattern=[[1, P]], compare_op=ALU.is_ge, fill=NEG, base=0, channel_multiplier=-1)
                pool.memset(mask[:, 2, 1, :], NEG)
                pool.wait_ge(s["w_in"], 16 * 5)
                pool.tensor_scalar(gain_rot[:, :, 0, :], gain[:, :, 1, :], -1.0, None, ALU.mult)
                pool.tensor_copy(gain_rot[:, :, 1, :], gain[:, :, 0, :]).then_inc(s["consts"], 1)
                pool.wait_ge(s["consts"], 1)

                def load_y(w, u):
                    need(pool, s["y_t"], w - 1)
                    pool.tensor_copy(y_now[:, u:u + 1, :], m.y[:, bass.ts(w, 1), :]).then_inc(s["y_now"], 1)

                def tables(w, u):
                    need(pool, s["rot"], w - 1)
                    for n, g in ((0, gain), (1, gain_rot)):
                        t = pool.tensor_tensor(cs[:, u, n, :].rearrange("p (q h d) -> p q h d", q=2, h=2),
                                               table[:, bass.ts(w, 1), 2 * n:2 * n + 2, :].rearrange("p o q d -> p (o q) d")
                                               .unsqueeze(2).broadcast_to([P, 2, 2, HALF]), g[:, :, :, :], ALU.mult)
                    t.then_inc(s["cs"], 1)

                def normalise(w, u):
                    need(pool, s["rot"], w + 1)
                    pool.tensor_tensor(straight[:, u, :], straight[:, u, :], crossed[:, :], ALU.add).then_inc(s["crossed"], 1)
                    need(pool, s["ss"], w + 1)
                    pool.tensor_tensor(rnorm[:, :], ss[:, :], m.minus_half[:, 0:2 * HEADS], ALU.pow).then_inc(s["rnorm"], 1)
                    need(pool, s["rnorm"], w + 1)
                    need(pool, s["crossed"], w + 1)
                    need(pool, s["exp"], PAIRS * (w - 1))
                    kk = straight[:, u, INNER:QK].rearrange("p (h d) -> p h d", d=DH)
                    pool.tensor_tensor(kk, kk, rnorm[:, HEADS:2 * HEADS].unsqueeze(2).broadcast_to([P, HEADS, DH]), ALU.mult)
                    pool.tensor_scalar(qscale[:, u, :], rnorm[:, 0:HEADS], QK_SCALE, None, ALU.mult).then_inc(s["qk"], 1)

                def step(i, u):
                    if exists(i + 3):
                        load_y(i + 3, 1 - u)
                    if exists(i + 2):
                        tables(i + 2, u)
                        normalise(i + 2, u)

                run(step, pool.Fori)

            @block.tensor
            def _(pe):
                credit(pe, s["y_t"], s["qk_mm"], s["v_mm"], s["qk_t"], s["score"], s["p_t"], s["pv"], s["o_t"], s["proj"])
                pe.wait_ge(s["w_in"], 16 * 5)


                def turn_y(w, u):
                    need(pe, s["y_now"], w + 1)
                    if isinstance(w, int):
                        need(pe, s["yt"], w)
                        need(pe, s["qk_ev"], 2 * (w - 1))
                    need(pe, s["ot"], w - 3)
                    for k in range(KD):
                        t = pe.transpose(m.ps[:, TURN, k * P:(k + 1) * P], y_now[:, u, k * P:(k + 1) * P], m.ident[:, :])
                    t.then_inc(s["y_t"], 1)

                def project_qk(w, u, n):
                    need(pe, s["yt"], w + 1)
                    need(pe, s["rot"], w)
                    need(pe, s["squares"], w)
                    for k in range(KD):
                        mm = pe.matmul(m.ps[:, n, :], yt[:, u, k, 0:P], wqkv[:, k, n * INNER:(n + 1) * INNER],
                                       start=(k == 0), stop=(k == KD - 1))
                    mm.then_inc(s["qk_mm"], 1)

                def project_v(w, u):
                    need(pe, s["v"], w)
                    for k in range(KD):
                        mm = pe.matmul(m.ps[:, V_BANK, :], yt[:, u, k, 0:P], wqkv[:, k, QK:], start=(k == 0), stop=(k == KD - 1))
                    mm.then_inc(s["v_mm"], 1)

                def turn_qk(w, u, n):
                    if n == 0:
                        need(pe, s["qk"], w + 1)
                        if exists(w + 1):
                            need(pe, s["yt"], w + 2)
                    else:
                        need(pe, s["qk_ev"], 2 * w + 1)
                    for g in range(PAIRS):
                        t = pe.transpose(m.ps[:, TURN, g * P:(g + 1) * P],
                                         straight[:, u, n * INNER + g * P:n * INNER + (g + 1) * P], m.ident[:, :])
                    t.then_inc(s["qk_t"], 1)

                def turn_o(w):
                    need(pe, s["o"], w + 1)
                    if exists(w + 2):
                        need(pe, s["qk_ev"], 2 * (w + 2) + 2)
                    else:
                        need(pe, s["ot"], w)
                    for k in range(INNER // P):
                        t = pe.transpose(m.ps[:, TURN, k * P:(k + 1) * P], o[:, k * P:(k + 1) * P], m.ident[:, :])
                    t.then_inc(s["o_t"], 1)

                def score(w, g):
                    need(pe, s["qk_ev"], 2 * w + 2)
                    need(pe, s["masked"], PAIRS * w + g - 2 + 1)
                    for h in range(2):
                        mm = pe.matmul(m.ps[:, SCORE + g % 2, h * 2 * P:(h + 1) * 2 * P], qz[:, 2 * g + h, :],
                                       kt[:, g, :, :].rearrange("p b k -> p (b k)"), start=True, stop=True)
                    mm.then_inc(s["score"], 1)

                def turn_weights(w, g):
                    need(pe, s["exp"], PAIRS * w + g + 1)
                    if g % 2:
                        need(pe, s["p_dve"], 2 * w + g // 2 + 1)
                    else:
                        need(pe, s["p_act"], 2 * w + g // 2)
                    for n in range(4):
                        t = pe.transpose(m.ps[:, PTURN, n * P:(n + 1) * P],
                                         scores[:, 2 * g + n // 2, (n % 2) * P:(n % 2 + 1) * P], m.ident[:, :])
                    t.then_inc(s["p_t"], 1)

                def weigh(w):
                    need(pe, s["p_dve"], 2 * w + 2)
                    need(pe, s["p_act"], 2 * w + 2)
                    need(pe, s["v"], w + 1)
                    need(pe, s["y"], w)
                    for h in range(HEADS):
                        for b in range(2):
                            mm = pe.matmul(m.ps[:, OUT, h * DH:(h + 1) * DH], pt[:, h // 2, (h % 2) * 2 + b, :],
                                           v[:, b, h * DH:(h + 1) * DH], start=(b == 0), stop=(b == 1))
                    mm.then_inc(s["pv"], 1)

                def project_o(w):
                    need(pe, s["ot"], w + 1)
                    for k in range(INNER // P):
                        mm = pe.matmul(m.ps[:, OUT, 0:D], ot[:, k, :], wo[:, k, :], start=(k == 0), stop=(k == INNER // P - 1))
                    mm.then_inc(s["proj"], 1)

                def step(i, u):
                    now, ahead, far, last = exists(i), exists(i + 1), exists(i + 2), exists(i - 1)
                    if now:
                        turn_weights(i, 0)
                    if far:
                        project_qk(i + 2, u, 0)
                    if now:
                        turn_weights(i, 1)
                    if far:
                        project_qk(i + 2, u, 1)
                    if ahead:
                        turn_qk(i + 1, 1 - u, 0)
                    if now:
                        turn_weights(i, 2)
                    if ahead:
                        project_v(i + 1, 1 - u)
                        turn_qk(i + 1, 1 - u, 1)
                    if now:
                        turn_weights(i, 3)
                    if last:
                        turn_o(i - 1)
                    if ahead:
                        score(i + 1, 0)
                        score(i + 1, 1)
                    if last:
                        project_o(i - 1)
                    if exists(i + 3):
                        turn_y(i + 3, 1 - u)
                    if ahead:
                        score(i + 1, 2)
                    if now:
                        weigh(i)
                    if ahead:
                        score(i + 1, 3)

                run(step, pe.Fori)

            @block.scalar
            def _(act):
                credit(act, s["yt"], s["squares"], s["v"], s["qk_ev"], s["exp"], s["p_act"], s["ot"])
                act.wait_ge(s["consts"], 1)

                def shifted(w, u):
                    need(act, s["y_t"], w + 1)
                    need(act, s["qk_mm"], 2 * (w - 1))
                    need(act, s["v_mm"], w - 1)
                    need(act, s["yt"], w)
                    act.copy(yt[:, u, 0, 0:P], m.ps[:, TURN, 0:P])
                    act.copy(yt[:, u, 1, 0:1], yt[:, 1 - u, 1, P:P + 1])
                    act.copy(yt[:, u, 1, 1:P + 1], m.ps[:, TURN, P:2 * P]).then_inc(s["yt"], 1)

                def square(w):
                    need(act, s["qk_mm"], 2 * w + 2)
                    need(act, s["ss"], w)
                    act.activation(squares[:, :], m.ps[:, Q_BANK:K_BANK + 1, :].rearrange("p b e -> p (b e)"),
                                   ACT.Square).then_inc(s["squares"], 1)

                def take_v(w, u):
                    need(act, s["v_mm"], w + 1)
                    need(act, s["pv"], w)
                    act.copy(v[:, u, :], m.ps[:, V_BANK, :]).then_inc(s["v"], 1)

                def take_q(w):
                    need(act, s["qk_t"], 2 * w + 1)
                    need(act, s["score"], PAIRS * w)
                    for h in range(2):
                        rows = slice(h * DH, (h + 1) * DH)
                        e = act.copy(qz[rows, h:HEADS:2, :], m.ps[rows, TURN, :].rearrange("p (g k) -> p g k", k=P))
                    e.then_inc(s["qk_ev"], 1)

                def take_k(w, u):
                    need(act, s["qk_t"], 2 * w + 2)
                    act.copy(kt[:, :, u, :], m.ps[:, TURN, :].rearrange("p (g k) -> p g k", k=P)).then_inc(s["qk_ev"], 1)

                def soften(w, u, g):
                    need(act, s["bias"], PAIRS * w + g + 1)
                    if g == 0:
                        need(act, s["recip"], w)
                    for h in (2 * g, 2 * g + 1):
                        e = act.activation(scores[:, h, :], scores[:, h, :], ACT.Exp, bias=bias[:, h:h + 1],
                                           scale=qscale[:, u, h:h + 1], accum_out=total[:, h:h + 1])
                    e.then_inc(s["exp"], 1)

                def take_weights(w, g):
                    need(act, s["p_t"], PAIRS * w + g + 1)
                    need(act, s["pv"], w)
                    act.copy(pt[:, g, :, :].rearrange("p n k -> p (n k)"), m.ps[:, PTURN, :]).then_inc(s["p_act"], 1)

                def take_o(w):
                    need(act, s["o_t"], w + 1)
                    need(act, s["proj"], w)
                    act.copy(ot[:, :, :].rearrange("p k t -> p (k t)"), m.ps[:, TURN, :]).then_inc(s["ot"], 1)

                def step(i, u):
                    now, ahead = exists(i), exists(i + 1)
                    if now:
                        take_weights(i, 1)
                    if exists(i + 2):
                        square(i + 2)
                    if ahead:
                        take_q(i + 1)
                        take_k(i + 1, 1 - u)
                    if now:
                        take_weights(i, 3)
                    if exists(i - 1):
                        take_o(i - 1)
                    if ahead:
                        soften(i + 1, 1 - u, 0)
                        soften(i + 1, 1 - u, 1)
                    if exists(i + 3):
                        shifted(i + 3, 1 - u)
                    if ahead:
                        soften(i + 1, 1 - u, 2)
                        take_v(i + 1, 1 - u)
                        soften(i + 1, 1 - u, 3)

                run(step, act.Fori)

            @block.vector
            def _(dve):
                credit(dve, s["rot"], s["summed"], s["ss"], s["masked"], s["bias"], s["p_dve"], s["recip"], s["o"], s["y"])
                dve.wait_ge(s["consts"], 1)

                def rotate(w, u):
                    need(dve, s["qk_mm"], 2 * w + 2)
                    need(dve, s["squares"], w + 1)
                    need(dve, s["cs"], w + 1)
                    need(dve, s["qk_t"], 2 * (w - 1))
                    need(dve, s["qk"], w)
                    qk = m.ps[:, Q_BANK:K_BANK + 1, :].rearrange("p b (h d) -> p b h d", d=DH)
                    to = straight[:, u, :].rearrange("p (b h d) -> p b h d", b=2, d=DH)
                    to_crossed = crossed[:, :].rearrange("p (b h d) -> p b h d", b=2, d=DH)
                    cos, sin = (cs[:, u, n, :].rearrange("p (b d) -> p b d", b=2).unsqueeze(2) for n in range(2))
                    dve.tensor_tensor(to, qk, cos.broadcast_to([P, 2, HEADS, DH]), ALU.mult)
                    for half in range(2):
                        here, there = slice(half * HALF, (half + 1) * HALF), slice((1 - half) * HALF, (2 - half) * HALF)
                        r = dve.tensor_tensor(to_crossed[:, :, :, here], qk[:, :, :, there],
                                              sin[:, :, :, here].broadcast_to([P, 2, HEADS, HALF]), ALU.mult)
                    r.then_inc(s["rot"], 1)
                    dve.tensor_reduce(ss[:, :], squares[:, :].rearrange("p (h d) -> p h d", d=DH), AX.X, ALU.add).then_inc(s["summed"], 1)
                    need(dve, s["summed"], w + 1)
                    dve.tensor_scalar(ss[:, :], ss[:, :], 1e-24, None, ALU.max).then_inc(s["ss"], 1)

                def biases(w, g):
                    need(dve, s["masked"], PAIRS * w + g + 1)
                    heads = slice(2 * g, 2 * g + 2)
                    dve.tensor_tensor(bias[:, heads], top[:, heads], minus_qscale[:, heads], ALU.mult).then_inc(s["bias"], 1)

                def masked(w, u, g):
                    kind = 2 if isinstance(w, int) and w == 0 else u
                    need(dve, s["score"], PAIRS * w + g + 1)
                    if g == 0:
                        need(dve, s["qk"], w + 1)
                        need(dve, s["p_t"], PAIRS * w)
                        dve.tensor_scalar(minus_qscale[:, :], qscale[:, u, :], -1.0, None, ALU.mult)
                    else:
                        biases(w, g - 1)
                    for h in range(2):
                        r = dve.tensor_tensor_reduce(scores[:, 2 * g + h, :], m.ps[:, SCORE + g % 2, h * 2 * P:(h + 1) * 2 * P],
                                                     mask[:, kind, :, :].rearrange("p b k -> p (b k)"), 1.0, -3e38,
                                                     ALU.add, ALU.max, top[:, 2 * g + h:2 * g + h + 1])
                    r.then_inc(s["masked"], 1)
                    if g == PAIRS - 1:
                        biases(w, g)

                def take_weights(w, g):
                    need(dve, s["p_t"], PAIRS * w + g + 1)
                    need(dve, s["pv"], w)
                    dve.tensor_copy(pt[:, g, :, :].rearrange("p n k -> p (n k)"), m.ps[:, PTURN, :]).then_inc(s["p_dve"], 1)

                def divide(w):
                    need(dve, s["exp"], PAIRS * (w + 1))
                    dve.reciprocal(rtotal[:, :], total[:, :]).then_inc(s["recip"], 1)

                def take_o(w):
                    need(dve, s["recip"], w + 1)
                    need(dve, s["pv"], w + 1)
                    need(dve, s["o_t"], w)
                    dve.tensor_tensor(o[:, :].rearrange("p (h d) -> p h d", d=DH), m.ps[:, OUT, :].rearrange("p (h d) -> p h d", d=DH),
                                      rtotal[:, :].unsqueeze(2).broadcast_to([P, HEADS, DH]), ALU.mult).then_inc(s["o"], 1)

                def residual(w):
                    need(dve, s["proj"], w + 1)
                    y = m.y[:, bass.ts(w, 1), :]
                    dve.tensor_tensor(y, y, m.ps[:, OUT:OUT + 1, 0:D], ALU.add).then_inc(s["y"], 1)

                def step(i, u):
                    now, ahead = exists(i), exists(i + 1)
                    if now:
                        take_weights(i, 0)
                        take_weights(i, 2)
                        divide(i)
                    if exists(i + 2):
                        rotate(i + 2, u)
                    if ahead:
                        masked(i + 1, 1 - u, 0)
                        masked(i + 1, 1 - u, 1)
                    if exists(i - 1):
                        residual(i - 1)
                    if ahead:
                        masked(i + 1, 1 - u, 2)
                    if now:
                        take_o(i)
                    if ahead:
                        masked(i + 1, 1 - u, 3)

                run(step, dve.Fori)


def gated_mlp_statistics(nc, m):
    with ExitStack() as ctx:
        def sb(name, shape, dt=F32):
            return ctx.enter_context(nc.sbuf_tensor(f"gs_{name}", shape, dt))

        six = sb("six", [P, 2, TILES, 6])
        gap = sb("gap", [P, 2, TILES])
        mean2 = sb("mean2", [P, 2, TILES])
        sq = sb("sq", [P, 2, TILES])
        moved = sb("moved", [P, 2, TILES])
        own = sb("own", [P, 2, TILES])
        pick = sb("pick", [P, P])
        minus = sb("minus", [P, 1])
        with stage(nc, "gs", "six", "dve", "half", "zeroed", "shifted", "var", "rstd", "back", "pick", "minus", "mm", "end") as (block, s):
            last = TILES - 1

            @block.gpsimd
            def _(pool):
                pool.memset(moved[:, :, :], 0.0)
                pool.memset(m.next[:, :, :], 0.0)
                pool.memset(pick[:, :], 0.0).then_inc(s["zeroed"], 1)
                pool.wait_ge(s["zeroed"], 1)
                pool.memset(pick[0:1, :], 1.0).then_inc(s["pick"], 1)
                pool.wait_ge(s["var"], 1)
                pool.tensor_tensor(own[:, 1, :], own[:, 1, :], m.minus_half[:, 0:TILES], ALU.pow).then_inc(s["rstd"], 1)

            @block.sync
            def _(sp):
                sp.wait_ge(s["zeroed"], 1)
                sp.wait_ge(s["half"], 1)
                for n, src in enumerate((mean2[:, 1, :], sq[:, 1, :])):
                    sp.dma_start(moved[1:P, n, :], src[0:P - 1, :]).then_inc(s["shifted"], 16)
                    sp.dma_start(moved[0:1, n, 1:TILES], src[P - 1:P, 0:last]).then_inc(s["shifted"], 16)
                sp.wait_ge(s["rstd"], 1)
                sp.dma_start(m.next[0:P - 1, :, :], own[1:P, :, :]).then_inc(s["back"], 16)
                sp.dma_start(m.next[P - 1:P, :, 0:last], own[0:1, :, 1:TILES]).then_inc(s["back"], 16)
                sp.wait_ge(s["back"], 32)

            @block.vector
            def _(dve):
                with dve.Fori(0, TILES // 4) as k:
                    for u in range(4):
                        for h in range(2):
                            t = bass.ts(k * 4 + u, 1)
                            dve.bn_stats(six[:, h, t, :], m.y[:, t, h * P:(h + 1) * P]).then_inc(s["six"], 1)
                dve.wait_ge(s["six"], 2 * TILES)
                even, odd = six[:, :, :, 1], six[:, :, :, 4]
                dve.tensor_tensor(gap[:, :, :], even, odd, ALU.subtract).then_inc(s["dve"], 1)
                dve.tensor_tensor(mean2[:, :, :], even, odd, ALU.add).then_inc(s["dve"], 1)
                dve.tensor_tensor(sq[:, :, :], six[:, :, :, 2], six[:, :, :, 5], ALU.add).then_inc(s["dve"], 1)
                dve.wait_ge(s["dve"], 3)
                dve.tensor_scalar(mean2[:, :, :], mean2[:, :, :], 0.5, None, ALU.mult).then_inc(s["dve"], 1)
                dve.scalar_tensor_tensor(gap[:, :, :], gap[:, :, :], P / 4.0, gap[:, :, :], ALU.mult, ALU.mult).then_inc(s["dve"], 1)
                dve.wait_ge(s["dve"], 5)
                dve.tensor_tensor(sq[:, :, :], sq[:, :, :], gap[:, :, :], ALU.add).then_inc(s["half"], 1)
                dve.wait_ge(s["half"], 1)
                dve.wait_ge(s["shifted"], 64)
                first, second = mean2[:, 0, :], moved[:, 0, :]
                dve.tensor_tensor(own[:, 0, :], first, second, ALU.add).then_inc(s["dve"], 1)
                dve.tensor_tensor(gap[:, 0, :], first, second, ALU.subtract).then_inc(s["dve"], 1)
                dve.tensor_tensor(own[:, 1, :], sq[:, 0, :], moved[:, 1, :], ALU.add).then_inc(s["dve"], 1)
                dve.wait_ge(s["dve"], 8)
                dve.tensor_scalar(own[:, 0, :], own[:, 0, :], 0.5, None, ALU.mult).then_inc(s["dve"], 1)
                dve.tensor_scalar(own[:, 1, :], own[:, 1, :], 1.0 / D, LN_EPS, ALU.mult, ALU.add).then_inc(s["dve"], 1)
                dve.scalar_tensor_tensor(gap[:, 0, :], gap[:, 0, :], 0.25, gap[:, 0, :], ALU.mult, ALU.mult).then_inc(s["dve"], 1)
                dve.wait_ge(s["dve"], 11)
                dve.tensor_tensor(own[:, 1, :], own[:, 1, :], gap[:, 0, :], ALU.add).then_inc(s["var"], 1)
                dve.wait_ge(s["rstd"], 1)
                dve.tensor_copy(m.mean[:, :], own[:, 0, :])
                dve.tensor_copy(m.rstd[:, :], own[:, 1, :])
                dve.scalar_tensor_tensor(minus[:, :], own[:, 0, 0:1], -1.0, own[:, 1, 0:1], ALU.mult, ALU.mult).then_inc(s["minus"], 1)
                dve.wait_ge(s["mm"], 1)
                dve.tensor_copy(m.first[:, :], m.ps[:, 0, 0:1]).then_inc(s["end"], 1)

            @block.tensor
            def _(pe):
                pe.wait_ge(s["pick"], 1)
                pe.wait_ge(s["minus"], 1)
                pe.matmul(m.ps[:, 0, 0:1], pick[:, :], minus[:, :], start=True, stop=True).then_inc(s["mm"], 1)


def gated_mlp(nc, m, a, layer):
    ET = -(-HID // P)
    sizes = [min(P, HID - e * P) for e in range(ET)]
    with ExitStack() as ctx:
        def sb(name, shape, dt=F32):
            return ctx.enter_context(nc.sbuf_tensor(f"gm_{name}", shape, dt))

        w1 = sb("w1", [P, KD, 2 * HID])
        w2 = sb("w2", [P, ET, D])
        b1 = sb("b1", [P, 2, ET])
        b2 = sb("b2", [P, D])
        lng, lnb = sb("lng", [P, KD]), sb("lnb", [P, KD])
        normed = sb("normed", [P, 2, TPC, D])
        ht = sb("ht", [P, 2, KD, CHUNK + 4])
        gelu = sb("gelu", [P, 2, CHUNK])
        hid = sb("hid", [P, 2, ET, CHUNK])
        with stage(nc, "gm", "w_in", "zeroed", "before", "normed", "turned", "ht", "a_mm", "g_mm", "gelu", "hid", "out", "b2", "y") as (block, s):
            full = (ET - 1) * P
            LOADS = 10

            @block.sync
            def _(sp):
                sp.dma_start(w1[:, :, :], layer_of(a["w1"], layer).rearrange("o (k p) e -> p (o k) e", p=P)).then_inc(s["w_in"], 16)
                sp.wait_ge(s["zeroed"], 1)
                w2_l = layer_of(a["w2"], layer).rearrange("o e d -> (o e) d")
                sp.dma_start(w2[:, 0:ET - 1, :], w2_l[0:full, :].rearrange("(t p) d -> p t d", p=P)).then_inc(s["w_in"], 16)
                sp.dma_start(w2[0:sizes[-1], ET - 1, :], w2_l[full:HID, :]).then_inc(s["w_in"], 16)
                b1_l = layer_of(a["b1"], layer).rearrange("o e -> (o e)")
                for n in range(2):
                    part = b1_l[n * HID:(n + 1) * HID]
                    sp.dma_start(b1[:, n, 0:ET - 1], part[0:full].rearrange("(t p) -> p t", p=P), allow_slow_non_contiguous=True).then_inc(s["w_in"], 16)
                    sp.dma_start(b1[0:sizes[-1], n, ET - 1:ET], part[full:HID].rearrange("(p t) -> p t", t=1), allow_slow_non_contiguous=True).then_inc(s["w_in"], 16)
                sp.dma_start(b2[:, :], layer_of(a["b2"], layer).rearrange("o d -> (o d)").partition_broadcast(P)).then_inc(s["w_in"], 16)
                for to, name in ((lng, "ln_g"), (lnb, "ln_b")):
                    sp.dma_start(to[:, :], layer_of(a[name], layer).rearrange("o (k p) -> p (o k)", p=P), allow_slow_non_contiguous=True).then_inc(s["w_in"], 16)

            @block.gpsimd
            def _(pool):
                credit(pool, s["b2"])
                pool.memset(hid[:, :, :, :], 0.0)
                pool.memset(w2[:, ET - 1, :], 0.0).then_inc(s["zeroed"], 1)
                pool.wait_ge(s["w_in"], 16 * (LOADS))

                def bias(c, u):
                    need(pool, s["normed"], c + 1)
                    y = m.y[:, bass.ts(c, TPC), :]
                    pool.tensor_tensor(y, y, b2[:, :].unsqueeze(1).broadcast_to([P, TPC, D]), ALU.add).then_inc(s["b2"], 1)

                in_pairs(pool, CHUNKS, bias)

            @block.vector
            def _(dve):
                credit(dve, s["normed"], s["hid"], s["y"])
                dve.wait_ge(s["w_in"], 16 * (LOADS))
                dve.wait_ge(s["zeroed"], 1)

                def norm(c, u):
                    need(dve, s["turned"], KD * (c - 1))
                    for j in range(TPC):
                        t = bass.ts(c * TPC + j, 1)
                        for h, (mean, rstd) in enumerate(((m.mean, m.rstd), (m.next[:, 0, :], m.next[:, 1, :]))):
                            n = dve.tensor_scalar(normed[:, u, j:j + 1, h * P:(h + 1) * P], m.y[:, t, h * P:(h + 1) * P],
                                                  mean[:, t], rstd[:, t], ALU.subtract, ALU.mult)
                    n.then_inc(s["normed"], 1)

                def gate(c, u):
                    need(dve, s["out"], TPC * (c - 1))
                    for e in range(ET):
                        need(dve, s["a_mm"], ET * c + e + 1)
                        need(dve, s["gelu"], ET * c + e + 1)
                        rows = slice(0, sizes[e])
                        dve.scalar_tensor_tensor(hid[rows, u, e, :], m.ps[rows, 2 + 2 * (e % 2), :], b1[rows, 0, e:e + 1],
                                                 gelu[rows, e % 2, :], ALU.add, ALU.mult).then_inc(s["hid"], 1)
                    need(dve, s["b2"], c + 1)
                    for j in range(TPC):
                        need(dve, s["out"], TPC * c + j + 1)
                        y = m.y[:, bass.ts(c * TPC + j, 1), :]
                        dve.tensor_tensor(y, y, m.ps[:, 6 + j % 2:7 + j % 2, 0:D], ALU.add).then_inc(s["y"], 1)

                ahead_in_pairs(dve, CHUNKS, norm, gate)

            @block.scalar
            def _(act):
                credit(act, s["ht"], s["gelu"])
                act.wait_ge(s["w_in"], 16 * (LOADS))
                act.activation(ht[:, 1, 1, CHUNK:CHUNK + 1], m.first[:, :], ACT.Identity, bias=lnb[:, 1:2],
                               scale=lng[:, 1:2]).then_inc(s["before"], 1)
                act.wait_ge(s["before"], 1)

                def scaled(c, u):
                    need(act, s["g_mm"], ET * (c - 1))
                    need(act, s["a_mm"], ET * (c - 1))
                    need(act, s["turned"], KD * c + 1)
                    act.activation(ht[:, u, 0, 0:CHUNK], m.ps[:, 0, :], ACT.Identity, bias=lnb[:, 0:1], scale=lng[:, 0:1]).then_inc(s["ht"], 1)
                    need(act, s["turned"], KD * c + 2)
                    need(act, s["ht"], KD * c)
                    act.copy(ht[:, u, 1, 0:1], ht[:, 1 - u, 1, CHUNK:CHUNK + 1])
                    act.activation(ht[:, u, 1, 1:CHUNK + 1], m.ps[:, 1, :], ACT.Identity, bias=lnb[:, 1:2], scale=lng[:, 1:2]).then_inc(s["ht"], 1)

                def gelus(c, u):
                    for e in range(ET):
                        need(act, s["g_mm"], ET * c + e + 1)
                        need(act, s["hid"], ET * c + e - 2 + 1)
                        rows = slice(0, sizes[e])
                        act.activation(gelu[rows, e % 2, :], m.ps[rows, 3 + 2 * (e % 2), :], ACT.Gelu, bias=b1[rows, 1, e:e + 1]).then_inc(s["gelu"], 1)

                ahead_in_pairs(act, CHUNKS, scaled, gelus)

            @block.tensor
            def _(pe):
                credit(pe, s["turned"], s["a_mm"], s["g_mm"], s["out"])
                pe.wait_ge(s["w_in"], 16 * (LOADS))

                def turn(c, u):
                    need(pe, s["normed"], c + 1)
                    for k in range(KD):
                        need(pe, s["ht"], KD * (c - 1) + k + 1)
                        for j in range(TPC):
                            t = pe.transpose(m.ps[:, k, j * P:(j + 1) * P], normed[:, u, j, k * P:(k + 1) * P], m.ident[:, :])
                        t.then_inc(s["turned"], 1)

                def products(c, u):
                    need(pe, s["ht"], KD * (c + 1))
                    for e in range(ET):
                        for part, mm_sem, free in ((1, s["g_mm"], s["gelu"]), (0, s["a_mm"], s["hid"])):
                            need(pe, free, ET * c + e - 2 + 1)
                            for k in range(KD):
                                mm = pe.matmul(m.ps[0:sizes[e], 2 + 2 * (e % 2) + part, :],
                                               w1[:, k, part * HID + e * P:part * HID + e * P + sizes[e]], ht[:, u, k, 0:CHUNK],
                                               start=(k == 0), stop=(k == KD - 1))
                            mm.then_inc(mm_sem, 1)
                    need(pe, s["hid"], ET * (c + 1))
                    for j in range(TPC):
                        need(pe, s["y"], TPC * c + j - 2 + 1)
                        for e in range(ET):
                            mm = pe.matmul(m.ps[:, 6 + j % 2, 0:D], hid[:, u, e, j * P:(j + 1) * P], w2[:, e, :],
                                           start=(e == 0), stop=(e == ET - 1))
                        mm.then_inc(s["out"], 1)

                ahead_in_pairs(pe, CHUNKS, turn, products)



GROUP = 4
GROUPS = L1_HEADS // GROUP
QUAD = 32
ROWS = 4 * L1_DH
MPARTS = 3
MASKED = -1e30


def attention1_projections(nc, m, a):
    OUTS = 2 * KD
    with ExitStack() as ctx:
        def sb(name, shape, dt=F32):
            return ctx.enter_context(nc.sbuf_tensor(f"a1_{name}", shape, dt))

        w = sb("w", [P, 5, KD, D])
        normed = sb("normed", [P, 2, TPC, D])
        ht = sb("ht", [P, 2, KD, CHUNK])
        table = sb("table", [P, 2, 2, CHUNK])
        straight = sb("straight", [P, 2, CHUNK])
        crossed = sb("crossed", [P, 2, CHUNK])
        parts = sb("parts", [P, 2, 2, CHUNK], F16)
        with stage(nc, "a1", "w_in", "table_even", "table_odd", "ones", "normed", "turned", "ht", "mm", "v_mm", "rot", "sum", "high", "low", "v", "out_even", "out_odd") as (block, s):

            table_in, parts_out = (s["table_even"], s["table_odd"]), (s["out_even"], s["out_odd"])

            @block.sync
            def _(sp):
                for n, name in enumerate(("WQ", "WK", "WQ_swapped", "WK_swapped", "WV")):
                    sp.dma_start(w[:, n, :, :], a[name].rearrange("(k p) e -> p k e", p=P)).then_inc(s["w_in"], 16)

            @block.gpsimd
            def _(pool):
                credit(pool, s["sum"])
                pool.memset(m.v17[:, :, :, L1_DH:L1_DH + 1], 1.0).then_inc(s["ones"], 1)

                def load(c, u):
                    need(pool, s["rot"], OUTS * (c - 1))
                    pool.dma_start(table[:, u, :, :], a["rope"][:, :, bass.ts(c, CHUNK)]).then_inc(table_in[u], 16)

                def add(c, u):
                    for n in range(OUTS):
                        need(pool, s["rot"], OUTS * c + n + 1)
                        pool.tensor_tensor(straight[:, n % 2, :], straight[:, n % 2, :], crossed[:, n % 2, :], ALU.add).then_inc(s["sum"], 1)

                ahead_in_pairs(pool, CHUNKS, load, add)

            @block.vector
            def _(dve):
                credit(dve, s["normed"], s["rot"], s["low"])

                def norm(c, u):
                    need(dve, s["turned"], KD * (c - 1))
                    for j in range(TPC):
                        t = bass.ts(c * TPC + j, 1)
                        n = dve.tensor_scalar(normed[:, u, j:j + 1, :], m.x[:, t, :], m.mean[:, t], m.rstd[:, t], ALU.subtract, ALU.mult)
                    n.then_inc(s["normed"], 1)

                def rotate(c, u):
                    dve.wait_ge(table_in[u], (c - u) * 8 + 16)

                    def low(n):
                        need(dve, s["high"], OUTS * c + n + 1)
                        dve.tensor_tensor(parts[:, n % 2, 1, :], straight[:, n % 2, :], parts[:, n % 2, 0, :], ALU.subtract).then_inc(s["low"], 1)

                    for n in range(OUTS):
                        need(dve, s["mm"], OUTS * c + n + 1)
                        scale = L1_DH ** -0.5 if n < KD else 1.0
                        need(dve, s["low"], OUTS * c + n - 2 + 1)
                        for k, to in enumerate((straight, crossed)):
                            r = dve.scalar_tensor_tensor(to[:, n % 2, :], m.ps[:, 2 + 2 * (n % 2) + k, :], scale, table[:, u, k, :],
                                                         ALU.mult, ALU.mult)
                        r.then_inc(s["rot"], 1)
                        if n:
                            low(n - 1)
                    low(OUTS - 1)

                ahead_in_pairs(dve, CHUNKS, norm, rotate)

            @block.scalar
            def _(act):
                credit(act, s["ht"], s["high"], s["v"], s["out_even"], s["out_odd"])
                act.wait_ge(s["ones"], 1)

                def scaled(c, u):
                    need(act, s["mm"], OUTS * (c - 1))
                    need(act, s["v_mm"], 2 * (c - 1))
                    for k in range(KD):
                        need(act, s["turned"], KD * c + k + 1)
                        act.activation(ht[:, u, k, :], m.ps[:, k, :], ACT.Identity, bias=m.modc[:, k:k + 1],
                                       scale=m.modc[:, KD + k:KD + k + 1]).then_inc(s["ht"], 1)

                def store(c, n):
                    need(act, s["low"], OUTS * c + n + 1)
                    act.dma_start(m.qk[n // KD, :, (n % KD) * P:(n % KD + 1) * P, bass.ts(c, CHUNK)].rearrange("i p t -> p i t"),
                                  parts[:, n % 2, :, :]).then_inc(parts_out[n % 2], 16)

                def high(c, u):
                    for n in range(OUTS):
                        need(act, s["sum"], OUTS * c + n + 1)
                        need(act, parts_out[n % 2], 16 * (OUTS // 2 * c + n // 2))
                        act.copy(parts[:, n % 2, 0, :], straight[:, n % 2, :]).then_inc(s["high"], 1)
                        if n:
                            store(c, n - 1)
                    for b in range(2):
                        need(act, s["v_mm"], 2 * c + b + 1)
                        act.copy(m.v17[:, bass.ts(c * 2 + b, 2), :, 0:L1_DH],
                                 m.ps[:, 6 + b, :].rearrange("p (j h d) -> p j h d", j=2, d=L1_DH)).then_inc(s["v"], 1)
                    store(c, OUTS - 1)

                ahead_in_pairs(act, CHUNKS, scaled, high)
                for done in parts_out:
                    need(act, done, 16 * OUTS // 2 * CHUNKS)

            @block.tensor
            def _(pe):
                credit(pe, s["turned"], s["mm"], s["v_mm"])
                pe.wait_ge(s["w_in"], 16 * 5)

                def turn(c, u):
                    need(pe, s["normed"], c + 1)
                    for k in range(KD):
                        need(pe, s["ht"], KD * (c - 1) + k + 1)
                        for j in range(TPC):
                            t = pe.transpose(m.ps[:, k, j * P:(j + 1) * P], normed[:, u, j, k * P:(k + 1) * P], m.ident[:, :])
                        t.then_inc(s["turned"], 1)

                def products(c, u):
                    need(pe, s["ht"], KD * (c + 1))
                    for n in range(OUTS):
                        need(pe, s["rot"], OUTS * c + n - 2 + 1)
                        o = n % KD
                        for swapped in range(2):
                            for k in range(KD):
                                mm = pe.matmul(m.ps[:, 2 + 2 * (n % 2) + swapped, :], w[:, n // KD + 2 * swapped, k, o * P:(o + 1) * P],
                                               ht[:, u, k, :], start=(k == 0), stop=(k == KD - 1))
                        mm.then_inc(s["mm"], 1)
                    for b in range(2):
                        need(pe, s["v"], 2 * (c - 1) + b + 1)
                        for j in range(2):
                            for k in range(KD):
                                mm = pe.matmul(m.ps[:, 6 + b, j * D:(j + 1) * D], ht[:, u, k, (2 * b + j) * P:(2 * b + j + 1) * P],
                                               w[:, 4, k, :], start=(k == 0), stop=(k == KD - 1))
                        mm.then_inc(s["v_mm"], 1)

                ahead_in_pairs(pe, CHUNKS, turn, products)


def attention1(nc, m):
    with ExitStack() as ctx:
        def sb(name, shape, dt=F32):
            return ctx.enter_context(nc.sbuf_tensor(f"s1_{name}", shape, dt))

        b = Memory()
        b.keys_max = sb("keys_max", [P, GROUP, N], F16)
        b.keys_now = sb("keys_now", [P, GROUP, N], F16)
        b.q_max = sb("q_max", [P, 2, GROUP, CHUNK], F16)
        b.q_now = sb("q_now", [P, 2, GROUP, CHUNK], F16)
        b.v_now = sb("v_now", [P, 4, GROUP, QUAD])
        b.weights = sb("weights", [P, 2, 2, 2, CHUNK])
        b.tops = sb("tops", [P, CHUNKS, TILES, GROUP])
        b.minus_top = sb("minus_top", [P, GROUP, TILES])
        b.zero16 = sb("zero16", [P, P], F16)
        b.rest = sb("rest", [P, P])
        b.top_parts = sb("top_parts", [P, MPARTS, P], F16)
        b.ident16 = sb("ident16", [P, P], BF16)
        b.later_key = sb("later_key", [P, P], BF16)
        b.later_key_t = sb("later_key_t", [P, P], BF16)
        b.o_t = sb("o_t", [P, CHUNK])
        b.recip = sb("recip", [P, TPC, GROUP])
        b.o_now = sb("o_now", [P, 2, TPC, GROUP, L1_DH])
        with stage(nc, "c1", "rows", "ones", "zeroed", "consts") as (block, s):

            @block.vector
            def _(dve):
                for buffer in (b.q_max, b.q_now):
                    dve.memset(buffer[ROWS:P, :, :, :], 0.0)
                dve.memset(b.keys_max[ROWS:P, :, :], 0.0)
                dve.memset(b.keys_now[ROWS:P, :, :], 0.0).then_inc(s["rows"], 1)
                dve.wait_ge(s["rows"], 1)
                dve.memset(b.keys_now[ROWS:ROWS + MPARTS, :, :], 1.0).then_inc(s["ones"], 1)

            @block.gpsimd
            def _(pool):
                pool.memset(b.v_now[:, :, :, :], 0.0)
                for square in (b.zero16, b.ident16, b.later_key, b.later_key_t):
                    z = pool.memset(square[:, :], 0.0)
                z.then_inc(s["zeroed"], 1)
                pool.wait_ge(s["zeroed"], 1)
                pool.affine_select(b.ident16[:, :], b.ident16[:, :], pattern=[[-1, P]], compare_op=ALU.not_equal, fill=1.0,
                                   base=0, channel_multiplier=1)
                pool.affine_select(b.later_key[:, :], b.later_key[:, :], pattern=[[-1, P]], compare_op=ALU.is_ge, fill=MASKED,
                                   base=0, channel_multiplier=1)
                pool.affine_select(b.later_key_t[:, :], b.later_key_t[:, :], pattern=[[1, P]], compare_op=ALU.is_ge, fill=MASKED,
                                   base=0, channel_multiplier=-1).then_inc(s["consts"], 1)

        attend_and_find(nc, m, b, "f1", None, 0)
        with nc.Fori(0, GROUPS - 1) as g:
            attend_and_find(nc, m, b, "g1", g, g + 1)
        attend_and_find(nc, m, b, "h1", GROUPS - 1, None)


def attend_and_find(nc, m, b, name, group, next_group):
    MAX_BANK, SCORE, OUT = 0, 2, 6
    attends, finds = group is not None, next_group is not None
    MAX_BANKS = 2 if attends else 4
    PARTS = 4

    def before(j):
        return 2 * j * (j + 1)

    def steps(eng, j, step):
        step(0, 0, j, 0)
        if j:
            with eng.Fori(0, j) as c:
                for u in range(TPC):
                    step(c * TPC + 1 + u, None, c, u)
        for r in range(1, TPC):
            step(TPC * j + r, r, j, r)

    def parity(r, u, n):
        return (1 + u if r is None else r) % n

    with stage(nc, name, "k_first", "k_in", "qm_in_even", "qm_in_odd", "q_in_even", "q_in_odd", "v_now", "max_mm", "max", "cleared", "top", "top_t", "split", "split_step",
               "top_out", "score", "exp", "pv", "o_t", "o_turned", "recip", "o_now", "o_out_even", "o_out_odd") as (block, s):
        qm_in, q_in, o_out = (s["qm_in_even"], s["qm_in_odd"]), (s["q_in_even"], s["q_in_odd"]), (s["o_out_even"], s["o_out_odd"])

        @block.sync
        def _(sp):
            credit(sp, *o_out)

            def parts_of(part):
                return slice(part * L1_DH, (part + 1) * L1_DH)

            def load_q(to, g, j, sem):
                for part in range(PARTS):
                    sp.dma_start(to[parts_of(part), j % 2, :, :],
                                 m.qk[0, part // 2, bass.ts(g, GROUP * L1_DH), j * CHUNK:(j + 1) * CHUNK]
                                 .rearrange("(h d) t -> d h t", d=L1_DH)).then_inc(sem, 16)

            def store(j):
                need(sp, s["o_now"], j + 1)
                sp.dma_start(m.o[j * CHUNK:(j + 1) * CHUNK, bass.ts(group, GROUP * L1_DH)].rearrange("(t p) e -> p t e", p=P),
                             b.o_now[:, j % 2, :, :, :].rearrange("p t h d -> p t (h d)")).then_inc(o_out[j % 2], 16)

            def load_k(to, g, columns, sem):
                for part in range(PARTS):
                    sp.dma_start(to[parts_of(part), :, columns],
                                 m.qk[1, part % 2, bass.ts(g, GROUP * L1_DH), columns].rearrange("(h d) t -> d h t", d=L1_DH)).then_inc(sem, 16)

            def load_queries(j):
                if attends:
                    need(sp, s["score"], 2 * before(j - 1))
                    load_q(b.q_now, group, j, q_in[j % 2])
                    sp.dma_start(b.q_now[ROWS:ROWS + MPARTS, j % 2, :, :], m.tops[:, :, j * CHUNK:(j + 1) * CHUNK]).then_inc(q_in[j % 2], 16)
                if finds:
                    need(sp, s["max_mm"], GROUP * before(j - 1))
                    load_q(b.q_max, next_group, j, qm_in[j % 2])

            def load_keys(columns, sem):
                if attends:
                    load_k(b.keys_now, group, columns, sem)
                if finds:
                    load_k(b.keys_max, next_group, columns, sem)

            load_keys(slice(0, CHUNK), s["k_first"])
            load_queries(0)
            load_keys(slice(CHUNK, N), s["k_in"])
            for j in range(1, CHUNKS):
                load_queries(j)
                if attends and j >= 2:
                    store(j - 2)
            if attends:
                store(CHUNKS - 2)
                store(CHUNKS - 1)
                for n in range(2):
                    sp.wait_ge(q_in[n], 16 * (PARTS + 1) * CHUNKS // 2)
                    need(sp, o_out[n], 16 * CHUNKS // 2)
            if finds:
                sp.wait_ge(s["split"], 1)
                sp.dma_start(m.tops.rearrange("n h (i q) -> (h i) n q", q=P), b.top_parts[:, :, :]).then_inc(s["top_out"], 16)
                sp.wait_ge(s["top_out"], 16)

        @block.gpsimd
        def _(pool):
            credit(pool, s["v_now"])
            for j in range(CHUNKS if attends else 0):
                def step(p, r, c, t):
                    n = before(j) + p
                    need(pool, s["pv"], 2 * (n - 4) + 2)
                    pool.tensor_copy(b.v_now[:, parity(r, t, 4), :, 0:L1_DH + 1],
                                     m.v17[:, bass.ts(c * TPC + t, 1), bass.ts(group, GROUP), :].rearrange("p o h d -> p (o h) d")).then_inc(s["v_now"], 1)

                steps(pool, j, step)

        @block.tensor
        def _(pe):
            credit(pe, s["max_mm"], s["score"], s["pv"], s["o_turned"])

            def find_max(j, p, r, c, t, h):
                if not finds:
                    return
                width = CHUNK if r is None else (r + 1) * P
                need(pe, s["max"], GROUP * (before(j) + p) + h - MAX_BANKS + 1)
                mm = pe.matmul(m.ps[:, MAX_BANK + h % MAX_BANKS, 0:width], b.q_max[:, j % 2, h, t * P:(t + 1) * P],
                               b.keys_max[:, h, bass.ds(c * CHUNK, width)], start=True, stop=(r is None))
                if r is not None:
                    mm = pe.matmul(m.ps[:, MAX_BANK + h % MAX_BANKS, r * P:(r + 1) * P], b.ident16[:, :], b.later_key[:, :], start=False, stop=True)
                mm.then_inc(s["max_mm"], 1)

            def score(j, p, r, c, t, pair):
                if not attends:
                    return
                need(pe, s["exp"], 2 * (before(j) + p - 1) + pair + 1)
                skip = 0 if r is None else r * P
                for h in (2 * pair, 2 * pair + 1):
                    mm = pe.matmul(m.ps[:, SCORE + h, skip:CHUNK], b.keys_now[:, h, bass.ds((c * TPC + t) * P, P)],
                                   b.q_now[:, j % 2, h, skip:CHUNK], start=True, stop=(r is None))
                    if r is not None:
                        mm = pe.matmul(m.ps[:, SCORE + h, skip:skip + P], b.ident16[:, :], b.later_key_t[:, :], start=False, stop=True)
                mm.then_inc(s["score"], 1)

            def weigh(j, p, r, slot, pair):
                n = before(j) + p
                need(pe, s["exp"], 2 * n + pair + 1)
                need(pe, s["v_now"], n + 1)
                skip = 0 if r is None else r * P
                for h in (2 * pair, 2 * pair + 1):
                    mm = pe.matmul(m.ps[h * QUAD:(h + 1) * QUAD, OUT + j % 2, skip:CHUNK], b.v_now[:, slot % 4, h, :],
                                   b.weights[:, slot % 2, pair, h % 2, skip:CHUNK], start=False, stop=(r == TPC - 1), skip_group_check=True)
                mm.then_inc(s["pv"], 1)

            def weigh_before(j, p, r, t, pair):
                if not attends:
                    return
                if r is None:
                    weigh(j, p - 1, None, t, pair)
                elif r:
                    weigh(j, p - 1, r - 1 if r > 1 else None, r - 1, pair)
                elif j:
                    weigh(j - 1, TPC * j - 1, TPC - 1, TPC - 1, pair)

            def turn_o(j):
                need(pe, s["o_t"], j + 1)
                for t in range(TPC):
                    x = pe.transpose(m.ps[:, OUT + j % 2, t * P:(t + 1) * P], b.o_t[:, t * P:(t + 1) * P], m.ident[:, :])
                x.then_inc(s["o_turned"], 1)

            def step(j, p, r, c, t):
                find_max(j, p, r, c, t, 0)
                score(j, p, r, c, t, 0)
                find_max(j, p, r, c, t, 1)
                score(j, p, r, c, t, 1)
                find_max(j, p, r, c, t, 2)
                weigh_before(j, p, r, t, 0)
                weigh_before(j, p, r, t, 1)
                find_max(j, p, r, c, t, 3)
                if attends and r == 0:
                    need(pe, s["o_now"], j - 1)
                    pe.matmul(m.ps[:, OUT + j % 2, :], b.zero16[:, :], b.q_now[:, j % 2, 0, :], start=True, stop=False, skip_group_check=True)
                if attends and r == 1 and j:
                    turn_o(j - 1)

            pe.wait_ge(s["k_first"], 16 * PARTS * (attends + finds))
            for j in range(CHUNKS):
                if j == 1:
                    pe.wait_ge(s["k_in"], 16 * PARTS * (attends + finds))
                if attends:
                    pe.wait_ge(q_in[j % 2], 16 * (PARTS + 1) * (j // 2 + 1))
                if finds:
                    pe.wait_ge(qm_in[j % 2], 16 * PARTS * (j // 2 + 1))
                steps(pe, j, lambda p, r, c, t: step(j, p, r, c, t))
            if attends:
                for pair in range(2):
                    weigh(CHUNKS - 1, TPC * CHUNKS - 1, TPC - 1, TPC - 1, pair)
                turn_o(CHUNKS - 1)
            if finds:
                pe.wait_ge(s["top"], 1)
                pe.transpose(m.ps[:, MAX_BANK, 0:P], b.minus_top[:, :, :].rearrange("p h i -> p (h i)"), m.ident[:, :]).then_inc(s["top_t"], 1)

        @block.scalar
        def _(act):
            credit(act, s["exp"])
            for j in range(CHUNKS if attends else 0):
                def step(p, r, c, t):
                    n = before(j) + p
                    skip = 0 if r is None else r * P
                    for pair in range(2):
                        need(act, s["score"], 2 * n + pair + 1)
                        need(act, s["pv"], 2 * (n - 2) + pair + 1)
                        act.activation(b.weights[:, parity(r, t, 2), pair, :, skip:CHUNK],
                                       m.ps[:, SCORE + 2 * pair:SCORE + 2 * pair + 2, skip:CHUNK], ACT.Exp).then_inc(s["exp"], 1)

                steps(act, j, step)

        @block.vector
        def _(dve):
            credit(dve, s["max"], s["o_t"], s["recip"], s["o_now"])
            dve.memset(b.tops[:, :, :, :], -3e38).then_inc(s["cleared"], 1)
            dve.wait_ge(s["cleared"], 1)

            def row_max(j, p, r, c, t):
                n = GROUP * (before(j) + p)
                width = CHUNK if r is None else (r + 1) * P
                for h in range(GROUP if finds else 0):
                    need(dve, s["max_mm"], n + h + 1)
                    dve.tensor_reduce(b.tops[:, bass.ts(c, 1), j * TPC + t, h], m.ps[:, MAX_BANK + h % MAX_BANKS, 0:width], AX.X, ALU.max).then_inc(s["max"], 1)

            def take_o(j):
                need(dve, s["pv"], 2 * before(j + 1))
                need(dve, s["o_turned"], j)
                dve.tensor_copy(b.o_t[:, :], m.ps[:, OUT + j % 2, :]).then_inc(s["o_t"], 1)

            def divide_o(j):
                need(dve, s["o_turned"], j + 1)
                turned = m.ps[:, OUT + j % 2, :].rearrange("p (t h e) -> p t h e", t=TPC, e=QUAD)
                dve.reciprocal(b.recip[:, :, :], turned[:, :, :, L1_DH]).then_inc(s["recip"], 1)
                need(dve, s["recip"], j + 1)
                need(dve, o_out[j % 2], 16 * (j // 2))
                dve.tensor_tensor(b.o_now[:, j % 2, :, :, :], turned[:, :, :, 0:L1_DH],
                                  b.recip[:, :, :].unsqueeze(3).broadcast_to([P, TPC, GROUP, L1_DH]), ALU.mult).then_inc(s["o_now"], 1)

            for j in range(CHUNKS):
                def step(p, r, c, t):
                    row_max(j, p, r, c, t)
                    if attends and r == 0 and j:
                        take_o(j - 1)
                    if attends and r == 1 and j:
                        divide_o(j - 1)

                steps(dve, j, step)
            if attends:
                take_o(CHUNKS - 1)
                divide_o(CHUNKS - 1)
            if not finds:
                return
            need(dve, s["max"], GROUP * before(CHUNKS))
            dve.tensor_reduce(b.minus_top[:, :, :], b.tops[:, :, :, :].rearrange("p c i h -> p h i c"), AX.X, ALU.max, negate=True).then_inc(s["top"], 1)
            dve.wait_ge(s["top_t"], 1)
            dve.tensor_copy(b.rest[:, :], m.ps[:, MAX_BANK, 0:P]).then_inc(s["split_step"], 1)
            for n in range(MPARTS):
                dve.wait_ge(s["split_step"], 2 * n + 1)
                x = dve.tensor_copy(b.top_parts[:, n, :], b.rest[:, :])
                if n == MPARTS - 1:
                    x.then_inc(s["split"], 1)
                else:
                    x.then_inc(s["split_step"], 1)
                    dve.wait_ge(s["split_step"], 2 * n + 2)
                    dve.tensor_tensor(b.rest[:, :], b.rest[:, :], b.top_parts[:, n, :], ALU.subtract).then_inc(s["split_step"], 1)


def attention1_output(nc, m, a):
    with ExitStack() as ctx:
        def sb(name, shape, dt=F32):
            return ctx.enter_context(nc.sbuf_tensor(f"o1_{name}", shape, dt))

        wo = sb("wo", [P, KD, D])
        o = sb("o", [P, 2, TPC, D])
        ot = sb("ot", [P, 2, KD, CHUNK])
        gated = sb("gated", [P, 2, TPC, D])
        with stage(nc, "o1", "w_in", "o_in_even", "o_in_odd", "turned", "ot", "mm", "gated", "x") as (block, s):
            o_in = s["o_in_even"], s["o_in_odd"]

            @block.sync
            def _(sp):
                sp.dma_start(wo[:, :, :], a["WO"].rearrange("(k p) e -> p k e", p=P)).then_inc(s["w_in"], 16)

            @block.tensor
            def _(pe):
                credit(pe, s["turned"], s["mm"])
                pe.wait_ge(s["w_in"], 16)

                def turn(c, u):
                    pe.wait_ge(o_in[u], (c - u) * 8 + 16)
                    for k in range(KD):
                        need(pe, s["ot"], KD * (c - 1) + k + 1)
                        for j in range(TPC):
                            t = pe.transpose(m.ps[:, k, j * P:(j + 1) * P], o[:, u, j, k * P:(k + 1) * P], m.ident[:, :])
                        t.then_inc(s["turned"], 1)

                def products(c, u):
                    need(pe, s["ot"], KD * (c + 1))
                    for j in range(TPC):
                        need(pe, s["gated"], TPC * (c - 1) + j + 1)
                        for k in range(KD):
                            mm = pe.matmul(m.ps[:, 2 + j, 0:D], ot[:, u, k, j * P:(j + 1) * P], wo[:, k, :],
                                           start=(k == 0), stop=(k == KD - 1))
                        mm.then_inc(s["mm"], 1)

                ahead_in_pairs(pe, CHUNKS, turn, products)

            @block.scalar
            def _(act):
                credit(act, s["ot"])

                def load(c, u):
                    need(act, s["turned"], KD * (c - 1))
                    act.dma_start(o[:, u, :, :], m.o[bass.ts(c, CHUNK), :].rearrange("(t p) e -> p t e", p=P)).then_inc(o_in[u], 16)

                def take(c, u):
                    need(act, s["mm"], TPC * (c - 1))
                    for k in range(KD):
                        need(act, s["turned"], KD * c + k + 1)
                        act.copy(ot[:, u, k, :], m.ps[:, k, :]).then_inc(s["ot"], 1)

                ahead_in_pairs(act, CHUNKS, load, take)

            @block.vector
            def _(dve):
                credit(dve, s["gated"])

                def gate(c, u):
                    need(dve, s["x"], c - 1)
                    for j in range(TPC):
                        need(dve, s["mm"], TPC * c + j + 1)
                        dve.tensor_tensor(gated[:, u, j, :], m.ps[:, 2 + j, 0:D], m.modb[:, 2, :], ALU.mult).then_inc(s["gated"], 1)

                in_pairs(dve, CHUNKS, gate)

            @block.gpsimd
            def _(pool):
                credit(pool, s["x"])

                def residual(c, u):
                    need(pool, s["gated"], TPC * (c + 1))
                    x = m.x[:, bass.ts(c, TPC), :]
                    pool.tensor_tensor(x, x, gated[:, u, :, :], ALU.add).then_inc(s["x"], 1)

                in_pairs(pool, CHUNKS, residual)



TE = TILES * EXPERTS
SLOT_TILES = TOPK // P


def expert_scores(nc, m, a):
    with ExitStack() as ctx:
        def sb(name, shape, dt=F32):
            return ctx.enter_context(nc.sbuf_tensor(f"es_{name}", shape, dt))

        gate = sb("gate", [P, KD, EXPERTS])
        h = sb("h", [P, 2, TPC, D])
        ht = sb("ht", [P, 2, KD, CHUNK])
        top = sb("top", [P, TILES])
        total = sb("total", [P, TILES])
        with stage(nc, "es", "w_in", "normed", "scaled", "h", "h_even", "h_odd", "turned", "ht", "mm", "scores", "top", "less", "exp", "total", "recip", "probs") as (block, s):
            h_out = s["h_even"], s["h_odd"]
            probs = m.probs[:, :, :]

            @block.sync
            def _(sp):
                sp.dma_start(gate[:, :, :], a["L1_ffn_gate_w"].rearrange("(k p) e -> p k e", p=P)).then_inc(s["w_in"], 16)

            @block.vector
            def _(dve):
                credit(dve, s["normed"], s["scores"])

                def norm(c, u):
                    need(dve, s["turned"], KD * (c - 1))
                    need(dve, h_out[u], (c - u) * 8)
                    for j in range(TPC):
                        t = bass.ts(c * TPC + j, 1)
                        n = dve.tensor_scalar(h[:, u, j:j + 1, :], m.x[:, t, :], m.mean[:, t], m.rstd[:, t], ALU.subtract, ALU.mult)
                    n.then_inc(s["normed"], 1)

                def take(c, u):
                    need(dve, s["mm"], c + 1)
                    dve.tensor_copy(m.probs[:, bass.ts(c, TPC), :],
                                    m.ps[:, 2 + u, 0:TPC * EXPERTS].rearrange("p (t e) -> p t e", e=EXPERTS)).then_inc(s["scores"], 1)

                ahead_in_pairs(dve, CHUNKS, norm, take)
                need(dve, s["scores"], CHUNKS)
                dve.tensor_reduce(top[:, :], probs, AX.X, ALU.max).then_inc(s["top"], 1)
                dve.wait_ge(s["top"], 1)
                dve.tensor_tensor(probs, probs, top[:, :].unsqueeze(2).broadcast_to([P, TILES, EXPERTS]), ALU.subtract).then_inc(s["less"], 1)
                dve.wait_ge(s["exp"], 1)
                dve.tensor_reduce(total[:, :], probs, AX.X, ALU.add).then_inc(s["total"], 1)
                dve.wait_ge(s["total"], 1)
                dve.reciprocal(total[:, :], total[:, :]).then_inc(s["recip"], 1)
                dve.wait_ge(s["recip"], 1)
                dve.tensor_tensor(probs, probs, total[:, :].unsqueeze(2).broadcast_to([P, TILES, EXPERTS]), ALU.mult).then_inc(s["probs"], 1)

            @block.gpsimd
            def _(pool):
                credit(pool, s["scaled"], s["h"])

                def modulate(c, u):
                    need(pool, s["normed"], c + 1)
                    pool.tensor_tensor(h[:, u, :, :], h[:, u, :, :], m.modb[:, 4:5, :].broadcast_to([P, TPC, D]), ALU.mult).then_inc(s["scaled"], 1)
                    need(pool, s["scaled"], c + 1)
                    pool.tensor_tensor(h[:, u, :, :], h[:, u, :, :], m.modb[:, 3:4, :].broadcast_to([P, TPC, D]), ALU.add).then_inc(s["h"], 1)

                in_pairs(pool, CHUNKS, modulate)

            @block.tensor
            def _(pe):
                credit(pe, s["turned"], s["mm"])
                pe.wait_ge(s["w_in"], 16)

                def turn(c, u):
                    need(pe, s["h"], c + 1)
                    for k in range(KD):
                        need(pe, s["ht"], KD * (c - 1) + k + 1)
                        for j in range(TPC):
                            t = pe.transpose(m.ps[:, k, j * P:(j + 1) * P], h[:, u, j, k * P:(k + 1) * P], m.ident[:, :])
                        t.then_inc(s["turned"], 1)

                def products(c, u):
                    need(pe, s["ht"], KD * (c + 1))
                    need(pe, s["scores"], c - 1)
                    for j in range(TPC):
                        for k in range(KD):
                            mm = pe.matmul(m.ps[:, 2 + u, j * EXPERTS:(j + 1) * EXPERTS], ht[:, u, k, j * P:(j + 1) * P], gate[:, k, :],
                                           start=(k == 0), stop=(k == KD - 1))
                    mm.then_inc(s["mm"], 1)

                ahead_in_pairs(pe, CHUNKS, turn, products)

            @block.scalar
            def _(act):
                credit(act, s["ht"], *h_out)

                def take(c, u):
                    need(act, s["h"], c + 1)
                    act.dma_start(m.h[bass.ts(c, CHUNK), :].rearrange("(t p) d -> p t d", p=P), h[:, u, :, :]).then_inc(h_out[u], 16)
                    need(act, s["mm"], c - 1)
                    for k in range(KD):
                        need(act, s["turned"], KD * c + k + 1)
                        act.copy(ht[:, u, k, :], m.ps[:, k, :]).then_inc(s["ht"], 1)

                in_pairs(act, CHUNKS, take)
                for stored in h_out:
                    need(act, stored, 16 * CHUNKS // 2)
                act.wait_ge(s["less"], 1)
                act.activation(probs, probs, ACT.Exp).then_inc(s["exp"], 1)


def choose_tokens(nc, m):
    BITS = 30
    with ExitStack() as ctx:
        def sb(name, shape, dt=F32):
            return ctx.enter_context(nc.sbuf_tensor(f"ct_{name}", shape, dt))

        bound = sb("bound", [P, EXPERTS], I32)
        trial = sb("trial", [P, EXPERTS], I32)
        bit = sb("bit", [P, EXPERTS], I32)
        enough = sb("enough", [P, EXPERTS], I32)
        by_expert = sb("by_expert", [P, EXPERTS, TILES])
        hits = sb("hits", [P, EXPERTS, TILES])
        equal = sb("equal", [P, EXPERTS, TILES])
        count = sb("count", [P, EXPERTS])
        wanted = sb("wanted", [P, EXPERTS])
        ones = sb("ones", [P, P])
        earlier = sb("earlier", [P, P])
        inclusive = sb("inclusive", [P, EXPERTS, TILES])
        rank = sb("rank", [P, EXPERTS, TILES])
        slot = sb("slot", [P, EXPERTS, TILES], I32)
        slot_row = sb("slot_row", [P, EXPERTS, TILES])
        slot_tile = sb("slot_tile", [P, EXPERTS, TILES])
        piece = sb("piece", [P, EXPERTS, TILES], I32)
        token = sb("token", [P, TILES])
        lane = sb("lane", [P, P])
        carried = sb("carried", [P, EXPERTS, TILES, 2, SLOT_TILES])
        row_hot = sb("row_hot", [P, 4, P])
        with stage(nc, "ct", "consts", "zeroed", "dve", "trial", "count", "sum", "kept", "rank_in", "rank_mm", "row_hot", "gather", "taken") as (block, s):
            flat = lambda x: x[:, :, :].rearrange("p e t -> p (e t)")
            wide = lambda x: x.unsqueeze(2).broadcast_to([P, EXPERTS, TILES])
            PREFIX, TOTAL = 1, 2

            @block.gpsimd
            def _(pool):
                pool.memset(ones[:, :], 1.0)
                pool.memset(earlier[:, :], 1.0).then_inc(s["zeroed"], 1)
                pool.iota(token[:, :], pattern=[[P, TILES]], base=0, channel_multiplier=1, allow_small_or_imprecise_dtypes=True)
                pool.iota(lane[:, :], pattern=[[1, P]], base=0, channel_multiplier=0, allow_small_or_imprecise_dtypes=True)
                pool.wait_ge(s["zeroed"], 1)
                pool.affine_select(earlier[:, :], earlier[:, :], pattern=[[1, P]], compare_op=ALU.is_gt, fill=0.0, base=0,
                                   channel_multiplier=-1).then_inc(s["consts"], 1)

            @block.tensor
            def _(pe):
                pe.wait_ge(s["consts"], 1)
                with pe.Fori(0, BITS + 1) as i:
                    pe.wait_ge(s["count"], i + 1)
                    pe.matmul(m.ps[:, 0, 0:EXPERTS], ones[:, :], count[:, :], start=True, stop=True).then_inc(s["sum"], 1)
                for n in range(2):
                    pe.wait_ge(s["rank_in"], n + 1)
                    src = flat(equal) if n == 0 else flat(hits)
                    pe.matmul(m.ps[:, PREFIX, 0:TE], earlier[:, :], src, start=True, stop=True)
                    pe.matmul(m.ps[:, TOTAL, 0:TE], ones[:, :], src, start=True, stop=True).then_inc(s["rank_mm"], 1)
                with pe.Fori(0, EXPERTS) as e:
                    for t in range(TILES):
                        pe.wait_ge(s["row_hot"], e * TILES + t + 1)
                        mm = pe.matmul(m.ps[:, 3, bass.ts(e, 2 * SLOT_TILES)], row_hot[:, t % 4, :],
                                       carried[:, bass.ts(e, 1), t, :, :].rearrange("p o i s -> p (o i s)"),
                                       start=(t == 0), stop=(t == TILES - 1), skip_group_check=True)
                        mm.then_inc(s["gather"], 1)

            @block.vector
            def _(dve):
                done = 0

                def chain(instruction):
                    nonlocal done
                    instruction.then_inc(s["dve"], 1)
                    done += 1
                    dve.wait_ge(s["dve"], done)

                dve.tensor_copy(by_expert[:, :, :], m.probs[:, :, :].rearrange("p t e -> p e t"))
                dve.memset(bound[:, :], 0)
                chain(dve.memset(bit[:, :], 1 << (BITS - 1)))
                with dve.Fori(0, BITS) as i:
                    dve.tensor_tensor(trial[:, :], bound[:, :], bit[:, :], ALU.bitwise_or).then_inc(s["trial"], 1)
                    dve.wait_ge(s["trial"], i * 4 + 1)
                    dve.tensor_tensor(hits[:, :, :], by_expert[:, :, :], wide(trial[:, :].bitcast(F32)), ALU.is_ge).then_inc(s["trial"], 1)
                    dve.wait_ge(s["trial"], i * 4 + 2)
                    dve.tensor_reduce(count[:, :], hits[:, :, :], AX.X, ALU.add).then_inc(s["count"], 1)
                    dve.wait_ge(s["sum"], i + 1)
                    dve.tensor_scalar(enough[:, :], m.ps[:, 0, 0:EXPERTS], float(TOPK), None, ALU.is_ge).then_inc(s["trial"], 1)
                    dve.wait_ge(s["trial"], i * 4 + 3)
                    dve.tensor_scalar(bit[:, :], bit[:, :], 1, None, ALU.logical_shift_right).then_inc(s["trial"], 1)
                    dve.copy_predicated(bound[:, :], enough[:, :], trial[:, :]).then_inc(s["kept"], 1)
                    dve.wait_ge(s["trial"], i * 4 + 4)
                    dve.wait_ge(s["kept"], i + 1)
                limit = wide(bound[:, :].bitcast(F32))
                dve.tensor_tensor(equal[:, :, :], by_expert[:, :, :], limit, ALU.is_equal).then_inc(s["rank_in"], 1)
                chain(dve.tensor_tensor(hits[:, :, :], by_expert[:, :, :], limit, ALU.is_gt))
                dve.tensor_reduce(count[:, :], hits[:, :, :], AX.X, ALU.add).then_inc(s["count"], 1)
                dve.wait_ge(s["sum"], BITS + 1)
                chain(dve.tensor_scalar(wanted[:, :], m.ps[:, 0, 0:EXPERTS], -1.0, float(TOPK), ALU.mult, ALU.add))

                def ranks(n):
                    dve.wait_ge(s["rank_mm"], n + 1)
                    for e in range(EXPERTS):
                        x = dve.tensor_tensor_scan(inclusive[:, e, :], ones[:, 0:TILES], m.ps[:, TOTAL, e * TILES:(e + 1) * TILES], 0.0,
                                                   ALU.mult, ALU.add)
                    chain(x)
                    chain(dve.tensor_tensor(flat(rank), flat(inclusive), m.ps[:, TOTAL, 0:TE], ALU.subtract))
                    chain(dve.tensor_tensor(flat(rank), flat(rank), m.ps[:, PREFIX, 0:TE], ALU.add))

                ranks(0)
                chain(dve.tensor_tensor(rank[:, :, :], rank[:, :, :], wide(wanted[:, :]), ALU.is_lt))
                chain(dve.tensor_tensor(equal[:, :, :], equal[:, :, :], rank[:, :, :], ALU.mult))
                dve.tensor_tensor(hits[:, :, :], hits[:, :, :], equal[:, :, :], ALU.add).then_inc(s["rank_in"], 1)
                ranks(1)
                chain(dve.tensor_copy(slot[:, :, :], rank[:, :, :]))
                chain(dve.tensor_scalar(piece[:, :, :], slot[:, :, :], P - 1, None, ALU.bitwise_and))
                dve.tensor_copy(slot_row[:, :, :], piece[:, :, :])
                chain(dve.tensor_scalar(slot[:, :, :], slot[:, :, :], 7, None, ALU.logical_shift_right))
                chain(dve.tensor_copy(slot_tile[:, :, :], slot[:, :, :]))
                chain(dve.scalar_tensor_tensor(slot_tile[:, :, :], slot_tile[:, :, :], 1.0, hits[:, :, :], ALU.add, ALU.mult))
                chain(dve.tensor_scalar(slot_tile[:, :, :], slot_tile[:, :, :], -1.0, None, ALU.add))
                hot = carried[:, :, :, 1, :].rearrange("p e t s -> p (e t) s")
                lanes = lane[:, 0:SLOT_TILES].unsqueeze(1).broadcast_to([P, TE, SLOT_TILES])
                chain(dve.tensor_tensor(hot, lanes, flat(slot_tile).unsqueeze(2).broadcast_to([P, TE, SLOT_TILES]), ALU.is_equal))
                for e in range(EXPERTS):
                    x = dve.tensor_tensor(carried[:, e, :, 0, :], carried[:, e, :, 1, :],
                                          token[:, :].unsqueeze(2).broadcast_to([P, TILES, SLOT_TILES]), ALU.mult)
                chain(x)
                chain(dve.tensor_tensor(hot, hot, flat(by_expert).unsqueeze(2).broadcast_to([P, TE, SLOT_TILES]), ALU.mult))
                with dve.Fori(0, EXPERTS) as e:
                    for t in range(TILES):
                        if t >= 4:
                            dve.wait_ge(s["gather"], e * TILES + t - 3)
                        dve.tensor_scalar(row_hot[:, t % 4, :], lane[:, :], slot_row[:, bass.ts(e, 1), t], None, ALU.is_equal).then_inc(s["row_hot"], 1)
                    dve.wait_ge(s["gather"], e * TILES + TILES)
                found = m.ps[:, 3, 0:EXPERTS * 2 * SLOT_TILES].rearrange("p (e i s) -> p e i s", e=EXPERTS, i=2)
                dve.tensor_copy(m.chosen[:, :, :], found[:, :, 0, :])
                dve.tensor_copy(m.gates[:, :, :], found[:, :, 1, :]).then_inc(s["taken"], 1)


def experts(nc, m, a):
    HALVES = TOPK // CHUNK
    FT = EHID // P
    with ExitStack() as ctx:
        def sb(name, shape, dt=F32):
            return ctx.enter_context(nc.sbuf_tensor(f"ex_{name}", shape, dt))

        w1 = sb("w1", [P, 2, KD, EHID])
        w2 = sb("w2", [P, 2, FT, D])
        which = sb("which", [P, 2, SLOT_TILES], U32)
        gate = sb("gate", [P, 2, SLOT_TILES])
        h = sb("h", [P, 2, SLOT_TILES, D])
        ht = sb("ht", [P, 2, KD, CHUNK])
        hid = sb("hid", [P, 2, FT, CHUNK])
        y = sb("y", [P, 2, SLOT_TILES, D])
        zero = sb("zero", [P, TPC, D])
        with stage(nc, "ex", "zeroed", "cleared", "w_even", "w_odd", "which", "h_even", "h_odd", "turned", "ht", "up", "hid", "down", "y", "added", "summed", "issue") as (block, s):
            w_in, h_in = (s["w_even"], s["w_odd"]), (s["h_even"], s["h_odd"])

            @block.sync
            def _(sp):
                sp.wait_ge(s["zeroed"], 1)
                for c in range(CHUNKS):
                    sp.dma_start(m.mix[c * CHUNK:(c + 1) * CHUNK, :].rearrange("(t p) d -> p t d", p=P), zero[:, :, :]).then_inc(s["cleared"], 16)

            @block.scalar
            def _(act):
                credit(act, s["ht"], s["hid"])

                def load(e, u):
                    need(act, s["up"], HALVES * FT * (e - 1))
                    need(act, s["down"], SLOT_TILES * (e - 1))
                    act.dma_start(w1[:, u, :, :], a["L1_ffn_w1"][bass.ts(e, 1)].rearrange("o (k p) f -> p (o k) f", p=P)).then_inc(w_in[u], 16)
                    act.dma_start(w2[:, u, :, :], a["L1_ffn_w2"][bass.ts(e, 1)].rearrange("o (f p) d -> p (o f) d", p=P)).then_inc(w_in[u], 16)

                def take(e, x):
                    n = e * HALVES + x
                    need(act, s["up"], FT * (n - 1))
                    for k in range(KD):
                        need(act, s["turned"], KD * n + k + 1)
                        act.copy(ht[:, x, k, :], m.ps[:, k, :]).then_inc(s["ht"], 1)

                def gelu(e, x):
                    n = e * HALVES + x
                    need(act, s["down"], TPC * (n - 1))
                    for f in range(FT):
                        need(act, s["up"], FT * n + f + 1)
                        act.activation(hid[:, x, f, :], m.ps[:, 2 + f % 2, :], ACT.Gelu_apprx_tanh).then_inc(s["hid"], 1)

                def expert(e, u):
                    take(e, 1)
                    gelu(e, 0)
                    if not isinstance(e, int) or e + 1 < EXPERTS:
                        load(e + 1, 1 - u)
                        take(e + 1, 0)
                    gelu(e, 1)

                load(0, 0)
                take(0, 0)
                expert(0, 0)
                with act.Fori(0, EXPERTS // 2 - 1) as k:
                    expert(k * 2 + 1, 1)
                    expert(k * 2 + 2, 0)
                expert(EXPERTS - 1, 1)

            @block.gpsimd
            def _(pool):
                credit(pool, s["which"], s["summed"], s["issue"])
                pool.memset(zero[:, :, :], 0.0).then_inc(s["zeroed"], 1)

                def gather(e, u):
                    need(pool, s["turned"], KD * HALVES * (e - 1))
                    pool.tensor_copy(which[:, u, :].unsqueeze(1), m.chosen[:, bass.ts(e, 1), :])
                    pool.tensor_copy(gate[:, u, :].unsqueeze(1), m.gates[:, bass.ts(e, 1), :]).then_inc(s["which"], 1)
                    need(pool, s["which"], e + 1)
                    pool.sem_inc(s["issue"], 1)
                    for t in range(SLOT_TILES):
                        pool.indirect_dma_start(h[:, u, t, :], None, m.h, bass.IndirectOffsetOnAxis(which[:, u, t:t + 1], 0)).then_inc(h_in[u], 16)

                def add(e, u):
                    for t in range(SLOT_TILES):
                        need(pool, s["y"], SLOT_TILES * e + t + 1)
                        pool.sem_inc(s["issue"], 1)
                        pool.indirect_dma_start(m.mix, bass.IndirectOffsetOnAxis(which[:, u, t:t + 1], 0), y[:, u, t, :], None,
                                                compute_op=ALU.add).then_inc(s["added"], 16)

                gather(0, 0)
                pool.wait_ge(s["cleared"], 16 * CHUNKS)

                def expert(e, u):
                    if not isinstance(e, int) or e > 0:
                        pool.wait_ge(s["added"], 16 * SLOT_TILES * e)
                        pool.sem_inc(s["summed"], 1)
                    if not isinstance(e, int) or e + 1 < EXPERTS:
                        gather(e + 1, 1 - u)
                    add(e, u)

                expert(0, 0)
                with pool.Fori(0, EXPERTS // 2 - 1) as k:
                    expert(k * 2 + 1, 1)
                    expert(k * 2 + 2, 0)
                expert(EXPERTS - 1, 1)
                pool.wait_ge(s["added"], 16 * SLOT_TILES * EXPERTS)

            @block.tensor
            def _(pe):
                credit(pe, s["turned"], s["up"], s["down"])

                def turn(e, u, x):
                    n = e * HALVES + x
                    if x == 0:
                        pe.wait_ge(h_in[u], (e - u) * 8 * SLOT_TILES + 16 * SLOT_TILES)
                    for k in range(KD):
                        need(pe, s["ht"], KD * (n - 1) + k + 1)
                        for j in range(TPC):
                            t = pe.transpose(m.ps[:, k, j * P:(j + 1) * P], h[:, u, x * TPC + j, k * P:(k + 1) * P], m.ident[:, :])
                        t.then_inc(s["turned"], 1)

                def up(e, u, x):
                    n = e * HALVES + x
                    need(pe, s["ht"], KD * (n + 1))
                    if x == 0:
                        pe.wait_ge(w_in[u], (e - u) * 16 + 32)
                    for f in range(FT):
                        need(pe, s["hid"], FT * n + f - 2 + 1)
                        for k in range(KD):
                            mm = pe.matmul(m.ps[:, 2 + f % 2, :], w1[:, u, k, f * P:(f + 1) * P], ht[:, x, k, :],
                                           start=(k == 0), stop=(k == KD - 1))
                        mm.then_inc(s["up"], 1)

                def down(e, u, x):
                    n = e * HALVES + x
                    need(pe, s["hid"], FT * (n + 1))
                    for j in range(TPC):
                        need(pe, s["y"], TPC * n + j - 4 + 1)
                        for f in range(FT):
                            mm = pe.matmul(m.ps[:, 4 + j, 0:D], hid[:, x, f, j * P:(j + 1) * P], w2[:, u, f, :],
                                           start=(f == 0), stop=(f == FT - 1))
                        mm.then_inc(s["down"], 1)

                def expert(e, u):
                    turn(e, u, 1)
                    up(e, u, 0)
                    down(e, u, 0)
                    if not isinstance(e, int) or e + 1 < EXPERTS:
                        turn(e + 1, 1 - u, 0)
                    up(e, u, 1)
                    down(e, u, 1)

                turn(0, 0, 0)
                expert(0, 0)
                with pe.Fori(0, EXPERTS // 2 - 1) as k:
                    expert(k * 2 + 1, 1)
                    expert(k * 2 + 2, 0)
                expert(EXPERTS - 1, 1)

            @block.vector
            def _(dve):
                credit(dve, s["y"])

                def expert(e, u):
                    need(dve, s["which"], e + 1)
                    need(dve, s["summed"], e - 1)
                    for t in range(SLOT_TILES):
                        need(dve, s["down"], SLOT_TILES * e + t + 1)
                        dve.tensor_scalar(y[:, u, t, :], m.ps[:, 4 + t % TPC, 0:D], gate[:, u, t:t + 1], None, ALU.mult).then_inc(s["y"], 1)

                in_pairs(dve, EXPERTS, expert)


def mixture_output(nc, m, out):
    with ExitStack() as ctx:
        mix = ctx.enter_context(nc.sbuf_tensor("mo_mix", [P, TILES, D], F32))
        rounded = ctx.enter_context(nc.sbuf_tensor("mo_rounded", [P, 2, TPC, D], BF16))
        with stage(nc, "mo", *(f"in{c}" for c in range(CHUNKS)), "rounded", "gated", "x", "out") as (block, s):
            mix_in = [s[f"in{c}"] for c in range(CHUNKS)]

            @block.sync
            def _(sp):
                for c in range(CHUNKS):
                    rows = slice(c * CHUNK, (c + 1) * CHUNK)
                    sp.dma_start(mix[:, c * TPC:(c + 1) * TPC, :], m.mix[rows, :].rearrange("(t p) d -> p t d", p=P)).then_inc(mix_in[c], 16)
                for c in range(CHUNKS):
                    rows = slice(c * CHUNK, (c + 1) * CHUNK)
                    sp.wait_ge(s["x"], c + 1)
                    sp.dma_start(out[rows, :].rearrange("(t p) d -> p t d", p=P), m.x[:, c * TPC:(c + 1) * TPC, :]).then_inc(s["out"], 16)
                sp.wait_ge(s["out"], 16 * CHUNKS)

            @block.vector
            def _(dve):
                for c in range(CHUNKS):
                    tiles = slice(c * TPC, (c + 1) * TPC)
                    dve.wait_ge(mix_in[c], 16)
                    if c >= 2:
                        dve.wait_ge(s["gated"], c - 1)
                    dve.tensor_copy(rounded[:, c % 2, :, :], mix[:, tiles, :]).then_inc(s["rounded"], 1)
                    dve.wait_ge(s["rounded"], c + 1)
                    dve.tensor_tensor(mix[:, tiles, :], rounded[:, c % 2, :, :], m.modb[:, 5:6, :].broadcast_to([P, TPC, D]), ALU.mult).then_inc(s["gated"], 1)

            @block.gpsimd
            def _(pool):
                for c in range(CHUNKS):
                    tiles = slice(c * TPC, (c + 1) * TPC)
                    pool.wait_ge(s["gated"], c + 1)
                    pool.tensor_tensor(m.x[:, tiles, :], m.x[:, tiles, :], mix[:, tiles, :], ALU.add).then_inc(s["x"], 1)



def rotary_table():
    f = np.float32
    half_idx = np.arange(0, DH, 2, dtype=f)
    inv_freq = f(1.0) / f(10000.0) ** (half_idx / f(DH))
    t = np.arange(N, dtype=f)
    freqs = t[:, None] * inv_freq[None, :]
    base = (half_idx + f(0.4 * DH)) / f(1.4 * DH)
    power = (t - f(N // 2)) / f(WINDOW // 2)
    scale = base[None, :] ** power[:, None]
    cos, sin = np.cos(freqs), np.sin(freqs)
    return np.stack([cos * scale, cos / scale, sin * scale, sin / scale], axis=1).astype(f)


def rope_table():
    f = np.float32
    k = np.arange(L1_DH // 2, dtype=f)
    inv_freq = f(10000.0) ** (f(-2.0) * k / f(L1_DH))
    angle = np.arange(N, dtype=f)[:, None] * inv_freq
    cos, sin = np.cos(angle).T, np.sin(angle).T
    pairs = np.stack([np.stack([cos, cos], axis=1).reshape(L1_DH, N), np.stack([-sin, sin], axis=1).reshape(L1_DH, N)], axis=1)
    return np.tile(pairs, (P // L1_DH, 1, 1)).astype(f)


def layout(inputs):
    a = dict(inputs)
    a["x"] = np.asarray(a.pop("L0_attn_X")).reshape(N, D)
    a["rotary"], a["rope"] = rotary_table(), rope_table()
    swap = np.arange(D) ^ 1
    for n in "QK":
        w = np.asarray(a.pop(f"L1_attn_W_{n}"))
        a[f"W{n}"], a[f"W{n}_swapped"] = w.T, w[swap].T
    for n in "VO":
        a[f"W{n}"] = np.asarray(a.pop(f"L1_attn_W_{n}")).T
    a = {n: np.ascontiguousarray(v) for n, v in a.items()}
    return a



def load_x(nc, m, x, name):
    with stage(nc, name, "x_in", "zeroed", "ident", "ident16") as (block, s):

        @block.sync
        def _(sp):
            for h in range(4):
                t = TILES // 4
                sp.dma_start(m.x[:, h * t:(h + 1) * t, :],
                             x[h * t * P:(h + 1) * t * P, :].rearrange("(t p) d -> p t d", p=P)).then_inc(s["x_in"], 16)
            sp.wait_ge(s["x_in"], 64)

        @block.gpsimd
        def _(pool):
            pool.memset(m.minus_half[:, :], -0.5)
            pool.memset(m.ident[:, :], 0.0).then_inc(s["zeroed"], 1)
            pool.wait_ge(s["zeroed"], 1)
            pool.affine_select(m.ident[:, :], m.ident[:, :], pattern=[[-1, P]], compare_op=ALU.not_equal, fill=1.0,
                               base=0, channel_multiplier=1).then_inc(s["ident"], 1)
            pool.wait_ge(s["ident"], 1)
            pool.tensor_copy(m.ident16[:, :], m.ident[:, :]).then_inc(s["ident16"], 1)


def program(nc, a, out):
    m = Memory()
    with ExitStack() as ctx:
        def sb(name, shape, dt=F32):
            return ctx.enter_context(nc.sbuf_tensor(name, shape, dt))

        m.ps = ctx.enter_context(nc.psum_tensor("ps", [P, 8, 512], F32))
        m.x = sb("x", [P, TILES, D])
        m.ident = sb("ident", [P, P])
        m.ident16 = sb("ident16", [P, P], F16)
        m.minus_half = sb("minus_half", [P, TILES])
        m.modb = sb("modb", [P, 6, D])
        m.modc = sb("modc", [P, 6 * KD])
        m.mean = sb("mean", [P, TILES])
        m.rstd = sb("rstd", [P, TILES])

        load_x(nc, m, a["x"], "load")
        modulation(nc, m, "m0", a["L0_c"], a["L0_wmod"])
        norm_statistics(nc, m, "n0")
        with ExitStack() as scope:
            m.qt = scope.enter_context(nc.sbuf_tensor("a0_qt", [P, KD, 2, N], F16))
            m.kt = scope.enter_context(nc.sbuf_tensor("a0_kt", [P, KD, 2, N], F16))
            m.v = scope.enter_context(nc.sbuf_tensor("a0_v", [P, TILES, 2, D], F16))
            attention0_projections(nc, m, {k: a["L0_attn_" + k] for k in ("Wq", "Wk", "Wv", "bq", "bk", "bv")})
            attention0(nc, m)

        with ExitStack() as scope:
            def sc(name, shape):
                return scope.enter_context(nc.sbuf_tensor(name, shape, F32))

            m.y = sc("y", [P, TILES, D])
            m.next = sc("next", [P, 2, TILES])
            m.first = sc("first", [P, 1])
            f = {k: a["L0_ffn_" + k] for k in ("wqkv", "q_scale", "k_scale", "wo", "ln_g", "ln_b", "w1", "b1", "w2", "b2")}
            f["rotary"] = a["rotary"]
            norm_statistics(nc, m, "n1")
            transformer_input(nc, m)
            with nc.Fori(0, DEPTH) as layer:
                local_attention(nc, m, f, layer)
                gated_mlp_statistics(nc, m)
                gated_mlp(nc, m, f, layer)
            transformer_output(nc, m)

        m.qk = nc.dram_tensor("qk_parts", [2, 2, D, N], F16).ap()
        m.tops = nc.dram_tensor("top_parts", [MPARTS, GROUP, N], F16).ap()
        m.o = nc.dram_tensor("heads_out", [N, D], F32).ap()
        modulation(nc, m, "m1", a["L1_c"], a["L1_wmod"])
        norm_statistics(nc, m, "n2")
        with ExitStack() as scope:
            m.v17 = scope.enter_context(nc.sbuf_tensor("v17", [P, TILES, L1_HEADS, L1_DH + 1], F32))
            attention1_projections(nc, m, a)
            attention1(nc, m)
        attention1_output(nc, m, a)

        m.h = nc.dram_tensor("expert_in", [N, D], F32).ap()
        m.mix = nc.dram_tensor("expert_out", [N, D], F32).ap()
        m.probs = sb("probs", [P, TILES, EXPERTS])
        m.chosen = sb("chosen", [P, EXPERTS, SLOT_TILES], U32)
        m.gates = sb("gates", [P, EXPERTS, SLOT_TILES])
        norm_statistics(nc, m, "n3")
        expert_scores(nc, m, a)
        choose_tokens(nc, m)
        experts(nc, m, a)
        mixture_output(nc, m, out)


def kernel(**inputs):
    import concourse.bacc as bacc
    from concourse.bass_utils import run_bass_kernel_spmd

    nc = bacc.Bacc("TRN2", target_bir_lowering=False, num_devices=1)
    arrays, a = {}, {}
    for name, array in layout(inputs).items():
        arrays[f"in_{name}_dram"] = array
        a[name] = nc.dram_tensor(f"in_{name}_dram", array.shape, mybir.dt.from_np(array.dtype), kind="ExternalInput").ap()
    out = nc.dram_tensor("out_dram", (N, D), F32, kind="ExternalOutput").ap()
    program(nc, a, out)
    result = run_bass_kernel_spmd(nc, [arrays], core_ids=[0])
    return result.results[0]["out_dram"].reshape(1, N, D)
```

```python
from contextlib import ExitStack, contextmanager

import numpy as np

import concourse.bass as bass
from concourse import mybir

F32 = mybir.dt.float32
F16 = mybir.dt.float16
BF16 = mybir.dt.bfloat16
I32 = mybir.dt.int32
U32 = mybir.dt.uint32
ACT = mybir.ActivationFunctionType
ALU = mybir.AluOpType
AX = mybir.AxisListType

P = 128
N = 4096
D = 256
KD = D // P
TILES = N // P
CHUNK = 512
TPC = CHUNK // P
CHUNKS = N // CHUNK
LN_EPS = 1e-5

DEPTH, HEADS, DH, WINDOW = 2, 8, 64, 128
INNER = HEADS * DH
HID = D * 4 * 2 // 3
QK_SCALE = 8.0
HALF = DH // 2
ROTARY_N = 4096

L1_HEADS, L1_DH = 16, 16
EXPERTS, TOPK, EHID = 8, 1024, 1024

CREDIT = 64


def need(eng, sem, n):
    eng.wait_ge(sem, n + CREDIT)


def credit(eng, *sems):
    for sem in sems:
        eng.sem_inc(sem, CREDIT)


class Memory:
    pass


@contextmanager
def stage(nc, name, *names):
    with ExitStack() as ctx:
        sems = [ctx.enter_context(nc.semaphore(f"{name}_{n}")) for n in names]
        with nc.Block() as block:
            yield block, dict(zip(names, sems))
        numbers = [sem.num for sem in sems]
        nc.all_engine_barrier(sems_to_clear=range(min(numbers), max(numbers) + 1))


def in_pairs(eng, count, step):
    with eng.Fori(0, count // 2) as k:
        step(k * 2, 0)
        step(k * 2 + 1, 1)


def ahead_in_pairs(eng, count, first, second):
    first(0, 0)
    with eng.Fori(0, count // 2 - 1) as k:
        first(k * 2 + 1, 1)
        second(k * 2, 0)
        first(k * 2 + 2, 0)
        second(k * 2 + 1, 1)
    first(count - 1, 1)
    second(count - 2, 0)
    second(count - 1, 1)



def modulation(nc, m, name, c, wmod):
    with ExitStack() as ctx:
        ccol = ctx.enter_context(nc.sbuf_tensor(f"{name}_ccol", [P, KD], F32))
        crep = ctx.enter_context(nc.sbuf_tensor(f"{name}_crep", [P, KD, P], F32))
        w = ctx.enter_context(nc.sbuf_tensor(f"{name}_wmod", [P, KD, 6 * D], F32))
        sign = ctx.enter_context(nc.sbuf_tensor(f"{name}_sign", [P, 2, D], F32))
        size = ctx.enter_context(nc.sbuf_tensor(f"{name}_size", [P, 2, D], F32))
        modb = m.modb[:, :, :].rearrange("p i d -> p (i d)")
        gates = m.modb[:, 2:6:3, :]
        with stage(nc, name, "c_in", "w_in", "silu", "rep", "col_mm", "row_mm", "col_ev", "row_ev", "dve") as (block, s):

            @block.sync
            def _(sp):
                sp.dma_start(ccol[:, :], c.rearrange("o (k p) -> p (o k)", p=P),
                             allow_slow_non_contiguous=True).then_inc(s["c_in"], 16)
                sp.dma_start(w[:, :, :], wmod.rearrange("(k p) e -> p k e", p=P)).then_inc(s["w_in"], 16)

            @block.scalar
            def _(act):
                act.wait_ge(s["c_in"], 16)
                act.activation(ccol[:, :], ccol[:, :], ACT.Silu).then_inc(s["silu"], 1)

            @block.tensor
            def _(pe):
                pe.wait_ge(s["w_in"], 16)
                pe.wait_ge(s["silu"], 1)
                for j in range(6 * KD):
                    for k in range(KD):
                        mm = pe.matmul(m.ps[:, 0, j:j + 1], w[:, k, j * P:(j + 1) * P], ccol[:, k:k + 1],
                                       start=(k == 0), stop=(k == KD - 1))
                mm.then_inc(s["col_mm"], 1)
                pe.wait_ge(s["rep"], 1)
                for j in range(3):
                    for k in range(KD):
                        mm = pe.matmul(m.ps[:, 1 + j, :], crep[:, k, :], w[:, k, j * 512:(j + 1) * 512],
                                       start=(k == 0), stop=(k == KD - 1))
                mm.then_inc(s["row_mm"], 1)

            @block.vector
            def _(dve):
                dve.wait_ge(s["silu"], 1)
                dve.tensor_copy(crep[:, :, :], ccol[:, :].unsqueeze(2).broadcast_to([P, KD, P])).then_inc(s["rep"], 1)
                dve.wait_ge(s["col_mm"], 1)
                dve.tensor_copy(m.modc[:, :], m.ps[:, 0, 0:6 * KD]).then_inc(s["col_ev"], 1)
                dve.wait_ge(s["row_mm"], 1)
                dve.tensor_copy(modb, m.ps[:, 1:4, :].rearrange("p b e -> p (b e)")).then_inc(s["row_ev"], 1)
                dve.wait_ge(s["col_ev"], 1)
                scales = m.modc[:, :].rearrange("p (i k) -> p i k", k=KD)[:, 1:6:3, :]
                dve.tensor_scalar(scales, scales, 1.0, None, ALU.add).then_inc(s["dve"], 1)
                dve.wait_ge(s["row_ev"], 1)
                rows = m.modb[:, 1:6:3, :]
                dve.tensor_scalar(rows, rows, 1.0, None, ALU.add).then_inc(s["dve"], 1)
                dve.tensor_scalar(sign[:, :, :], gates, 0.0, 2.0, ALU.is_ge, ALU.mult).then_inc(s["dve"], 1)
                dve.scalar_tensor_tensor(size[:, :, :], gates, -1.0, gates, ALU.mult, ALU.max).then_inc(s["dve"], 1)
                dve.wait_ge(s["dve"], 4)
                dve.tensor_scalar(size[:, :, :], size[:, :, :], 0.25, None, ALU.max).then_inc(s["dve"], 1)
                dve.wait_ge(s["dve"], 5)
                dve.scalar_tensor_tensor(gates, sign[:, :, :], -1.0, size[:, :, :], ALU.add, ALU.mult)



def norm_statistics(nc, m, name):
    with ExitStack() as ctx:
        six = ctx.enter_context(nc.sbuf_tensor(f"{name}_six", [P, TILES, 6], F32))
        half_gap = ctx.enter_context(nc.sbuf_tensor(f"{name}_half_gap", [P, TILES], F32))
        var = ctx.enter_context(nc.sbuf_tensor(f"{name}_var", [P, TILES], F32))
        with stage(nc, name, "six", "dve", "var", "rstd") as (block, s):

            @block.vector
            def _(dve):
                with dve.Fori(0, TILES // 4) as k:
                    for u in range(4):
                        t = bass.ts(k * 4 + u, 1)
                        dve.bn_stats(six[:, t, :], m.x[:, t, :]).then_inc(s["six"], 1)
                dve.wait_ge(s["six"], TILES)
                even, odd, sq_even, sq_odd = six[:, :, 1], six[:, :, 4], six[:, :, 2], six[:, :, 5]
                dve.tensor_tensor(half_gap[:, :], even, odd, ALU.subtract).then_inc(s["dve"], 1)
                dve.tensor_tensor(m.mean[:, :], even, odd, ALU.add).then_inc(s["dve"], 1)
                dve.tensor_tensor(var[:, :], sq_even, sq_odd, ALU.add).then_inc(s["dve"], 1)
                dve.wait_ge(s["dve"], 3)
                dve.tensor_scalar(m.mean[:, :], m.mean[:, :], 0.5, None, ALU.mult)
                dve.tensor_scalar(var[:, :], var[:, :], 1.0 / D, LN_EPS, ALU.mult, ALU.add).then_inc(s["dve"], 1)
                dve.scalar_tensor_tensor(half_gap[:, :], half_gap[:, :], 0.25, half_gap[:, :], ALU.mult, ALU.mult).then_inc(s["dve"], 1)
                dve.wait_ge(s["dve"], 5)
                dve.tensor_tensor(m.rstd[:, :], var[:, :], half_gap[:, :], ALU.add).then_inc(s["var"], 1)

            @block.gpsimd
            def _(pool):
                pool.wait_ge(s["var"], 1)
                pool.tensor_tensor(m.rstd[:, :], m.rstd[:, :], m.minus_half[:, 0:TILES], ALU.pow).then_inc(s["rstd"], 1)



def attention0_projections(nc, m, a):
    with ExitStack() as ctx:
        def sb(name, shape, dt=F32):
            return ctx.enter_context(nc.sbuf_tensor(f"a0_{name}", shape, dt))

        w = {n: sb(f"w{n}", [P, KD, D]) for n in "qkv"}
        bcol = {n: sb(f"b{n}", [P, KD]) for n in "qk"}
        bv = sb("bv", [P, D])
        normed = sb("normed", [P, 2, TPC, D])
        ht = sb("ht", [P, 2, KD, CHUNK])
        v = sb("v_whole", [P, 2, 2, D])
        with stage(nc, "a0", "w_in", "normed", "turned", "ht", "mm", "high", "ev", "v", "v_high", "v_low") as (block, s):

            @block.sync
            def _(sp):
                for n in "qkv":
                    sp.dma_start(w[n][:, :, :], a[f"W{n}"].rearrange("(k p) e -> p k e", p=P)).then_inc(s["w_in"], 16)
                for n in "qk":
                    sp.dma_start(bcol[n][:, :], a[f"b{n}"].rearrange("(k p) -> p k", p=P),
                                 allow_slow_non_contiguous=True).then_inc(s["w_in"], 16)
                sp.dma_start(bv[:, :], a["bv"].partition_broadcast(P)).then_inc(s["w_in"], 16)

            @block.vector
            def _(dve):
                credit(dve, s["normed"], s["ev"], s["v"])
                dve.wait_ge(s["w_in"], 16 * 6)

                def norm(c, u):
                    need(dve, s["turned"], KD * (c - 1))
                    for j in range(TPC):
                        t = c * TPC + j
                        n = dve.tensor_scalar(normed[:, u, j:j + 1, :], m.x[:, bass.ts(t, 1), :], m.mean[:, bass.ts(t, 1)],
                                              m.rstd[:, bass.ts(t, 1)], ALU.subtract, ALU.mult)
                    n.then_inc(s["normed"], 1)

                def outputs(c, u):
                    for n in range(2 * KD):
                        need(dve, s["high"], 2 * KD * c + n + 1)
                        to, b = (m.qt, bcol["q"]) if n < KD else (m.kt, bcol["k"])
                        dve.scalar_tensor_tensor(to[:, n % KD, 1, bass.ts(c, CHUNK)], m.ps[:, 2 + n, :], b[:, n % KD:n % KD + 1],
                                                 to[:, n % KD, 0, bass.ts(c, CHUNK)], ALU.add, ALU.subtract).then_inc(s["ev"], 1)
                    for b in range(2):
                        need(dve, s["mm"], 6 * c + 2 * KD + b + 1)
                        need(dve, s["v_low"], 2 * (c - 1) + b + 1)
                        dve.tensor_tensor(v[:, b, :, :], m.ps[:, 6 + b, :].rearrange("p (j e) -> p j e", e=D),
                                          bv[:, :].unsqueeze(1).broadcast_to([P, 2, D]), ALU.add).then_inc(s["v"], 1)

                ahead_in_pairs(dve, CHUNKS, norm, outputs)

            @block.scalar
            def _(act):
                credit(act, s["ht"], s["high"], s["v_high"])
                act.wait_ge(s["w_in"], 16 * 6)

                def high(c, u):
                    for n in range(2 * KD):
                        need(act, s["mm"], 6 * c + n + 1)
                        to, b = (m.qt, bcol["q"]) if n < KD else (m.kt, bcol["k"])
                        act.activation(to[:, n % KD, 0, bass.ts(c, CHUNK)], m.ps[:, 2 + n, :], ACT.Identity,
                                       bias=b[:, n % KD:n % KD + 1]).then_inc(s["high"], 1)
                    for b in range(2):
                        need(act, s["v"], 2 * c + b + 1)
                        act.copy(m.v[:, bass.ts(c * 2 + b, 2), 0, :], v[:, b, :, :]).then_inc(s["v_high"], 1)

                def scaled(c, u):
                    need(act, s["mm"], 6 * (c - 1))
                    for k in range(KD):
                        need(act, s["turned"], KD * c + k + 1)
                        act.activation(ht[:, u, k, :], m.ps[:, k, :], ACT.Identity, bias=m.modc[:, k:k + 1],
                                       scale=m.modc[:, KD + k:KD + k + 1]).then_inc(s["ht"], 1)

                ahead_in_pairs(act, CHUNKS, scaled, high)

            @block.gpsimd
            def _(pool):
                credit(pool, s["v_low"])

                def low(c, u):
                    for b in range(2):
                        need(pool, s["v_high"], 2 * c + b + 1)
                        pool.tensor_tensor(m.v[:, bass.ts(c * 2 + b, 2), 1, :], v[:, b, :, :], m.v[:, bass.ts(c * 2 + b, 2), 0, :],
                                           ALU.subtract).then_inc(s["v_low"], 1)

                in_pairs(pool, CHUNKS, low)

            @block.tensor
            def _(pe):
                credit(pe, s["turned"], s["mm"])
                pe.wait_ge(s["w_in"], 16 * 6)

                def turn(c, u):
                    need(pe, s["normed"], c + 1)
                    for k in range(KD):
                        need(pe, s["ht"], KD * (c - 1) + k + 1)
                        for j in range(TPC):
                            t = pe.transpose(m.ps[:, k, j * P:(j + 1) * P], normed[:, u, j, k * P:(k + 1) * P], m.ident[:, :])
                        t.then_inc(s["turned"], 1)

                def products(c, u):
                    need(pe, s["ht"], KD * (c + 1))
                    for n in range(2 * KD):
                        need(pe, s["ev"], 2 * KD * (c - 1) + n + 1)
                        o = n % KD
                        for k in range(KD):
                            mm = pe.matmul(m.ps[:, 2 + n, :], w["qk"[n // KD]][:, k, o * P:(o + 1) * P], ht[:, u, k, :],
                                           start=(k == 0), stop=(k == KD - 1))
                        mm.then_inc(s["mm"], 1)
                    for b in range(2):
                        need(pe, s["v"], 2 * (c - 1) + b + 1)
                        for j in range(2):
                            for k in range(KD):
                                mm = pe.matmul(m.ps[:, 6 + b, j * D:(j + 1) * D],
                                               ht[:, u, k, (2 * b + j) * P:(2 * b + j + 1) * P], w["v"][:, k, :],
                                               start=(k == 0), stop=(k == KD - 1))
                        mm.then_inc(s["mm"], 1)

                ahead_in_pairs(pe, CHUNKS, turn, products)


def attention0(nc, m):
    KC = N // CHUNK
    PIECES = 4
    PIECE = N // PIECES
    CPP = KC // PIECES
    with ExitStack() as ctx:
        def sb(name, shape, dt=F32):
            return ctx.enter_context(nc.sbuf_tensor(f"s0_{name}", shape, dt))

        scores = sb("scores", [P, 2, N])
        parts = sb("parts", [P, 2, N], F16)
        pt = sb("pt", [P, 2, 2, CHUNK], F16)
        top = sb("top", [P, 2, KC])
        minus_top = sb("minus_top", [P, 2])
        total = sb("total", [P, 2])
        rtotal = sb("rtotal", [P, 2])
        add = sb("add", [P, 2, D])
        with stage(nc, "s0", "mm", "copied", "max", "top", "exp", "high", "low", "turned", "pt_act", "pt_dve", "pv", "recip", "summed",
                   "gated", "x") as (block, s):

            def run(step, loop):
                with loop(0, TILES // 2 - 1) as k:
                    step(k * 2, 0)
                    step(k * 2 + 1, 1)
                step(TILES - 2, 0)
                step(TILES - 1, 1)

            def exists(i):
                return not isinstance(i, int) or i < TILES

            def turned_bank(c):
                return m.ps[:, 4 + c % 2, :].bitcast(F16)

            @block.gpsimd
            def _(pool):
                credit(pool, s["x"])

                def residual(i, u):
                    need(pool, s["gated"], i + 1)
                    x = m.x[:, bass.ts(i, 1), :]
                    pool.tensor_tensor(x, x, add[:, u:u + 1, :], ALU.add).then_inc(s["x"], 1)

                in_pairs(pool, TILES, residual)

            @block.tensor
            def _(pe):
                credit(pe, s["mm"], s["turned"], s["pv"])

                def score(i):
                    for c in range(KC):
                        need(pe, s["copied"], KC * i + c - 4 + 1)
                        keys = slice(c * CHUNK, (c + 1) * CHUNK)
                        terms = [(k, a, b) for k in range(KD) for a, b in ((0, 0), (0, 1), (1, 0))]
                        for n, (k, a, b) in enumerate(terms):
                            mm = pe.matmul(m.ps[:, c % 4, :], m.qt[:, k, a, bass.ts(i, P)], m.kt[:, k, b, keys],
                                           start=(n == 0), stop=(n == len(terms) - 1))
                        mm.then_inc(s["mm"], 1)

                def turn(i, c):
                    need(pe, s["low"], PIECES * i + c // CPP + 1)
                    if c % 2:
                        need(pe, s["pt_dve"], KC // 2 * i + c // 2)
                    else:
                        need(pe, s["pt_act"], KC // 2 * i + c // 2)
                    for part in range(2):
                        for j in range(TPC):
                            kt = c * TPC + j
                            t = pe.transpose(turned_bank(c)[:, (part * TPC + j) * P:(part * TPC + j + 1) * P],
                                             parts[:, part, kt * P:(kt + 1) * P], m.ident16[:, :])
                    t.then_inc(s["turned"], 1)

                def weigh(i, u):
                    turn(i, 0)
                    need(pe, s["summed"], 2 * (i - 1))
                    for c in range(KC):
                        if c + 1 < KC:
                            turn(i, c + 1)
                        need(pe, s["pt_dve" if c % 2 else "pt_act"], KC // 2 * i + c // 2 + 1)
                        for j in range(TPC):
                            kt = c * TPC + j
                            pe.matmul(m.ps[:, 6 + u, :], pt[:, c % 2, 0, j * P:(j + 1) * P], m.v[:, kt, :, :].rearrange("p i e -> p (i e)"),
                                      start=(kt == 0), stop=False, skip_group_check=True)
                            mm = pe.matmul(m.ps[:, 6 + u, 0:D], pt[:, c % 2, 1, j * P:(j + 1) * P], m.v[:, kt, 0, :],
                                           start=False, stop=(kt == TILES - 1), skip_group_check=True)
                        mm.then_inc(s["pv"], 1)

                def step(i, u):
                    if exists(i + 1):
                        score(i + 1)
                    weigh(i, u)

                score(0)
                run(step, pe.Fori)

            @block.vector
            def _(dve):
                credit(dve, s["copied"], s["max"], s["top"], s["low"], s["pt_dve"], s["recip"], s["summed"], s["gated"])

                def row_max(i, u, c):
                    need(dve, s["mm"], KC * i + c + 1)
                    dve.tensor_scalar(scores[:, u, c * CHUNK:(c + 1) * CHUNK], m.ps[:, c % 4, :], 1.0, None, ALU.mult, ALU.max,
                                      accum_out=top[:, u, c:c + 1]).then_inc(s["copied"], 1)

                def row_top(i, u):
                    need(dve, s["copied"], KC * (i + 1))
                    dve.tensor_reduce(minus_top[:, u:u + 1], top[:, u, :], AX.X, ALU.max, negate=True).then_inc(s["max"], 1)
                    need(dve, s["max"], i + 1)
                    dve.tensor_scalar(minus_top[:, u:u + 1], minus_top[:, u:u + 1], float(10 * np.log(2)), None, ALU.add).then_inc(s["top"], 1)

                def low(i, u, g):
                    need(dve, s["high"], PIECES * i + g + 1)
                    piece = slice(g * PIECE, (g + 1) * PIECE)
                    dve.tensor_tensor(parts[:, 1, piece], scores[:, u, piece], parts[:, 0, piece], ALU.subtract).then_inc(s["low"], 1)

                def step(i, u):
                    for c in range(KC):
                        if exists(i + 1):
                            row_max(i + 1, 1 - u, c)
                        if c >= KC - PIECES:
                            low(i, u, c - (KC - PIECES))
                    if exists(i + 1):
                        row_top(i + 1, 1 - u)
                    dve.reciprocal(rtotal[:, u:u + 1], total[:, u:u + 1]).then_inc(s["recip"], 1)
                    for c in range(1, KC, 2):
                        need(dve, s["turned"], KC * i + c + 1)
                        need(dve, s["pv"], KC * i + c - 2 + 1)
                        dve.tensor_copy(pt[:, c % 2, :, :].rearrange("p i k -> p (i k)"), turned_bank(c)).then_inc(s["pt_dve"], 1)
                    need(dve, s["recip"], i + 1)
                    need(dve, s["pv"], KC * (i + 1))
                    need(dve, s["x"], i - 1)
                    dve.tensor_copy(add[:, u, :], m.ps[:, 6 + u, D:2 * D]).then_inc(s["summed"], 1)
                    need(dve, s["summed"], 2 * i + 1)
                    dve.tensor_tensor(add[:, u, :], m.ps[:, 6 + u, 0:D], add[:, u, :], ALU.add).then_inc(s["summed"], 1)
                    need(dve, s["summed"], 2 * i + 2)
                    dve.scalar_tensor_tensor(add[:, u, :], add[:, u, :], rtotal[:, u:u + 1], m.modb[:, 2, :],
                                             ALU.mult, ALU.mult).then_inc(s["gated"], 1)

                for c in range(KC):
                    row_max(0, 0, c)
                row_top(0, 0)
                run(step, dve.Fori)

            @block.scalar
            def _(act):
                credit(act, s["exp"], s["high"], s["pt_act"])

                def step(i, u):
                    need(act, s["top"], i + 1)
                    need(act, s["recip"], i - 1)
                    act.activation(scores[:, u, :], scores[:, u, :], ACT.Exp, bias=minus_top[:, u:u + 1],
                                   accum_out=total[:, u:u + 1]).then_inc(s["exp"], 1)
                    need(act, s["exp"], i + 1)
                    need(act, s["turned"], KC * i)
                    for g in range(PIECES):
                        piece = slice(g * PIECE, (g + 1) * PIECE)
                        act.copy(parts[:, 0, piece], scores[:, u, piece]).then_inc(s["high"], 1)
                    for c in range(0, KC, 2):
                        need(act, s["turned"], KC * i + c + 1)
                        need(act, s["pv"], KC * i + c - 2 + 1)
                        act.copy(pt[:, c % 2, :, :].rearrange("p i k -> p (i k)"), turned_bank(c)).then_inc(s["pt_act"], 1)

                run(step, act.Fori)



def load_attention(eng, m, f, layer, loaded):
    eng.dma_start(m.wqkv[:, :, :], layer_of(f["wqkv"], layer).rearrange("o (k p) e -> p (o k) e", p=P)).then_inc(loaded, 16)
    eng.dma_start(m.wo[:, :, :], layer_of(f["wo"], layer).rearrange("o (k p) e -> p (o k) e", p=P)).then_inc(loaded, 16)
    for n, name in enumerate(("q_scale", "k_scale")):
        src = layer_of(f[name], layer).rearrange("o d -> (o d)")
        eng.dma_start(m.gain[:, n, :, :].rearrange("p h d -> p (h d)"), src.partition_broadcast(P)).then_inc(loaded, 16)


ATTENTION_LOADS = 4


def transformer_input(nc, m, f):
    NEG = -1e30
    with ExitStack() as ctx:
        normed = ctx.enter_context(nc.sbuf_tensor("y0_normed", [P, 2, TPC, D], F32))
        with stage(nc, "y0", "table_in", "w_in", "zeroed", "normed", "scaled", "y") as (block, s):

            @block.sync
            def _(sp):
                load_attention(sp, m, f, 0, s["w_in"])
                sp.dma_start(m.table[:, :, :, :], f["rotary"].rearrange("(t p) i d -> p t i d", p=P)).then_inc(s["table_in"], 16)
                sp.wait_ge(s["w_in"], 16 * ATTENTION_LOADS)
                sp.wait_ge(s["table_in"], 16)

            @block.vector
            def _(dve):
                credit(dve, s["normed"], s["scaled"])

                def norm(c, u):
                    need(dve, s["y"], c - 1)
                    for j in range(TPC):
                        t = bass.ts(c * TPC + j, 1)
                        n = dve.tensor_scalar(normed[:, u, j:j + 1, :], m.x[:, t, :], m.mean[:, t], m.rstd[:, t], ALU.subtract, ALU.mult)
                    n.then_inc(s["normed"], 1)
                    need(dve, s["normed"], c + 1)
                    dve.tensor_tensor(normed[:, u, :, :], normed[:, u, :, :], m.modb[:, 4:5, :].broadcast_to([P, TPC, D]),
                                      ALU.mult).then_inc(s["scaled"], 1)

                in_pairs(dve, CHUNKS, norm)

            @block.gpsimd
            def _(pool):
                credit(pool, s["y"])
                pool.memset(m.mask[:, :, :, :], 0.0).then_inc(s["zeroed"], 1)
                pool.wait_ge(s["zeroed"], 1)
                for own in (m.mask[:, 0, 0, :], m.mask[:, 1, 1, :], m.mask[:, 2, 0, :]):
                    pool.affine_select(own, own, pattern=[[-1, P]], compare_op=ALU.is_ge, fill=NEG, base=0, channel_multiplier=1)
                for before in (m.mask[:, 0, 1, :], m.mask[:, 1, 0, :]):
                    pool.affine_select(before, before, pattern=[[1, P]], compare_op=ALU.is_ge, fill=NEG, base=0, channel_multiplier=-1)
                pool.memset(m.mask[:, 2, 1, :], NEG)

                def shift(c, u):
                    need(pool, s["scaled"], c + 1)
                    pool.tensor_tensor(m.y[:, bass.ts(c, TPC), :], normed[:, u, :, :], m.modb[:, 3:4, :].broadcast_to([P, TPC, D]),
                                       ALU.add).then_inc(s["y"], 1)

                in_pairs(pool, CHUNKS, shift)


def transformer_output(nc, m):
    with stage(nc, "y1", "gated", "x") as (block, s):

        @block.vector
        def _(dve):
            with dve.Fori(0, CHUNKS) as c:
                y = m.y[:, bass.ts(c, TPC), :]
                dve.tensor_tensor(y, y, m.modb[:, 5:6, :].broadcast_to([P, TPC, D]), ALU.mult).then_inc(s["gated"], 1)

        @block.gpsimd
        def _(pool):
            with pool.Fori(0, CHUNKS) as c:
                pool.wait_ge(s["gated"], c + 1)
                x = m.x[:, bass.ts(c, TPC), :]
                pool.tensor_tensor(x, x, m.y[:, bass.ts(c, TPC), :], ALU.add).then_inc(s["x"], 1)


def layer_of(weights, layer):
    return weights[bass.ts(layer, 1)]


def local_attention(nc, m):
    QK = 2 * INNER
    PAIRS = HEADS // 2
    wqkv, wo, table, mask, gain = m.wqkv, m.wo, m.table, m.mask, m.gain
    with ExitStack() as ctx:
        def sb(name, shape, dt=F32):
            return ctx.enter_context(nc.sbuf_tensor(f"la_{name}", shape, dt))

        gain_rot = sb("gain_rot", [P, 2, 2, HALF])
        y_now = sb("y_now", [P, 2, D])
        yt = sb("yt", [P, 2, KD, P + 4])
        cs = sb("cs", [P, 2, 2, 2 * DH])
        squares = sb("squares", [P, QK])
        straight = sb("straight", [P, 2, QK])
        crossed = sb("crossed", [P, QK])
        ss = sb("ss", [P, 2 * HEADS])
        rnorm = sb("rnorm", [P, 2 * HEADS])
        qscale = sb("qscale", [P, 2, HEADS])
        qz = sb("qz", [P, HEADS, P])
        kt = sb("kt", [P, PAIRS, 2, P])
        v = sb("v", [P, 2, INNER])
        scores = sb("scores", [P, HEADS, 2 * P])
        top = sb("top", [P, HEADS])
        bias = sb("bias", [P, HEADS])
        minus_qscale = sb("minus_qscale", [P, HEADS])
        total = sb("total", [P, HEADS])
        rtotal = sb("rtotal", [P, HEADS])
        pt = sb("pt", [P, PAIRS, 4, P])
        o = sb("o", [P, INNER])
        ot = sb("ot", [P, INNER // P, P])
        Q_BANK, K_BANK, V_BANK, TURN, SCORE, PTURN, OUT = 0, 1, 2, 3, 4, 6, 7

        def run(step, loop):
            for i in range(-3, 2):
                step(i, i % 2)
            with loop(1, TILES // 2 - 2) as k:
                step(k * 2, 0)
                step(k * 2 + 1, 1)
            for i in range(TILES - 4, TILES + 1):
                step(i, i % 2)

        def exists(w):
            return not isinstance(w, int) or 0 <= w < TILES

        with stage(nc, "la", "consts", "zeroed", "y_now", "y_t", "yt", "qk_mm", "v_mm", "cs", "rot", "squares", "summed", "ss", "rnorm", "crossed",
                   "qk", "qk_t", "qk_ev", "v", "score", "masked", "bias", "exp", "p_t", "p_act", "p_dve", "pv", "recip",
                   "o", "o_t", "ot", "proj", "y") as (block, s):

            @block.gpsimd
            def _(pool):
                credit(pool, s["y_now"], s["cs"], s["rnorm"], s["crossed"], s["qk"])
                pool.memset(yt[:, 1, :, P:P + 1], 0.0)
                pool.memset(qz[:, :, :], 0.0)
                pool.tensor_scalar(gain_rot[:, :, 0, :], gain[:, :, 1, :], -1.0, None, ALU.mult)
                pool.tensor_copy(gain_rot[:, :, 1, :], gain[:, :, 0, :]).then_inc(s["consts"], 1)
                pool.wait_ge(s["consts"], 1)

                def load_y(w, u):
                    need(pool, s["y_t"], w - 1)
                    pool.tensor_copy(y_now[:, u:u + 1, :], m.y[:, bass.ts(w, 1), :]).then_inc(s["y_now"], 1)

                def tables(w, u):
                    need(pool, s["rot"], w - 1)
                    for n, g in ((0, gain), (1, gain_rot)):
                        t = pool.tensor_tensor(cs[:, u, n, :].rearrange("p (q h d) -> p q h d", q=2, h=2),
                                               table[:, bass.ts(w, 1), 2 * n:2 * n + 2, :].rearrange("p o q d -> p (o q) d")
                                               .unsqueeze(2).broadcast_to([P, 2, 2, HALF]), g[:, :, :, :], ALU.mult)
                    t.then_inc(s["cs"], 1)

                def normalise(w, u):
                    need(pool, s["rot"], w + 1)
                    pool.tensor_tensor(straight[:, u, :], straight[:, u, :], crossed[:, :], ALU.add).then_inc(s["crossed"], 1)
                    need(pool, s["ss"], w + 1)
                    pool.tensor_tensor(rnorm[:, :], ss[:, :], m.minus_half[:, 0:2 * HEADS], ALU.pow).then_inc(s["rnorm"], 1)
                    need(pool, s["rnorm"], w + 1)
                    need(pool, s["crossed"], w + 1)
                    need(pool, s["exp"], PAIRS * (w - 1))
                    kk = straight[:, u, INNER:QK].rearrange("p (h d) -> p h d", d=DH)
                    pool.tensor_tensor(kk, kk, rnorm[:, HEADS:2 * HEADS].unsqueeze(2).broadcast_to([P, HEADS, DH]), ALU.mult)
                    pool.tensor_scalar(qscale[:, u, :], rnorm[:, 0:HEADS], QK_SCALE, None, ALU.mult).then_inc(s["qk"], 1)

                def step(i, u):
                    if exists(i + 3):
                        load_y(i + 3, 1 - u)
                    if exists(i + 2):
                        tables(i + 2, u)
                        normalise(i + 2, u)

                run(step, pool.Fori)

            @block.tensor
            def _(pe):
                credit(pe, s["y_t"], s["qk_mm"], s["v_mm"], s["qk_t"], s["score"], s["p_t"], s["pv"], s["o_t"], s["proj"])

                def turn_y(w, u):
                    need(pe, s["y_now"], w + 1)
                    if isinstance(w, int):
                        need(pe, s["yt"], w)
                        need(pe, s["qk_ev"], 2 * (w - 1))
                    need(pe, s["ot"], w - 3)
                    for k in range(KD):
                        t = pe.transpose(m.ps[:, TURN, k * P:(k + 1) * P], y_now[:, u, k * P:(k + 1) * P], m.ident[:, :])
                    t.then_inc(s["y_t"], 1)

                def project_qk(w, u, n):
                    need(pe, s["yt"], w + 1)
                    need(pe, s["rot"], w)
                    need(pe, s["squares"], w)
                    for k in range(KD):
                        mm = pe.matmul(m.ps[:, n, :], yt[:, u, k, 0:P], wqkv[:, k, n * INNER:(n + 1) * INNER],
                                       start=(k == 0), stop=(k == KD - 1))
                    mm.then_inc(s["qk_mm"], 1)

                def project_v(w, u):
                    need(pe, s["v"], w)
                    for k in range(KD):
                        mm = pe.matmul(m.ps[:, V_BANK, :], yt[:, u, k, 0:P], wqkv[:, k, QK:], start=(k == 0), stop=(k == KD - 1))
                    mm.then_inc(s["v_mm"], 1)

                def turn_qk(w, u, n):
                    if n == 0:
                        need(pe, s["qk"], w + 1)
                        if exists(w + 1):
                            need(pe, s["yt"], w + 2)
                    else:
                        need(pe, s["qk_ev"], 2 * w + 1)
                    for g in range(PAIRS):
                        t = pe.transpose(m.ps[:, TURN, g * P:(g + 1) * P],
                                         straight[:, u, n * INNER + g * P:n * INNER + (g + 1) * P], m.ident[:, :])
                    t.then_inc(s["qk_t"], 1)

                def turn_o(w):
                    need(pe, s["o"], w + 1)
                    if exists(w + 2):
                        need(pe, s["qk_ev"], 2 * (w + 2) + 2)
                    else:
                        need(pe, s["ot"], w)
                    for k in range(INNER // P):
                        t = pe.transpose(m.ps[:, TURN, k * P:(k + 1) * P], o[:, k * P:(k + 1) * P], m.ident[:, :])
                    t.then_inc(s["o_t"], 1)

                def score(w, g):
                    need(pe, s["qk_ev"], 2 * w + 2)
                    need(pe, s["masked"], PAIRS * w + g - 2 + 1)
                    for h in range(2):
                        mm = pe.matmul(m.ps[:, SCORE + g % 2, h * 2 * P:(h + 1) * 2 * P], qz[:, 2 * g + h, :],
                                       kt[:, g, :, :].rearrange("p b k -> p (b k)"), start=True, stop=True)
                    mm.then_inc(s["score"], 1)

                def turn_weights(w, g):
                    need(pe, s["exp"], PAIRS * w + g + 1)
                    if g % 2:
                        need(pe, s["p_dve"], 2 * w + g // 2 + 1)
                    else:
                        need(pe, s["p_act"], 2 * w + g // 2)
                    for n in range(4):
                        t = pe.transpose(m.ps[:, PTURN, n * P:(n + 1) * P],
                                         scores[:, 2 * g + n // 2, (n % 2) * P:(n % 2 + 1) * P], m.ident[:, :])
                    t.then_inc(s["p_t"], 1)

                def weigh(w):
                    need(pe, s["p_dve"], 2 * w + 2)
                    need(pe, s["p_act"], 2 * w + 2)
                    need(pe, s["v"], w + 1)
                    need(pe, s["y"], w)
                    for h in range(HEADS):
                        for b in range(2):
                            mm = pe.matmul(m.ps[:, OUT, h * DH:(h + 1) * DH], pt[:, h // 2, (h % 2) * 2 + b, :],
                                           v[:, b, h * DH:(h + 1) * DH], start=(b == 0), stop=(b == 1))
                    mm.then_inc(s["pv"], 1)

                def project_o(w):
                    need(pe, s["ot"], w + 1)
                    for k in range(INNER // P):
                        mm = pe.matmul(m.ps[:, OUT, 0:D], ot[:, k, :], wo[:, k, :], start=(k == 0), stop=(k == INNER // P - 1))
                    mm.then_inc(s["proj"], 1)

                def step(i, u):
                    now, ahead, far, last = exists(i), exists(i + 1), exists(i + 2), exists(i - 1)
                    if now:
                        turn_weights(i, 0)
                    if far:
                        project_qk(i + 2, u, 0)
                    if now:
                        turn_weights(i, 1)
                    if far:
                        project_qk(i + 2, u, 1)
                    if ahead:
                        turn_qk(i + 1, 1 - u, 0)
                    if now:
                        turn_weights(i, 2)
                    if ahead:
                        project_v(i + 1, 1 - u)
                        turn_qk(i + 1, 1 - u, 1)
                    if now:
                        turn_weights(i, 3)
                    if last:
                        turn_o(i - 1)
                    if ahead:
                        score(i + 1, 0)
                        score(i + 1, 1)
                    if last:
                        project_o(i - 1)
                    if exists(i + 3):
                        turn_y(i + 3, 1 - u)
                    if ahead:
                        score(i + 1, 2)
                    if now:
                        weigh(i)
                    if ahead:
                        score(i + 1, 3)

                run(step, pe.Fori)

            @block.scalar
            def _(act):
                credit(act, s["yt"], s["squares"], s["v"], s["qk_ev"], s["exp"], s["p_act"], s["ot"])
                act.wait_ge(s["consts"], 1)
                act.wait_ge(s["zeroed"], 1)

                def shifted(w, u):
                    need(act, s["y_t"], w + 1)
                    need(act, s["qk_mm"], 2 * (w - 1))
                    need(act, s["v_mm"], w - 1)
                    need(act, s["yt"], w)
                    act.copy(yt[:, u, 0, 0:P], m.ps[:, TURN, 0:P])
                    act.copy(yt[:, u, 1, 0:1], yt[:, 1 - u, 1, P:P + 1])
                    act.copy(yt[:, u, 1, 1:P + 1], m.ps[:, TURN, P:2 * P]).then_inc(s["yt"], 1)

                def square(w):
                    need(act, s["qk_mm"], 2 * w + 2)
                    need(act, s["ss"], w)
                    act.activation(squares[:, :], m.ps[:, Q_BANK:K_BANK + 1, :].rearrange("p b e -> p (b e)"),
                                   ACT.Square).then_inc(s["squares"], 1)

                def take_v(w, u):
                    need(act, s["v_mm"], w + 1)
                    need(act, s["pv"], w)
                    act.copy(v[:, u, :], m.ps[:, V_BANK, :]).then_inc(s["v"], 1)

                def take_q(w):
                    need(act, s["qk_t"], 2 * w + 1)
                    need(act, s["score"], PAIRS * w)
                    for h in range(2):
                        rows = slice(h * DH, (h + 1) * DH)
                        e = act.copy(qz[rows, h:HEADS:2, :], m.ps[rows, TURN, :].rearrange("p (g k) -> p g k", k=P))
                    e.then_inc(s["qk_ev"], 1)

                def take_k(w, u):
                    need(act, s["qk_t"], 2 * w + 2)
                    act.copy(kt[:, :, u, :], m.ps[:, TURN, :].rearrange("p (g k) -> p g k", k=P)).then_inc(s["qk_ev"], 1)

                def soften(w, u, g):
                    need(act, s["bias"], PAIRS * w + g + 1)
                    if g == 0:
                        need(act, s["recip"], w)
                    for h in (2 * g, 2 * g + 1):
                        e = act.activation(scores[:, h, :], scores[:, h, :], ACT.Exp, bias=bias[:, h:h + 1],
                                           scale=qscale[:, u, h:h + 1], accum_out=total[:, h:h + 1])
                    e.then_inc(s["exp"], 1)

                def take_weights(w, g):
                    need(act, s["p_t"], PAIRS * w + g + 1)
                    need(act, s["pv"], w)
                    act.copy(pt[:, g, :, :].rearrange("p n k -> p (n k)"), m.ps[:, PTURN, :]).then_inc(s["p_act"], 1)

                def take_o(w):
                    need(act, s["o_t"], w + 1)
                    need(act, s["proj"], w)
                    act.copy(ot[:, :, :].rearrange("p k t -> p (k t)"), m.ps[:, TURN, :]).then_inc(s["ot"], 1)

                def step(i, u):
                    now, ahead = exists(i), exists(i + 1)
                    if now:
                        take_weights(i, 1)
                    if exists(i + 2):
                        square(i + 2)
                    if ahead:
                        take_q(i + 1)
                        take_k(i + 1, 1 - u)
                    if now:
                        take_weights(i, 3)
                    if exists(i - 1):
                        take_o(i - 1)
                    if ahead:
                        soften(i + 1, 1 - u, 0)
                        soften(i + 1, 1 - u, 1)
                    if exists(i + 3):
                        shifted(i + 3, 1 - u)
                    if ahead:
                        soften(i + 1, 1 - u, 2)
                        take_v(i + 1, 1 - u)
                        soften(i + 1, 1 - u, 3)

                run(step, act.Fori)

            @block.vector
            def _(dve):
                credit(dve, s["rot"], s["summed"], s["ss"], s["masked"], s["bias"], s["p_dve"], s["recip"], s["o"], s["y"])
                dve.memset(kt[:, :, 1, :], 0.0)
                dve.memset(v[:, 1, :], 0.0).then_inc(s["zeroed"], 1)
                dve.wait_ge(s["consts"], 1)

                def rotate(w, u):
                    need(dve, s["qk_mm"], 2 * w + 2)
                    need(dve, s["squares"], w + 1)
                    need(dve, s["cs"], w + 1)
                    need(dve, s["qk_t"], 2 * (w - 1))
                    need(dve, s["qk"], w)
                    qk = m.ps[:, Q_BANK:K_BANK + 1, :].rearrange("p b (h d) -> p b h d", d=DH)
                    to = straight[:, u, :].rearrange("p (b h d) -> p b h d", b=2, d=DH)
                    to_crossed = crossed[:, :].rearrange("p (b h d) -> p b h d", b=2, d=DH)
                    cos, sin = (cs[:, u, n, :].rearrange("p (b d) -> p b d", b=2).unsqueeze(2) for n in range(2))
                    dve.tensor_tensor(to, qk, cos.broadcast_to([P, 2, HEADS, DH]), ALU.mult)
                    for half in range(2):
                        here, there = slice(half * HALF, (half + 1) * HALF), slice((1 - half) * HALF, (2 - half) * HALF)
                        r = dve.tensor_tensor(to_crossed[:, :, :, here], qk[:, :, :, there],
                                              sin[:, :, :, here].broadcast_to([P, 2, HEADS, HALF]), ALU.mult)
                    r.then_inc(s["rot"], 1)
                    dve.tensor_reduce(ss[:, :], squares[:, :].rearrange("p (h d) -> p h d", d=DH), AX.X, ALU.add).then_inc(s["summed"], 1)
                    need(dve, s["summed"], w + 1)
                    dve.tensor_scalar(ss[:, :], ss[:, :], 1e-24, None, ALU.max).then_inc(s["ss"], 1)

                def biases(w, g):
                    need(dve, s["masked"], PAIRS * w + g + 1)
                    heads = slice(2 * g, 2 * g + 2)
                    dve.tensor_tensor(bias[:, heads], top[:, heads], minus_qscale[:, heads], ALU.mult).then_inc(s["bias"], 1)

                def masked(w, u, g):
                    kind = 2 if isinstance(w, int) and w == 0 else u
                    need(dve, s["score"], PAIRS * w + g + 1)
                    if g == 0:
                        need(dve, s["qk"], w + 1)
                        need(dve, s["p_t"], PAIRS * w)
                        dve.tensor_scalar(minus_qscale[:, :], qscale[:, u, :], -1.0, None, ALU.mult)
                    else:
                        biases(w, g - 1)
                    for h in range(2):
                        r = dve.tensor_tensor_reduce(scores[:, 2 * g + h, :], m.ps[:, SCORE + g % 2, h * 2 * P:(h + 1) * 2 * P],
                                                     mask[:, kind, :, :].rearrange("p b k -> p (b k)"), 1.0, -3e38,
                                                     ALU.add, ALU.max, top[:, 2 * g + h:2 * g + h + 1])
                    r.then_inc(s["masked"], 1)
                    if g == PAIRS - 1:
                        biases(w, g)

                def take_weights(w, g):
                    need(dve, s["p_t"], PAIRS * w + g + 1)
                    need(dve, s["pv"], w)
                    dve.tensor_copy(pt[:, g, :, :].rearrange("p n k -> p (n k)"), m.ps[:, PTURN, :]).then_inc(s["p_dve"], 1)

                def divide(w):
                    need(dve, s["exp"], PAIRS * (w + 1))
                    dve.reciprocal(rtotal[:, :], total[:, :]).then_inc(s["recip"], 1)

                def take_o(w):
                    need(dve, s["recip"], w + 1)
                    need(dve, s["pv"], w + 1)
                    need(dve, s["o_t"], w)
                    dve.tensor_tensor(o[:, :].rearrange("p (h d) -> p h d", d=DH), m.ps[:, OUT, :].rearrange("p (h d) -> p h d", d=DH),
                                      rtotal[:, :].unsqueeze(2).broadcast_to([P, HEADS, DH]), ALU.mult).then_inc(s["o"], 1)

                def residual(w):
                    need(dve, s["proj"], w + 1)
                    y = m.y[:, bass.ts(w, 1), :]
                    dve.tensor_tensor(y, y, m.ps[:, OUT:OUT + 1, 0:D], ALU.add).then_inc(s["y"], 1)

                def step(i, u):
                    now, ahead = exists(i), exists(i + 1)
                    if now:
                        take_weights(i, 0)
                        take_weights(i, 2)
                        divide(i)
                    if exists(i + 2):
                        rotate(i + 2, u)
                    if ahead:
                        masked(i + 1, 1 - u, 0)
                        masked(i + 1, 1 - u, 1)
                    if exists(i - 1):
                        residual(i - 1)
                    if ahead:
                        masked(i + 1, 1 - u, 2)
                    if now:
                        take_o(i)
                    if ahead:
                        masked(i + 1, 1 - u, 3)

                run(step, dve.Fori)


MLP_SCALE = 64.0
MLP_TILES = -(-HID // P)


def gated_mlp_statistics(nc, m, b, a, layer):
    ET, LOADS = MLP_TILES, 10
    full, rest = (ET - 1) * P, HID - (ET - 1) * P
    with ExitStack() as ctx:
        def sb(name, shape, dt=F32):
            return ctx.enter_context(nc.sbuf_tensor(f"gs_{name}", shape, dt))

        six = sb("six", [P, 2, TILES, 6])
        gap = sb("gap", [P, 2, TILES])
        mean2 = sb("mean2", [P, 2, TILES])
        sq = sb("sq", [P, 2, TILES])
        moved = sb("moved", [P, 2, TILES])
        own = sb("own", [P, 2, TILES])
        pick = sb("pick", [P, P])
        minus = sb("minus", [P, 1])
        w1_whole = sb("w1_whole", [P, KD, 2 * HID])
        w2_whole = sb("w2_whole", [P, ET, D])
        with stage(nc, "gs", "w_in", "w_high", "w_low", "w_zeroed", "six", "dve", "half", "zeroed", "shifted", "var", "rstd", "back", "pick", "minus", "mm", "end") as (block, s):
            last = TILES - 1

            @block.scalar
            def _(act):
                act.dma_start(w1_whole[:, :, :], layer_of(a["w1"], layer).rearrange("o (k p) e -> p (o k) e", p=P)).then_inc(s["w_in"], 16)
                w2_l = layer_of(a["w2"], layer).rearrange("o e d -> (o e) d")
                act.dma_start(w2_whole[:, 0:ET - 1, :], w2_l[0:full, :].rearrange("(t p) d -> p t d", p=P)).then_inc(s["w_in"], 16)
                act.dma_start(b.b2[:, :], layer_of(a["b2"], layer).rearrange("o d -> (o d)").partition_broadcast(P)).then_inc(s["w_in"], 16)
                for to, name in ((b.lng, "ln_g"), (b.lnb, "ln_b")):
                    act.dma_start(to[:, :], layer_of(a[name], layer).rearrange("o (k p) -> p (o k)", p=P), allow_slow_non_contiguous=True).then_inc(s["w_in"], 16)
                act.wait_ge(s["w_zeroed"], 1)
                act.dma_start(w2_whole[0:rest, ET - 1, :], w2_l[full:HID, :]).then_inc(s["w_in"], 16)
                b1_l = layer_of(a["b1"], layer).rearrange("o e -> (o e)")
                for n in range(2):
                    part = b1_l[n * HID:(n + 1) * HID]
                    act.dma_start(b.b1[:, n, 0:ET - 1], part[0:full].rearrange("(t p) -> p t", p=P), allow_slow_non_contiguous=True).then_inc(s["w_in"], 16)
                    act.dma_start(b.b1[0:rest, n, ET - 1:ET], part[full:HID].rearrange("(p t) -> p t", t=1), allow_slow_non_contiguous=True).then_inc(s["w_in"], 16)
                act.wait_ge(s["w_in"], 16 * LOADS)
                for whole, to in ((w1_whole, b.w1), (w2_whole, b.w2)):
                    act.activation(to[:, 0, :, :], whole[:, :, :], ACT.Copy, scale=MLP_SCALE).then_inc(s["w_high"], 1)

            @block.gpsimd
            def _(pool):
                pool.memset(w2_whole[:, ET - 1, :], 0.0)
                pool.memset(b.b1[:, :, ET - 1:ET], 0.0).then_inc(s["w_zeroed"], 1)
                pool.memset(moved[:, :, :], 0.0)
                pool.memset(m.next[:, :, :], 0.0)
                pool.memset(pick[:, :], 0.0).then_inc(s["zeroed"], 1)
                pool.wait_ge(s["zeroed"], 1)
                pool.memset(pick[0:1, :], 1.0).then_inc(s["pick"], 1)
                pool.wait_ge(s["var"], 1)
                pool.tensor_tensor(own[:, 1, :], own[:, 1, :], m.minus_half[:, 0:TILES], ALU.pow).then_inc(s["rstd"], 1)

            @block.sync
            def _(sp):
                sp.wait_ge(s["zeroed"], 1)
                sp.wait_ge(s["half"], 1)
                for n, src in enumerate((mean2[:, 1, :], sq[:, 1, :])):
                    sp.dma_start(moved[1:P, n, :], src[0:P - 1, :]).then_inc(s["shifted"], 16)
                    sp.dma_start(moved[0:1, n, 1:TILES], src[P - 1:P, 0:last]).then_inc(s["shifted"], 16)
                sp.wait_ge(s["rstd"], 1)
                sp.dma_start(m.next[0:P - 1, :, :], own[1:P, :, :]).then_inc(s["back"], 16)
                sp.dma_start(m.next[P - 1:P, :, 0:last], own[0:1, :, 1:TILES]).then_inc(s["back"], 16)
                sp.wait_ge(s["back"], 32)

            @block.vector
            def _(dve):
                with dve.Fori(0, TILES // 4) as k:
                    for u in range(4):
                        for h in range(2):
                            t = bass.ts(k * 4 + u, 1)
                            dve.bn_stats(six[:, h, t, :], m.y[:, t, h * P:(h + 1) * P]).then_inc(s["six"], 1)
                dve.wait_ge(s["six"], 2 * TILES)
                even, odd = six[:, :, :, 1], six[:, :, :, 4]
                dve.tensor_tensor(gap[:, :, :], even, odd, ALU.subtract).then_inc(s["dve"], 1)
                dve.tensor_tensor(mean2[:, :, :], even, odd, ALU.add).then_inc(s["dve"], 1)
                dve.tensor_tensor(sq[:, :, :], six[:, :, :, 2], six[:, :, :, 5], ALU.add).then_inc(s["dve"], 1)
                dve.wait_ge(s["dve"], 3)
                dve.tensor_scalar(mean2[:, :, :], mean2[:, :, :], 0.5, None, ALU.mult).then_inc(s["dve"], 1)
                dve.scalar_tensor_tensor(gap[:, :, :], gap[:, :, :], P / 4.0, gap[:, :, :], ALU.mult, ALU.mult).then_inc(s["dve"], 1)
                dve.wait_ge(s["dve"], 5)
                dve.tensor_tensor(sq[:, :, :], sq[:, :, :], gap[:, :, :], ALU.add).then_inc(s["half"], 1)
                dve.wait_ge(s["w_in"], 16 * LOADS)
                dve.tensor_scalar(b.b1_scaled[:, :], b.b1[:, 0, :], MLP_SCALE, None, ALU.mult)
                for n, (whole, to) in enumerate(((w1_whole, b.w1), (w2_whole, b.w2))):
                    dve.wait_ge(s["w_high"], n + 1)
                    dve.scalar_tensor_tensor(to[:, 1, :, :], whole[:, :, :], MLP_SCALE, to[:, 0, :, :], ALU.mult, ALU.subtract).then_inc(s["w_low"], 1)
                dve.wait_ge(s["half"], 1)
                dve.wait_ge(s["shifted"], 64)
                first, second = mean2[:, 0, :], moved[:, 0, :]
                dve.tensor_tensor(own[:, 0, :], first, second, ALU.add).then_inc(s["dve"], 1)
                dve.tensor_tensor(gap[:, 0, :], first, second, ALU.subtract).then_inc(s["dve"], 1)
                dve.tensor_tensor(own[:, 1, :], sq[:, 0, :], moved[:, 1, :], ALU.add).then_inc(s["dve"], 1)
                dve.wait_ge(s["dve"], 8)
                dve.tensor_scalar(own[:, 0, :], own[:, 0, :], 0.5, None, ALU.mult).then_inc(s["dve"], 1)
                dve.tensor_scalar(own[:, 1, :], own[:, 1, :], 1.0 / D, LN_EPS, ALU.mult, ALU.add).then_inc(s["dve"], 1)
                dve.scalar_tensor_tensor(gap[:, 0, :], gap[:, 0, :], 0.25, gap[:, 0, :], ALU.mult, ALU.mult).then_inc(s["dve"], 1)
                dve.wait_ge(s["dve"], 11)
                dve.tensor_tensor(own[:, 1, :], own[:, 1, :], gap[:, 0, :], ALU.add).then_inc(s["var"], 1)
                dve.wait_ge(s["rstd"], 1)
                dve.tensor_copy(m.mean[:, :], own[:, 0, :])
                dve.tensor_copy(m.rstd[:, :], own[:, 1, :])
                dve.scalar_tensor_tensor(minus[:, :], own[:, 0, 0:1], -1.0, own[:, 1, 0:1], ALU.mult, ALU.mult).then_inc(s["minus"], 1)
                dve.wait_ge(s["mm"], 1)
                dve.tensor_copy(m.first[:, :], m.ps[:, 0, 0:1]).then_inc(s["end"], 1)

            @block.tensor
            def _(pe):
                pe.wait_ge(s["pick"], 1)
                pe.wait_ge(s["minus"], 1)
                pe.matmul(m.ps[:, 0, 0:1], pick[:, :], minus[:, :], start=True, stop=True).then_inc(s["mm"], 1)


def gated_mlp(nc, m, b, a, layer):
    SCALE = MLP_SCALE
    TERMS = (0, 0), (0, 1), (1, 0)
    ET = MLP_TILES
    sizes = [min(P, HID - e * P) for e in range(ET)]
    with ExitStack() as ctx:
        def sb(name, shape, dt=F32):
            return ctx.enter_context(nc.sbuf_tensor(f"gm_{name}", shape, dt))

        normed = sb("normed", [P, 2, TPC, D])
        ht_whole = sb("ht_whole", [P, 2, KD, CHUNK + 4])
        ht = sb("ht", [P, 2, 2, KD, CHUNK], F16)
        gelu = sb("gelu", [P, 2, CHUNK])
        hid_whole = sb("hid_whole", [P, 2, CHUNK])
        hid = sb("hid", [P, 2, 2, ET, CHUNK], F16)
        with stage(nc, "gm", "next_in", "zeroed", "before", "normed", "turned", "ht_whole", "ht_high", "ht", "a_mm", "g_mm", "gelu",
                   "hid_whole", "hid_high", "hid", "out", "b2", "y") as (block, s):
            def run(step, loop):
                with loop(0, CHUNKS // 2 - 1) as k:
                    step(k * 2, 0)
                    step(k * 2 + 1, 1)
                step(CHUNKS - 2, 0)
                step(CHUNKS - 1, 1)

            def exists(c):
                return not isinstance(c, int) or c < CHUNKS

            @block.sync
            def _(sp):
                load_attention(sp, m, a, DEPTH - 1 - layer, s["next_in"])
                sp.wait_ge(s["next_in"], 16 * ATTENTION_LOADS)

            @block.gpsimd
            def _(pool):
                credit(pool, s["b2"])
                pool.memset(hid[:, :, :, ET - 1, :], 0.0).then_inc(s["zeroed"], 1)

                def bias(c, u):
                    need(pool, s["normed"], c + 1)
                    y = m.y[:, bass.ts(c, TPC), :]
                    pool.tensor_tensor(y, y, b.b2[:, :].unsqueeze(1).broadcast_to([P, TPC, D]), ALU.add).then_inc(s["b2"], 1)

                in_pairs(pool, CHUNKS, bias)

            @block.vector
            def _(dve):
                credit(dve, s["normed"], s["ht"], s["hid_whole"], s["hid"], s["y"])
                dve.wait_ge(s["zeroed"], 1)

                def norm(c, u):
                    need(dve, s["turned"], KD * (c - 1))
                    for j in range(TPC):
                        t = bass.ts(c * TPC + j, 1)
                        for h, (mean, rstd) in enumerate(((m.mean, m.rstd), (m.next[:, 0, :], m.next[:, 1, :]))):
                            n = dve.tensor_scalar(normed[:, u, j:j + 1, h * P:(h + 1) * P], m.y[:, t, h * P:(h + 1) * P],
                                                  mean[:, t], rstd[:, t], ALU.subtract, ALU.mult)
                    n.then_inc(s["normed"], 1)

                def ht_low(c, u):
                    need(dve, s["a_mm"], ET * (c - 1))
                    for k in range(KD):
                        need(dve, s["ht_high"], KD * c + k + 1)
                        dve.tensor_tensor(ht[:, u, 1, k, :], ht_whole[:, u, k, 0:CHUNK], ht[:, u, 0, k, :], ALU.subtract).then_inc(s["ht"], 1)

                def gate(c, u):
                    def low(e):
                        need(dve, s["hid_high"], ET * c + e + 1)
                        rows = slice(0, sizes[e])
                        dve.scalar_tensor_tensor(hid[rows, u, 1, e, :], hid_whole[rows, e % 2, :], 1 / SCALE, hid[rows, u, 0, e, :],
                                                 ALU.mult, ALU.subtract).then_inc(s["hid"], 1)

                    need(dve, s["out"], TPC * (c - 1))
                    for e in range(ET):
                        need(dve, s["a_mm"], ET * c + e + 1)
                        need(dve, s["gelu"], ET * c + e + 1)
                        need(dve, s["hid"], ET * c + e - 2 + 1)
                        rows = slice(0, sizes[e])
                        dve.scalar_tensor_tensor(hid_whole[rows, e % 2, :], m.ps[rows, 2 + 2 * (e % 2), :], b.b1_scaled[rows, e:e + 1],
                                                 gelu[rows, e % 2, :], ALU.add, ALU.mult).then_inc(s["hid_whole"], 1)
                        if e:
                            low(e - 1)
                    low(ET - 1)

                def residual(c):
                    need(dve, s["b2"], c + 1)
                    for j in range(TPC):
                        need(dve, s["out"], TPC * c + j + 1)
                        y = m.y[:, bass.ts(c * TPC + j, 1), :]
                        dve.scalar_tensor_tensor(y, m.ps[:, 6 + j % 2:7 + j % 2, 0:D], 1 / SCALE, y, ALU.mult, ALU.add).then_inc(s["y"], 1)

                def step(c, u):
                    gate(c, u)
                    if exists(c + 1):
                        ht_low(c + 1, 1 - u)
                    residual(c)
                    if exists(c + 2):
                        norm(c + 2, u)

                norm(0, 0)
                norm(1, 1)
                ht_low(0, 0)
                run(step, dve.Fori)

            @block.scalar
            def _(act):
                credit(act, s["ht_whole"], s["ht_high"], s["gelu"], s["hid_high"])
                act.activation(ht_whole[:, 1, 1, CHUNK:CHUNK + 1], m.first[:, :], ACT.Identity, bias=b.lnb[:, 1:2],
                               scale=b.lng[:, 1:2]).then_inc(s["before"], 1)
                act.wait_ge(s["before"], 1)
                act.wait_ge(s["zeroed"], 1)

                def scaled(c, u):
                    need(act, s["ht"], KD * (c - 1))
                    need(act, s["turned"], KD * c + 1)
                    act.activation(ht_whole[:, u, 0, 0:CHUNK], m.ps[:, 0, :], ACT.Identity, bias=b.lnb[:, 0:1], scale=b.lng[:, 0:1]).then_inc(s["ht_whole"], 1)
                    need(act, s["turned"], KD * c + 2)
                    need(act, s["ht_whole"], KD * c)
                    act.copy(ht_whole[:, u, 1, 0:1], ht_whole[:, 1 - u, 1, CHUNK:CHUNK + 1])
                    act.activation(ht_whole[:, u, 1, 1:CHUNK + 1], m.ps[:, 1, :], ACT.Identity, bias=b.lnb[:, 1:2], scale=b.lng[:, 1:2]).then_inc(s["ht_whole"], 1)
                    need(act, s["a_mm"], ET * (c - 1))
                    for k in range(KD):
                        need(act, s["ht_whole"], KD * c + k + 1)
                        act.copy(ht[:, u, 0, k, :], ht_whole[:, u, k, 0:CHUNK]).then_inc(s["ht_high"], 1)

                def gelus(c, u):
                    def high(e):
                        need(act, s["hid_whole"], ET * c + e + 1)
                        rows = slice(0, sizes[e])
                        act.activation(hid[rows, u, 0, e, :], hid_whole[rows, e % 2, :], ACT.Copy, scale=1 / SCALE).then_inc(s["hid_high"], 1)

                    for e in range(ET):
                        need(act, s["g_mm"], ET * c + e + 1)
                        need(act, s["hid_whole"], ET * c + e - 2 + 1)
                        rows = slice(0, sizes[e])
                        act.activation(gelu[rows, e % 2, :], m.ps[rows, 3 + 2 * (e % 2), :], ACT.Gelu, bias=b.b1[rows, 1, e:e + 1],
                                       scale=1 / SCALE).then_inc(s["gelu"], 1)
                        if e:
                            high(e - 1)
                    high(ET - 1)

                def step(c, u):
                    gelus(c, u)
                    if exists(c + 1):
                        scaled(c + 1, 1 - u)

                scaled(0, 0)
                run(step, act.Fori)

            @block.tensor
            def _(pe):
                credit(pe, s["turned"], s["a_mm"], s["g_mm"], s["out"])

                def turn(c, u):
                    need(pe, s["normed"], c + 1)
                    for k in range(KD):
                        need(pe, s["ht_whole"], KD * (c - 1) + k + 1)
                        for j in range(TPC):
                            t = pe.transpose(m.ps[:, k, j * P:(j + 1) * P], normed[:, u, j, k * P:(k + 1) * P], m.ident[:, :])
                        t.then_inc(s["turned"], 1)

                def up(c, u):
                    need(pe, s["ht"], KD * (c + 1))
                    for e in range(ET):
                        for part, mm_sem, free in ((1, s["g_mm"], s["gelu"]), (0, s["a_mm"], s["hid_whole"])):
                            need(pe, free, ET * c + e - 2 + 1)
                            terms = [(k, p, q) for k in range(KD) for p, q in TERMS]
                            for i, (k, p, q) in enumerate(terms):
                                mm = pe.matmul(m.ps[0:sizes[e], 2 + 2 * (e % 2) + part, :],
                                               b.w1[:, p, k, part * HID + e * P:part * HID + e * P + sizes[e]], ht[:, u, q, k, :],
                                               start=(i == 0), stop=(i == len(terms) - 1))
                            mm.then_inc(mm_sem, 1)

                def down(c, u):
                    need(pe, s["hid"], ET * (c + 1))
                    for j in range(TPC):
                        need(pe, s["y"], TPC * c + j - 2 + 1)
                        terms = [(e, p, q) for e in range(ET) for p, q in TERMS]
                        for i, (e, p, q) in enumerate(terms):
                            mm = pe.matmul(m.ps[:, 6 + j % 2, 0:D], hid[:, u, p, e, j * P:(j + 1) * P], b.w2[:, q, e, :],
                                           start=(i == 0), stop=(i == len(terms) - 1))
                        mm.then_inc(s["out"], 1)

                def step(c, u):
                    up(c, u)
                    if exists(c + 1):
                        turn(c + 1, 1 - u)
                    down(c, u)

                turn(0, 0)
                run(step, pe.Fori)


def gated_mlp_layer(nc, m, f, layer):
    with ExitStack() as ctx:
        def sb(name, shape, dt=F32):
            return ctx.enter_context(nc.sbuf_tensor(f"gw_{name}", shape, dt))

        b = Memory()
        b.w1 = sb("w1", [P, 2, KD, 2 * HID], F16)
        b.w2 = sb("w2", [P, 2, MLP_TILES, D], F16)
        b.b1, b.b1_scaled = sb("b1", [P, 2, MLP_TILES]), sb("b1_scaled", [P, MLP_TILES])
        b.b2 = sb("b2", [P, D])
        b.lng, b.lnb = sb("lng", [P, KD]), sb("lnb", [P, KD])
        gated_mlp_statistics(nc, m, b, f, layer)
        gated_mlp(nc, m, b, f, layer)



GROUP = 4
GROUPS = L1_HEADS // GROUP
QUAD = 32
ROWS = 4 * L1_DH
MPARTS = 3
MASKED = -1e30


def attention1_projections(nc, m, a):
    OUTS = 2 * KD
    with ExitStack() as ctx:
        def sb(name, shape, dt=F32):
            return ctx.enter_context(nc.sbuf_tensor(f"a1_{name}", shape, dt))

        w = sb("w", [P, 5, KD, D])
        normed = sb("normed", [P, 2, TPC, D])
        ht = sb("ht", [P, 2, KD, CHUNK])
        table = sb("table", [P, 2, 2, CHUNK])
        straight = sb("straight", [P, 2, CHUNK])
        crossed = sb("crossed", [P, 2, CHUNK])
        parts = sb("parts", [P, 2, 2, CHUNK], F16)
        with stage(nc, "a1", "w_in", "table_even", "table_odd", "ones", "normed", "turned", "ht", "mm", "v_mm", "rot", "sum", "high", "low", "v", "out_even", "out_odd") as (block, s):

            table_in, parts_out = (s["table_even"], s["table_odd"]), (s["out_even"], s["out_odd"])

            @block.sync
            def _(sp):
                for n, name in enumerate(("WQ", "WK", "WQ_swapped", "WK_swapped", "WV")):
                    sp.dma_start(w[:, n, :, :], a[name].rearrange("(k p) e -> p k e", p=P)).then_inc(s["w_in"], 16)

            @block.gpsimd
            def _(pool):
                credit(pool, s["sum"])
                pool.memset(m.v17[:, :, :, L1_DH:L1_DH + 1], 1.0).then_inc(s["ones"], 1)

                def load(c, u):
                    need(pool, s["rot"], OUTS * (c - 1))
                    pool.dma_start(table[:, u, :, :], a["rope"][:, :, bass.ts(c, CHUNK)]).then_inc(table_in[u], 16)

                def add(c, u):
                    for n in range(OUTS):
                        need(pool, s["rot"], OUTS * c + n + 1)
                        pool.tensor_tensor(straight[:, n % 2, :], straight[:, n % 2, :], crossed[:, n % 2, :], ALU.add).then_inc(s["sum"], 1)

                ahead_in_pairs(pool, CHUNKS, load, add)

            @block.vector
            def _(dve):
                credit(dve, s["normed"], s["rot"], s["low"])

                def norm(c, u):
                    need(dve, s["turned"], KD * (c - 1))
                    for j in range(TPC):
                        t = bass.ts(c * TPC + j, 1)
                        n = dve.tensor_scalar(normed[:, u, j:j + 1, :], m.x[:, t, :], m.mean[:, t], m.rstd[:, t], ALU.subtract, ALU.mult)
                    n.then_inc(s["normed"], 1)

                def rotate(c, u):
                    dve.wait_ge(table_in[u], (c - u) * 8 + 16)

                    def low(n):
                        need(dve, s["high"], OUTS * c + n + 1)
                        dve.tensor_tensor(parts[:, n % 2, 1, :], straight[:, n % 2, :], parts[:, n % 2, 0, :], ALU.subtract).then_inc(s["low"], 1)

                    for n in range(OUTS):
                        need(dve, s["mm"], OUTS * c + n + 1)
                        scale = L1_DH ** -0.5 if n < KD else 1.0
                        need(dve, s["low"], OUTS * c + n - 2 + 1)
                        for k, to in enumerate((straight, crossed)):
                            r = dve.scalar_tensor_tensor(to[:, n % 2, :], m.ps[:, 2 + 2 * (n % 2) + k, :], scale, table[:, u, k, :],
                                                         ALU.mult, ALU.mult)
                        r.then_inc(s["rot"], 1)
                        if n:
                            low(n - 1)
                    low(OUTS - 1)

                ahead_in_pairs(dve, CHUNKS, norm, rotate)

            @block.scalar
            def _(act):
                credit(act, s["ht"], s["high"], s["v"], s["out_even"], s["out_odd"])
                act.wait_ge(s["ones"], 1)

                def scaled(c, u):
                    need(act, s["mm"], OUTS * (c - 1))
                    need(act, s["v_mm"], 2 * (c - 1))
                    for k in range(KD):
                        need(act, s["turned"], KD * c + k + 1)
                        act.activation(ht[:, u, k, :], m.ps[:, k, :], ACT.Identity, bias=m.modc[:, k:k + 1],
                                       scale=m.modc[:, KD + k:KD + k + 1]).then_inc(s["ht"], 1)

                def store(c, n):
                    need(act, s["low"], OUTS * c + n + 1)
                    act.dma_start(m.qk[n // KD, :, (n % KD) * P:(n % KD + 1) * P, bass.ts(c, CHUNK)].rearrange("i p t -> p i t"),
                                  parts[:, n % 2, :, :]).then_inc(parts_out[n % 2], 16)

                def high(c, u):
                    for n in range(OUTS):
                        need(act, s["sum"], OUTS * c + n + 1)
                        need(act, parts_out[n % 2], 16 * (OUTS // 2 * c + n // 2))
                        act.copy(parts[:, n % 2, 0, :], straight[:, n % 2, :]).then_inc(s["high"], 1)
                        if n:
                            store(c, n - 1)
                    for b in range(2):
                        need(act, s["v_mm"], 2 * c + b + 1)
                        act.copy(m.v17[:, bass.ts(c * 2 + b, 2), :, 0:L1_DH],
                                 m.ps[:, 6 + b, :].rearrange("p (j h d) -> p j h d", j=2, d=L1_DH)).then_inc(s["v"], 1)
                    store(c, OUTS - 1)

                ahead_in_pairs(act, CHUNKS, scaled, high)
                for done in parts_out:
                    need(act, done, 16 * OUTS // 2 * CHUNKS)

            @block.tensor
            def _(pe):
                credit(pe, s["turned"], s["mm"], s["v_mm"])
                pe.wait_ge(s["w_in"], 16 * 5)

                def turn(c, u):
                    need(pe, s["normed"], c + 1)
                    for k in range(KD):
                        need(pe, s["ht"], KD * (c - 1) + k + 1)
                        for j in range(TPC):
                            t = pe.transpose(m.ps[:, k, j * P:(j + 1) * P], normed[:, u, j, k * P:(k + 1) * P], m.ident[:, :])
                        t.then_inc(s["turned"], 1)

                def products(c, u):
                    need(pe, s["ht"], KD * (c + 1))
                    for n in range(OUTS):
                        need(pe, s["rot"], OUTS * c + n - 2 + 1)
                        o = n % KD
                        for swapped in range(2):
                            for k in range(KD):
                                mm = pe.matmul(m.ps[:, 2 + 2 * (n % 2) + swapped, :], w[:, n // KD + 2 * swapped, k, o * P:(o + 1) * P],
                                               ht[:, u, k, :], start=(k == 0), stop=(k == KD - 1))
                        mm.then_inc(s["mm"], 1)
                    for b in range(2):
                        need(pe, s["v"], 2 * (c - 1) + b + 1)
                        for j in range(2):
                            for k in range(KD):
                                mm = pe.matmul(m.ps[:, 6 + b, j * D:(j + 1) * D], ht[:, u, k, (2 * b + j) * P:(2 * b + j + 1) * P],
                                               w[:, 4, k, :], start=(k == 0), stop=(k == KD - 1))
                        mm.then_inc(s["v_mm"], 1)

                ahead_in_pairs(pe, CHUNKS, turn, products)


def attention1(nc, m):
    with ExitStack() as ctx:
        def sb(name, shape, dt=F32):
            return ctx.enter_context(nc.sbuf_tensor(f"s1_{name}", shape, dt))

        b = Memory()
        b.keys_max = sb("keys_max", [P, GROUP, N], F16)
        b.keys_now = sb("keys_now", [P, GROUP, N], F16)
        b.q_max = sb("q_max", [P, 2, GROUP, CHUNK], F16)
        b.q_now = sb("q_now", [P, 2, GROUP, CHUNK], F16)
        b.v_now = sb("v_now", [P, 4, GROUP, QUAD])
        b.weights = sb("weights", [P, 2, 2, 2, CHUNK])
        b.tops = sb("tops", [P, CHUNKS, TILES, GROUP])
        b.minus_top = sb("minus_top", [P, GROUP, TILES])
        b.zero16 = sb("zero16", [P, P], F16)
        b.rest = sb("rest", [P, P])
        b.top_parts = sb("top_parts", [P, MPARTS, P], F16)
        b.ident16 = sb("ident16", [P, P], BF16)
        b.later_key = sb("later_key", [P, P], BF16)
        b.later_key_t = sb("later_key_t", [P, P], BF16)
        b.o_t = sb("o_t", [P, CHUNK])
        b.recip = sb("recip", [P, TPC, GROUP])
        b.o_now = sb("o_now", [P, 2, TPC, GROUP, L1_DH])
        with stage(nc, "c1", "rows", "ones", "zeroed", "consts") as (block, s):

            @block.vector
            def _(dve):
                for buffer in (b.q_max, b.q_now):
                    dve.memset(buffer[ROWS:P, :, :, :], 0.0)
                dve.memset(b.keys_max[ROWS:P, :, :], 0.0)
                dve.memset(b.keys_now[ROWS:P, :, :], 0.0).then_inc(s["rows"], 1)
                dve.wait_ge(s["rows"], 1)
                dve.memset(b.keys_now[ROWS:ROWS + MPARTS, :, :], 1.0).then_inc(s["ones"], 1)

            @block.gpsimd
            def _(pool):
                pool.memset(b.v_now[:, :, :, :], 0.0)
                for square in (b.zero16, b.ident16, b.later_key, b.later_key_t):
                    z = pool.memset(square[:, :], 0.0)
                z.then_inc(s["zeroed"], 1)
                pool.wait_ge(s["zeroed"], 1)
                pool.affine_select(b.ident16[:, :], b.ident16[:, :], pattern=[[-1, P]], compare_op=ALU.not_equal, fill=1.0,
                                   base=0, channel_multiplier=1)
                pool.affine_select(b.later_key[:, :], b.later_key[:, :], pattern=[[-1, P]], compare_op=ALU.is_ge, fill=MASKED,
                                   base=0, channel_multiplier=1)
                pool.affine_select(b.later_key_t[:, :], b.later_key_t[:, :], pattern=[[1, P]], compare_op=ALU.is_ge, fill=MASKED,
                                   base=0, channel_multiplier=-1).then_inc(s["consts"], 1)

        attend_and_find(nc, m, b, "f1", None, 0)
        with nc.Fori(0, GROUPS - 1) as g:
            attend_and_find(nc, m, b, "g1", g, g + 1)
        attend_and_find(nc, m, b, "h1", GROUPS - 1, None)


def attend_and_find(nc, m, b, name, group, next_group):
    MAX_BANK, SCORE, OUT = 0, 2, 6
    attends, finds = group is not None, next_group is not None
    MAX_BANKS = 2 if attends else 4
    PARTS = 4

    def before(j):
        return 2 * j * (j + 1)

    def steps(eng, j, step):
        step(0, 0, j, 0)
        if j:
            with eng.Fori(0, j) as c:
                for u in range(TPC):
                    step(c * TPC + 1 + u, None, c, u)
        for r in range(1, TPC):
            step(TPC * j + r, r, j, r)

    def parity(r, u, n):
        return (1 + u if r is None else r) % n

    with stage(nc, name, "k_first", "k_in", "qm_in_even", "qm_in_odd", "q_in_even", "q_in_odd", "v_now", "max_mm", "max", "cleared", "top", "top_t", "split", "split_step",
               "top_out", "score", "exp", "pv", "o_t", "o_turned", "recip", "o_now", "o_out_even", "o_out_odd") as (block, s):
        qm_in, q_in, o_out = (s["qm_in_even"], s["qm_in_odd"]), (s["q_in_even"], s["q_in_odd"]), (s["o_out_even"], s["o_out_odd"])

        @block.sync
        def _(sp):
            credit(sp, *o_out)

            def parts_of(part):
                return slice(part * L1_DH, (part + 1) * L1_DH)

            def load_q(to, g, j, sem):
                for part in range(PARTS):
                    sp.dma_start(to[parts_of(part), j % 2, :, :],
                                 m.qk[0, part // 2, bass.ts(g, GROUP * L1_DH), j * CHUNK:(j + 1) * CHUNK]
                                 .rearrange("(h d) t -> d h t", d=L1_DH)).then_inc(sem, 16)

            def store(j):
                need(sp, s["o_now"], j + 1)
                sp.dma_start(m.o[j * CHUNK:(j + 1) * CHUNK, bass.ts(group, GROUP * L1_DH)].rearrange("(t p) e -> p t e", p=P),
                             b.o_now[:, j % 2, :, :, :].rearrange("p t h d -> p t (h d)")).then_inc(o_out[j % 2], 16)

            def load_k(to, g, columns, sem):
                for part in range(PARTS):
                    sp.dma_start(to[parts_of(part), :, columns],
                                 m.qk[1, part % 2, bass.ts(g, GROUP * L1_DH), columns].rearrange("(h d) t -> d h t", d=L1_DH)).then_inc(sem, 16)

            def load_queries(j):
                if attends:
                    need(sp, s["score"], 2 * before(j - 1))
                    load_q(b.q_now, group, j, q_in[j % 2])
                    sp.dma_start(b.q_now[ROWS:ROWS + MPARTS, j % 2, :, :], m.tops[:, :, j * CHUNK:(j + 1) * CHUNK]).then_inc(q_in[j % 2], 16)
                if finds:
                    need(sp, s["max_mm"], GROUP * before(j - 1))
                    load_q(b.q_max, next_group, j, qm_in[j % 2])

            def load_keys(columns, sem):
                if attends:
                    load_k(b.keys_now, group, columns, sem)
                if finds:
                    load_k(b.keys_max, next_group, columns, sem)

            load_keys(slice(0, CHUNK), s["k_first"])
            load_queries(0)
            load_keys(slice(CHUNK, N), s["k_in"])
            for j in range(1, CHUNKS):
                load_queries(j)
                if attends and j >= 2:
                    store(j - 2)
            if attends:
                store(CHUNKS - 2)
                store(CHUNKS - 1)
                for n in range(2):
                    sp.wait_ge(q_in[n], 16 * (PARTS + 1) * CHUNKS // 2)
                    need(sp, o_out[n], 16 * CHUNKS // 2)
            if finds:
                sp.wait_ge(s["split"], 1)
                sp.dma_start(m.tops.rearrange("n h (i q) -> (h i) n q", q=P), b.top_parts[:, :, :]).then_inc(s["top_out"], 16)
                sp.wait_ge(s["top_out"], 16)

        @block.gpsimd
        def _(pool):
            credit(pool, s["v_now"])
            for j in range(CHUNKS if attends else 0):
                def step(p, r, c, t):
                    n = before(j) + p
                    need(pool, s["pv"], 2 * (n - 4) + 2)
                    pool.tensor_copy(b.v_now[:, parity(r, t, 4), :, 0:L1_DH + 1],
                                     m.v17[:, bass.ts(c * TPC + t, 1), bass.ts(group, GROUP), :].rearrange("p o h d -> p (o h) d")).then_inc(s["v_now"], 1)

                steps(pool, j, step)

        @block.tensor
        def _(pe):
            credit(pe, s["max_mm"], s["score"], s["pv"], s["o_turned"])

            def find_max(j, p, r, c, t, h):
                if not finds:
                    return
                width = CHUNK if r is None else (r + 1) * P
                need(pe, s["max"], GROUP * (before(j) + p) + h - MAX_BANKS + 1)
                mm = pe.matmul(m.ps[:, MAX_BANK + h % MAX_BANKS, 0:width], b.q_max[:, j % 2, h, t * P:(t + 1) * P],
                               b.keys_max[:, h, bass.ds(c * CHUNK, width)], start=True, stop=(r is None))
                if r is not None:
                    mm = pe.matmul(m.ps[:, MAX_BANK + h % MAX_BANKS, r * P:(r + 1) * P], b.ident16[:, :], b.later_key[:, :], start=False, stop=True)
                mm.then_inc(s["max_mm"], 1)

            def score(j, p, r, c, t, pair):
                if not attends:
                    return
                need(pe, s["exp"], 2 * (before(j) + p - 1) + pair + 1)
                skip = 0 if r is None else r * P
                for h in (2 * pair, 2 * pair + 1):
                    mm = pe.matmul(m.ps[:, SCORE + h, skip:CHUNK], b.keys_now[:, h, bass.ds((c * TPC + t) * P, P)],
                                   b.q_now[:, j % 2, h, skip:CHUNK], start=True, stop=(r is None))
                    if r is not None:
                        mm = pe.matmul(m.ps[:, SCORE + h, skip:skip + P], b.ident16[:, :], b.later_key_t[:, :], start=False, stop=True)
                mm.then_inc(s["score"], 1)

            def weigh(j, p, r, slot, pair):
                n = before(j) + p
                need(pe, s["exp"], 2 * n + pair + 1)
                need(pe, s["v_now"], n + 1)
                skip = 0 if r is None else r * P
                for h in (2 * pair, 2 * pair + 1):
                    mm = pe.matmul(m.ps[h * QUAD:(h + 1) * QUAD, OUT + j % 2, skip:CHUNK], b.v_now[:, slot % 4, h, :],
                                   b.weights[:, slot % 2, pair, h % 2, skip:CHUNK], start=False, stop=(r == TPC - 1), skip_group_check=True)
                mm.then_inc(s["pv"], 1)

            def weigh_before(j, p, r, t, pair):
                if not attends:
                    return
                if r is None:
                    weigh(j, p - 1, None, t, pair)
                elif r:
                    weigh(j, p - 1, r - 1 if r > 1 else None, r - 1, pair)
                elif j:
                    weigh(j - 1, TPC * j - 1, TPC - 1, TPC - 1, pair)

            def turn_o(j):
                need(pe, s["o_t"], j + 1)
                for t in range(TPC):
                    x = pe.transpose(m.ps[:, OUT + j % 2, t * P:(t + 1) * P], b.o_t[:, t * P:(t + 1) * P], m.ident[:, :])
                x.then_inc(s["o_turned"], 1)

            def step(j, p, r, c, t):
                find_max(j, p, r, c, t, 0)
                score(j, p, r, c, t, 0)
                find_max(j, p, r, c, t, 1)
                weigh_before(j, p, r, t, 0)
                weigh_before(j, p, r, t, 1)
                find_max(j, p, r, c, t, 2)
                score(j, p, r, c, t, 1)
                find_max(j, p, r, c, t, 3)
                if attends and r == 0:
                    need(pe, s["o_now"], j - 1)
                    pe.matmul(m.ps[:, OUT + j % 2, :], b.zero16[:, :], b.q_now[:, j % 2, 0, :], start=True, stop=False, skip_group_check=True)
                if attends and r == 1 and j:
                    turn_o(j - 1)

            pe.wait_ge(s["k_first"], 16 * PARTS * (attends + finds))
            for j in range(CHUNKS):
                if j == 1:
                    pe.wait_ge(s["k_in"], 16 * PARTS * (attends + finds))
                if attends:
                    pe.wait_ge(q_in[j % 2], 16 * (PARTS + 1) * (j // 2 + 1))
                if finds:
                    pe.wait_ge(qm_in[j % 2], 16 * PARTS * (j // 2 + 1))
                steps(pe, j, lambda p, r, c, t: step(j, p, r, c, t))
            if attends:
                for pair in range(2):
                    weigh(CHUNKS - 1, TPC * CHUNKS - 1, TPC - 1, TPC - 1, pair)
                turn_o(CHUNKS - 1)
            if finds:
                pe.wait_ge(s["top"], 1)
                pe.transpose(m.ps[:, MAX_BANK, 0:P], b.minus_top[:, :, :].rearrange("p h i -> p (h i)"), m.ident[:, :]).then_inc(s["top_t"], 1)

        @block.scalar
        def _(act):
            credit(act, s["exp"])
            for j in range(CHUNKS if attends else 0):
                def step(p, r, c, t):
                    n = before(j) + p
                    skip = 0 if r is None else r * P
                    for pair in range(2):
                        need(act, s["score"], 2 * n + pair + 1)
                        need(act, s["pv"], 2 * (n - 2) + pair + 1)
                        act.activation(b.weights[:, parity(r, t, 2), pair, :, skip:CHUNK],
                                       m.ps[:, SCORE + 2 * pair:SCORE + 2 * pair + 2, skip:CHUNK], ACT.Exp).then_inc(s["exp"], 1)

                steps(act, j, step)

        @block.vector
        def _(dve):
            credit(dve, s["max"], s["o_t"], s["recip"], s["o_now"])
            dve.memset(b.tops[:, :, :, :], -3e38).then_inc(s["cleared"], 1)
            dve.wait_ge(s["cleared"], 1)

            def row_max(j, p, r, c, t):
                n = GROUP * (before(j) + p)
                width = CHUNK if r is None else (r + 1) * P
                for h in range(GROUP if finds else 0):
                    need(dve, s["max_mm"], n + h + 1)
                    dve.tensor_reduce(b.tops[:, bass.ts(c, 1), j * TPC + t, h], m.ps[:, MAX_BANK + h % MAX_BANKS, 0:width], AX.X, ALU.max).then_inc(s["max"], 1)

            def take_o(j):
                need(dve, s["pv"], 2 * before(j + 1))
                need(dve, s["o_turned"], j)
                dve.tensor_copy(b.o_t[:, :], m.ps[:, OUT + j % 2, :]).then_inc(s["o_t"], 1)

            def divide_o(j):
                need(dve, s["o_turned"], j + 1)
                turned = m.ps[:, OUT + j % 2, :].rearrange("p (t h e) -> p t h e", t=TPC, e=QUAD)
                dve.reciprocal(b.recip[:, :, :], turned[:, :, :, L1_DH]).then_inc(s["recip"], 1)
                need(dve, s["recip"], j + 1)
                need(dve, o_out[j % 2], 16 * (j // 2))
                dve.tensor_tensor(b.o_now[:, j % 2, :, :, :], turned[:, :, :, 0:L1_DH],
                                  b.recip[:, :, :].unsqueeze(3).broadcast_to([P, TPC, GROUP, L1_DH]), ALU.mult).then_inc(s["o_now"], 1)

            for j in range(CHUNKS):
                def step(p, r, c, t):
                    row_max(j, p, r, c, t)
                    if attends and r == 0 and j:
                        take_o(j - 1)
                    if attends and r == 1 and j:
                        divide_o(j - 1)

                steps(dve, j, step)
            if attends:
                take_o(CHUNKS - 1)
                divide_o(CHUNKS - 1)
            if not finds:
                return
            need(dve, s["max"], GROUP * before(CHUNKS))
            dve.tensor_reduce(b.minus_top[:, :, :], b.tops[:, :, :, :].rearrange("p c i h -> p h i c"), AX.X, ALU.max, negate=True).then_inc(s["top"], 1)
            dve.wait_ge(s["top_t"], 1)
            dve.tensor_copy(b.rest[:, :], m.ps[:, MAX_BANK, 0:P]).then_inc(s["split_step"], 1)
            for n in range(MPARTS):
                dve.wait_ge(s["split_step"], 2 * n + 1)
                x = dve.tensor_copy(b.top_parts[:, n, :], b.rest[:, :])
                if n == MPARTS - 1:
                    x.then_inc(s["split"], 1)
                else:
                    x.then_inc(s["split_step"], 1)
                    dve.wait_ge(s["split_step"], 2 * n + 2)
                    dve.tensor_tensor(b.rest[:, :], b.rest[:, :], b.top_parts[:, n, :], ALU.subtract).then_inc(s["split_step"], 1)


def attention1_output(nc, m, a):
    with ExitStack() as ctx:
        def sb(name, shape, dt=F32):
            return ctx.enter_context(nc.sbuf_tensor(f"o1_{name}", shape, dt))

        wo = sb("wo", [P, KD, D])
        o = sb("o", [P, 2, TPC, D])
        ot = sb("ot", [P, 2, KD, CHUNK])
        gated = sb("gated", [P, 2, TPC, D])
        with stage(nc, "o1", "w_in", "o_in_even", "o_in_odd", "turned", "ot", "mm", "gated", "x") as (block, s):
            o_in = s["o_in_even"], s["o_in_odd"]

            @block.sync
            def _(sp):
                sp.dma_start(wo[:, :, :], a["WO"].rearrange("(k p) e -> p k e", p=P)).then_inc(s["w_in"], 16)

            @block.tensor
            def _(pe):
                credit(pe, s["turned"], s["mm"])
                pe.wait_ge(s["w_in"], 16)

                def turn(c, u):
                    pe.wait_ge(o_in[u], (c - u) * 8 + 16)
                    for k in range(KD):
                        need(pe, s["ot"], KD * (c - 1) + k + 1)
                        for j in range(TPC):
                            t = pe.transpose(m.ps[:, k, j * P:(j + 1) * P], o[:, u, j, k * P:(k + 1) * P], m.ident[:, :])
                        t.then_inc(s["turned"], 1)

                def products(c, u):
                    need(pe, s["ot"], KD * (c + 1))
                    for j in range(TPC):
                        need(pe, s["gated"], TPC * (c - 1) + j + 1)
                        for k in range(KD):
                            mm = pe.matmul(m.ps[:, 2 + j, 0:D], ot[:, u, k, j * P:(j + 1) * P], wo[:, k, :],
                                           start=(k == 0), stop=(k == KD - 1))
                        mm.then_inc(s["mm"], 1)

                ahead_in_pairs(pe, CHUNKS, turn, products)

            @block.scalar
            def _(act):
                credit(act, s["ot"])

                def load(c, u):
                    need(act, s["turned"], KD * (c - 1))
                    act.dma_start(o[:, u, :, :], m.o[bass.ts(c, CHUNK), :].rearrange("(t p) e -> p t e", p=P)).then_inc(o_in[u], 16)

                def take(c, u):
                    need(act, s["mm"], TPC * (c - 1))
                    for k in range(KD):
                        need(act, s["turned"], KD * c + k + 1)
                        act.copy(ot[:, u, k, :], m.ps[:, k, :]).then_inc(s["ot"], 1)

                ahead_in_pairs(act, CHUNKS, load, take)

            @block.vector
            def _(dve):
                credit(dve, s["gated"])

                def gate(c, u):
                    need(dve, s["x"], c - 1)
                    for j in range(TPC):
                        need(dve, s["mm"], TPC * c + j + 1)
                        dve.tensor_tensor(gated[:, u, j, :], m.ps[:, 2 + j, 0:D], m.modb[:, 2, :], ALU.mult).then_inc(s["gated"], 1)

                in_pairs(dve, CHUNKS, gate)

            @block.gpsimd
            def _(pool):
                credit(pool, s["x"])

                def residual(c, u):
                    need(pool, s["gated"], TPC * (c + 1))
                    x = m.x[:, bass.ts(c, TPC), :]
                    pool.tensor_tensor(x, x, gated[:, u, :, :], ALU.add).then_inc(s["x"], 1)

                in_pairs(pool, CHUNKS, residual)



TE = TILES * EXPERTS
SLOT_TILES = TOPK // P


def expert_scores(nc, m, a):
    with ExitStack() as ctx:
        def sb(name, shape, dt=F32):
            return ctx.enter_context(nc.sbuf_tensor(f"es_{name}", shape, dt))

        gate = sb("gate", [P, KD, EXPERTS])
        h = sb("h", [P, 2, TPC, D])
        ht = sb("ht", [P, 2, KD, CHUNK])
        top = sb("top", [P, TILES])
        total = sb("total", [P, TILES])
        with stage(nc, "es", "w_in", "normed", "scaled", "h", "h_even", "h_odd", "turned", "ht", "mm", "scores", "top", "less", "exp", "total", "recip", "probs") as (block, s):
            h_out = s["h_even"], s["h_odd"]
            probs = m.probs[:, :, :]

            @block.sync
            def _(sp):
                sp.dma_start(gate[:, :, :], a["L1_ffn_gate_w"].rearrange("(k p) e -> p k e", p=P)).then_inc(s["w_in"], 16)

            @block.vector
            def _(dve):
                credit(dve, s["normed"], s["scaled"])

                def norm(c, u):
                    need(dve, s["turned"], KD * (c - 1))
                    need(dve, h_out[u], (c - u) * 8)
                    for j in range(TPC):
                        t = bass.ts(c * TPC + j, 1)
                        n = dve.tensor_scalar(h[:, u, j:j + 1, :], m.x[:, t, :], m.mean[:, t], m.rstd[:, t], ALU.subtract, ALU.mult)
                    n.then_inc(s["normed"], 1)
                    need(dve, s["normed"], c + 1)
                    dve.tensor_tensor(h[:, u, :, :], h[:, u, :, :], m.modb[:, 4:5, :].broadcast_to([P, TPC, D]), ALU.mult).then_inc(s["scaled"], 1)

                in_pairs(dve, CHUNKS, norm)
                need(dve, s["scores"], CHUNKS)
                dve.tensor_reduce(top[:, :], probs, AX.X, ALU.max).then_inc(s["top"], 1)
                dve.wait_ge(s["top"], 1)
                dve.tensor_tensor(probs, probs, top[:, :].unsqueeze(2).broadcast_to([P, TILES, EXPERTS]), ALU.subtract).then_inc(s["less"], 1)
                dve.wait_ge(s["exp"], 1)
                dve.tensor_reduce(total[:, :], probs, AX.X, ALU.add).then_inc(s["total"], 1)
                dve.wait_ge(s["total"], 1)
                dve.reciprocal(total[:, :], total[:, :]).then_inc(s["recip"], 1)
                dve.wait_ge(s["recip"], 1)
                dve.tensor_tensor(probs, probs, total[:, :].unsqueeze(2).broadcast_to([P, TILES, EXPERTS]), ALU.mult).then_inc(s["probs"], 1)

            @block.gpsimd
            def _(pool):
                credit(pool, s["h"])

                def shift(c, u):
                    need(pool, s["scaled"], c + 1)
                    pool.tensor_tensor(h[:, u, :, :], h[:, u, :, :], m.modb[:, 3:4, :].broadcast_to([P, TPC, D]), ALU.add).then_inc(s["h"], 1)

                in_pairs(pool, CHUNKS, shift)

            @block.tensor
            def _(pe):
                credit(pe, s["turned"], s["mm"])
                pe.wait_ge(s["w_in"], 16)

                def turn(c, u):
                    need(pe, s["h"], c + 1)
                    for k in range(KD):
                        need(pe, s["ht"], KD * (c - 1) + k + 1)
                        for j in range(TPC):
                            t = pe.transpose(m.ps[:, k, j * P:(j + 1) * P], h[:, u, j, k * P:(k + 1) * P], m.ident[:, :])
                        t.then_inc(s["turned"], 1)

                def products(c, u):
                    need(pe, s["ht"], KD * (c + 1))
                    need(pe, s["scores"], c - 1)
                    for j in range(TPC):
                        for k in range(KD):
                            mm = pe.matmul(m.ps[:, 2 + u, j * EXPERTS:(j + 1) * EXPERTS], ht[:, u, k, j * P:(j + 1) * P], gate[:, k, :],
                                           start=(k == 0), stop=(k == KD - 1))
                    mm.then_inc(s["mm"], 1)

                ahead_in_pairs(pe, CHUNKS, turn, products)

            @block.scalar
            def _(act):
                credit(act, s["ht"], s["scores"], *h_out)

                def take(c, u):
                    need(act, s["h"], c + 1)
                    act.dma_start(m.h[bass.ts(c, CHUNK), :].rearrange("(t p) d -> p t d", p=P), h[:, u, :, :]).then_inc(h_out[u], 16)
                    need(act, s["mm"], c - 1)
                    for k in range(KD):
                        need(act, s["turned"], KD * c + k + 1)
                        act.copy(ht[:, u, k, :], m.ps[:, k, :]).then_inc(s["ht"], 1)

                def take_scores(c, u):
                    need(act, s["mm"], c + 1)
                    act.copy(m.probs[:, bass.ts(c, TPC), :],
                             m.ps[:, 2 + u, 0:TPC * EXPERTS].rearrange("p (t e) -> p t e", e=EXPERTS)).then_inc(s["scores"], 1)

                ahead_in_pairs(act, CHUNKS, take, take_scores)
                for stored in h_out:
                    need(act, stored, 16 * CHUNKS // 2)
                act.wait_ge(s["less"], 1)
                act.activation(probs, probs, ACT.Exp).then_inc(s["exp"], 1)


def choose_tokens(nc, m):
    BITS = 30
    CARRIED = 5
    WIDE = 8
    GROUPS_OF_TILES = TILES // WIDE
    with ExitStack() as ctx:
        def sb(name, shape, dt=F32):
            return ctx.enter_context(nc.sbuf_tensor(f"ct_{name}", shape, dt))

        bound = sb("bound", [P, EXPERTS], I32)
        trial = sb("trial", [P, EXPERTS], I32)
        bit = sb("bit", [P, EXPERTS], I32)
        enough = sb("enough", [P, EXPERTS], I32)
        by_expert = sb("by_expert", [P, EXPERTS, TILES])
        hits = sb("hits", [P, EXPERTS, TILES])
        equal = sb("equal", [P, EXPERTS, TILES])
        count = sb("count", [P, EXPERTS])
        wanted = sb("wanted", [P, EXPERTS])
        ones = sb("ones", [P, P])
        earlier = sb("earlier", [P, P])
        inclusive = sb("inclusive", [P, EXPERTS, TILES])
        rank = sb("rank", [P, EXPERTS, TILES])
        slot = sb("slot", [P, EXPERTS, TILES], I32)
        slot_tile = sb("slot_tile", [P, EXPERTS, TILES])
        piece = sb("piece", [P, EXPERTS, TILES], I32)
        tile = sb("tile", [P, TILES])
        row = sb("row", [P, 1])
        lane = sb("lane", [P, P])
        lane16 = sb("lane16", [P, P], BF16)
        slot_row16 = sb("slot_row16", [P, EXPERTS, TILES], BF16)
        hot = sb("hot", [P, TE, SLOT_TILES])
        part = sb("part", [P, 3, EXPERTS, TILES], BF16)
        carried = sb("carried", [P, EXPERTS, TILES, CARRIED, SLOT_TILES], BF16)
        row_hot = sb("row_hot", [P, 2, WIDE, P], BF16)
        found = sb("found", [P, EXPERTS, CARRIED, SLOT_TILES])
        with stage(nc, "ct", "consts", "zeroed", "dve", "trial", "count", "sum", "kept", "rank_in", "rank_mm", "hot", "carried", "row_hot", "gather", "taken") as (block, s):
            flat = lambda x: x[:, :, :].rearrange("p e t -> p (e t)")
            wide = lambda x: x.unsqueeze(2).broadcast_to([P, EXPERTS, TILES])
            PREFIX, TOTAL = 1, 2

            @block.gpsimd
            def _(pool):
                pool.memset(ones[:, :], 1.0)
                pool.memset(earlier[:, :], 1.0).then_inc(s["zeroed"], 1)
                pool.iota(tile[:, :], pattern=[[1, TILES]], base=0, channel_multiplier=0, allow_small_or_imprecise_dtypes=True)
                pool.iota(row[:, :], pattern=[[0, 1]], base=0, channel_multiplier=1, allow_small_or_imprecise_dtypes=True)
                pool.iota(lane[:, :], pattern=[[1, P]], base=0, channel_multiplier=0, allow_small_or_imprecise_dtypes=True)
                pool.wait_ge(s["zeroed"], 1)
                pool.affine_select(earlier[:, :], earlier[:, :], pattern=[[1, P]], compare_op=ALU.is_gt, fill=0.0, base=0,
                                   channel_multiplier=-1).then_inc(s["consts"], 1)
                pool.wait_ge(s["consts"], 1)
                pool.wait_ge(s["hot"], 1)
                hot4 = hot[:, :, :].rearrange("p (e t) s -> p e t s", e=EXPERTS)
                pool.tensor_tensor(carried[:, :, :, 0, :], hot4,
                                   tile[:, :].unsqueeze(1).unsqueeze(3).broadcast_to([P, EXPERTS, TILES, SLOT_TILES]), ALU.mult)
                pool.tensor_scalar(carried[:, :, :, 1, :], hot4, row[:, :], None, ALU.mult).then_inc(s["carried"], 1)

            @block.tensor
            def _(pe):
                pe.wait_ge(s["consts"], 1)
                with pe.Fori(0, BITS + 1) as i:
                    pe.wait_ge(s["count"], i + 1)
                    pe.matmul(m.ps[:, 0, 0:EXPERTS], ones[:, :], count[:, :], start=True, stop=True).then_inc(s["sum"], 1)
                for n in range(2):
                    pe.wait_ge(s["rank_in"], n + 1)
                    src = flat(equal) if n == 0 else flat(hits)
                    pe.matmul(m.ps[:, PREFIX, 0:TE], earlier[:, :], src, start=True, stop=True)
                    pe.matmul(m.ps[:, TOTAL, 0:TE], ones[:, :], src, start=True, stop=True).then_inc(s["rank_mm"], 1)
                pe.wait_ge(s["carried"], 2)
                with pe.Fori(0, EXPERTS) as e:
                    for g in range(GROUPS_OF_TILES):
                        pe.wait_ge(s["row_hot"], e * GROUPS_OF_TILES + g + 1)
                        for j in range(WIDE):
                            t = g * WIDE + j
                            mm = pe.matmul(m.ps[:, 3, bass.ts(e, CARRIED * SLOT_TILES)], row_hot[:, g % 2, j, :],
                                           carried[:, bass.ts(e, 1), t, :, :].rearrange("p o i s -> p (o i s)"),
                                           start=(t == 0), stop=(t == TILES - 1), skip_group_check=True)
                        mm.then_inc(s["gather"], 1)

            @block.vector
            def _(dve):
                done = 0

                def chain(instruction):
                    nonlocal done
                    instruction.then_inc(s["dve"], 1)
                    done += 1
                    dve.wait_ge(s["dve"], done)

                dve.tensor_copy(by_expert[:, :, :], m.probs[:, :, :].rearrange("p t e -> p e t"))
                dve.memset(bound[:, :], 0)
                chain(dve.memset(bit[:, :], 1 << (BITS - 1)))
                with dve.Fori(0, BITS) as i:
                    dve.tensor_tensor(trial[:, :], bound[:, :], bit[:, :], ALU.bitwise_or).then_inc(s["trial"], 1)
                    dve.wait_ge(s["trial"], i * 4 + 1)
                    dve.tensor_tensor(hits[:, :, :], by_expert[:, :, :], wide(trial[:, :].bitcast(F32)), ALU.is_ge).then_inc(s["trial"], 1)
                    dve.wait_ge(s["trial"], i * 4 + 2)
                    dve.tensor_reduce(count[:, :], hits[:, :, :], AX.X, ALU.add).then_inc(s["count"], 1)
                    dve.wait_ge(s["sum"], i + 1)
                    dve.tensor_scalar(enough[:, :], m.ps[:, 0, 0:EXPERTS], float(TOPK), None, ALU.is_ge).then_inc(s["trial"], 1)
                    dve.wait_ge(s["trial"], i * 4 + 3)
                    dve.tensor_scalar(bit[:, :], bit[:, :], 1, None, ALU.logical_shift_right).then_inc(s["trial"], 1)
                    dve.copy_predicated(bound[:, :], enough[:, :], trial[:, :]).then_inc(s["kept"], 1)
                    dve.wait_ge(s["trial"], i * 4 + 4)
                    dve.wait_ge(s["kept"], i + 1)
                limit = wide(bound[:, :].bitcast(F32))
                dve.tensor_tensor(equal[:, :, :], by_expert[:, :, :], limit, ALU.is_equal).then_inc(s["rank_in"], 1)
                chain(dve.tensor_tensor(hits[:, :, :], by_expert[:, :, :], limit, ALU.is_gt))
                dve.tensor_reduce(count[:, :], hits[:, :, :], AX.X, ALU.add).then_inc(s["count"], 1)
                dve.wait_ge(s["sum"], BITS + 1)
                chain(dve.tensor_scalar(wanted[:, :], m.ps[:, 0, 0:EXPERTS], -1.0, float(TOPK), ALU.mult, ALU.add))

                def ranks(n):
                    dve.wait_ge(s["rank_mm"], n + 1)
                    for e in range(EXPERTS):
                        x = dve.tensor_tensor_scan(inclusive[:, e, :], ones[:, 0:TILES], m.ps[:, TOTAL, e * TILES:(e + 1) * TILES], 0.0,
                                                   ALU.mult, ALU.add)
                    chain(x)
                    chain(dve.tensor_tensor(flat(rank), flat(inclusive), m.ps[:, TOTAL, 0:TE], ALU.subtract))
                    chain(dve.tensor_tensor(flat(rank), flat(rank), m.ps[:, PREFIX, 0:TE], ALU.add))

                ranks(0)
                chain(dve.tensor_tensor(rank[:, :, :], rank[:, :, :], wide(wanted[:, :]), ALU.is_lt))
                chain(dve.tensor_tensor(equal[:, :, :], equal[:, :, :], rank[:, :, :], ALU.mult))
                dve.tensor_tensor(hits[:, :, :], hits[:, :, :], equal[:, :, :], ALU.add).then_inc(s["rank_in"], 1)
                ranks(1)
                chain(dve.tensor_copy(slot[:, :, :], rank[:, :, :]))
                chain(dve.tensor_scalar(piece[:, :, :], slot[:, :, :], P - 1, None, ALU.bitwise_and))
                dve.tensor_copy(slot_row16[:, :, :], piece[:, :, :])
                dve.tensor_copy(lane16[:, :], lane[:, :])
                chain(dve.tensor_scalar(slot[:, :, :], slot[:, :, :], 7, None, ALU.logical_shift_right))
                chain(dve.tensor_copy(slot_tile[:, :, :], slot[:, :, :]))
                chain(dve.scalar_tensor_tensor(slot_tile[:, :, :], slot_tile[:, :, :], 1.0, hits[:, :, :], ALU.add, ALU.mult))
                chain(dve.tensor_scalar(slot_tile[:, :, :], slot_tile[:, :, :], -1.0, None, ALU.add))
                lanes = lane[:, 0:SLOT_TILES].unsqueeze(1).broadcast_to([P, TE, SLOT_TILES])
                dve.tensor_tensor(hot[:, :, :], lanes, flat(slot_tile).unsqueeze(2).broadcast_to([P, TE, SLOT_TILES]),
                                  ALU.is_equal).then_inc(s["hot"], 1)
                dve.wait_ge(s["hot"], 1)
                hot4 = hot[:, :, :].rearrange("p (e t) s -> p e t s", e=EXPERTS)
                for n in range(3):
                    chain(dve.tensor_copy(part[:, n, :, :], by_expert[:, :, :]))
                    if n < 2:
                        dve.tensor_tensor(by_expert[:, :, :], by_expert[:, :, :], part[:, n, :, :], ALU.subtract).then_inc(s["dve"], 1)
                        done += 1
                    x = dve.tensor_tensor(carried[:, :, :, 2 + n, :], hot4,
                                          part[:, n, :, :].unsqueeze(3).broadcast_to([P, EXPERTS, TILES, SLOT_TILES]), ALU.mult)
                    if n < 2:
                        dve.wait_ge(s["dve"], done)
                x.then_inc(s["carried"], 1)
                lanes16 = lane16[:, :].unsqueeze(1).broadcast_to([P, WIDE, P])
                with dve.Fori(0, EXPERTS) as e:
                    for g in range(GROUPS_OF_TILES):
                        if g >= 2:
                            dve.wait_ge(s["gather"], e * GROUPS_OF_TILES + g - 1)
                        tiles = slice(g * WIDE, (g + 1) * WIDE)
                        dve.tensor_tensor(row_hot[:, g % 2, :, :], lanes16,
                                          slot_row16[:, bass.ts(e, 1), tiles].rearrange("p o t -> p (o t)").unsqueeze(2).broadcast_to([P, WIDE, P]),
                                          ALU.is_equal).then_inc(s["row_hot"], 1)
                    dve.wait_ge(s["gather"], e * GROUPS_OF_TILES + GROUPS_OF_TILES)
                chain(dve.tensor_copy(found[:, :, :, :].rearrange("p e i s -> p (e i s)"), m.ps[:, 3, 0:EXPERTS * CARRIED * SLOT_TILES]))
                dve.scalar_tensor_tensor(m.chosen[:, :, :], found[:, :, 0, :], float(P), found[:, :, 1, :], ALU.mult, ALU.add)
                chain(dve.tensor_tensor(m.gates[:, :, :], found[:, :, 2, :], found[:, :, 3, :], ALU.add))
                dve.tensor_tensor(m.gates[:, :, :], m.gates[:, :, :], found[:, :, 4, :], ALU.add).then_inc(s["taken"], 1)


def experts(nc, m, a):
    HALVES = TOPK // CHUNK
    FT = EHID // P
    SCALE = 64.0
    TERMS = (0, 0), (0, 1), (1, 0)
    with ExitStack() as ctx:
        def sb(name, shape, dt=F32):
            return ctx.enter_context(nc.sbuf_tensor(f"ex_{name}", shape, dt))

        w1_whole = sb("w1_whole", [P, KD * EHID])
        w2_whole = sb("w2_whole", [P, FT * D])
        w1 = sb("w1", [P, 2, 2, KD, EHID], F16)
        w2 = sb("w2", [P, 2, 2, FT, D], F16)
        which = sb("which", [P, 2, SLOT_TILES], U32)
        gate = sb("gate", [P, 2, SLOT_TILES])
        h = sb("h", [P, 2, SLOT_TILES, D])
        ht = sb("ht", [P, 2, 2, KD, CHUNK], F16)
        hid_whole = sb("hid_whole", [P, 2, CHUNK])
        hid = sb("hid", [P, 2, 2, FT, CHUNK], F16)
        y = sb("y", [P, 2, SLOT_TILES, D])
        zero = sb("zero", [P, TPC, D])
        with stage(nc, "ex", "zeroed", "cleared", "w_in", "w_high", "w_low", "which", "h_even", "h_odd", "turned", "ht_high", "ht", "up", "gelu",
                   "hid_high", "hid", "down", "y", "added", "summed", "issue") as (block, s):
            h_in = s["h_even"], s["h_odd"]

            def exists(e):
                return not isinstance(e, int) or e < EXPERTS

            def run(expert, loop):
                expert(0, 0)
                with loop(0, EXPERTS // 2 - 1) as k:
                    expert(k * 2 + 1, 1)
                    expert(k * 2 + 2, 0)
                expert(EXPERTS - 1, 1)

            @block.sync
            def _(sp):
                sp.wait_ge(s["zeroed"], 1)
                for c in range(CHUNKS):
                    sp.dma_start(m.mix[c * CHUNK:(c + 1) * CHUNK, :].rearrange("(t p) d -> p t d", p=P), zero[:, :, :]).then_inc(s["cleared"], 16)

            @block.scalar
            def _(act):
                credit(act, s["w_high"], s["ht_high"], s["gelu"], s["hid_high"])

                def load(e):
                    need(act, s["w_low"], 2 * e)
                    act.dma_start(w1_whole[:, :].rearrange("p (k f) -> p k f", k=KD),
                                  a["L1_ffn_w1"][bass.ts(e, 1)].rearrange("o (k p) f -> p (o k) f", p=P)).then_inc(s["w_in"], 16)
                    act.dma_start(w2_whole[:, :].rearrange("p (f d) -> p f d", f=FT),
                                  a["L1_ffn_w2"][bass.ts(e, 1)].rearrange("o (f p) d -> p (o f) d", p=P)).then_inc(s["w_in"], 16)

                def split(e, u):
                    act.wait_ge(s["w_in"], e * 32 + 32)
                    need(act, s["up"], HALVES * FT * (e - 1))
                    need(act, s["down"], SLOT_TILES * (e - 1))
                    for whole, to in ((w1_whole, w1), (w2_whole, w2)):
                        act.activation(to[:, u, 0, :, :].rearrange("p k f -> p (k f)"), whole[:, :], ACT.Copy, scale=SCALE).then_inc(s["w_high"], 1)

                def take(e, x):
                    n = e * HALVES + x
                    need(act, s["up"], FT * (n - 1))
                    for k in range(KD):
                        need(act, s["turned"], KD * n + k + 1)
                        act.copy(ht[:, x, 0, k, :], m.ps[:, k, :]).then_inc(s["ht_high"], 1)

                def gelu(e, x):
                    n = e * HALVES + x
                    need(act, s["down"], TPC * (n - 1))
                    for f in range(FT):
                        need(act, s["up"], FT * n + f + 1)
                        need(act, s["hid"], FT * n + f - 2 + 1)
                        act.activation(hid_whole[:, f % 2, :], m.ps[:, 2 + f % 2, :], ACT.Gelu_apprx_tanh, scale=1 / SCALE).then_inc(s["gelu"], 1)
                        need(act, s["gelu"], FT * n + f + 1)
                        act.copy(hid[:, x, 0, f, :], hid_whole[:, f % 2, :]).then_inc(s["hid_high"], 1)

                def expert(e, u):
                    take(e, 1)
                    if exists(e + 1):
                        load(e + 1)
                    gelu(e, 0)
                    if exists(e + 1):
                        split(e + 1, 1 - u)
                        take(e + 1, 0)
                    gelu(e, 1)

                load(0)
                split(0, 0)
                take(0, 0)
                run(expert, act.Fori)

            @block.gpsimd
            def _(pool):
                credit(pool, s["which"], s["summed"], s["issue"])
                pool.memset(zero[:, :, :], 0.0).then_inc(s["zeroed"], 1)

                def gather(e, u):
                    need(pool, s["turned"], KD * HALVES * (e - 1))
                    pool.tensor_copy(which[:, u, :].unsqueeze(1), m.chosen[:, bass.ts(e, 1), :])
                    pool.tensor_copy(gate[:, u, :].unsqueeze(1), m.gates[:, bass.ts(e, 1), :]).then_inc(s["which"], 1)
                    need(pool, s["which"], e + 1)
                    pool.sem_inc(s["issue"], 1)
                    for t in range(SLOT_TILES):
                        pool.indirect_dma_start(h[:, u, t, :], None, m.h, bass.IndirectOffsetOnAxis(which[:, u, t:t + 1], 0)).then_inc(h_in[u], 16)

                def add(e, u):
                    for t in range(SLOT_TILES):
                        need(pool, s["y"], SLOT_TILES * e + t + 1)
                        pool.sem_inc(s["issue"], 1)
                        pool.indirect_dma_start(m.mix, bass.IndirectOffsetOnAxis(which[:, u, t:t + 1], 0), y[:, u, t, :], None,
                                                compute_op=ALU.add).then_inc(s["added"], 16)

                gather(0, 0)
                pool.wait_ge(s["cleared"], 16 * CHUNKS)

                def expert(e, u):
                    if not isinstance(e, int) or e > 0:
                        pool.wait_ge(s["added"], 16 * SLOT_TILES * e)
                        pool.sem_inc(s["summed"], 1)
                    if exists(e + 1):
                        gather(e + 1, 1 - u)
                    add(e, u)

                run(expert, pool.Fori)
                pool.wait_ge(s["added"], 16 * SLOT_TILES * EXPERTS)

            @block.tensor
            def _(pe):
                credit(pe, s["turned"], s["up"], s["down"])

                def turn(e, u, x):
                    n = e * HALVES + x
                    if x == 0:
                        pe.wait_ge(h_in[u], (e - u) * 8 * SLOT_TILES + 16 * SLOT_TILES)
                    for k in range(KD):
                        need(pe, s["ht"], KD * (n - 1) + k + 1)
                        for j in range(TPC):
                            t = pe.transpose(m.ps[:, k, j * P:(j + 1) * P], h[:, u, x * TPC + j, k * P:(k + 1) * P], m.ident[:, :])
                        t.then_inc(s["turned"], 1)

                def up(e, u, x, between=None):
                    n = e * HALVES + x
                    need(pe, s["ht"], KD * (n + 1))
                    if x == 0:
                        need(pe, s["w_low"], 2 * e + 2)
                    terms = [(k, i, j) for k in range(KD) for i, j in TERMS]
                    for f in range(FT):
                        need(pe, s["gelu"], FT * n + f - 2 + 1)
                        for i, (k, p, q) in enumerate(terms):
                            mm = pe.matmul(m.ps[:, 2 + f % 2, :], w1[:, u, p, k, f * P:(f + 1) * P], ht[:, x, q, k, :],
                                           start=(i == 0), stop=(i == len(terms) - 1))
                        mm.then_inc(s["up"], 1)
                        if between and f % 2:
                            between(f // 2)

                def down(e, u, x, j):
                    n = e * HALVES + x
                    need(pe, s["hid"], FT * (n + 1))
                    terms = [(f, p, q) for f in range(FT) for p, q in TERMS]
                    need(pe, s["y"], TPC * n + j - 4 + 1)
                    for i, (f, p, q) in enumerate(terms):
                        mm = pe.matmul(m.ps[:, 4 + j, 0:D], hid[:, x, p, f, j * P:(j + 1) * P], w2[:, u, q, f, :],
                                       start=(i == 0), stop=(i == len(terms) - 1))
                    mm.then_inc(s["down"], 1)

                def expert(e, u):
                    turn(e, u, 1)
                    up(e, u, 0)
                    if exists(e + 1):
                        turn(e + 1, 1 - u, 0)
                    up(e, u, 1, lambda j: down(e, u, 0, j))
                    for j in range(TPC):
                        down(e, u, 1, j)

                turn(0, 0, 0)
                run(expert, pe.Fori)

            @block.vector
            def _(dve):
                credit(dve, s["w_low"], s["ht"], s["hid"], s["y"])

                def split(e, u):
                    for n, (whole, to) in enumerate(((w1_whole, w1), (w2_whole, w2))):
                        need(dve, s["w_high"], 2 * e + n + 1)
                        high, low = (to[:, u, i, :, :].rearrange("p k f -> p (k f)") for i in range(2))
                        dve.scalar_tensor_tensor(low, whole[:, :], SCALE, high, ALU.mult, ALU.subtract).then_inc(s["w_low"], 1)

                def take(e, x):
                    n = e * HALVES + x
                    for k in range(KD):
                        need(dve, s["ht_high"], KD * n + k + 1)
                        dve.tensor_tensor(ht[:, x, 1, k, :], m.ps[:, k, :], ht[:, x, 0, k, :], ALU.subtract).then_inc(s["ht"], 1)

                def low(e, x, between=None):
                    n = e * HALVES + x
                    for f in range(FT):
                        need(dve, s["hid_high"], FT * n + f + 1)
                        dve.tensor_tensor(hid[:, x, 1, f, :], hid_whole[:, f % 2, :], hid[:, x, 0, f, :], ALU.subtract).then_inc(s["hid"], 1)
                        if between and f % 2:
                            between(f // 2)

                def weigh(e, u, x, j):
                    t = x * TPC + j
                    need(dve, s["which"], e + 1)
                    need(dve, s["summed"], e - 1)
                    need(dve, s["down"], SLOT_TILES * e + t + 1)
                    dve.tensor_scalar(y[:, u, t, :], m.ps[:, 4 + j, 0:D], gate[:, u, t:t + 1], 1 / SCALE, ALU.mult, ALU.mult).then_inc(s["y"], 1)

                def expert(e, u):
                    take(e, 1)
                    low(e, 0)
                    if exists(e + 1):
                        split(e + 1, 1 - u)
                        take(e + 1, 0)
                    low(e, 1, lambda j: weigh(e, u, 0, j))
                    for j in range(TPC):
                        weigh(e, u, 1, j)

                split(0, 0)
                take(0, 0)
                run(expert, dve.Fori)


def mixture_output(nc, m, out):
    with ExitStack() as ctx:
        mix = ctx.enter_context(nc.sbuf_tensor("mo_mix", [P, TILES, D], F32))
        rounded = ctx.enter_context(nc.sbuf_tensor("mo_rounded", [P, 2, TPC, D], BF16))
        with stage(nc, "mo", *(f"in{c}" for c in range(CHUNKS)), "rounded", "gated", "x", "out") as (block, s):
            mix_in = [s[f"in{c}"] for c in range(CHUNKS)]

            @block.sync
            def _(sp):
                for c in range(CHUNKS):
                    rows = slice(c * CHUNK, (c + 1) * CHUNK)
                    sp.dma_start(mix[:, c * TPC:(c + 1) * TPC, :], m.mix[rows, :].rearrange("(t p) d -> p t d", p=P)).then_inc(mix_in[c], 16)
                for c in range(CHUNKS):
                    rows = slice(c * CHUNK, (c + 1) * CHUNK)
                    sp.wait_ge(s["x"], c + 1)
                    sp.dma_start(out[rows, :].rearrange("(t p) d -> p t d", p=P), m.x[:, c * TPC:(c + 1) * TPC, :]).then_inc(s["out"], 16)
                sp.wait_ge(s["out"], 16 * CHUNKS)

            @block.vector
            def _(dve):
                for c in range(CHUNKS):
                    tiles = slice(c * TPC, (c + 1) * TPC)
                    dve.wait_ge(mix_in[c], 16)
                    if c >= 2:
                        dve.wait_ge(s["gated"], c - 1)
                    dve.tensor_copy(rounded[:, c % 2, :, :], mix[:, tiles, :]).then_inc(s["rounded"], 1)
                    dve.wait_ge(s["rounded"], c + 1)
                    dve.tensor_tensor(mix[:, tiles, :], rounded[:, c % 2, :, :], m.modb[:, 5:6, :].broadcast_to([P, TPC, D]), ALU.mult).then_inc(s["gated"], 1)

            @block.gpsimd
            def _(pool):
                for c in range(CHUNKS):
                    tiles = slice(c * TPC, (c + 1) * TPC)
                    pool.wait_ge(s["gated"], c + 1)
                    pool.tensor_tensor(m.x[:, tiles, :], m.x[:, tiles, :], mix[:, tiles, :], ALU.add).then_inc(s["x"], 1)



def rotary_table():
    f = np.float32
    half_idx = np.arange(0, DH, 2, dtype=f)
    inv_freq = f(1.0) / f(10000.0) ** (half_idx / f(DH))
    t = np.arange(N, dtype=f)
    freqs = t[:, None] * inv_freq[None, :]
    base = (half_idx + f(0.4 * DH)) / f(1.4 * DH)
    power = (t - f(N // 2)) / f(WINDOW // 2)
    scale = base[None, :] ** power[:, None]
    cos, sin = np.cos(freqs), np.sin(freqs)
    return np.stack([cos * scale, cos / scale, sin * scale, sin / scale], axis=1).astype(f)


def rope_table():
    f = np.float32
    k = np.arange(L1_DH // 2, dtype=f)
    inv_freq = f(10000.0) ** (f(-2.0) * k / f(L1_DH))
    angle = np.arange(N, dtype=f)[:, None] * inv_freq
    cos, sin = np.cos(angle).T, np.sin(angle).T
    pairs = np.stack([np.stack([cos, cos], axis=1).reshape(L1_DH, N), np.stack([-sin, sin], axis=1).reshape(L1_DH, N)], axis=1)
    return np.tile(pairs, (P // L1_DH, 1, 1)).astype(f)


def layout(inputs):
    a = dict(inputs)
    a["x"] = np.asarray(a.pop("L0_attn_X")).reshape(N, D)
    a["rotary"], a["rope"] = rotary_table(), rope_table()
    swap = np.arange(D) ^ 1
    for n in "QK":
        w = np.asarray(a.pop(f"L1_attn_W_{n}"))
        a[f"W{n}"], a[f"W{n}_swapped"] = w.T, w[swap].T
    for n in "VO":
        a[f"W{n}"] = np.asarray(a.pop(f"L1_attn_W_{n}")).T
    a = {n: np.ascontiguousarray(v) for n, v in a.items()}
    return a



def load_x(nc, m, x, name):
    with stage(nc, name, "x_in", "zeroed", "ident", "ident16") as (block, s):

        @block.sync
        def _(sp):
            for h in range(4):
                t = TILES // 4
                sp.dma_start(m.x[:, h * t:(h + 1) * t, :],
                             x[h * t * P:(h + 1) * t * P, :].rearrange("(t p) d -> p t d", p=P)).then_inc(s["x_in"], 16)
            sp.wait_ge(s["x_in"], 64)

        @block.gpsimd
        def _(pool):
            pool.memset(m.minus_half[:, :], -0.5)
            pool.memset(m.ident[:, :], 0.0).then_inc(s["zeroed"], 1)
            pool.wait_ge(s["zeroed"], 1)
            pool.affine_select(m.ident[:, :], m.ident[:, :], pattern=[[-1, P]], compare_op=ALU.not_equal, fill=1.0,
                               base=0, channel_multiplier=1).then_inc(s["ident"], 1)
            pool.wait_ge(s["ident"], 1)
            pool.tensor_copy(m.ident16[:, :], m.ident[:, :]).then_inc(s["ident16"], 1)


def program(nc, a, out):
    m = Memory()
    with ExitStack() as ctx:
        def sb(name, shape, dt=F32):
            return ctx.enter_context(nc.sbuf_tensor(name, shape, dt))

        m.ps = ctx.enter_context(nc.psum_tensor("ps", [P, 8, 512], F32))
        m.x = sb("x", [P, TILES, D])
        m.ident = sb("ident", [P, P])
        m.ident16 = sb("ident16", [P, P], F16)
        m.minus_half = sb("minus_half", [P, TILES])
        m.modb = sb("modb", [P, 6, D])
        m.modc = sb("modc", [P, 6 * KD])
        m.mean = sb("mean", [P, TILES])
        m.rstd = sb("rstd", [P, TILES])

        load_x(nc, m, a["x"], "load")
        modulation(nc, m, "m0", a["L0_c"], a["L0_wmod"])
        norm_statistics(nc, m, "n0")
        with ExitStack() as scope:
            m.qt = scope.enter_context(nc.sbuf_tensor("a0_qt", [P, KD, 2, N], F16))
            m.kt = scope.enter_context(nc.sbuf_tensor("a0_kt", [P, KD, 2, N], F16))
            m.v = scope.enter_context(nc.sbuf_tensor("a0_v", [P, TILES, 2, D], F16))
            attention0_projections(nc, m, {k: a["L0_attn_" + k] for k in ("Wq", "Wk", "Wv", "bq", "bk", "bv")})
            attention0(nc, m)

        with ExitStack() as scope:
            def sc(name, shape):
                return scope.enter_context(nc.sbuf_tensor(name, shape, F32))

            m.y = sc("y", [P, TILES, D])
            m.next = sc("next", [P, 2, TILES])
            m.wqkv = sc("wqkv", [P, KD, 3 * INNER])
            m.wo = sc("wo", [P, INNER // P, D])
            m.table = sc("table", [P, TILES, 4, HALF])
            m.gain = sc("gain", [P, 2, 2, HALF])
            m.mask = sc("mask", [P, 3, 2, P])
            m.first = sc("first", [P, 1])
            f = {k: a["L0_ffn_" + k] for k in ("wqkv", "q_scale", "k_scale", "wo", "ln_g", "ln_b", "w1", "b1", "w2", "b2")}
            f["rotary"] = a["rotary"]
            norm_statistics(nc, m, "n1")
            transformer_input(nc, m, f)
            with nc.Fori(0, DEPTH) as layer:
                local_attention(nc, m)
                gated_mlp_layer(nc, m, f, layer)
            transformer_output(nc, m)

        m.qk = nc.dram_tensor("qk_parts", [2, 2, D, N], F16).ap()
        m.tops = nc.dram_tensor("top_parts", [MPARTS, GROUP, N], F16).ap()
        m.o = nc.dram_tensor("heads_out", [N, D], F32).ap()
        modulation(nc, m, "m1", a["L1_c"], a["L1_wmod"])
        norm_statistics(nc, m, "n2")
        with ExitStack() as scope:
            m.v17 = scope.enter_context(nc.sbuf_tensor("v17", [P, TILES, L1_HEADS, L1_DH + 1], F32))
            attention1_projections(nc, m, a)
            attention1(nc, m)
        attention1_output(nc, m, a)

        m.h = nc.dram_tensor("expert_in", [N, D], F32).ap()
        m.mix = nc.dram_tensor("expert_out", [N, D], F32).ap()
        m.probs = sb("probs", [P, TILES, EXPERTS])
        m.chosen = sb("chosen", [P, EXPERTS, SLOT_TILES], U32)
        m.gates = sb("gates", [P, EXPERTS, SLOT_TILES])
        norm_statistics(nc, m, "n3")
        expert_scores(nc, m, a)
        choose_tokens(nc, m)
        experts(nc, m, a)
        mixture_output(nc, m, out)


def kernel(**inputs):
    import concourse.bacc as bacc
    from concourse.bass_utils import run_bass_kernel_spmd

    nc = bacc.Bacc("TRN2", target_bir_lowering=False, num_devices=1)
    arrays, a = {}, {}
    for name, array in layout(inputs).items():
        arrays[f"in_{name}_dram"] = array
        a[name] = nc.dram_tensor(f"in_{name}_dram", array.shape, mybir.dt.from_np(array.dtype), kind="ExternalInput").ap()
    out = nc.dram_tensor("out_dram", (N, D), F32, kind="ExternalOutput").ap()
    program(nc, a, out)
    result = run_bass_kernel_spmd(nc, [arrays], core_ids=[0])
    return result.results[0]["out_dram"].reshape(1, N, D)
```

```python
from contextlib import ExitStack, contextmanager

import numpy as np

import concourse.bass as bass
from concourse import mybir

F32 = mybir.dt.float32
F16 = mybir.dt.float16
BF16 = mybir.dt.bfloat16
I32 = mybir.dt.int32
U32 = mybir.dt.uint32
ACT = mybir.ActivationFunctionType
ALU = mybir.AluOpType
AX = mybir.AxisListType

P = 128
N = 4096
D = 256
KD = D // P
TILES = N // P
CHUNK = 512
TPC = CHUNK // P
CHUNKS = N // CHUNK
LN_EPS = 1e-5

DEPTH, HEADS, DH, WINDOW = 2, 8, 64, 128
INNER = HEADS * DH
HID = D * 4 * 2 // 3
QK_SCALE = 8.0
HALF = DH // 2
ROTARY_N = 4096

L1_HEADS, L1_DH = 16, 16
EXPERTS, TOPK, EHID = 8, 1024, 1024

CREDIT = 64


def need(eng, sem, n):
    eng.wait_ge(sem, n + CREDIT)


def credit(eng, *sems):
    for sem in sems:
        eng.sem_inc(sem, CREDIT)


class Memory:
    pass


@contextmanager
def stage(nc, name, *names):
    with ExitStack() as ctx:
        sems = [ctx.enter_context(nc.semaphore(f"{name}_{n}")) for n in names]
        with nc.Block() as block:
            yield block, dict(zip(names, sems))
        numbers = [sem.num for sem in sems]
        nc.all_engine_barrier(sems_to_clear=range(min(numbers), max(numbers) + 1))


def in_pairs(eng, count, step, slots=2):
    with eng.Fori(0, count // slots) as k:
        for u in range(slots):
            step(k * slots + u, u)


def ahead_in_pairs(eng, count, first, second, slots=2):
    first(0, 0)
    with eng.Fori(0, count // slots - 1) as k:
        for u in range(slots):
            first(k * slots + u + 1, (u + 1) % slots)
            second(k * slots + u, u)
    for u in range(slots):
        if u + 1 < slots:
            first(count - slots + u + 1, u + 1)
        second(count - slots + u, u)


def two_ahead_in_pairs(eng, count, first, second):
    first(0, 0)
    first(1, 1)
    with eng.Fori(0, count // 2 - 1) as k:
        for u in range(2):
            first(k * 2 + u + 2, u)
            second(k * 2 + u, u)
    for u in range(2):
        second(count - 2 + u, u)



STATISTICS = "six", "moments", "var", "rstd"


def statistics_buffers(nc, ctx, name):
    b = Memory()
    b.half_gap = ctx.enter_context(nc.sbuf_tensor(f"{name}_half_gap", [P, TILES], F32))
    b.var = ctx.enter_context(nc.sbuf_tensor(f"{name}_var", [P, TILES], F32))
    return b


def halves_on_vector(dve, m, s):
    with dve.Fori(0, TILES // 4) as k:
        for u in range(4):
            t = bass.ts(k * 4 + u, 1)
            dve.bn_stats(m.six[:, t, :], m.x[:, t, :]).then_inc(s["six"], 1)
    dve.wait_ge(s["six"], TILES)


def statistics_on_vector(dve, m, b, s):
    even, odd, sq_even, sq_odd = m.six[:, :, 1], m.six[:, :, 4], m.six[:, :, 2], m.six[:, :, 5]
    dve.tensor_tensor(b.half_gap[:, :], even, odd, ALU.subtract).then_inc(s["moments"], 1)
    dve.tensor_tensor(m.mean[:, :], even, odd, ALU.add).then_inc(s["moments"], 1)
    dve.tensor_tensor(b.var[:, :], sq_even, sq_odd, ALU.add).then_inc(s["moments"], 1)
    dve.wait_ge(s["moments"], 3)
    dve.tensor_scalar(m.mean[:, :], m.mean[:, :], 0.5, None, ALU.mult)
    dve.tensor_scalar(b.var[:, :], b.var[:, :], 1.0 / D, LN_EPS, ALU.mult, ALU.add).then_inc(s["moments"], 1)
    dve.scalar_tensor_tensor(b.half_gap[:, :], b.half_gap[:, :], 0.25, b.half_gap[:, :], ALU.mult, ALU.mult).then_inc(s["moments"], 1)
    dve.wait_ge(s["moments"], 5)
    dve.tensor_tensor(m.rstd[:, :], b.var[:, :], b.half_gap[:, :], ALU.add).then_inc(s["var"], 1)


def statistics_on_gpsimd(pool, m, s):
    pool.wait_ge(s["var"], 1)
    pool.tensor_tensor(m.rstd[:, :], m.rstd[:, :], m.minus_half[:, 0:TILES], ALU.pow).then_inc(s["rstd"], 1)


def norm_statistics(nc, m, name):
    with ExitStack() as ctx:
        b = statistics_buffers(nc, ctx, name)
        with stage(nc, name, *STATISTICS) as (block, s):

            @block.vector
            def _(dve):
                statistics_on_vector(dve, m, b, s)

            @block.gpsimd
            def _(pool):
                statistics_on_gpsimd(pool, m, s)



def modulation_and_statistics(nc, m, name, c, wmod, beside=None):
    with ExitStack() as ctx:
        ccol = ctx.enter_context(nc.sbuf_tensor(f"{name}_ccol", [P, KD], F32))
        crep = ctx.enter_context(nc.sbuf_tensor(f"{name}_crep", [P, KD, P], F32))
        w = ctx.enter_context(nc.sbuf_tensor(f"{name}_wmod", [P, KD, 6 * D], F32))
        sign = ctx.enter_context(nc.sbuf_tensor(f"{name}_sign", [P, 2, D], F32))
        size = ctx.enter_context(nc.sbuf_tensor(f"{name}_size", [P, 2, D], F32))
        b = statistics_buffers(nc, ctx, name)
        modb = m.modb[:, :, :].rearrange("p i d -> p (i d)")
        gates = m.modb[:, 2:6:3, :]
        with stage(nc, name, "c_in", "w_in", "silu", "rep", "col_mm", "row_mm", "col_ev", "row_ev", "dve", "beside", *STATISTICS) as (block, s):

            @block.sync
            def _(sp):
                sp.dma_start(ccol[:, :], c.rearrange("o (k p) -> p (o k)", p=P),
                             allow_slow_non_contiguous=True).then_inc(s["c_in"], 16)
                sp.dma_start(w[:, :, :], wmod.rearrange("(k p) e -> p k e", p=P)).then_inc(s["w_in"], 16)

            @block.gpsimd
            def _(pool):
                if beside:
                    beside(pool, s["beside"])
                statistics_on_gpsimd(pool, m, s)

            @block.scalar
            def _(act):
                act.wait_ge(s["c_in"], 16)
                act.activation(ccol[:, :], ccol[:, :], ACT.Silu).then_inc(s["silu"], 1)

            @block.tensor
            def _(pe):
                pe.wait_ge(s["w_in"], 16)
                pe.wait_ge(s["silu"], 1)
                for j in range(6 * KD):
                    for k in range(KD):
                        mm = pe.matmul(m.ps[:, 0, j:j + 1], w[:, k, j * P:(j + 1) * P], ccol[:, k:k + 1],
                                       start=(k == 0), stop=(k == KD - 1))
                mm.then_inc(s["col_mm"], 1)
                pe.wait_ge(s["rep"], 1)
                for j in range(3):
                    for k in range(KD):
                        mm = pe.matmul(m.ps[:, 1 + j, :], crep[:, k, :], w[:, k, j * 512:(j + 1) * 512],
                                       start=(k == 0), stop=(k == KD - 1))
                mm.then_inc(s["row_mm"], 1)

            @block.vector
            def _(dve):
                dve.wait_ge(s["silu"], 1)
                dve.tensor_copy(crep[:, :, :], ccol[:, :].unsqueeze(2).broadcast_to([P, KD, P])).then_inc(s["rep"], 1)
                halves_on_vector(dve, m, s)
                statistics_on_vector(dve, m, b, s)
                dve.wait_ge(s["col_mm"], 1)
                dve.tensor_copy(m.modc[:, :], m.ps[:, 0, 0:6 * KD]).then_inc(s["col_ev"], 1)
                dve.wait_ge(s["row_mm"], 1)
                dve.tensor_copy(modb, m.ps[:, 1:4, :].rearrange("p b e -> p (b e)")).then_inc(s["row_ev"], 1)
                dve.wait_ge(s["col_ev"], 1)
                scales = m.modc[:, :].rearrange("p (i k) -> p i k", k=KD)[:, 1:6:3, :]
                dve.tensor_scalar(scales, scales, 1.0, None, ALU.add).then_inc(s["dve"], 1)
                dve.wait_ge(s["row_ev"], 1)
                rows = m.modb[:, 1:6:3, :]
                dve.tensor_scalar(rows, rows, 1.0, None, ALU.add).then_inc(s["dve"], 1)
                dve.tensor_scalar(sign[:, :, :], gates, 0.0, 2.0, ALU.is_ge, ALU.mult).then_inc(s["dve"], 1)
                dve.scalar_tensor_tensor(size[:, :, :], gates, -1.0, gates, ALU.mult, ALU.max).then_inc(s["dve"], 1)
                dve.wait_ge(s["dve"], 4)
                dve.tensor_scalar(size[:, :, :], size[:, :, :], 0.25, None, ALU.max).then_inc(s["dve"], 1)
                dve.wait_ge(s["dve"], 5)
                dve.scalar_tensor_tensor(gates, sign[:, :, :], -1.0, size[:, :, :], ALU.add, ALU.mult)



def attention0_projections(nc, m, a):
    with ExitStack() as ctx:
        def sb(name, shape, dt=F32):
            return ctx.enter_context(nc.sbuf_tensor(f"a0_{name}", shape, dt))

        LOADS = 6

        w = {n: sb(f"w{n}", [P, KD, D]) for n in "qkv"}
        bcol = {n: sb(f"b{n}", [P, KD]) for n in "qk"}
        bv = sb("bv", [P, D])
        normed = sb("normed", [P, 2, TPC, D])
        ht = sb("ht", [P, 2, KD, CHUNK])
        v = sb("v_whole", [P, 2, 2, D])
        with stage(nc, "a0", "w_in", "normed", "turned", "ht", "mm", "high", "ev", "v", "v_high", "v_low") as (block, s):

            @block.sync
            def _(sp):
                for n in "qkv":
                    sp.dma_start(w[n][:, :, :], a[f"W{n}"].rearrange("(k p) e -> p k e", p=P)).then_inc(s["w_in"], 16)
                for n in "qk":
                    sp.dma_start(bcol[n][:, :], a[f"b{n}"].rearrange("(k p) -> p k", p=P),
                                 allow_slow_non_contiguous=True).then_inc(s["w_in"], 16)
                sp.dma_start(bv[:, :], a["bv"].partition_broadcast(P)).then_inc(s["w_in"], 16)

            @block.vector
            def _(dve):
                credit(dve, s["normed"], s["ev"], s["v"])

                def norm(c, u):
                    need(dve, s["turned"], KD * (c - 1))
                    for j in range(TPC):
                        t = c * TPC + j
                        n = dve.tensor_scalar(normed[:, u, j:j + 1, :], m.x[:, bass.ts(t, 1), :], m.mean[:, bass.ts(t, 1)],
                                              m.rstd[:, bass.ts(t, 1)], ALU.subtract, ALU.mult)
                    n.then_inc(s["normed"], 1)

                def outputs(c, u):
                    dve.wait_ge(s["w_in"], 16 * LOADS)
                    for n in range(2 * KD):
                        need(dve, s["high"], 2 * KD * c + n + 1)
                        to, b = (m.qt, bcol["q"]) if n < KD else (m.kt, bcol["k"])
                        dve.scalar_tensor_tensor(to[:, n % KD, 1, bass.ts(c, CHUNK)], m.ps[:, 2 + n, :], b[:, n % KD:n % KD + 1],
                                                 to[:, n % KD, 0, bass.ts(c, CHUNK)], ALU.add, ALU.subtract).then_inc(s["ev"], 1)
                    for b in range(2):
                        need(dve, s["mm"], 6 * c + 2 * KD + b + 1)
                        need(dve, s["v_low"], 2 * (c - 1) + b + 1)
                        dve.tensor_tensor(v[:, b, :, :], m.ps[:, 6 + b, :].rearrange("p (j e) -> p j e", e=D),
                                          bv[:, :].unsqueeze(1).broadcast_to([P, 2, D]), ALU.add).then_inc(s["v"], 1)

                two_ahead_in_pairs(dve, CHUNKS, norm, outputs)

            @block.scalar
            def _(act):
                credit(act, s["ht"], s["high"], s["v_high"])

                def high(c, u):
                    act.wait_ge(s["w_in"], 16 * LOADS)
                    for n in range(2 * KD):
                        need(act, s["mm"], 6 * c + n + 1)
                        to, b = (m.qt, bcol["q"]) if n < KD else (m.kt, bcol["k"])
                        act.activation(to[:, n % KD, 0, bass.ts(c, CHUNK)], m.ps[:, 2 + n, :], ACT.Identity,
                                       bias=b[:, n % KD:n % KD + 1]).then_inc(s["high"], 1)
                    for b in range(2):
                        need(act, s["v"], 2 * c + b + 1)
                        act.copy(m.v[:, bass.ts(c * 2 + b, 2), 0, :], v[:, b, :, :]).then_inc(s["v_high"], 1)

                def scaled(c, u):
                    need(act, s["mm"], 6 * (c - 1))
                    for k in range(KD):
                        need(act, s["turned"], KD * c + k + 1)
                        act.activation(ht[:, u, k, :], m.ps[:, k, :], ACT.Identity, bias=m.modc[:, k:k + 1],
                                       scale=m.modc[:, KD + k:KD + k + 1]).then_inc(s["ht"], 1)

                ahead_in_pairs(act, CHUNKS, scaled, high)

            @block.gpsimd
            def _(pool):
                credit(pool, s["v_low"])

                def low(c, u):
                    for b in range(2):
                        need(pool, s["v_high"], 2 * c + b + 1)
                        pool.tensor_tensor(m.v[:, bass.ts(c * 2 + b, 2), 1, :], v[:, b, :, :], m.v[:, bass.ts(c * 2 + b, 2), 0, :],
                                           ALU.subtract).then_inc(s["v_low"], 1)

                in_pairs(pool, CHUNKS, low)

            @block.tensor
            def _(pe):
                credit(pe, s["turned"], s["mm"])

                def turn(c, u):
                    need(pe, s["normed"], c + 1)
                    for k in range(KD):
                        need(pe, s["ht"], KD * (c - 1) + k + 1)
                        for j in range(TPC):
                            t = pe.transpose(m.ps[:, k, j * P:(j + 1) * P], normed[:, u, j, k * P:(k + 1) * P], m.ident[:, :])
                        t.then_inc(s["turned"], 1)

                def products(c, u):
                    pe.wait_ge(s["w_in"], 16 * LOADS)
                    need(pe, s["ht"], KD * (c + 1))
                    for n in range(2 * KD):
                        need(pe, s["ev"], 2 * KD * (c - 1) + n + 1)
                        o = n % KD
                        for k in range(KD):
                            mm = pe.matmul(m.ps[:, 2 + n, :], w["qk"[n // KD]][:, k, o * P:(o + 1) * P], ht[:, u, k, :],
                                           start=(k == 0), stop=(k == KD - 1))
                        mm.then_inc(s["mm"], 1)
                    for b in range(2):
                        need(pe, s["v"], 2 * (c - 1) + b + 1)
                        for j in range(2):
                            for k in range(KD):
                                mm = pe.matmul(m.ps[:, 6 + b, j * D:(j + 1) * D],
                                               ht[:, u, k, (2 * b + j) * P:(2 * b + j + 1) * P], w["v"][:, k, :],
                                               start=(k == 0), stop=(k == KD - 1))
                        mm.then_inc(s["mm"], 1)

                ahead_in_pairs(pe, CHUNKS, turn, products)


def attention0(nc, m):
    KC = N // CHUNK
    PIECES = 4
    PIECE = N // PIECES
    CPP = KC // PIECES
    FIRST_LOW = KC - PIECES - 1
    with ExitStack() as ctx:
        def sb(name, shape, dt=F32):
            return ctx.enter_context(nc.sbuf_tensor(f"s0_{name}", shape, dt))

        scores = sb("scores", [P, 2, N])
        parts = sb("parts", [P, 2, N], F16)
        pt = sb("pt", [P, 2, 2, CHUNK], F16)
        top = sb("top", [P, 2, KC])
        minus_top = sb("minus_top", [P, 2])
        total = sb("total", [P, 2])
        rtotal = sb("rtotal", [P, 2])
        add = sb("add", [P, 2, D])
        with stage(nc, "s0", "mm", "copied", "max", "top", "exp", "high", "low", "turned", "pt_act", "pt_dve", "pv", "recip", "summed",
                   "gated", "x") as (block, s):

            def run(step, loop):
                step(0, 0)
                with loop(0, TILES // 2 - 1) as k:
                    step(k * 2 + 1, 1)
                    step(k * 2 + 2, 0)
                step(TILES - 1, 1)

            def exists(i):
                return not isinstance(i, int) or i < TILES

            def turned_bank(c):
                return m.ps[:, 4 + c % 2, :].bitcast(F16)

            @block.gpsimd
            def _(pool):
                credit(pool, s["x"])

                def residual(i, u):
                    need(pool, s["gated"], i + 1)
                    x = m.x[:, bass.ts(i, 1), :]
                    pool.tensor_tensor(x, x, add[:, u:u + 1, :], ALU.add).then_inc(s["x"], 1)

                in_pairs(pool, TILES, residual)

            @block.tensor
            def _(pe):
                credit(pe, s["mm"], s["turned"], s["pv"])

                def score(i, chunks):
                    for c in chunks:
                        need(pe, s["copied"], KC * i + c - 4 + 1)
                        keys = slice(c * CHUNK, (c + 1) * CHUNK)
                        terms = [(k, a, b) for k in range(KD) for a, b in ((0, 0), (0, 1), (1, 0))]
                        for n, (k, a, b) in enumerate(terms):
                            mm = pe.matmul(m.ps[:, c % 4, :], m.qt[:, k, a, bass.ts(i, P)], m.kt[:, k, b, keys],
                                           start=(n == 0), stop=(n == len(terms) - 1))
                        mm.then_inc(s["mm"], 1)

                def turn(i, c):
                    need(pe, s["low"], PIECES * i + c // CPP + 1)
                    if c % 2:
                        need(pe, s["pt_dve"], KC // 2 * i + c // 2)
                    else:
                        need(pe, s["pt_act"], KC // 2 * i + c // 2)
                    for part in range(2):
                        for j in range(TPC):
                            kt = c * TPC + j
                            t = pe.transpose(turned_bank(c)[:, (part * TPC + j) * P:(part * TPC + j + 1) * P],
                                             parts[:, part, kt * P:(kt + 1) * P], m.ident16[:, :])
                    t.then_inc(s["turned"], 1)

                def weigh(i, u):
                    need(pe, s["summed"], 2 * (i - 1))
                    for c in range(KC):
                        if 2 <= c + 1 < KC:
                            turn(i, c + 1)
                        need(pe, s["pt_dve" if c % 2 else "pt_act"], KC // 2 * i + c // 2 + 1)
                        for j in range(TPC):
                            kt = c * TPC + j
                            pe.matmul(m.ps[:, 6 + u, :], pt[:, c % 2, 0, j * P:(j + 1) * P], m.v[:, kt, :, :].rearrange("p i e -> p (i e)"),
                                      start=(kt == 0), stop=False, skip_group_check=True)
                            mm = pe.matmul(m.ps[:, 6 + u, 0:D], pt[:, c % 2, 1, j * P:(j + 1) * P], m.v[:, kt, 0, :],
                                           start=False, stop=(kt == TILES - 1), skip_group_check=True)
                        mm.then_inc(s["pv"], 1)

                def step(i, u):
                    for chunks, c in ((range(KC - 2), 0), (range(KC - 2, KC - 1), 1), (range(KC - 1, KC), None)):
                        if exists(i + 1):
                            score(i + 1, chunks)
                        if c is not None:
                            turn(i, c)
                    weigh(i, u)

                score(0, range(KC))
                run(step, pe.Fori)

            @block.vector
            def _(dve):
                credit(dve, s["copied"], s["max"], s["top"], s["low"], s["pt_dve"], s["recip"], s["summed"], s["gated"])

                def row_max(i, u, c):
                    need(dve, s["mm"], KC * i + c + 1)
                    dve.tensor_scalar(scores[:, u, c * CHUNK:(c + 1) * CHUNK], m.ps[:, c % 4, :], 1.0, None, ALU.mult, ALU.max,
                                      accum_out=top[:, u, c:c + 1]).then_inc(s["copied"], 1)

                def row_top(i, u):
                    need(dve, s["copied"], KC * (i + 1))
                    dve.tensor_reduce(minus_top[:, u:u + 1], top[:, u, :], AX.X, ALU.max, negate=True).then_inc(s["max"], 1)
                    need(dve, s["max"], i + 1)
                    dve.tensor_scalar(minus_top[:, u:u + 1], minus_top[:, u:u + 1], float(10 * np.log(2)), None, ALU.add).then_inc(s["top"], 1)

                def low(i, u, g):
                    need(dve, s["high"], PIECES * i + g + 1)
                    piece = slice(g * PIECE, (g + 1) * PIECE)
                    dve.tensor_tensor(parts[:, 1, piece], scores[:, u, piece], parts[:, 0, piece], ALU.subtract).then_inc(s["low"], 1)

                def take_turned(i, c):
                    need(dve, s["turned"], KC * i + c + 1)
                    need(dve, s["pv"], KC * i + c - 2 + 1)
                    dve.tensor_copy(pt[:, c % 2, :, :].rearrange("p i k -> p (i k)"), turned_bank(c)).then_inc(s["pt_dve"], 1)

                def step(i, u):
                    for c in range(KC):
                        if c == KC - 1:
                            take_turned(i, 1)
                        if exists(i + 1):
                            row_max(i + 1, 1 - u, c)
                        if 0 <= c - FIRST_LOW < PIECES:
                            low(i, u, c - FIRST_LOW)
                    if exists(i + 1):
                        row_top(i + 1, 1 - u)
                    dve.reciprocal(rtotal[:, u:u + 1], total[:, u:u + 1]).then_inc(s["recip"], 1)
                    for c in range(3, KC, 2):
                        take_turned(i, c)
                    need(dve, s["recip"], i + 1)
                    need(dve, s["pv"], KC * (i + 1))
                    need(dve, s["x"], i)
                    dve.tensor_copy(add[:, u, :], m.ps[:, 6 + u, D:2 * D]).then_inc(s["summed"], 1)
                    need(dve, s["summed"], 2 * i + 1)
                    dve.tensor_tensor(add[:, u, :], m.ps[:, 6 + u, 0:D], add[:, u, :], ALU.add).then_inc(s["summed"], 1)
                    need(dve, s["summed"], 2 * i + 2)
                    dve.scalar_tensor_tensor(add[:, u, :], add[:, u, :], rtotal[:, u:u + 1], m.modb[:, 2, :],
                                             ALU.mult, ALU.mult).then_inc(s["gated"], 1)
                    if not isinstance(i, int) or i:
                        halves(i - 1)

                def halves(i):
                    dve.bn_stats(m.six[:, bass.ts(i, 1), :], m.x[:, bass.ts(i, 1), :])

                for c in range(KC):
                    row_max(0, 0, c)
                row_top(0, 0)
                run(step, dve.Fori)
                need(dve, s["x"], TILES)
                halves(TILES - 1)

            @block.scalar
            def _(act):
                credit(act, s["exp"], s["high"], s["pt_act"])

                def step(i, u):
                    need(act, s["top"], i + 1)
                    need(act, s["recip"], i - 1)
                    act.activation(scores[:, u, :], scores[:, u, :], ACT.Exp, bias=minus_top[:, u:u + 1],
                                   accum_out=total[:, u:u + 1]).then_inc(s["exp"], 1)
                    need(act, s["exp"], i + 1)
                    need(act, s["turned"], KC * i)
                    for g in range(PIECES):
                        piece = slice(g * PIECE, (g + 1) * PIECE)
                        act.copy(parts[:, 0, piece], scores[:, u, piece]).then_inc(s["high"], 1)
                    for c in range(0, KC, 2):
                        need(act, s["turned"], KC * i + c + 1)
                        need(act, s["pv"], KC * i + c - 2 + 1)
                        act.copy(pt[:, c % 2, :, :].rearrange("p i k -> p (i k)"), turned_bank(c)).then_inc(s["pt_act"], 1)

                run(step, act.Fori)



def load_attention(eng, m, f, layer, loaded):
    eng.dma_start(m.wqkv[:, :, :], layer_of(f["wqkv"], layer).rearrange("o (k p) e -> p (o k) e", p=P)).then_inc(loaded, 16)
    eng.dma_start(m.wo[:, :, :], layer_of(f["wo"], layer).rearrange("o (k p) e -> p (o k) e", p=P)).then_inc(loaded, 16)
    for n, name in enumerate(("q_scale", "k_scale")):
        src = layer_of(f[name], layer).rearrange("o d -> (o d)")
        eng.dma_start(m.gain[:, n, :, :].rearrange("p h d -> p (h d)"), src.partition_broadcast(P)).then_inc(loaded, 16)


ATTENTION_LOADS = 4


def transformer_input(nc, m, f):
    NEG = -1e30
    with ExitStack() as ctx:
        normed = ctx.enter_context(nc.sbuf_tensor("y0_normed", [P, 2, TPC, D], F32))
        with stage(nc, "y0", "table_in", "w_in", "zeroed", "normed", "scaled", "y") as (block, s):

            @block.sync
            def _(sp):
                load_attention(sp, m, f, 0, s["w_in"])
                sp.dma_start(m.table[:, :, :, :], f["rotary"].rearrange("(t p) i d -> p t i d", p=P)).then_inc(s["table_in"], 16)
                sp.wait_ge(s["w_in"], 16 * ATTENTION_LOADS)
                sp.wait_ge(s["table_in"], 16)

            @block.vector
            def _(dve):
                credit(dve, s["normed"], s["scaled"])

                def norm(c, u):
                    need(dve, s["y"], c - 1)
                    for j in range(TPC):
                        t = bass.ts(c * TPC + j, 1)
                        n = dve.tensor_scalar(normed[:, u, j:j + 1, :], m.x[:, t, :], m.mean[:, t], m.rstd[:, t], ALU.subtract, ALU.mult)
                    n.then_inc(s["normed"], 1)
                    need(dve, s["normed"], c + 1)
                    dve.tensor_tensor(normed[:, u, :, :], normed[:, u, :, :], m.modb[:, 4:5, :].broadcast_to([P, TPC, D]),
                                      ALU.mult).then_inc(s["scaled"], 1)

                in_pairs(dve, CHUNKS, norm)

            @block.gpsimd
            def _(pool):
                credit(pool, s["y"])
                pool.memset(m.mask[:, :, :, :], 0.0).then_inc(s["zeroed"], 1)
                pool.wait_ge(s["zeroed"], 1)
                for own in (m.mask[:, 0, 0, :], m.mask[:, 1, 1, :], m.mask[:, 2, 0, :]):
                    pool.affine_select(own, own, pattern=[[-1, P]], compare_op=ALU.is_ge, fill=NEG, base=0, channel_multiplier=1)
                for before in (m.mask[:, 0, 1, :], m.mask[:, 1, 0, :]):
                    pool.affine_select(before, before, pattern=[[1, P]], compare_op=ALU.is_ge, fill=NEG, base=0, channel_multiplier=-1)
                pool.memset(m.mask[:, 2, 1, :], NEG)

                def shift(c, u):
                    need(pool, s["scaled"], c + 1)
                    pool.tensor_tensor(m.y[:, bass.ts(c, TPC), :], normed[:, u, :, :], m.modb[:, 3:4, :].broadcast_to([P, TPC, D]),
                                       ALU.add).then_inc(s["y"], 1)

                in_pairs(pool, CHUNKS, shift)


def transformer_output(nc, m):
    ON_GPSIMD = 5
    with stage(nc, "y1", "gated", "x") as (block, s):

        def add(eng, c):
            eng.wait_ge(s["gated"], c + 1)
            x = m.x[:, bass.ts(c, TPC), :]
            eng.tensor_tensor(x, x, m.y[:, bass.ts(c, TPC), :], ALU.add).then_inc(s["x"], 1)

        @block.vector
        def _(dve):
            with dve.Fori(0, CHUNKS) as c:
                y = m.y[:, bass.ts(c, TPC), :]
                dve.tensor_tensor(y, y, m.modb[:, 5:6, :].broadcast_to([P, TPC, D]), ALU.mult).then_inc(s["gated"], 1)
            with dve.Fori(ON_GPSIMD, CHUNKS) as c:
                add(dve, c)

        @block.gpsimd
        def _(pool):
            with pool.Fori(0, ON_GPSIMD) as c:
                add(pool, c)


def layer_of(weights, layer):
    return weights[bass.ts(layer, 1)]


def local_attention(nc, m):
    SCALE = 64.0
    TERMS = (0, 0), (0, 1), (1, 0)
    QK = 2 * INNER
    PAIRS = HEADS // 2
    table, mask, gain = m.table, m.mask, m.gain
    with ExitStack() as ctx:
        def sb(name, shape, dt=F32):
            return ctx.enter_context(nc.sbuf_tensor(f"la_{name}", shape, dt))

        gain_rot = sb("gain_rot", [P, 2, 2, HALF])
        y_now = sb("y_now", [P, 2, D])
        yt_whole = sb("yt_whole", [P, 2, KD, P + 4])
        yt = sb("yt", [P, 2, 2, KD, P], F16)
        wqkv = sb("wqkv16", [P, 2, KD, 3 * INNER], F16)
        wo = sb("wo16", [P, 2, INNER // P, D], F16)
        cs = sb("cs", [P, 2, 2, 2 * DH])
        squares = sb("squares", [P, QK])
        straight = sb("straight", [P, 2, QK])
        crossed = sb("crossed", [P, QK])
        ss = sb("ss", [P, 2 * HEADS])
        rnorm = sb("rnorm", [P, 2 * HEADS])
        qscale = sb("qscale", [P, 2, HEADS])
        qz = sb("qz", [P, HEADS, P])
        kt = sb("kt", [P, PAIRS, 2, P])
        v = sb("v", [P, 2, INNER])
        scores = sb("scores", [P, HEADS, 2 * P])
        top = sb("top", [P, HEADS])
        bias = sb("bias", [P, HEADS])
        minus_qscale = sb("minus_qscale", [P, HEADS])
        total = sb("total", [P, HEADS])
        rtotal = sb("rtotal", [P, HEADS])
        pt = sb("pt", [P, PAIRS, 4, P])
        o = sb("o", [P, INNER])
        ot = sb("ot", [P, 2, INNER // P, P], F16)
        Q_BANK, K_BANK, V_BANK, TURN, SCORE, PTURN, OUT = 0, 1, 2, 3, 4, 6, 7

        def run(step, loop):
            for i in range(-3, 2):
                step(i, i % 2)
            with loop(1, TILES // 2 - 2) as k:
                step(k * 2, 0)
                step(k * 2 + 1, 1)
            for i in range(TILES - 4, TILES + 1):
                step(i, i % 2)

        def exists(w):
            return not isinstance(w, int) or 0 <= w < TILES

        with stage(nc, "la", "w_high", "w_low", "yt_high", "yt_low", "ot_high", "consts", "zeroed", "y_now", "y_t", "yt", "qk_mm", "v_mm", "cs", "rot", "squares", "summed", "ss", "rnorm", "crossed",
                   "qk", "qk_t", "qk_ev", "v", "score", "masked", "bias", "exp", "p_t", "p_act", "p_dve", "pv", "recip",
                   "o", "o_t", "ot", "proj", "y") as (block, s):

            @block.gpsimd
            def _(pool):
                credit(pool, s["y_now"], s["cs"], s["rnorm"], s["crossed"], s["qk"])
                pool.memset(yt_whole[:, 1, :, P:P + 1], 0.0)
                pool.memset(qz[:, :, :], 0.0)
                pool.tensor_scalar(gain_rot[:, :, 0, :], gain[:, :, 1, :], -1.0, None, ALU.mult)
                pool.tensor_copy(gain_rot[:, :, 1, :], gain[:, :, 0, :]).then_inc(s["consts"], 1)
                pool.wait_ge(s["consts"], 1)

                def load_y(w, u):
                    need(pool, s["y_t"], w - 1)
                    pool.tensor_copy(y_now[:, u:u + 1, :], m.y[:, bass.ts(w, 1), :]).then_inc(s["y_now"], 1)

                def tables(w, u):
                    need(pool, s["rot"], w - 1)
                    for n, g in ((0, gain), (1, gain_rot)):
                        t = pool.tensor_tensor(cs[:, u, n, :].rearrange("p (q h d) -> p q h d", q=2, h=2),
                                               table[:, bass.ts(w, 1), 2 * n:2 * n + 2, :].rearrange("p o q d -> p (o q) d")
                                               .unsqueeze(2).broadcast_to([P, 2, 2, HALF]), g[:, :, :, :], ALU.mult)
                    t.then_inc(s["cs"], 1)

                def normalise(w, u):
                    need(pool, s["rot"], w + 1)
                    pool.tensor_tensor(straight[:, u, :], straight[:, u, :], crossed[:, :], ALU.add).then_inc(s["crossed"], 1)
                    need(pool, s["ss"], w + 1)
                    pool.tensor_tensor(rnorm[:, :], ss[:, :], m.minus_half[:, 0:2 * HEADS], ALU.pow).then_inc(s["rnorm"], 1)
                    need(pool, s["rnorm"], w + 1)
                    need(pool, s["crossed"], w + 1)
                    need(pool, s["exp"], PAIRS * (w - 1))
                    kk = straight[:, u, INNER:QK].rearrange("p (h d) -> p h d", d=DH)
                    pool.tensor_tensor(kk, kk, rnorm[:, HEADS:2 * HEADS].unsqueeze(2).broadcast_to([P, HEADS, DH]), ALU.mult)
                    pool.tensor_scalar(qscale[:, u, :], rnorm[:, 0:HEADS], QK_SCALE, None, ALU.mult).then_inc(s["qk"], 1)

                def step(i, u):
                    if exists(i + 3):
                        load_y(i + 3, 1 - u)
                    if exists(i + 2):
                        tables(i + 2, u)
                        normalise(i + 2, u)

                run(step, pool.Fori)

            @block.tensor
            def _(pe):
                credit(pe, s["y_t"], s["qk_mm"], s["v_mm"], s["qk_t"], s["score"], s["p_t"], s["pv"], s["o_t"], s["proj"])
                pe.wait_ge(s["w_low"], 2)


                def turn_y(w, u):
                    need(pe, s["y_now"], w + 1)
                    if isinstance(w, int):
                        need(pe, s["yt"], w)
                    need(pe, s["qk_ev"], 2 * (w - 1))
                    for k in range(KD):
                        t = pe.transpose(m.ps[:, TURN, k * P:(k + 1) * P], y_now[:, u, k * P:(k + 1) * P], m.ident[:, :])
                    t.then_inc(s["y_t"], 1)

                def project(n, u):
                    terms = [(k, p, q) for k in range(KD) for p, q in TERMS]
                    for i, (k, p, q) in enumerate(terms):
                        mm = pe.matmul(m.ps[:, n, :], yt[:, u, p, k, :], wqkv[:, q, k, n * INNER:(n + 1) * INNER],
                                       start=(i == 0), stop=(i == len(terms) - 1))
                    return mm

                def project_qk(w, u, n):
                    need(pe, s["yt_low"], w + 1)
                    need(pe, s["rot"], w)
                    need(pe, s["squares"], w)
                    project(n, u).then_inc(s["qk_mm"], 1)

                def project_v(w, u):
                    need(pe, s["v"], w)
                    need(pe, s["ot"], w - 1)
                    project(V_BANK, u).then_inc(s["v_mm"], 1)

                def turn_qk(w, u, n):
                    if n == 0:
                        need(pe, s["qk"], w + 1)
                        if exists(w + 1):
                            need(pe, s["yt"], w + 2)
                        else:
                            need(pe, s["qk_ev"], 2 * w)
                    else:
                        need(pe, s["qk_ev"], 2 * w + 1)
                    for g in range(PAIRS):
                        t = pe.transpose(m.ps[:, TURN, g * P:(g + 1) * P],
                                         straight[:, u, n * INNER + g * P:n * INNER + (g + 1) * P], m.ident[:, :])
                    t.then_inc(s["qk_t"], 1)

                def turn_o(w):
                    need(pe, s["o"], w + 1)
                    need(pe, s["v"], w + 2 if exists(w + 1) else w + 1)
                    for k in range(INNER // P):
                        t = pe.transpose(m.ps[:, V_BANK, k * P:(k + 1) * P], o[:, k * P:(k + 1) * P], m.ident[:, :])
                    t.then_inc(s["o_t"], 1)

                def score(w, g):
                    need(pe, s["qk_ev"], 2 * w + 2)
                    need(pe, s["masked"], PAIRS * w + g - 2 + 1)
                    for h in range(2):
                        mm = pe.matmul(m.ps[:, SCORE + g % 2, h * 2 * P:(h + 1) * 2 * P], qz[:, 2 * g + h, :],
                                       kt[:, g, :, :].rearrange("p b k -> p (b k)"), start=True, stop=True)
                    mm.then_inc(s["score"], 1)

                def turn_weights(w, g):
                    need(pe, s["exp"], PAIRS * w + g + 1)
                    if g % 2:
                        need(pe, s["p_dve"], 2 * w + g // 2 + 1)
                    else:
                        need(pe, s["p_act"], 2 * w + g // 2)
                    for n in range(4):
                        t = pe.transpose(m.ps[:, PTURN, n * P:(n + 1) * P],
                                         scores[:, 2 * g + n // 2, (n % 2) * P:(n % 2 + 1) * P], m.ident[:, :])
                    t.then_inc(s["p_t"], 1)

                def weigh(w):
                    need(pe, s["p_dve"], 2 * w + 2)
                    need(pe, s["p_act"], 2 * w + 2)
                    need(pe, s["v"], w + 1)
                    need(pe, s["y"], w)
                    for h in range(HEADS):
                        for b in range(2):
                            mm = pe.matmul(m.ps[:, OUT, h * DH:(h + 1) * DH], pt[:, h // 2, (h % 2) * 2 + b, :],
                                           v[:, b, h * DH:(h + 1) * DH], start=(b == 0), stop=(b == 1))
                    mm.then_inc(s["pv"], 1)

                def project_o(w):
                    need(pe, s["ot"], w + 1)
                    terms = [(k, p, q) for k in range(INNER // P) for p, q in TERMS]
                    for i, (k, p, q) in enumerate(terms):
                        mm = pe.matmul(m.ps[:, OUT, 0:D], ot[:, p, k, :], wo[:, q, k, :], start=(i == 0), stop=(i == len(terms) - 1))
                    mm.then_inc(s["proj"], 1)

                def step(i, u):
                    now, ahead, far, last = exists(i), exists(i + 1), exists(i + 2), exists(i - 1)
                    if now:
                        turn_weights(i, 0)
                    if far:
                        project_qk(i + 2, u, 0)
                    if now:
                        turn_weights(i, 1)
                    if last:
                        turn_o(i - 1)
                    if far:
                        project_qk(i + 2, u, 1)
                    if ahead:
                        turn_qk(i + 1, 1 - u, 0)
                    if now:
                        turn_weights(i, 2)
                    if last:
                        project_o(i - 1)
                    if ahead:
                        turn_qk(i + 1, 1 - u, 1)
                        project_v(i + 1, 1 - u)
                    if now:
                        turn_weights(i, 3)
                    if ahead:
                        score(i + 1, 0)
                        score(i + 1, 1)
                    if exists(i + 3):
                        turn_y(i + 3, 1 - u)
                    if ahead:
                        score(i + 1, 2)
                    if now:
                        weigh(i)
                    if ahead:
                        score(i + 1, 3)

                run(step, pe.Fori)

            @block.scalar
            def _(act):
                credit(act, s["yt"], s["yt_high"], s["squares"], s["v"], s["qk_ev"], s["exp"], s["p_act"], s["ot_high"])
                for whole, to in ((m.wqkv, wqkv), (m.wo, wo)):
                    act.activation(to[:, 0, :, :], whole[:, :, :], ACT.Copy, scale=SCALE).then_inc(s["w_high"], 1)
                act.wait_ge(s["consts"], 1)
                act.wait_ge(s["zeroed"], 1)

                def shifted(w, u):
                    need(act, s["y_t"], w + 1)
                    need(act, s["yt_low"], w - 1)
                    need(act, s["yt"], w)
                    act.copy(yt_whole[:, u, 0, 0:P], m.ps[:, TURN, 0:P])
                    act.copy(yt_whole[:, u, 1, 0:1], yt_whole[:, 1 - u, 1, P:P + 1])
                    act.copy(yt_whole[:, u, 1, 1:P + 1], m.ps[:, TURN, P:2 * P]).then_inc(s["yt"], 1)
                    need(act, s["yt"], w + 1)
                    need(act, s["qk_mm"], 2 * (w - 1))
                    need(act, s["v_mm"], w - 1)
                    act.copy(yt[:, u, 0, :, :], yt_whole[:, u, :, 0:P]).then_inc(s["yt_high"], 1)

                def square(w):
                    need(act, s["qk_mm"], 2 * w + 2)
                    need(act, s["ss"], w)
                    act.activation(squares[:, :], m.ps[:, Q_BANK:K_BANK + 1, :].rearrange("p b e -> p (b e)"),
                                   ACT.Square).then_inc(s["squares"], 1)

                def take_v(w, u):
                    need(act, s["v_mm"], w + 1)
                    need(act, s["pv"], w)
                    act.activation(v[:, u, :], m.ps[:, V_BANK, :], ACT.Copy, scale=1 / SCALE).then_inc(s["v"], 1)

                def take_q(w):
                    need(act, s["qk_t"], 2 * w + 1)
                    need(act, s["score"], PAIRS * w)
                    for h in range(2):
                        rows = slice(h * DH, (h + 1) * DH)
                        e = act.copy(qz[rows, h:HEADS:2, :], m.ps[rows, TURN, :].rearrange("p (g k) -> p g k", k=P))
                    e.then_inc(s["qk_ev"], 1)

                def take_k(w, u):
                    need(act, s["qk_t"], 2 * w + 2)
                    act.copy(kt[:, :, u, :], m.ps[:, TURN, :].rearrange("p (g k) -> p g k", k=P)).then_inc(s["qk_ev"], 1)

                def soften(w, u, g):
                    need(act, s["bias"], PAIRS * w + g + 1)
                    if g == 0:
                        need(act, s["recip"], w)
                    for h in (2 * g, 2 * g + 1):
                        e = act.activation(scores[:, h, :], scores[:, h, :], ACT.Exp, bias=bias[:, h:h + 1],
                                           scale=qscale[:, u, h:h + 1], accum_out=total[:, h:h + 1])
                    e.then_inc(s["exp"], 1)

                def take_weights(w, g):
                    need(act, s["p_t"], PAIRS * w + g + 1)
                    need(act, s["pv"], w)
                    act.copy(pt[:, g, :, :].rearrange("p n k -> p (n k)"), m.ps[:, PTURN, :]).then_inc(s["p_act"], 1)

                def take_o(w):
                    need(act, s["o_t"], w + 1)
                    need(act, s["proj"], w)
                    act.copy(ot[:, 0, :, :].rearrange("p k t -> p (k t)"), m.ps[:, V_BANK, :]).then_inc(s["ot_high"], 1)

                def step(i, u):
                    now, ahead = exists(i), exists(i + 1)
                    if now:
                        take_weights(i, 1)
                    if exists(i - 1):
                        take_o(i - 1)
                    if exists(i + 2):
                        square(i + 2)
                    if ahead:
                        take_q(i + 1)
                        take_k(i + 1, 1 - u)
                    if now:
                        take_weights(i, 3)
                    if ahead:
                        soften(i + 1, 1 - u, 0)
                        soften(i + 1, 1 - u, 1)
                    if exists(i + 3):
                        shifted(i + 3, 1 - u)
                    if ahead:
                        soften(i + 1, 1 - u, 2)
                        take_v(i + 1, 1 - u)
                        soften(i + 1, 1 - u, 3)

                run(step, act.Fori)

            @block.vector
            def _(dve):
                credit(dve, s["yt_low"], s["rot"], s["summed"], s["ss"], s["masked"], s["bias"], s["p_dve"], s["recip"], s["o"], s["ot"], s["y"])
                for n, (whole, to) in enumerate(((m.wqkv, wqkv), (m.wo, wo))):
                    dve.wait_ge(s["w_high"], n + 1)
                    dve.scalar_tensor_tensor(to[:, 1, :, :], whole[:, :, :], SCALE, to[:, 0, :, :], ALU.mult, ALU.subtract).then_inc(s["w_low"], 1)
                dve.memset(kt[:, :, 1, :], 0.0)
                dve.memset(v[:, 1, :], 0.0).then_inc(s["zeroed"], 1)
                dve.wait_ge(s["consts"], 1)

                def rotate(w, u):
                    need(dve, s["qk_mm"], 2 * w + 2)
                    need(dve, s["squares"], w + 1)
                    need(dve, s["cs"], w + 1)
                    need(dve, s["qk_t"], 2 * (w - 1))
                    need(dve, s["qk"], w)
                    qk = m.ps[:, Q_BANK:K_BANK + 1, :].rearrange("p b (h d) -> p b h d", d=DH)
                    to = straight[:, u, :].rearrange("p (b h d) -> p b h d", b=2, d=DH)
                    to_crossed = crossed[:, :].rearrange("p (b h d) -> p b h d", b=2, d=DH)
                    cos, sin = (cs[:, u, n, :].rearrange("p (b d) -> p b d", b=2).unsqueeze(2) for n in range(2))
                    dve.tensor_tensor(to, qk, cos.broadcast_to([P, 2, HEADS, DH]), ALU.mult)
                    for half in range(2):
                        here, there = slice(half * HALF, (half + 1) * HALF), slice((1 - half) * HALF, (2 - half) * HALF)
                        r = dve.tensor_tensor(to_crossed[:, :, :, here], qk[:, :, :, there],
                                              sin[:, :, :, here].broadcast_to([P, 2, HEADS, HALF]), ALU.mult)
                    r.then_inc(s["rot"], 1)

                def sums(w):
                    dve.tensor_reduce(ss[:, :], squares[:, :].rearrange("p (h d) -> p h d", d=DH), AX.X, ALU.add).then_inc(s["summed"], 1)
                    need(dve, s["summed"], w + 1)
                    dve.tensor_scalar(ss[:, :], ss[:, :], 1e-24 * SCALE ** 2, None, ALU.max).then_inc(s["ss"], 1)

                def biases(w, g):
                    need(dve, s["masked"], PAIRS * w + g + 1)
                    heads = slice(2 * g, 2 * g + 2)
                    dve.tensor_tensor(bias[:, heads], top[:, heads], minus_qscale[:, heads], ALU.mult).then_inc(s["bias"], 1)

                def scores_stand(w, g):
                    need(dve, s["score"], PAIRS * w + g + 1)

                def masked(w, u, g):
                    kind = 2 if isinstance(w, int) and w == 0 else u
                    if g == 0:
                        need(dve, s["qk"], w + 1)
                        need(dve, s["p_t"], PAIRS * w)
                        scores_stand(w, g)
                        dve.tensor_scalar(minus_qscale[:, 0:HEADS - 2], qscale[:, u, 0:HEADS - 2], -1.0, None, ALU.mult)
                    if g == PAIRS - 1:
                        scores_stand(w, g)
                        dve.tensor_scalar(minus_qscale[:, HEADS - 2:HEADS], qscale[:, u, HEADS - 2:HEADS], -1.0, None, ALU.mult)
                    for h in range(2):
                        r = dve.tensor_tensor_reduce(scores[:, 2 * g + h, :], m.ps[:, SCORE + g % 2, h * 2 * P:(h + 1) * 2 * P],
                                                     mask[:, kind, :, :].rearrange("p b k -> p (b k)"), 1.0, -3e38,
                                                     ALU.add, ALU.max, top[:, 2 * g + h:2 * g + h + 1])
                    r.then_inc(s["masked"], 1)

                def take_weights(w, g):
                    need(dve, s["p_t"], PAIRS * w + g + 1)
                    need(dve, s["pv"], w)
                    dve.tensor_copy(pt[:, g, :, :].rearrange("p n k -> p (n k)"), m.ps[:, PTURN, :]).then_inc(s["p_dve"], 1)

                def divide(w):
                    need(dve, s["exp"], PAIRS * (w + 1))
                    dve.reciprocal(rtotal[:, :], total[:, :]).then_inc(s["recip"], 1)

                def take_o(w):
                    need(dve, s["recip"], w + 1)
                    need(dve, s["pv"], w + 1)
                    need(dve, s["o_t"], w)
                    dve.tensor_tensor(o[:, :].rearrange("p (h d) -> p h d", d=DH), m.ps[:, OUT, :].rearrange("p (h d) -> p h d", d=DH),
                                      rtotal[:, :].unsqueeze(2).broadcast_to([P, HEADS, DH]), ALU.mult).then_inc(s["o"], 1)

                def low_y(w, u):
                    need(dve, s["yt_high"], w + 1)
                    dve.tensor_tensor(yt[:, u, 1, :, :], yt_whole[:, u, :, 0:P], yt[:, u, 0, :, :], ALU.subtract).then_inc(s["yt_low"], 1)

                def low_o(w):
                    need(dve, s["ot_high"], w + 1)
                    dve.tensor_tensor(ot[:, 1, :, :].rearrange("p k t -> p (k t)"), m.ps[:, V_BANK, :],
                                      ot[:, 0, :, :].rearrange("p k t -> p (k t)"), ALU.subtract).then_inc(s["ot"], 1)

                def residual(w):
                    need(dve, s["proj"], w + 1)
                    y = m.y[:, bass.ts(w, 1), :]
                    dve.scalar_tensor_tensor(y, m.ps[:, OUT:OUT + 1, 0:D], 1 / SCALE, y, ALU.mult, ALU.add).then_inc(s["y"], 1)

                def halves(w):
                    need(dve, s["y"], w + 1)
                    for h in range(2):
                        dve.bn_stats(m.y_six[:, h, bass.ts(w, 1), :], m.y[:, bass.ts(w, 1), h * P:(h + 1) * P])

                def step(i, u):
                    now, ahead = exists(i), exists(i + 1)
                    if exists(i - 1):
                        low_o(i - 1)
                    if now:
                        take_weights(i, 2)
                        divide(i)
                    if exists(i + 2):
                        rotate(i + 2, u)
                    if exists(i - 1):
                        residual(i - 1)
                    if ahead:
                        masked(i + 1, 1 - u, 0)
                        scores_stand(i + 1, 1)
                        biases(i + 1, 0)
                        masked(i + 1, 1 - u, 1)
                        scores_stand(i + 1, 2)
                        biases(i + 1, 1)
                        masked(i + 1, 1 - u, 2)
                        biases(i + 1, 2)
                    if exists(i + 2):
                        sums(i + 2)
                    if exists(i - 1):
                        halves(i - 1)
                    if exists(i + 3):
                        low_y(i + 3, 1 - u)
                    if now:
                        take_o(i)
                    if ahead:
                        masked(i + 1, 1 - u, 3)
                        biases(i + 1, 3)
                        take_weights(i + 1, 0)

                run(step, dve.Fori)


MLP_SCALE = 64.0
MLP_TILES = -(-HID // P)


def gated_mlp_statistics(nc, m, b, a, layer):
    ET, LOADS = MLP_TILES, 10
    full, rest = (ET - 1) * P, HID - (ET - 1) * P
    with ExitStack() as ctx:
        def sb(name, shape, dt=F32):
            return ctx.enter_context(nc.sbuf_tensor(f"gs_{name}", shape, dt))

        gap = sb("gap", [P, 2, TILES])
        mean2 = sb("mean2", [P, 2, TILES])
        sq = sb("sq", [P, 2, TILES])
        moved = sb("moved", [P, 2, TILES])
        own = sb("own", [P, 2, TILES])
        pick = sb("pick", [P, P])
        minus = sb("minus", [P, 1])
        w1_whole = sb("w1_whole", [P, KD, 2 * HID])
        w2_whole = sb("w2_whole", [P, ET, D])
        with stage(nc, "gs", "w_in", "w_high", "w_low", "w_zeroed", "dve", "half", "zeroed", "shifted", "var", "rstd", "back", "pick", "minus", "mm", "end") as (block, s):
            last = TILES - 1

            @block.scalar
            def _(act):
                act.dma_start(w1_whole[:, :, :], layer_of(a["w1"], layer).rearrange("o (k p) e -> p (o k) e", p=P)).then_inc(s["w_in"], 16)
                w2_l = layer_of(a["w2"], layer).rearrange("o e d -> (o e) d")
                act.dma_start(w2_whole[:, 0:ET - 1, :], w2_l[0:full, :].rearrange("(t p) d -> p t d", p=P)).then_inc(s["w_in"], 16)
                act.dma_start(b.b2[:, :], layer_of(a["b2"], layer).rearrange("o d -> (o d)").partition_broadcast(P)).then_inc(s["w_in"], 16)
                for to, name in ((b.lng, "ln_g"), (b.lnb, "ln_b")):
                    act.dma_start(to[:, :], layer_of(a[name], layer).rearrange("o (k p) -> p (o k)", p=P), allow_slow_non_contiguous=True).then_inc(s["w_in"], 16)
                act.wait_ge(s["w_zeroed"], 1)
                act.dma_start(w2_whole[0:rest, ET - 1, :], w2_l[full:HID, :]).then_inc(s["w_in"], 16)
                b1_l = layer_of(a["b1"], layer).rearrange("o e -> (o e)")
                for n in range(2):
                    part = b1_l[n * HID:(n + 1) * HID]
                    act.dma_start(b.b1[:, n, 0:ET - 1], part[0:full].rearrange("(t p) -> p t", p=P), allow_slow_non_contiguous=True).then_inc(s["w_in"], 16)
                    act.dma_start(b.b1[0:rest, n, ET - 1:ET], part[full:HID].rearrange("(p t) -> p t", t=1), allow_slow_non_contiguous=True).then_inc(s["w_in"], 16)
                act.wait_ge(s["w_in"], 16 * LOADS)
                for whole, to in ((w1_whole, b.w1), (w2_whole, b.w2)):
                    act.activation(to[:, 0, :, :], whole[:, :, :], ACT.Copy, scale=MLP_SCALE).then_inc(s["w_high"], 1)

            @block.gpsimd
            def _(pool):
                pool.memset(w2_whole[:, ET - 1, :], 0.0)
                pool.memset(b.b1[:, :, ET - 1:ET], 0.0).then_inc(s["w_zeroed"], 1)
                pool.memset(moved[:, :, :], 0.0)
                pool.memset(m.next[:, :, :], 0.0)
                pool.memset(pick[:, :], 0.0).then_inc(s["zeroed"], 1)
                pool.wait_ge(s["zeroed"], 1)
                pool.memset(pick[0:1, :], 1.0).then_inc(s["pick"], 1)
                pool.wait_ge(s["var"], 1)
                pool.tensor_tensor(own[:, 1, :], own[:, 1, :], m.minus_half[:, 0:TILES], ALU.pow).then_inc(s["rstd"], 1)

            @block.sync
            def _(sp):
                sp.wait_ge(s["zeroed"], 1)
                sp.wait_ge(s["half"], 1)
                for n, src in enumerate((mean2[:, 1, :], sq[:, 1, :])):
                    sp.dma_start(moved[1:P, n, :], src[0:P - 1, :]).then_inc(s["shifted"], 16)
                    sp.dma_start(moved[0:1, n, 1:TILES], src[P - 1:P, 0:last]).then_inc(s["shifted"], 16)
                sp.wait_ge(s["rstd"], 1)
                sp.dma_start(m.next[0:P - 1, :, :], own[1:P, :, :]).then_inc(s["back"], 16)
                sp.dma_start(m.next[P - 1:P, :, 0:last], own[0:1, :, 1:TILES]).then_inc(s["back"], 16)
                sp.wait_ge(s["back"], 32)

            @block.vector
            def _(dve):
                even, odd = m.y_six[:, :, :, 1], m.y_six[:, :, :, 4]
                dve.tensor_tensor(gap[:, :, :], even, odd, ALU.subtract).then_inc(s["dve"], 1)
                dve.tensor_tensor(mean2[:, :, :], even, odd, ALU.add).then_inc(s["dve"], 1)
                dve.tensor_tensor(sq[:, :, :], m.y_six[:, :, :, 2], m.y_six[:, :, :, 5], ALU.add).then_inc(s["dve"], 1)
                dve.wait_ge(s["dve"], 3)
                dve.tensor_scalar(mean2[:, :, :], mean2[:, :, :], 0.5, None, ALU.mult).then_inc(s["dve"], 1)
                dve.scalar_tensor_tensor(gap[:, :, :], gap[:, :, :], P / 4.0, gap[:, :, :], ALU.mult, ALU.mult).then_inc(s["dve"], 1)
                dve.wait_ge(s["dve"], 5)
                dve.tensor_tensor(sq[:, :, :], sq[:, :, :], gap[:, :, :], ALU.add).then_inc(s["half"], 1)
                dve.wait_ge(s["half"], 1)
                dve.wait_ge(s["shifted"], 64)
                first, second = mean2[:, 0, :], moved[:, 0, :]
                dve.tensor_tensor(own[:, 0, :], first, second, ALU.add).then_inc(s["dve"], 1)
                dve.tensor_tensor(gap[:, 0, :], first, second, ALU.subtract).then_inc(s["dve"], 1)
                dve.tensor_tensor(own[:, 1, :], sq[:, 0, :], moved[:, 1, :], ALU.add).then_inc(s["dve"], 1)
                dve.wait_ge(s["dve"], 8)
                dve.tensor_scalar(own[:, 0, :], own[:, 0, :], 0.5, None, ALU.mult).then_inc(s["dve"], 1)
                dve.tensor_scalar(own[:, 1, :], own[:, 1, :], 1.0 / D, LN_EPS, ALU.mult, ALU.add).then_inc(s["dve"], 1)
                dve.scalar_tensor_tensor(gap[:, 0, :], gap[:, 0, :], 0.25, gap[:, 0, :], ALU.mult, ALU.mult).then_inc(s["dve"], 1)
                dve.wait_ge(s["dve"], 11)
                dve.tensor_tensor(own[:, 1, :], own[:, 1, :], gap[:, 0, :], ALU.add).then_inc(s["var"], 1)
                dve.wait_ge(s["w_in"], 16 * LOADS)
                dve.tensor_scalar(b.b1_scaled[:, :], b.b1[:, 0, :], MLP_SCALE, None, ALU.mult)
                for n, (whole, to) in enumerate(((w1_whole, b.w1), (w2_whole, b.w2))):
                    dve.wait_ge(s["w_high"], n + 1)
                    dve.scalar_tensor_tensor(to[:, 1, :, :], whole[:, :, :], MLP_SCALE, to[:, 0, :, :], ALU.mult, ALU.subtract).then_inc(s["w_low"], 1)
                dve.wait_ge(s["rstd"], 1)
                dve.tensor_copy(m.mean[:, :], own[:, 0, :])
                dve.tensor_copy(m.rstd[:, :], own[:, 1, :])
                dve.scalar_tensor_tensor(minus[:, :], own[:, 0, 0:1], -1.0, own[:, 1, 0:1], ALU.mult, ALU.mult).then_inc(s["minus"], 1)
                dve.wait_ge(s["mm"], 1)
                dve.tensor_copy(m.first[:, :], m.ps[:, 0, 0:1]).then_inc(s["end"], 1)

            @block.tensor
            def _(pe):
                pe.wait_ge(s["pick"], 1)
                pe.wait_ge(s["minus"], 1)
                pe.matmul(m.ps[:, 0, 0:1], pick[:, :], minus[:, :], start=True, stop=True).then_inc(s["mm"], 1)


def gated_mlp(nc, m, b, a, layer):
    SCALE = MLP_SCALE
    TERMS = (0, 0), (0, 1), (1, 0)
    ET = MLP_TILES
    TURN_AT = ET - 4
    sizes = [min(P, HID - e * P) for e in range(ET)]
    with ExitStack() as ctx:
        def sb(name, shape, dt=F32):
            return ctx.enter_context(nc.sbuf_tensor(f"gm_{name}", shape, dt))

        normed = sb("normed", [P, 2, TPC, D])
        ht_whole = sb("ht_whole", [P, 2, KD, CHUNK + 4])
        ht = sb("ht", [P, 2, 2, KD, CHUNK], F16)
        gelu = sb("gelu", [P, 2, CHUNK])
        hid_whole = sb("hid_whole", [P, 2, CHUNK])
        hid = sb("hid", [P, 2, 2, ET, CHUNK], F16)
        with stage(nc, "gm", "next_in", "zeroed", "before", "normed", "turned", "ht_whole", "ht_high", "ht", "a_mm", "g_mm", "gelu",
                   "hid_whole", "hid_high", "hid", "out", "b2", "y") as (block, s):
            def run(step, loop):
                with loop(0, CHUNKS // 2 - 1) as k:
                    step(k * 2, 0)
                    step(k * 2 + 1, 1)
                step(CHUNKS - 2, 0)
                step(CHUNKS - 1, 1)

            def exists(c):
                return not isinstance(c, int) or c < CHUNKS

            @block.sync
            def _(sp):
                load_attention(sp, m, a, DEPTH - 1 - layer, s["next_in"])
                sp.wait_ge(s["next_in"], 16 * ATTENTION_LOADS)

            @block.gpsimd
            def _(pool):
                credit(pool, s["b2"])
                pool.memset(hid[:, :, :, ET - 1, :], 0.0).then_inc(s["zeroed"], 1)

                def bias(c, u):
                    need(pool, s["normed"], c + 1)
                    y = m.y[:, bass.ts(c, TPC), :]
                    pool.tensor_tensor(y, y, b.b2[:, :].unsqueeze(1).broadcast_to([P, TPC, D]), ALU.add).then_inc(s["b2"], 1)

                in_pairs(pool, CHUNKS, bias)

            @block.vector
            def _(dve):
                credit(dve, s["normed"], s["ht"], s["hid_whole"], s["hid"], s["y"])

                def norm(c, u):
                    need(dve, s["turned"], KD * (c - 1))
                    for j in range(TPC):
                        t = bass.ts(c * TPC + j, 1)
                        for h, (mean, rstd) in enumerate(((m.mean, m.rstd), (m.next[:, 0, :], m.next[:, 1, :]))):
                            n = dve.tensor_scalar(normed[:, u, j:j + 1, h * P:(h + 1) * P], m.y[:, t, h * P:(h + 1) * P],
                                                  mean[:, t], rstd[:, t], ALU.subtract, ALU.mult)
                    n.then_inc(s["normed"], 1)

                def ht_low(c, u):
                    need(dve, s["a_mm"], ET * (c - 1))
                    for k in range(KD):
                        need(dve, s["ht_high"], KD * c + k + 1)
                        dve.tensor_tensor(ht[:, u, 1, k, :], ht_whole[:, u, k, 0:CHUNK], ht[:, u, 0, k, :], ALU.subtract).then_inc(s["ht"], 1)

                def gate(c, u):
                    def low(e):
                        need(dve, s["hid_high"], ET * c + e + 1)
                        rows = slice(0, sizes[e])
                        dve.scalar_tensor_tensor(hid[rows, u, 1, e, :], hid_whole[rows, e % 2, :], 1 / SCALE, hid[rows, u, 0, e, :],
                                                 ALU.mult, ALU.subtract).then_inc(s["hid"], 1)

                    need(dve, s["out"], TPC * (c - 1))
                    for e in range(ET):
                        need(dve, s["a_mm"], ET * c + e + 1)
                        need(dve, s["gelu"], ET * c + e + 1)
                        need(dve, s["hid"], ET * c + e - 2 + 1)
                        rows = slice(0, sizes[e])
                        dve.scalar_tensor_tensor(hid_whole[rows, e % 2, :], m.ps[rows, 2 + 2 * (e % 2), :], b.b1_scaled[rows, e:e + 1],
                                                 gelu[rows, e % 2, :], ALU.add, ALU.mult).then_inc(s["hid_whole"], 1)
                        if e:
                            low(e - 1)
                        if e == TURN_AT + 1 and exists(c + 1):
                            ht_low(c + 1, 1 - u)
                    low(ET - 1)

                def residual(c):
                    need(dve, s["b2"], c + 1)
                    for j in range(TPC):
                        need(dve, s["out"], TPC * c + j + 1)
                        y = m.y[:, bass.ts(c * TPC + j, 1), :]
                        dve.scalar_tensor_tensor(y, m.ps[:, 6 + j % 2:7 + j % 2, 0:D], 1 / SCALE, y, ALU.mult, ALU.add).then_inc(s["y"], 1)

                def step(c, u):
                    gate(c, u)
                    residual(c)
                    if exists(c + 2):
                        norm(c + 2, u)

                norm(0, 0)
                norm(1, 1)
                ht_low(0, 0)
                dve.wait_ge(s["zeroed"], 1)
                run(step, dve.Fori)

            @block.scalar
            def _(act):
                credit(act, s["ht_whole"], s["ht_high"], s["gelu"], s["hid_high"])
                act.activation(ht_whole[:, 1, 1, CHUNK:CHUNK + 1], m.first[:, :], ACT.Identity, bias=b.lnb[:, 1:2],
                               scale=b.lng[:, 1:2]).then_inc(s["before"], 1)
                act.wait_ge(s["before"], 1)

                def scaled(c, u):
                    need(act, s["ht"], KD * (c - 1))
                    need(act, s["turned"], KD * c + 1)
                    act.activation(ht_whole[:, u, 0, 0:CHUNK], m.ps[:, 0, :], ACT.Identity, bias=b.lnb[:, 0:1], scale=b.lng[:, 0:1]).then_inc(s["ht_whole"], 1)
                    need(act, s["turned"], KD * c + 2)
                    need(act, s["ht_whole"], KD * c)
                    act.copy(ht_whole[:, u, 1, 0:1], ht_whole[:, 1 - u, 1, CHUNK:CHUNK + 1])
                    act.activation(ht_whole[:, u, 1, 1:CHUNK + 1], m.ps[:, 1, :], ACT.Identity, bias=b.lnb[:, 1:2], scale=b.lng[:, 1:2]).then_inc(s["ht_whole"], 1)
                    need(act, s["a_mm"], ET * (c - 1))
                    for k in range(KD):
                        need(act, s["ht_whole"], KD * c + k + 1)
                        act.copy(ht[:, u, 0, k, :], ht_whole[:, u, k, 0:CHUNK]).then_inc(s["ht_high"], 1)

                def gelus(c, u):
                    def high(e):
                        need(act, s["hid_whole"], ET * c + e + 1)
                        rows = slice(0, sizes[e])
                        act.activation(hid[rows, u, 0, e, :], hid_whole[rows, e % 2, :], ACT.Copy, scale=1 / SCALE).then_inc(s["hid_high"], 1)

                    for e in range(ET):
                        need(act, s["g_mm"], ET * c + e + 1)
                        need(act, s["hid_whole"], ET * c + e - 2 + 1)
                        rows = slice(0, sizes[e])
                        act.activation(gelu[rows, e % 2, :], m.ps[rows, 3 + 2 * (e % 2), :], ACT.Gelu, bias=b.b1[rows, 1, e:e + 1],
                                       scale=1 / SCALE).then_inc(s["gelu"], 1)
                        if e:
                            high(e - 1)
                        if e == TURN_AT and exists(c + 1):
                            scaled(c + 1, 1 - u)
                    high(ET - 1)

                scaled(0, 0)
                act.wait_ge(s["zeroed"], 1)
                run(gelus, act.Fori)

            @block.tensor
            def _(pe):
                credit(pe, s["turned"], s["a_mm"], s["g_mm"], s["out"])

                def turn(c, u):
                    need(pe, s["normed"], c + 1)
                    for k in range(KD):
                        need(pe, s["ht_whole"], KD * (c - 1) + k + 1)
                        for j in range(TPC):
                            t = pe.transpose(m.ps[:, k, j * P:(j + 1) * P], normed[:, u, j, k * P:(k + 1) * P], m.ident[:, :])
                        t.then_inc(s["turned"], 1)

                def up(c, u, tiles):
                    need(pe, s["ht"], KD * (c + 1))
                    for e in tiles:
                        for part, mm_sem, free in ((1, s["g_mm"], s["gelu"]), (0, s["a_mm"], s["hid_whole"])):
                            need(pe, free, ET * c + e - 2 + 1)
                            terms = [(k, p, q) for k in range(KD) for p, q in TERMS]
                            for i, (k, p, q) in enumerate(terms):
                                mm = pe.matmul(m.ps[0:sizes[e], 2 + 2 * (e % 2) + part, :],
                                               b.w1[:, p, k, part * HID + e * P:part * HID + e * P + sizes[e]], ht[:, u, q, k, :],
                                               start=(i == 0), stop=(i == len(terms) - 1))
                            mm.then_inc(mm_sem, 1)

                def down(c, u):
                    need(pe, s["hid"], ET * (c + 1))
                    for j in range(TPC):
                        need(pe, s["y"], TPC * c + j - 2 + 1)
                        terms = [(e, p, q) for e in range(ET) for p, q in TERMS]
                        for i, (e, p, q) in enumerate(terms):
                            mm = pe.matmul(m.ps[:, 6 + j % 2, 0:D], hid[:, u, p, e, j * P:(j + 1) * P], b.w2[:, q, e, :],
                                           start=(i == 0), stop=(i == len(terms) - 1))
                        mm.then_inc(s["out"], 1)

                def step(c, u):
                    up(c, u, range(1, TURN_AT + 1))
                    if exists(c + 1):
                        turn(c + 1, 1 - u)
                    up(c, u, range(TURN_AT + 1, ET))
                    if exists(c + 1):
                        up(c + 1, 1 - u, range(1))
                    down(c, u)

                turn(0, 0)
                up(0, 0, range(1))
                run(step, pe.Fori)


def gated_mlp_layer(nc, m, f, layer):
    with ExitStack() as ctx:
        def sb(name, shape, dt=F32):
            return ctx.enter_context(nc.sbuf_tensor(f"gw_{name}", shape, dt))

        b = Memory()
        b.w1 = sb("w1", [P, 2, KD, 2 * HID], F16)
        b.w2 = sb("w2", [P, 2, MLP_TILES, D], F16)
        b.b1, b.b1_scaled = sb("b1", [P, 2, MLP_TILES]), sb("b1_scaled", [P, MLP_TILES])
        b.b2 = sb("b2", [P, D])
        b.lng, b.lnb = sb("lng", [P, KD]), sb("lnb", [P, KD])
        gated_mlp_statistics(nc, m, b, f, layer)
        gated_mlp(nc, m, b, f, layer)



GROUP = 4
GROUPS = L1_HEADS // GROUP
QUAD = 32
ROWS = 4 * L1_DH
MPARTS = 3
MASKED = -1e30


def attention1_projections(nc, m, a):
    OUTS = 2 * KD
    HP = P // 2
    STORES = 2
    with ExitStack() as ctx:
        def sb(name, shape, dt=F32):
            return ctx.enter_context(nc.sbuf_tensor(f"a1_{name}", shape, dt))

        w = sb("w", [P, 3, KD, D])
        normed = sb("normed", [P, 2, TPC, D])
        ht = sb("ht", [P, 2, KD, CHUNK])
        table = sb("table", [P, 2, 2, CHUNK])
        straight = sb("straight", [P, OUTS, CHUNK])
        crossed = sb("crossed", [P, 2, CHUNK])
        parts = sb("parts", [P, OUTS, 2, CHUNK], F16)
        with stage(nc, "a1", "w_in", "table_even", "table_odd", "ones", "normed", "turned", "ht", "mm", "v_mm", "rot", "sum", "high", "low", "v", "out_0", "out_1", "out_2", "out_3") as (block, s):

            table_in, parts_out = (s["table_even"], s["table_odd"]), [s[f"out_{n}"] for n in range(OUTS)]

            @block.sync
            def _(sp):
                for n, name in enumerate(("WQ", "WK", "WV")):
                    sp.dma_start(w[:, n, :, :], a[name].rearrange("(k p) e -> p k e", p=P)).then_inc(s["w_in"], 16)

                def store(c, u):
                    for n in range(OUTS):
                        for part, made in enumerate((s["high"], s["low"])):
                            need(sp, made, OUTS * c + n + 1)
                            rows = m.qk[n // KD, part, :, :].rearrange("(d i h) t -> i d h t", d=L1_DH, i=KD)[n % KD]
                            sp.dma_start(rows[:, :, bass.ts(c, CHUNK)], parts[:, n, part, :]).then_inc(parts_out[n], 16)

                in_pairs(sp, CHUNKS, store)

            @block.gpsimd
            def _(pool):
                credit(pool, s["sum"])
                pool.memset(m.v17[:, :, :, L1_DH:L1_DH + 1], 1.0).then_inc(s["ones"], 1)

                def load(c, u):
                    need(pool, s["rot"], OUTS * (c - 1))
                    pool.dma_start(table[:, u, :, :], a["rope"][:, :, bass.ts(c, CHUNK)]).then_inc(table_in[u], 16)

                def add(c, u):
                    for n in range(OUTS):
                        need(pool, s["rot"], OUTS * c + n + 1)
                        pool.tensor_tensor(straight[:, n, :], straight[:, n, :], crossed[:, n % 2, :], ALU.add).then_inc(s["sum"], 1)

                ahead_in_pairs(pool, CHUNKS, load, add)

            @block.vector
            def _(dve):
                credit(dve, s["normed"], s["rot"], s["low"])

                def norm(c, u):
                    need(dve, s["turned"], KD * (c - 1))
                    for j in range(TPC):
                        t = bass.ts(c * TPC + j, 1)
                        n = dve.tensor_scalar(normed[:, u, j:j + 1, :], m.x[:, t, :], m.mean[:, t], m.rstd[:, t], ALU.subtract, ALU.mult)
                    n.then_inc(s["normed"], 1)

                def rotate(c, u):
                    dve.wait_ge(table_in[u], (c - u) * 8 + 16)

                    def low(n):
                        need(dve, s["high"], OUTS * c + n + 1)
                        dve.tensor_tensor(parts[:, n, 1, :], straight[:, n, :], parts[:, n, 0, :], ALU.subtract).then_inc(s["low"], 1)

                    for n in range(OUTS):
                        need(dve, s["mm"], OUTS * c + n + 1)
                        scale = L1_DH ** -0.5 if n < KD else 1.0
                        need(dve, s["low"], OUTS * (c - 1) + n + 1)
                        dve.scalar_tensor_tensor(straight[:, n, :], m.ps[:, 2 + n, :], scale, table[:, u, 0, :], ALU.mult, ALU.mult)
                        need(dve, s["sum"], OUTS * c + n - 2 + 1)
                        for here, there in ((slice(0, HP), slice(HP, P)), (slice(HP, P), slice(0, HP))):
                            r = dve.scalar_tensor_tensor(crossed[here, n % 2, :], m.ps[there, 2 + n, :], scale, table[there, u, 1, :],
                                                         ALU.mult, ALU.mult)
                        r.then_inc(s["rot"], 1)
                        if n > 1:
                            low(n - 2)
                    low(OUTS - 2)
                    low(OUTS - 1)

                two_ahead_in_pairs(dve, CHUNKS, norm, rotate)

            @block.scalar
            def _(act):
                credit(act, s["ht"], s["high"], s["v"], *parts_out)
                act.wait_ge(s["ones"], 1)

                def scaled(c, u):
                    need(act, s["mm"], OUTS * (c - 1))
                    need(act, s["v_mm"], 2 * (c - 1))
                    for k in range(KD):
                        need(act, s["turned"], KD * c + k + 1)
                        act.activation(ht[:, u, k, :], m.ps[:, k, :], ACT.Identity, bias=m.modc[:, k:k + 1],
                                       scale=m.modc[:, KD + k:KD + k + 1]).then_inc(s["ht"], 1)

                def high(c, u):
                    for n in range(OUTS):
                        need(act, s["sum"], OUTS * c + n + 1)
                        need(act, parts_out[n], 16 * STORES * c)
                        act.copy(parts[:, n, 0, :], straight[:, n, :]).then_inc(s["high"], 1)
                    for b in range(2):
                        need(act, s["v_mm"], 2 * c + b + 1)
                        act.copy(m.v17[:, bass.ts(c * 2 + b, 2), :, 0:L1_DH],
                                 m.ps[:, 6 + b, :].rearrange("p (j h d) -> p j h d", j=2, d=L1_DH)).then_inc(s["v"], 1)

                ahead_in_pairs(act, CHUNKS, scaled, high)
                for done in parts_out:
                    need(act, done, 16 * STORES * CHUNKS)

            @block.tensor
            def _(pe):
                credit(pe, s["turned"], s["mm"], s["v_mm"])

                def turn(c, u):
                    need(pe, s["normed"], c + 1)
                    for k in range(KD):
                        need(pe, s["ht"], KD * (c - 1) + k + 1)
                        for j in range(TPC):
                            t = pe.transpose(m.ps[:, k, j * P:(j + 1) * P], normed[:, u, j, k * P:(k + 1) * P], m.ident[:, :])
                        t.then_inc(s["turned"], 1)

                def products(c, u):
                    pe.wait_ge(s["w_in"], 16 * 3)
                    need(pe, s["ht"], KD * (c + 1))
                    for n in range(OUTS):
                        need(pe, s["rot"], OUTS * (c - 1) + n + 1)
                        o = n % KD
                        for k in range(KD):
                            mm = pe.matmul(m.ps[:, 2 + n, :], w[:, n // KD, k, o * P:(o + 1) * P], ht[:, u, k, :],
                                           start=(k == 0), stop=(k == KD - 1))
                        mm.then_inc(s["mm"], 1)
                    for b in range(2):
                        need(pe, s["v"], 2 * (c - 1) + b + 1)
                        for j in range(2):
                            for k in range(KD):
                                mm = pe.matmul(m.ps[:, 6 + b, j * D:(j + 1) * D], ht[:, u, k, (2 * b + j) * P:(2 * b + j + 1) * P],
                                               w[:, 2, k, :], start=(k == 0), stop=(k == KD - 1))
                        mm.then_inc(s["v_mm"], 1)

                ahead_in_pairs(pe, CHUNKS, turn, products)


def attention1_buffers(nc, ctx):
    def sb(name, shape, dt=F32):
        return ctx.enter_context(nc.sbuf_tensor(f"s1_{name}", shape, dt))

    b = Memory()
    b.keys_max = sb("keys_max", [P, GROUP, N], F16)
    b.keys_now = sb("keys_now", [P, GROUP, N], F16)
    b.q_max = sb("q_max", [P, 2, GROUP, CHUNK], F16)
    b.q_now = sb("q_now", [P, 2, GROUP, CHUNK], F16)
    b.v_now = sb("v_now", [P, 4, GROUP, QUAD])
    b.zero16 = sb("zero16", [P, P], F16)
    b.ident16 = sb("ident16", [P, P], BF16)
    b.later_key = sb("later_key", [P, P], BF16)
    b.later_key_t = sb("later_key_t", [P, P], BF16)
    return b


def attention1_constants(pool, b, done):
    pool.memset(b.v_now[:, :, :, :], 0.0)
    for square in (b.zero16, b.ident16, b.later_key, b.later_key_t):
        z = pool.memset(square[:, :], 0.0)
    z.then_inc(done, 1)
    pool.wait_ge(done, 1)
    pool.affine_select(b.ident16[:, :], b.ident16[:, :], pattern=[[-1, P]], compare_op=ALU.not_equal, fill=1.0,
                       base=0, channel_multiplier=1)
    pool.affine_select(b.later_key[:, :], b.later_key[:, :], pattern=[[-1, P]], compare_op=ALU.is_ge, fill=MASKED,
                       base=0, channel_multiplier=1)
    pool.affine_select(b.later_key_t[:, :], b.later_key_t[:, :], pattern=[[1, P]], compare_op=ALU.is_ge, fill=MASKED,
                       base=0, channel_multiplier=-1).then_inc(done, 1)
    pool.wait_ge(done, 2)
    for buffer in (b.q_max, b.q_now):
        pool.memset(buffer[ROWS:P, :, :, :].bitcast(F32), 0.0)
    pool.memset(b.keys_max[ROWS:P, :, :].bitcast(F32), 0.0)
    pool.memset(b.keys_now[ROWS:P, :, :].bitcast(F32), 0.0).then_inc(done, 1)
    pool.wait_ge(done, 3)
    pool.memset(b.keys_now[ROWS:ROWS + MPARTS, :, :], 1.0).then_inc(done, 1)
    pool.wait_ge(done, 4)


def attention1(nc, m, b):
    with ExitStack() as ctx:
        def sb(name, shape, dt=F32):
            return ctx.enter_context(nc.sbuf_tensor(f"s1_{name}", shape, dt))

        b.copied = sb("copied", [P, 2, GROUP - 1, CHUNK], BF16)
        b.weights = sb("weights", [P, 2, 2, 2, CHUNK])
        b.tops = sb("tops", [P, CHUNKS, TILES, GROUP])
        b.minus_top = sb("minus_top", [P, GROUP, TILES])
        b.rest = sb("rest", [P, P])
        b.top_parts = sb("top_parts", [P, MPARTS, P], F16)
        b.o_t = sb("o_t", [P, CHUNK])
        b.recip = sb("recip", [P, TPC, GROUP])
        b.o_now = sb("o_now", [P, 2, TPC, GROUP, L1_DH])
        attend_and_find(nc, m, b, "f1", None, 0)
        with nc.Fori(0, GROUPS - 1) as g:
            attend_and_find(nc, m, b, "g1", g, g + 1)
        attend_and_find(nc, m, b, "h1", GROUPS - 1, None)


def attend_and_find(nc, m, b, name, group, next_group):
    attends, finds = group is not None, next_group is not None
    MAX_BANK, USED, TURNS = ((0, 1, 0, 7), (2, 4, 2, 4), 1) if attends else ((0, 1, 2, 3), (8, 8, 8, 8), 2)
    SCORE, OUT, TURN = 2, 6, 7
    PARTS = 4

    def before(j):
        return 2 * j * (j + 1)

    def steps(eng, j, step):
        step(0, 0, j, 0)
        if j:
            with eng.Fori(0, j) as c:
                for u in range(TPC):
                    step(c * TPC + 1 + u, None, c, u)
        for r in range(1, TPC):
            step(TPC * j + r, r, j, r)

    def parity(r, u, n):
        return (1 + u if r is None else r) % n

    def max_bank(r, u, h):
        return GROUP * parity(r, u, TURNS) + MAX_BANK[h]

    with stage(nc, name, "k_first", "k_in", "qm_in_even", "qm_in_odd", "q_in_even", "q_in_odd", "v_now", "max_mm", "copied", "max", "cleared", "top", "top_t", "split", "split_step",
               "top_out", "score", "exp", "pv", "o_t", "o_turned", "recip", "o_now", "o_out_even", "o_out_odd") as (block, s):
        qm_in, q_in, o_out = (s["qm_in_even"], s["qm_in_odd"]), (s["q_in_even"], s["q_in_odd"]), (s["o_out_even"], s["o_out_odd"])

        @block.sync
        def _(sp):
            credit(sp, *o_out)

            def parts_of(part):
                return slice(part * L1_DH, (part + 1) * L1_DH)

            def load_q(to, g, j, sem):
                for part in range(PARTS):
                    sp.dma_start(to[parts_of(part), j % 2, :, :],
                                 m.qk[0, part // 2, :, j * CHUNK:(j + 1) * CHUNK]
                                 .rearrange("(d h) t -> d h t", d=L1_DH)[:, bass.ts(g, GROUP), :]).then_inc(sem, 16)

            def store(j):
                need(sp, s["o_now"], j + 1)
                sp.dma_start(m.o[j * CHUNK:(j + 1) * CHUNK, bass.ts(group, GROUP * L1_DH)].rearrange("(t p) e -> p t e", p=P),
                             b.o_now[:, j % 2, :, :, :].rearrange("p t h d -> p t (h d)")).then_inc(o_out[j % 2], 16)

            def load_k(to, g, columns, sem):
                for part in range(PARTS):
                    sp.dma_start(to[parts_of(part), :, columns],
                                 m.qk[1, part % 2, :, columns].rearrange("(d h) t -> d h t", d=L1_DH)[:, bass.ts(g, GROUP), :]).then_inc(sem, 16)

            def load_queries(j):
                if attends:
                    need(sp, s["score"], 2 * before(j - 1))
                    load_q(b.q_now, group, j, q_in[j % 2])
                    sp.dma_start(b.q_now[ROWS:ROWS + MPARTS, j % 2, :, :], m.tops[:, :, j * CHUNK:(j + 1) * CHUNK]).then_inc(q_in[j % 2], 16)
                if finds:
                    need(sp, s["max_mm"], GROUP * before(j - 1))
                    load_q(b.q_max, next_group, j, qm_in[j % 2])

            def load_keys(columns, sem):
                if attends:
                    load_k(b.keys_now, group, columns, sem)
                if finds:
                    load_k(b.keys_max, next_group, columns, sem)

            load_keys(slice(0, CHUNK), s["k_first"])
            load_queries(0)
            load_keys(slice(CHUNK, N), s["k_in"])
            for j in range(1, CHUNKS):
                load_queries(j)
                if attends and j >= 2:
                    store(j - 2)
            if attends:
                store(CHUNKS - 2)
                store(CHUNKS - 1)
                for n in range(2):
                    sp.wait_ge(q_in[n], 16 * (PARTS + 1) * CHUNKS // 2)
                    need(sp, o_out[n], 16 * CHUNKS // 2)
            if finds:
                sp.wait_ge(s["split"], 1)
                sp.dma_start(m.tops.rearrange("n h (i q) -> (h i) n q", q=P), b.top_parts[:, :, :]).then_inc(s["top_out"], 16)
                sp.wait_ge(s["top_out"], 16)

        @block.gpsimd
        def _(pool):
            credit(pool, s["v_now"])
            for j in range(CHUNKS if attends else 0):
                def step(p, r, c, t):
                    n = before(j) + p
                    need(pool, s["pv"], 2 * (n - 4) + 2)
                    pool.tensor_copy(b.v_now[:, parity(r, t, 4), :, 0:L1_DH + 1],
                                     m.v17[:, bass.ts(c * TPC + t, 1), bass.ts(group, GROUP), :].rearrange("p o h d -> p (o h) d")).then_inc(s["v_now"], 1)

                steps(pool, j, step)

        @block.tensor
        def _(pe):
            credit(pe, s["max_mm"], s["score"], s["pv"], s["o_turned"])

            def find_max(j, p, r, c, t, h):
                if not finds:
                    return
                width = CHUNK if r is None else (r + 1) * P
                need(pe, s["max"], GROUP * (before(j) + p) + h - USED[h] + 1)
                if attends and h == 3 and r == 2:
                    need(pe, s["o_now"], j)
                mm = pe.matmul(m.ps[:, max_bank(r, t, h), 0:width], b.q_max[:, j % 2, h, t * P:(t + 1) * P],
                               b.keys_max[:, h, bass.ds(c * CHUNK, width)], start=True, stop=(r is None))
                if r is not None:
                    mm = pe.matmul(m.ps[:, max_bank(r, t, h), r * P:(r + 1) * P], b.ident16[:, :], b.later_key[:, :], start=False, stop=True)
                mm.then_inc(s["max_mm"], 1)

            def score(j, p, r, c, t, pair):
                if not attends:
                    return
                need(pe, s["exp"], 2 * (before(j) + p - 1) + pair + 1)
                skip = 0 if r is None else r * P
                for h in (2 * pair, 2 * pair + 1):
                    mm = pe.matmul(m.ps[:, SCORE + h, skip:CHUNK], b.keys_now[:, h, bass.ds((c * TPC + t) * P, P)],
                                   b.q_now[:, j % 2, h, skip:CHUNK], start=True, stop=(r is None))
                    if r is not None:
                        mm = pe.matmul(m.ps[:, SCORE + h, skip:skip + P], b.ident16[:, :], b.later_key_t[:, :], start=False, stop=True)
                mm.then_inc(s["score"], 1)

            def weigh(j, p, r, slot, pair):
                n = before(j) + p
                need(pe, s["exp"], 2 * n + pair + 1)
                need(pe, s["v_now"], n + 1)
                skip = 0 if r is None else r * P
                for h in (2 * pair, 2 * pair + 1):
                    mm = pe.matmul(m.ps[h * QUAD:(h + 1) * QUAD, OUT, skip:CHUNK], b.v_now[:, slot % 4, h, :],
                                   b.weights[:, slot % 2, pair, h % 2, skip:CHUNK], start=False, stop=(r == TPC - 1), skip_group_check=True)
                mm.then_inc(s["pv"], 1)

            def weigh_before(j, p, r, t):
                for pair in range(2 if attends else 0):
                    if r is None:
                        weigh(j, p - 1, None, t, pair)
                    elif r:
                        weigh(j, p - 1, r - 1 if r > 1 else None, r - 1, pair)
                    elif j:
                        weigh(j - 1, TPC * j - 1, TPC - 1, TPC - 1, pair)

            def turn_o(j):
                need(pe, s["o_t"], j + 1)
                if finds:
                    need(pe, s["max"], GROUP * (before(j + 1) + TPC * (j + 1) + 2) if j < CHUNKS - 1 else GROUP * before(CHUNKS))
                else:
                    need(pe, s["o_now"], j)
                for t in range(TPC):
                    x = pe.transpose(m.ps[:, TURN, t * P:(t + 1) * P], b.o_t[:, t * P:(t + 1) * P], m.ident[:, :])
                x.then_inc(s["o_turned"], 1)

            def step(j, p, r, c, t):
                find_max(j, p, r, c, t, 0)
                find_max(j, p, r, c, t, 1)
                if r == 0:
                    weigh_before(j, p, r, t)
                score(j, p, r, c, t, 0)
                score(j, p, r, c, t, 1)
                find_max(j, p, r, c, t, 2)
                find_max(j, p, r, c, t, 3)
                if r != 0:
                    weigh_before(j, p, r, t)
                elif attends:
                    need(pe, s["o_t"], j)
                    pe.matmul(m.ps[:, OUT, :], b.zero16[:, :], b.q_now[:, j % 2, 0, :], start=True, stop=False, skip_group_check=True)
                if attends and r == 1 and j:
                    turn_o(j - 1)

            pe.wait_ge(s["k_first"], 16 * PARTS * (attends + finds))
            for j in range(CHUNKS):
                if j == 1:
                    pe.wait_ge(s["k_in"], 16 * PARTS * (attends + finds))
                if attends:
                    pe.wait_ge(q_in[j % 2], 16 * (PARTS + 1) * (j // 2 + 1))
                if finds:
                    pe.wait_ge(qm_in[j % 2], 16 * PARTS * (j // 2 + 1))
                steps(pe, j, lambda p, r, c, t: step(j, p, r, c, t))
            if attends:
                for pair in range(2):
                    weigh(CHUNKS - 1, TPC * CHUNKS - 1, TPC - 1, TPC - 1, pair)
                turn_o(CHUNKS - 1)
            if finds:
                pe.wait_ge(s["top"], 1)
                pe.transpose(m.ps[:, MAX_BANK[0], 0:P], b.minus_top[:, :, :].rearrange("p h i -> p (h i)"), m.ident[:, :]).then_inc(s["top_t"], 1)

        @block.scalar
        def _(act):
            credit(act, s["exp"], s["copied"])
            for j in range(0 if attends else CHUNKS):
                def copy(p, r, c, t):
                    n = before(j) + p
                    width = CHUNK if r is None else (r + 1) * P
                    need(act, s["max_mm"], GROUP * n + GROUP)
                    need(act, s["max"], GROUP * (n - 1))
                    bank = max_bank(r, t, 1)
                    act.copy(b.copied[:, parity(r, t, 2), :, 0:width], m.ps[:, bank:bank + GROUP - 1, 0:width]).then_inc(s["copied"], 1)

                steps(act, j, copy)
            for j in range(CHUNKS if attends else 0):
                def step(p, r, c, t):
                    n = before(j) + p
                    skip = 0 if r is None else r * P
                    for pair in range(2):
                        need(act, s["score"], 2 * n + pair + 1)
                        need(act, s["pv"], 2 * (n - 2) + pair + 1)
                        act.activation(b.weights[:, parity(r, t, 2), pair, :, skip:CHUNK],
                                       m.ps[:, SCORE + 2 * pair:SCORE + 2 * pair + 2, skip:CHUNK], ACT.Exp).then_inc(s["exp"], 1)

                steps(act, j, step)

        @block.vector
        def _(dve):
            credit(dve, s["max"], s["o_t"], s["recip"], s["o_now"])
            dve.memset(b.tops[:, :, :, :], -3e38).then_inc(s["cleared"], 1)
            dve.wait_ge(s["cleared"], 1)

            def row_max(j, p, r, c, t, heads):
                n = GROUP * (before(j) + p)
                width = CHUNK if r is None else (r + 1) * P
                for h in heads if finds else ():
                    top = b.tops[:, bass.ts(c, 1), j * TPC + t, h]
                    if attends or h == 0:
                        need(dve, s["max_mm"], n + h + 1)
                        x = dve.tensor_reduce(top, m.ps[:, max_bank(r, t, h), 0:width], AX.X, ALU.max)
                    else:
                        need(dve, s["copied"], before(j) + p + 1)
                        part = b.copied[:, parity(r, t, 2), h - 1, 0:width]
                        x = dve.tensor_scalar(part, part, 1.0, None, ALU.mult, ALU.max, accum_out=top)
                    x.then_inc(s["max"], 1)

            def take_o(j):
                need(dve, s["pv"], 2 * before(j + 1))
                need(dve, s["o_turned"], j)
                dve.tensor_copy(b.o_t[:, :], m.ps[:, OUT, :]).then_inc(s["o_t"], 1)

            def divide_o(j):
                need(dve, s["o_turned"], j + 1)
                turned = m.ps[:, TURN, :].rearrange("p (t h e) -> p t h e", t=TPC, e=QUAD)
                dve.reciprocal(b.recip[:, :, :], turned[:, :, :, L1_DH]).then_inc(s["recip"], 1)
                need(dve, s["recip"], j + 1)
                need(dve, o_out[j % 2], 16 * (j // 2))
                dve.tensor_tensor(b.o_now[:, j % 2, :, :, :], turned[:, :, :, 0:L1_DH],
                                  b.recip[:, :, :].unsqueeze(3).broadcast_to([P, TPC, GROUP, L1_DH]), ALU.mult).then_inc(s["o_now"], 1)

            for j in range(CHUNKS):
                def step(p, r, c, t):
                    row_max(j, p, r, c, t, (0, 1))
                    if attends and r == 0 and j:
                        take_o(j - 1)
                    row_max(j, p, r, c, t, (2, 3))
                    if attends and r == 1 and j:
                        divide_o(j - 1)

                steps(dve, j, step)
            if attends:
                take_o(CHUNKS - 1)
                divide_o(CHUNKS - 1)
            if not finds:
                return
            need(dve, s["max"], GROUP * before(CHUNKS))
            dve.tensor_reduce(b.minus_top[:, :, :], b.tops[:, :, :, :].rearrange("p c i h -> p h i c"), AX.X, ALU.max, negate=True).then_inc(s["top"], 1)
            dve.wait_ge(s["top_t"], 1)
            dve.tensor_copy(b.rest[:, :], m.ps[:, MAX_BANK[0], 0:P]).then_inc(s["split_step"], 1)
            for n in range(MPARTS):
                dve.wait_ge(s["split_step"], 2 * n + 1)
                x = dve.tensor_copy(b.top_parts[:, n, :], b.rest[:, :])
                if n == MPARTS - 1:
                    x.then_inc(s["split"], 1)
                else:
                    x.then_inc(s["split_step"], 1)
                    dve.wait_ge(s["split_step"], 2 * n + 2)
                    dve.tensor_tensor(b.rest[:, :], b.rest[:, :], b.top_parts[:, n, :], ALU.subtract).then_inc(s["split_step"], 1)


def attention1_output(nc, m, a):
    with ExitStack() as ctx:
        def sb(name, shape, dt=F32):
            return ctx.enter_context(nc.sbuf_tensor(f"o1_{name}", shape, dt))

        wo = sb("wo", [P, KD, D])
        o = sb("o", [P, 2, TPC, D])
        ot = sb("ot", [P, 2, KD, CHUNK])
        gated = sb("gated", [P, 2, TPC, D])
        with stage(nc, "o1", "w_in", "o_in_even", "o_in_odd", "turned", "ot", "mm", "gated", "x") as (block, s):
            o_in = s["o_in_even"], s["o_in_odd"]

            @block.sync
            def _(sp):
                sp.dma_start(wo[:, :, :], a["WO"].rearrange("(k p) e -> p k e", p=P)).then_inc(s["w_in"], 16)

            @block.tensor
            def _(pe):
                credit(pe, s["turned"], s["mm"])
                pe.wait_ge(s["w_in"], 16)

                def turn(c, u):
                    pe.wait_ge(o_in[u], (c - u) * 8 + 16)
                    for k in range(KD):
                        need(pe, s["ot"], KD * (c - 1) + k + 1)
                        for j in range(TPC):
                            t = pe.transpose(m.ps[:, k, j * P:(j + 1) * P], o[:, u, j, k * P:(k + 1) * P], m.ident[:, :])
                        t.then_inc(s["turned"], 1)

                def products(c, u):
                    need(pe, s["ot"], KD * (c + 1))
                    for j in range(TPC):
                        need(pe, s["gated"], TPC * (c - 1) + j + 1)
                        for k in range(KD):
                            mm = pe.matmul(m.ps[:, 2 + j, 0:D], ot[:, u, k, j * P:(j + 1) * P], wo[:, k, :],
                                           start=(k == 0), stop=(k == KD - 1))
                        mm.then_inc(s["mm"], 1)

                ahead_in_pairs(pe, CHUNKS, turn, products)

            @block.scalar
            def _(act):
                credit(act, s["ot"])

                def load(c, u):
                    need(act, s["turned"], KD * (c - 1))
                    act.dma_start(o[:, u, :, :], m.o[bass.ts(c, CHUNK), :].rearrange("(t p) e -> p t e", p=P)).then_inc(o_in[u], 16)

                def take(c, u):
                    need(act, s["mm"], TPC * (c - 1))
                    for k in range(KD):
                        need(act, s["turned"], KD * c + k + 1)
                        act.copy(ot[:, u, k, :], m.ps[:, k, :]).then_inc(s["ot"], 1)

                ahead_in_pairs(act, CHUNKS, load, take)

            @block.vector
            def _(dve):
                credit(dve, s["gated"])

                def gate(c, u):
                    need(dve, s["x"], c - 1)
                    for j in range(TPC):
                        need(dve, s["mm"], TPC * c + j + 1)
                        dve.tensor_tensor(gated[:, u, j, :], m.ps[:, 2 + j, 0:D], m.modb[:, 2, :], ALU.mult).then_inc(s["gated"], 1)

                def halves(c):
                    for j in range(TPC):
                        t = bass.ts(c * TPC + j, 1)
                        dve.bn_stats(m.six[:, t, :], m.x[:, t, :])

                for u in range(2):
                    gate(u, u)
                with dve.Fori(1, CHUNKS // 2) as k:
                    for u in range(2):
                        gate(k * 2 + u, u)
                        halves(k * 2 + u - 2)
                need(dve, s["x"], CHUNKS)
                for u in range(2):
                    halves(CHUNKS - 2 + u)

            @block.gpsimd
            def _(pool):
                credit(pool, s["x"])

                def residual(c, u):
                    need(pool, s["gated"], TPC * (c + 1))
                    x = m.x[:, bass.ts(c, TPC), :]
                    pool.tensor_tensor(x, x, gated[:, u, :, :], ALU.add).then_inc(s["x"], 1)

                in_pairs(pool, CHUNKS, residual)



TE = TILES * EXPERTS
SLOT_TILES = TOPK // P


def expert_scores(nc, m, a):
    with ExitStack() as ctx:
        def sb(name, shape, dt=F32):
            return ctx.enter_context(nc.sbuf_tensor(f"es_{name}", shape, dt))

        SLOTS = 4

        gate = sb("gate", [P, KD, EXPERTS])
        h = sb("h", [P, SLOTS, TPC, D])
        ht = sb("ht", [P, 2, KD, CHUNK])
        top = sb("top", [P, TILES])
        total = sb("total", [P, TILES])
        with stage(nc, "es", "w_in", "normed", "scaled", "h", "h_out_0", "h_out_1", "h_out_2", "h_out_3", "turned", "ht", "mm", "scores", "top", "less", "exp", "total", "recip", "probs") as (block, s):
            h_out = [s[f"h_out_{u}"] for u in range(SLOTS)]
            probs = m.probs[:, :, :]

            @block.sync
            def _(sp):
                sp.dma_start(gate[:, :, :], a["L1_ffn_gate_w"].rearrange("(k p) e -> p k e", p=P)).then_inc(s["w_in"], 16)

            @block.vector
            def _(dve):
                credit(dve, s["normed"], s["scaled"])

                def norm(c, u):
                    need(dve, s["turned"], KD * (c - SLOTS + 1))
                    need(dve, h_out[u], (c - u) * (16 // SLOTS))
                    for j in range(TPC):
                        t = bass.ts(c * TPC + j, 1)
                        n = dve.tensor_scalar(h[:, u, j:j + 1, :], m.x[:, t, :], m.mean[:, t], m.rstd[:, t], ALU.subtract, ALU.mult)
                    n.then_inc(s["normed"], 1)
                    need(dve, s["normed"], c + 1)
                    dve.tensor_tensor(h[:, u, :, :], h[:, u, :, :], m.modb[:, 4:5, :].broadcast_to([P, TPC, D]), ALU.mult).then_inc(s["scaled"], 1)

                in_pairs(dve, CHUNKS, norm, SLOTS)
                need(dve, s["scores"], CHUNKS)
                dve.tensor_reduce(top[:, :], probs, AX.X, ALU.max).then_inc(s["top"], 1)
                dve.wait_ge(s["top"], 1)
                dve.tensor_tensor(probs, probs, top[:, :].unsqueeze(2).broadcast_to([P, TILES, EXPERTS]), ALU.subtract).then_inc(s["less"], 1)
                dve.wait_ge(s["exp"], 1)
                dve.tensor_reduce(total[:, :], probs, AX.X, ALU.add).then_inc(s["total"], 1)
                dve.wait_ge(s["total"], 1)
                dve.reciprocal(total[:, :], total[:, :]).then_inc(s["recip"], 1)
                dve.wait_ge(s["recip"], 1)
                dve.tensor_tensor(probs, probs, total[:, :].unsqueeze(2).broadcast_to([P, TILES, EXPERTS]), ALU.mult).then_inc(s["probs"], 1)

            @block.gpsimd
            def _(pool):
                credit(pool, s["h"])

                def shift(c, u):
                    need(pool, s["scaled"], c + 1)
                    pool.tensor_tensor(h[:, u, :, :], h[:, u, :, :], m.modb[:, 3:4, :].broadcast_to([P, TPC, D]), ALU.add).then_inc(s["h"], 1)

                in_pairs(pool, CHUNKS, shift, SLOTS)

            @block.tensor
            def _(pe):
                credit(pe, s["turned"], s["mm"])
                pe.wait_ge(s["w_in"], 16)

                def turn(c, u):
                    need(pe, s["h"], c + 1)
                    for k in range(KD):
                        need(pe, s["ht"], KD * (c - 1) + k + 1)
                        for j in range(TPC):
                            t = pe.transpose(m.ps[:, k, j * P:(j + 1) * P], h[:, u, j, k * P:(k + 1) * P], m.ident[:, :])
                        t.then_inc(s["turned"], 1)

                def products(c, u):
                    need(pe, s["ht"], KD * (c + 1))
                    need(pe, s["scores"], c - 1)
                    for j in range(TPC):
                        for k in range(KD):
                            mm = pe.matmul(m.ps[:, 2 + u % 2, j * EXPERTS:(j + 1) * EXPERTS], ht[:, u % 2, k, j * P:(j + 1) * P], gate[:, k, :],
                                           start=(k == 0), stop=(k == KD - 1))
                    mm.then_inc(s["mm"], 1)

                ahead_in_pairs(pe, CHUNKS, turn, products, SLOTS)

            @block.scalar
            def _(act):
                credit(act, s["ht"], s["scores"], *h_out)

                def take(c, u):
                    need(act, s["h"], c + 1)
                    act.dma_start(m.h[bass.ts(c, CHUNK), :].rearrange("(t p) d -> p t d", p=P), h[:, u, :, :]).then_inc(h_out[u], 16)
                    need(act, s["mm"], c - 1)
                    for k in range(KD):
                        need(act, s["turned"], KD * c + k + 1)
                        act.copy(ht[:, u % 2, k, :], m.ps[:, k, :]).then_inc(s["ht"], 1)

                def take_scores(c, u):
                    need(act, s["mm"], c + 1)
                    act.copy(m.probs[:, bass.ts(c, TPC), :],
                             m.ps[:, 2 + u % 2, 0:TPC * EXPERTS].rearrange("p (t e) -> p t e", e=EXPERTS)).then_inc(s["scores"], 1)

                ahead_in_pairs(act, CHUNKS, take, take_scores, SLOTS)
                for stored in h_out:
                    need(act, stored, 16 * CHUNKS // SLOTS)
                act.wait_ge(s["less"], 1)
                act.activation(probs, probs, ACT.Exp).then_inc(s["exp"], 1)


def choose_tokens(nc, m):
    BITS = 30
    DIGITS = 3
    CARRIED = 5
    WIDE = 8
    GROUPS_OF_TILES = TILES // WIDE
    with ExitStack() as ctx:
        def sb(name, shape, dt=F32):
            return ctx.enter_context(nc.sbuf_tensor(f"ct_{name}", shape, dt))

        bound = sb("bound", [P, EXPERTS], I32)
        trial = sb("trial", [P, DIGITS, EXPERTS], I32)
        digit = sb("digit", [P, DIGITS, EXPERTS], I32)
        enough = sb("enough", [P, DIGITS, EXPERTS], I32)
        kept = sb("kept", [P, DIGITS, EXPERTS], I32)
        trial_hits = sb("trial_hits", [P, DIGITS, EXPERTS, TILES])
        trial_count = sb("trial_count", [P, DIGITS, EXPERTS])
        by_expert = sb("by_expert", [P, EXPERTS, TILES])
        hits = sb("hits", [P, EXPERTS, TILES])
        equal = sb("equal", [P, EXPERTS, TILES])
        count = sb("count", [P, EXPERTS])
        wanted = sb("wanted", [P, EXPERTS])
        ones = sb("ones", [P, P])
        earlier = sb("earlier", [P, P])
        inclusive = sb("inclusive", [P, EXPERTS, TILES])
        rank = sb("rank", [P, EXPERTS, TILES])
        slot = sb("slot", [P, EXPERTS, TILES], I32)
        slot_tile = sb("slot_tile", [P, EXPERTS, TILES])
        piece = sb("piece", [P, EXPERTS, TILES], I32)
        tile = sb("tile", [P, TILES])
        row = sb("row", [P, 1])
        lane = sb("lane", [P, P])
        lane16 = sb("lane16", [P, P], BF16)
        slot_row16 = sb("slot_row16", [P, EXPERTS, TILES], BF16)
        hot = sb("hot", [P, TE, SLOT_TILES])
        part = sb("part", [P, 3, EXPERTS, TILES], BF16)
        carried = sb("carried", [P, EXPERTS, TILES, CARRIED, SLOT_TILES], BF16)
        row_hot = sb("row_hot", [P, 2, WIDE, P], BF16)
        found = sb("found", [P, EXPERTS, CARRIED, SLOT_TILES])
        with stage(nc, "ct", "consts", "zeroed", "dve", "trial", "count", "sum", "kept", "rank_in", "rank_mm", "hot", "carried", "row_hot", "gather", "taken") as (block, s):
            flat = lambda x: x[:, :, :].rearrange("p e t -> p (e t)")
            wide = lambda x: x.unsqueeze(2).broadcast_to([P, EXPERTS, TILES])
            PREFIX, TOTAL = 1, 2

            @block.gpsimd
            def _(pool):
                pool.memset(ones[:, :], 1.0)
                pool.memset(earlier[:, :], 1.0).then_inc(s["zeroed"], 1)
                pool.iota(tile[:, :], pattern=[[1, TILES]], base=0, channel_multiplier=0, allow_small_or_imprecise_dtypes=True)
                pool.iota(row[:, :], pattern=[[0, 1]], base=0, channel_multiplier=1, allow_small_or_imprecise_dtypes=True)
                pool.iota(lane[:, :], pattern=[[1, P]], base=0, channel_multiplier=0, allow_small_or_imprecise_dtypes=True)
                pool.wait_ge(s["zeroed"], 1)
                pool.affine_select(earlier[:, :], earlier[:, :], pattern=[[1, P]], compare_op=ALU.is_gt, fill=0.0, base=0,
                                   channel_multiplier=-1).then_inc(s["consts"], 1)
                pool.wait_ge(s["consts"], 1)
                pool.wait_ge(s["hot"], 1)
                hot4 = hot[:, :, :].rearrange("p (e t) s -> p e t s", e=EXPERTS)
                pool.tensor_tensor(carried[:, :, :, 0, :], hot4,
                                   tile[:, :].unsqueeze(1).unsqueeze(3).broadcast_to([P, EXPERTS, TILES, SLOT_TILES]), ALU.mult)
                pool.tensor_scalar(carried[:, :, :, 1, :], hot4, row[:, :], None, ALU.mult).then_inc(s["carried"], 1)

            @block.tensor
            def _(pe):
                pe.wait_ge(s["consts"], 1)
                with pe.Fori(0, BITS // 2) as i:
                    pe.wait_ge(s["count"], i + 1)
                    pe.matmul(m.ps[:, 0, 0:DIGITS * EXPERTS], ones[:, :], trial_count[:, :, :].rearrange("p n e -> p (n e)"),
                              start=True, stop=True).then_inc(s["sum"], 1)
                pe.wait_ge(s["count"], BITS // 2 + 1)
                pe.matmul(m.ps[:, 0, 0:EXPERTS], ones[:, :], count[:, :], start=True, stop=True).then_inc(s["sum"], 1)
                for n in range(2):
                    pe.wait_ge(s["rank_in"], n + 1)
                    src = flat(equal) if n == 0 else flat(hits)
                    pe.matmul(m.ps[:, PREFIX, 0:TE], earlier[:, :], src, start=True, stop=True)
                    pe.matmul(m.ps[:, TOTAL, 0:TE], ones[:, :], src, start=True, stop=True).then_inc(s["rank_mm"], 1)
                pe.wait_ge(s["carried"], 2)
                with pe.Fori(0, EXPERTS) as e:
                    for g in range(GROUPS_OF_TILES):
                        pe.wait_ge(s["row_hot"], e * GROUPS_OF_TILES + g + 1)
                        for j in range(WIDE):
                            t = g * WIDE + j
                            mm = pe.matmul(m.ps[:, 3, bass.ts(e, CARRIED * SLOT_TILES)], row_hot[:, g % 2, j, :],
                                           carried[:, bass.ts(e, 1), t, :, :].rearrange("p o i s -> p (o i s)"),
                                           start=(t == 0), stop=(t == TILES - 1), skip_group_check=True)
                        mm.then_inc(s["gather"], 1)

            @block.vector
            def _(dve):
                done = 0

                def chain(instruction):
                    nonlocal done
                    instruction.then_inc(s["dve"], 1)
                    done += 1
                    dve.wait_ge(s["dve"], done)

                dve.tensor_copy(by_expert[:, :, :], m.probs[:, :, :].rearrange("p t e -> p e t"))
                dve.memset(bound[:, :], 0)
                for n in range(DIGITS):
                    x = dve.memset(digit[:, n, :], (n + 1) << (BITS - 2))
                chain(x)
                with dve.Fori(0, BITS // 2) as i:
                    dve.tensor_tensor(trial[:, :, :], digit[:, :, :], bound[:, :].unsqueeze(1).broadcast_to([P, DIGITS, EXPERTS]),
                                      ALU.bitwise_or).then_inc(s["trial"], 1)
                    dve.tensor_copy(kept[:, :, :], bound[:, :].unsqueeze(1).broadcast_to([P, DIGITS, EXPERTS])).then_inc(s["kept"], 1)
                    dve.wait_ge(s["trial"], i * 4 + 1)
                    dve.tensor_tensor(trial_hits[:, :, :, :], by_expert[:, :, :].unsqueeze(1).broadcast_to([P, DIGITS, EXPERTS, TILES]),
                                      trial[:, :, :].bitcast(F32).unsqueeze(3).broadcast_to([P, DIGITS, EXPERTS, TILES]),
                                      ALU.is_ge).then_inc(s["trial"], 1)
                    dve.wait_ge(s["trial"], i * 4 + 2)
                    dve.tensor_reduce(trial_count[:, :, :], trial_hits[:, :, :, :], AX.X, ALU.add).then_inc(s["count"], 1)
                    dve.wait_ge(s["sum"], i + 1)
                    dve.tensor_scalar(enough[:, :, :].rearrange("p n e -> p (n e)"), m.ps[:, 0, 0:DIGITS * EXPERTS], float(TOPK), None,
                                      ALU.is_ge).then_inc(s["trial"], 1)
                    dve.wait_ge(s["trial"], i * 4 + 3)
                    dve.wait_ge(s["kept"], i * 3 + 1)
                    dve.tensor_scalar(digit[:, :, :], digit[:, :, :], 2, None, ALU.logical_shift_right).then_inc(s["trial"], 1)
                    dve.copy_predicated(kept[:, :, :], enough[:, :, :], trial[:, :, :]).then_inc(s["kept"], 1)
                    dve.wait_ge(s["trial"], i * 4 + 4)
                    dve.wait_ge(s["kept"], i * 3 + 2)
                    dve.tensor_reduce(bound[:, :].bitcast(F32), kept[:, :, :].bitcast(F32).rearrange("p n e -> p e n"), AX.X, ALU.max).then_inc(s["kept"], 1)
                    dve.wait_ge(s["kept"], i * 3 + 3)
                limit = wide(bound[:, :].bitcast(F32))
                dve.tensor_tensor(equal[:, :, :], by_expert[:, :, :], limit, ALU.is_equal).then_inc(s["rank_in"], 1)
                chain(dve.tensor_tensor(hits[:, :, :], by_expert[:, :, :], limit, ALU.is_gt))
                dve.tensor_reduce(count[:, :], hits[:, :, :], AX.X, ALU.add).then_inc(s["count"], 1)
                dve.wait_ge(s["sum"], BITS // 2 + 1)
                chain(dve.tensor_scalar(wanted[:, :], m.ps[:, 0, 0:EXPERTS], -1.0, float(TOPK), ALU.mult, ALU.add))

                def ranks(n):
                    dve.wait_ge(s["rank_mm"], n + 1)
                    for e in range(EXPERTS):
                        x = dve.tensor_tensor_scan(inclusive[:, e, :], ones[:, 0:TILES], m.ps[:, TOTAL, e * TILES:(e + 1) * TILES], 0.0,
                                                   ALU.mult, ALU.add)
                    chain(x)
                    chain(dve.tensor_tensor(flat(rank), flat(inclusive), m.ps[:, TOTAL, 0:TE], ALU.subtract))
                    chain(dve.tensor_tensor(flat(rank), flat(rank), m.ps[:, PREFIX, 0:TE], ALU.add))

                ranks(0)
                chain(dve.tensor_tensor(rank[:, :, :], rank[:, :, :], wide(wanted[:, :]), ALU.is_lt))
                chain(dve.tensor_tensor(equal[:, :, :], equal[:, :, :], rank[:, :, :], ALU.mult))
                dve.tensor_tensor(hits[:, :, :], hits[:, :, :], equal[:, :, :], ALU.add).then_inc(s["rank_in"], 1)
                ranks(1)
                chain(dve.tensor_copy(slot[:, :, :], rank[:, :, :]))
                chain(dve.tensor_scalar(piece[:, :, :], slot[:, :, :], P - 1, None, ALU.bitwise_and))
                dve.tensor_copy(slot_row16[:, :, :], piece[:, :, :])
                dve.tensor_copy(lane16[:, :], lane[:, :])
                chain(dve.tensor_scalar(slot[:, :, :], slot[:, :, :], 7, None, ALU.logical_shift_right))
                chain(dve.tensor_copy(slot_tile[:, :, :], slot[:, :, :]))
                chain(dve.scalar_tensor_tensor(slot_tile[:, :, :], slot_tile[:, :, :], 1.0, hits[:, :, :], ALU.add, ALU.mult))
                chain(dve.tensor_scalar(slot_tile[:, :, :], slot_tile[:, :, :], -1.0, None, ALU.add))
                lanes = lane[:, 0:SLOT_TILES].unsqueeze(1).broadcast_to([P, TE, SLOT_TILES])
                dve.tensor_tensor(hot[:, :, :], lanes, flat(slot_tile).unsqueeze(2).broadcast_to([P, TE, SLOT_TILES]),
                                  ALU.is_equal).then_inc(s["hot"], 1)
                dve.wait_ge(s["hot"], 1)
                hot4 = hot[:, :, :].rearrange("p (e t) s -> p e t s", e=EXPERTS)
                for n in range(3):
                    chain(dve.tensor_copy(part[:, n, :, :], by_expert[:, :, :]))
                    if n < 2:
                        dve.tensor_tensor(by_expert[:, :, :], by_expert[:, :, :], part[:, n, :, :], ALU.subtract).then_inc(s["dve"], 1)
                        done += 1
                    x = dve.tensor_tensor(carried[:, :, :, 2 + n, :], hot4,
                                          part[:, n, :, :].unsqueeze(3).broadcast_to([P, EXPERTS, TILES, SLOT_TILES]), ALU.mult)
                    if n < 2:
                        dve.wait_ge(s["dve"], done)
                x.then_inc(s["carried"], 1)
                lanes16 = lane16[:, :].unsqueeze(1).broadcast_to([P, WIDE, P])
                with dve.Fori(0, EXPERTS) as e:
                    for g in range(GROUPS_OF_TILES):
                        if g >= 2:
                            dve.wait_ge(s["gather"], e * GROUPS_OF_TILES + g - 1)
                        tiles = slice(g * WIDE, (g + 1) * WIDE)
                        dve.tensor_tensor(row_hot[:, g % 2, :, :], lanes16,
                                          slot_row16[:, bass.ts(e, 1), tiles].rearrange("p o t -> p (o t)").unsqueeze(2).broadcast_to([P, WIDE, P]),
                                          ALU.is_equal).then_inc(s["row_hot"], 1)
                    dve.wait_ge(s["gather"], e * GROUPS_OF_TILES + GROUPS_OF_TILES)
                chain(dve.tensor_copy(found[:, :, :, :].rearrange("p e i s -> p (e i s)"), m.ps[:, 3, 0:EXPERTS * CARRIED * SLOT_TILES]))
                dve.scalar_tensor_tensor(m.chosen[:, :, :], found[:, :, 0, :], float(P), found[:, :, 1, :], ALU.mult, ALU.add)
                chain(dve.tensor_tensor(m.gates[:, :, :], found[:, :, 2, :], found[:, :, 3, :], ALU.add))
                dve.tensor_tensor(m.gates[:, :, :], m.gates[:, :, :], found[:, :, 4, :], ALU.add).then_inc(s["taken"], 1)


def experts(nc, m, a):
    HALVES = TOPK // CHUNK
    FT = EHID // P
    SCALE = 64.0
    TERMS = (0, 0), (0, 1), (1, 0)
    with ExitStack() as ctx:
        def sb(name, shape, dt=F32):
            return ctx.enter_context(nc.sbuf_tensor(f"ex_{name}", shape, dt))

        w1_whole = sb("w1_whole", [P, KD * EHID])
        w2_whole = sb("w2_whole", [P, FT * D])
        w1 = sb("w1", [P, 2, 2, KD, EHID], F16)
        w2 = sb("w2", [P, 2, 2, FT, D], F16)
        which = sb("which", [P, 2, SLOT_TILES], U32)
        gate = sb("gate", [P, 2, SLOT_TILES])
        h = sb("h", [P, 2, SLOT_TILES, D])
        ht = sb("ht", [P, 2, 2, KD, CHUNK], F16)
        hid_whole = sb("hid_whole", [P, 2, CHUNK])
        hid = sb("hid", [P, 2, 2, FT, CHUNK], F16)
        y = sb("y", [P, 2, SLOT_TILES, D])
        zero = sb("zero", [P, TPC, D])
        with stage(nc, "ex", "zeroed", "cleared", "w_in", "w_high", "w_low", "which", "h_even", "h_odd", "turned", "ht_high", "ht", "up", "gelu",
                   "hid_high", "hid", "down", "y", "added", "summed", "issue") as (block, s):
            h_in = s["h_even"], s["h_odd"]

            def exists(e):
                return not isinstance(e, int) or e < EXPERTS

            def run(expert, loop):
                expert(0, 0)
                with loop(0, EXPERTS // 2 - 1) as k:
                    expert(k * 2 + 1, 1)
                    expert(k * 2 + 2, 0)
                expert(EXPERTS - 1, 1)

            @block.sync
            def _(sp):
                sp.wait_ge(s["zeroed"], 1)
                for c in range(CHUNKS):
                    sp.dma_start(m.mix[c * CHUNK:(c + 1) * CHUNK, :].rearrange("(t p) d -> p t d", p=P), zero[:, :, :]).then_inc(s["cleared"], 16)

            @block.scalar
            def _(act):
                credit(act, s["w_high"], s["ht_high"], s["gelu"], s["hid_high"])

                def load(e):
                    need(act, s["w_low"], 2 * e)
                    act.dma_start(w1_whole[:, :].rearrange("p (k f) -> p k f", k=KD),
                                  a["L1_ffn_w1"][bass.ts(e, 1)].rearrange("o (k p) f -> p (o k) f", p=P)).then_inc(s["w_in"], 16)
                    act.dma_start(w2_whole[:, :].rearrange("p (f d) -> p f d", f=FT),
                                  a["L1_ffn_w2"][bass.ts(e, 1)].rearrange("o (f p) d -> p (o f) d", p=P)).then_inc(s["w_in"], 16)

                def split(e, u):
                    act.wait_ge(s["w_in"], e * 32 + 32)
                    need(act, s["up"], HALVES * FT * (e - 1))
                    need(act, s["down"], SLOT_TILES * (e - 1))
                    for whole, to in ((w1_whole, w1), (w2_whole, w2)):
                        act.activation(to[:, u, 0, :, :].rearrange("p k f -> p (k f)"), whole[:, :], ACT.Copy, scale=SCALE).then_inc(s["w_high"], 1)

                def take(e, x):
                    n = e * HALVES + x
                    need(act, s["up"], FT * (n - 1))
                    for k in range(KD):
                        need(act, s["turned"], KD * n + k + 1)
                        act.copy(ht[:, x, 0, k, :], m.ps[:, k, :]).then_inc(s["ht_high"], 1)

                def gelu(e, x):
                    n = e * HALVES + x
                    need(act, s["down"], TPC * (n - 1))
                    for f in range(FT):
                        need(act, s["up"], FT * n + f + 1)
                        need(act, s["hid"], FT * n + f - 2 + 1)
                        act.activation(hid_whole[:, f % 2, :], m.ps[:, 2 + f % 2, :], ACT.Gelu_apprx_tanh, scale=1 / SCALE).then_inc(s["gelu"], 1)
                        need(act, s["gelu"], FT * n + f + 1)
                        act.copy(hid[:, x, 0, f, :], hid_whole[:, f % 2, :]).then_inc(s["hid_high"], 1)

                def expert(e, u):
                    take(e, 1)
                    if exists(e + 1):
                        load(e + 1)
                    gelu(e, 0)
                    if exists(e + 1):
                        split(e + 1, 1 - u)
                    gelu(e, 1)
                    if exists(e + 1):
                        take(e + 1, 0)

                load(0)
                split(0, 0)
                take(0, 0)
                run(expert, act.Fori)

            @block.gpsimd
            def _(pool):
                credit(pool, s["which"], s["summed"], s["issue"])
                pool.memset(zero[:, :, :], 0.0).then_inc(s["zeroed"], 1)

                def gather(e, u):
                    need(pool, s["turned"], KD * HALVES * (e - 1))
                    pool.tensor_copy(which[:, u, :].unsqueeze(1), m.chosen[:, bass.ts(e, 1), :])
                    pool.tensor_copy(gate[:, u, :].unsqueeze(1), m.gates[:, bass.ts(e, 1), :]).then_inc(s["which"], 1)
                    need(pool, s["which"], e + 1)
                    pool.sem_inc(s["issue"], 1)
                    for t in range(SLOT_TILES):
                        pool.indirect_dma_start(h[:, u, t, :], None, m.h, bass.IndirectOffsetOnAxis(which[:, u, t:t + 1], 0)).then_inc(h_in[u], 16)

                def add(e, u):
                    for t in range(SLOT_TILES):
                        need(pool, s["y"], SLOT_TILES * e + t + 1)
                        pool.sem_inc(s["issue"], 1)
                        pool.indirect_dma_start(m.mix, bass.IndirectOffsetOnAxis(which[:, u, t:t + 1], 0), y[:, u, t, :], None,
                                                compute_op=ALU.add).then_inc(s["added"], 16)

                gather(0, 0)
                pool.wait_ge(s["cleared"], 16 * CHUNKS)

                def expert(e, u):
                    if not isinstance(e, int) or e > 0:
                        pool.wait_ge(s["added"], 16 * SLOT_TILES * e)
                        pool.sem_inc(s["summed"], 1)
                    if exists(e + 1):
                        gather(e + 1, 1 - u)
                    add(e, u)

                run(expert, pool.Fori)
                pool.wait_ge(s["added"], 16 * SLOT_TILES * EXPERTS)

            @block.tensor
            def _(pe):
                credit(pe, s["turned"], s["up"], s["down"])

                def turn(e, u, x):
                    n = e * HALVES + x
                    if x == 0:
                        pe.wait_ge(h_in[u], (e - u) * 8 * SLOT_TILES + 16 * SLOT_TILES)
                    for k in range(KD):
                        need(pe, s["ht"], KD * (n - 1) + k + 1)
                        for j in range(TPC):
                            t = pe.transpose(m.ps[:, k, j * P:(j + 1) * P], h[:, u, x * TPC + j, k * P:(k + 1) * P], m.ident[:, :])
                        t.then_inc(s["turned"], 1)

                def up(e, u, x, between=None):
                    n = e * HALVES + x
                    need(pe, s["ht"], KD * (n + 1))
                    if x == 0:
                        need(pe, s["w_low"], 2 * e + 2)
                    terms = [(k, i, j) for k in range(KD) for i, j in TERMS]
                    for f in range(FT):
                        need(pe, s["gelu"], FT * n + f - 2 + 1)
                        for i, (k, p, q) in enumerate(terms):
                            mm = pe.matmul(m.ps[:, 2 + f % 2, :], w1[:, u, p, k, f * P:(f + 1) * P], ht[:, x, q, k, :],
                                           start=(i == 0), stop=(i == len(terms) - 1))
                        mm.then_inc(s["up"], 1)
                        if between and f % 2:
                            between(f // 2)

                def down(e, u, x, j):
                    n = e * HALVES + x
                    need(pe, s["hid"], FT * (n + 1))
                    terms = [(f, p, q) for f in range(FT) for p, q in TERMS]
                    need(pe, s["y"], TPC * n + j - 4 + 1)
                    for i, (f, p, q) in enumerate(terms):
                        mm = pe.matmul(m.ps[:, 4 + j, 0:D], hid[:, x, p, f, j * P:(j + 1) * P], w2[:, u, q, f, :],
                                       start=(i == 0), stop=(i == len(terms) - 1))
                    mm.then_inc(s["down"], 1)

                def expert(e, u):
                    turn(e, u, 1)
                    up(e, u, 0)
                    up(e, u, 1, lambda j: down(e, u, 0, j))
                    if exists(e + 1):
                        turn(e + 1, 1 - u, 0)
                    for j in range(TPC):
                        down(e, u, 1, j)

                turn(0, 0, 0)
                run(expert, pe.Fori)

            @block.vector
            def _(dve):
                credit(dve, s["w_low"], s["ht"], s["hid"], s["y"])

                def split(e, u):
                    for n, (whole, to) in enumerate(((w1_whole, w1), (w2_whole, w2))):
                        need(dve, s["w_high"], 2 * e + n + 1)
                        high, low = (to[:, u, i, :, :].rearrange("p k f -> p (k f)") for i in range(2))
                        dve.scalar_tensor_tensor(low, whole[:, :], SCALE, high, ALU.mult, ALU.subtract).then_inc(s["w_low"], 1)

                def take(e, x):
                    n = e * HALVES + x
                    for k in range(KD):
                        need(dve, s["ht_high"], KD * n + k + 1)
                        dve.tensor_tensor(ht[:, x, 1, k, :], m.ps[:, k, :], ht[:, x, 0, k, :], ALU.subtract).then_inc(s["ht"], 1)

                def low(e, x, between=None):
                    n = e * HALVES + x
                    for f in range(FT):
                        need(dve, s["hid_high"], FT * n + f + 1)
                        dve.tensor_tensor(hid[:, x, 1, f, :], hid_whole[:, f % 2, :], hid[:, x, 0, f, :], ALU.subtract).then_inc(s["hid"], 1)
                        if between and f % 2:
                            between(f // 2)

                def weigh(e, u, x, j):
                    t = x * TPC + j
                    need(dve, s["which"], e + 1)
                    need(dve, s["summed"], e - 1)
                    need(dve, s["down"], SLOT_TILES * e + t + 1)
                    dve.tensor_scalar(y[:, u, t, :], m.ps[:, 4 + j, 0:D], gate[:, u, t:t + 1], 1 / SCALE, ALU.mult, ALU.mult).then_inc(s["y"], 1)

                def expert(e, u):
                    take(e, 1)
                    low(e, 0)
                    if exists(e + 1):
                        split(e + 1, 1 - u)
                    low(e, 1, lambda j: weigh(e, u, 0, j))
                    if exists(e + 1):
                        take(e + 1, 0)
                    for j in range(TPC):
                        weigh(e, u, 1, j)

                split(0, 0)
                take(0, 0)
                run(expert, dve.Fori)


def mixture_output(nc, m, out):
    with ExitStack() as ctx:
        mix = ctx.enter_context(nc.sbuf_tensor("mo_mix", [P, TILES, D], F32))
        rounded = ctx.enter_context(nc.sbuf_tensor("mo_rounded", [P, 2, TPC, D], BF16))
        with stage(nc, "mo", *(f"in{c}" for c in range(CHUNKS)), "rounded", "gated", "x", "out") as (block, s):
            mix_in = [s[f"in{c}"] for c in range(CHUNKS)]

            @block.sync
            def _(sp):
                for c in range(CHUNKS):
                    rows = slice(c * CHUNK, (c + 1) * CHUNK)
                    sp.dma_start(mix[:, c * TPC:(c + 1) * TPC, :], m.mix[rows, :].rearrange("(t p) d -> p t d", p=P)).then_inc(mix_in[c], 16)
                for c in range(CHUNKS):
                    rows = slice(c * CHUNK, (c + 1) * CHUNK)
                    sp.wait_ge(s["x"], c + 1)
                    sp.dma_start(out[rows, :].rearrange("(t p) d -> p t d", p=P), m.x[:, c * TPC:(c + 1) * TPC, :]).then_inc(s["out"], 16)
                sp.wait_ge(s["out"], 16 * CHUNKS)

            @block.vector
            def _(dve):
                for c in range(CHUNKS):
                    tiles = slice(c * TPC, (c + 1) * TPC)
                    dve.wait_ge(mix_in[c], 16)
                    if c >= 2:
                        dve.wait_ge(s["gated"], c - 1)
                    dve.tensor_copy(rounded[:, c % 2, :, :], mix[:, tiles, :]).then_inc(s["rounded"], 1)
                    dve.wait_ge(s["rounded"], c + 1)
                    dve.tensor_tensor(mix[:, tiles, :], rounded[:, c % 2, :, :], m.modb[:, 5:6, :].broadcast_to([P, TPC, D]), ALU.mult).then_inc(s["gated"], 1)

            @block.gpsimd
            def _(pool):
                for c in range(CHUNKS):
                    tiles = slice(c * TPC, (c + 1) * TPC)
                    pool.wait_ge(s["gated"], c + 1)
                    pool.tensor_tensor(m.x[:, tiles, :], m.x[:, tiles, :], mix[:, tiles, :], ALU.add).then_inc(s["x"], 1)



def rotary_table():
    f = np.float32
    half_idx = np.arange(0, DH, 2, dtype=f)
    inv_freq = f(1.0) / f(10000.0) ** (half_idx / f(DH))
    t = np.arange(N, dtype=f)
    freqs = t[:, None] * inv_freq[None, :]
    base = (half_idx + f(0.4 * DH)) / f(1.4 * DH)
    power = (t - f(N // 2)) / f(WINDOW // 2)
    scale = base[None, :] ** power[:, None]
    cos, sin = np.cos(freqs), np.sin(freqs)
    return np.stack([cos * scale, cos / scale, sin * scale, sin / scale], axis=1).astype(f)


def rope_table():
    f = np.float32
    k = np.arange(L1_DH // 2, dtype=f)
    inv_freq = f(10000.0) ** (f(-2.0) * k / f(L1_DH))
    angle = np.arange(N, dtype=f)[:, None] * inv_freq
    cos, sin = np.cos(angle).T, np.sin(angle).T
    heads = P // L1_DH
    rows = [np.repeat(half, heads, axis=0) for half in (cos, cos, sin, -sin)]
    return np.stack([np.concatenate(rows[:2]), np.concatenate(rows[2:])], axis=1).astype(f)


def layout(inputs):
    a = dict(inputs)
    a["x"] = np.asarray(a.pop("L0_attn_X")).reshape(N, D)
    a["rotary"], a["rope"] = rotary_table(), rope_table()
    halves = np.arange(D).reshape(D // P, P // L1_DH, L1_DH // 2, 2).transpose(0, 3, 2, 1).reshape(D)
    for n in "QK":
        a[f"W{n}"] = np.asarray(a.pop(f"L1_attn_W_{n}"))[halves].T
    for n in "VO":
        a[f"W{n}"] = np.asarray(a.pop(f"L1_attn_W_{n}")).T
    a = {n: np.ascontiguousarray(v) for n, v in a.items()}
    return a



def load_x(nc, m, x, name):
    with stage(nc, name, "x_in", "zeroed", "ident", "ident16") as (block, s):

        @block.sync
        def _(sp):
            for h in range(4):
                t = TILES // 4
                sp.dma_start(m.x[:, h * t:(h + 1) * t, :],
                             x[h * t * P:(h + 1) * t * P, :].rearrange("(t p) d -> p t d", p=P)).then_inc(s["x_in"], 16)
            sp.wait_ge(s["x_in"], 64)

        @block.gpsimd
        def _(pool):
            pool.memset(m.minus_half[:, :], -0.5)
            pool.memset(m.ident[:, :], 0.0).then_inc(s["zeroed"], 1)
            pool.wait_ge(s["zeroed"], 1)
            pool.affine_select(m.ident[:, :], m.ident[:, :], pattern=[[-1, P]], compare_op=ALU.not_equal, fill=1.0,
                               base=0, channel_multiplier=1).then_inc(s["ident"], 1)
            pool.wait_ge(s["ident"], 1)
            pool.tensor_copy(m.ident16[:, :], m.ident[:, :]).then_inc(s["ident16"], 1)


def program(nc, a, out):
    m = Memory()
    with ExitStack() as ctx:
        def sb(name, shape, dt=F32):
            return ctx.enter_context(nc.sbuf_tensor(name, shape, dt))

        m.ps = ctx.enter_context(nc.psum_tensor("ps", [P, 8, 512], F32))
        m.x = sb("x", [P, TILES, D])
        m.ident = sb("ident", [P, P])
        m.ident16 = sb("ident16", [P, P], F16)
        m.minus_half = sb("minus_half", [P, TILES])
        m.modb = sb("modb", [P, 6, D])
        m.modc = sb("modc", [P, 6 * KD])
        m.mean = sb("mean", [P, TILES])
        m.rstd = sb("rstd", [P, TILES])
        m.six = sb("six", [P, TILES, 6])

        load_x(nc, m, a["x"], "load")
        modulation_and_statistics(nc, m, "m0", a["L0_c"], a["L0_wmod"])
        with ExitStack() as scope:
            m.qt = scope.enter_context(nc.sbuf_tensor("a0_qt", [P, KD, 2, N], F16))
            m.kt = scope.enter_context(nc.sbuf_tensor("a0_kt", [P, KD, 2, N], F16))
            m.v = scope.enter_context(nc.sbuf_tensor("a0_v", [P, TILES, 2, D], F16))
            attention0_projections(nc, m, {k: a["L0_attn_" + k] for k in ("Wq", "Wk", "Wv", "bq", "bk", "bv")})
            attention0(nc, m)

        with ExitStack() as scope:
            def sc(name, shape):
                return scope.enter_context(nc.sbuf_tensor(name, shape, F32))

            m.y = sc("y", [P, TILES, D])
            m.y_six = sc("y_six", [P, 2, TILES, 6])
            m.next = sc("next", [P, 2, TILES])
            m.wqkv = sc("wqkv", [P, KD, 3 * INNER])
            m.wo = sc("wo", [P, INNER // P, D])
            m.table = sc("table", [P, TILES, 4, HALF])
            m.gain = sc("gain", [P, 2, 2, HALF])
            m.mask = sc("mask", [P, 3, 2, P])
            m.first = sc("first", [P, 1])
            f = {k: a["L0_ffn_" + k] for k in ("wqkv", "q_scale", "k_scale", "wo", "ln_g", "ln_b", "w1", "b1", "w2", "b2")}
            f["rotary"] = a["rotary"]
            norm_statistics(nc, m, "n1")
            transformer_input(nc, m, f)
            with nc.Fori(0, DEPTH) as layer:
                local_attention(nc, m)
                gated_mlp_layer(nc, m, f, layer)
            transformer_output(nc, m)

        m.qk = nc.dram_tensor("qk_parts", [2, 2, D, N], F16).ap()
        m.tops = nc.dram_tensor("top_parts", [MPARTS, GROUP, N], F16).ap()
        m.o = nc.dram_tensor("heads_out", [N, D], F32).ap()
        with ExitStack() as scope:
            b = attention1_buffers(nc, scope)
            modulation_and_statistics(nc, m, "m1", a["L1_c"], a["L1_wmod"], lambda pool, done: attention1_constants(pool, b, done))
            m.v17 = scope.enter_context(nc.sbuf_tensor("v17", [P, TILES, L1_HEADS, L1_DH + 1], F32))
            attention1_projections(nc, m, a)
            attention1(nc, m, b)
        attention1_output(nc, m, a)

        m.h = nc.dram_tensor("expert_in", [N, D], F32).ap()
        m.mix = nc.dram_tensor("expert_out", [N, D], F32).ap()
        m.probs = sb("probs", [P, TILES, EXPERTS])
        m.chosen = sb("chosen", [P, EXPERTS, SLOT_TILES], U32)
        m.gates = sb("gates", [P, EXPERTS, SLOT_TILES])
        norm_statistics(nc, m, "n3")
        expert_scores(nc, m, a)
        choose_tokens(nc, m)
        experts(nc, m, a)
        mixture_output(nc, m, out)


def kernel(**inputs):
    import concourse.bacc as bacc
    from concourse.bass_utils import run_bass_kernel_spmd

    nc = bacc.Bacc("TRN2", target_bir_lowering=False, num_devices=1)
    arrays, a = {}, {}
    for name, array in layout(inputs).items():
        arrays[f"in_{name}_dram"] = array
        a[name] = nc.dram_tensor(f"in_{name}_dram", array.shape, mybir.dt.from_np(array.dtype), kind="ExternalInput").ap()
    out = nc.dram_tensor("out_dram", (N, D), F32, kind="ExternalOutput").ap()
    program(nc, a, out)
    result = run_bass_kernel_spmd(nc, [arrays], core_ids=[0])
    return result.results[0]["out_dram"].reshape(1, N, D)
```
